# Optimizing a Trainium2 kernel written in Bass

```python
import numpy as np
import jax
import jax.numpy as jnp

def _softmax(x, axis=-1):
    return jax.nn.softmax(x, axis=axis)

def _gelu(x):
    return jax.nn.gelu(x, approximate=True)

def _silu(x):
    return jax.nn.silu(x)

def _sigmoid(x):
    return jax.nn.sigmoid(x)

def _layernorm(x, axis=-1, eps=1e-05):
    m = jnp.mean(x, axis=axis, keepdims=True)
    v = jnp.var(x, axis=axis, keepdims=True)
    return (x - m) / jnp.sqrt(v + eps)

def _scatter_add(tgt, idx, src, axis=0):
    return tgt.at[idx].add(src)

def _segment_sum(src, seg, n):
    return jax.ops.segment_sum(src, seg, n)
kernel_name = 'mk_adaln_d4_jaxref_r8_932501'

def setup_inputs(seed: int=0):
    np.random.seed(seed)
    _w = jnp.asarray

    def _L0_attn_setup():
        import jax, jax.numpy as jnp
        import numpy as np
        NEG_BIG = -1e+38

        def _wkv_scan(w, u, k, v, aa0, bb0, pp0):
            kT = jnp.moveaxis(k, 1, 0)
            vT = jnp.moveaxis(v, 1, 0)

            def step(carry, kv):
                aa, bb, pp = carry
                kt, vt = kv
                ww = u + kt
                p = jnp.maximum(pp, ww)
                e1 = jnp.exp(pp - p)
                e2 = jnp.exp(ww - p)
                y = (e1 * aa + e2 * vt) / (e1 * bb + e2)
                ww2 = pp + w
                p2 = jnp.maximum(ww2, kt)
                e1 = jnp.exp(ww2 - p2)
                e2 = jnp.exp(kt - p2)
                return ((e1 * aa + e2 * vt, e1 * bb + e2, p2), y)
            (aa, bb, pp), yT = jax.lax.scan(step, (aa0, bb0, pp0), (kT, vT))
            return (jnp.moveaxis(yT, 0, 1), aa, bb, pp)

        def _reference_tuple_inner(x, W_rvk, W_out, time_decay, time_first):
            B, T, C = x.shape
            rvk = jnp.einsum('btc,dc->btd', x, W_rvk)
            r, v, k = jnp.split(rvk, 3, axis=-1)
            w = -jnp.exp(time_decay)
            u = time_first
            aa0 = jnp.zeros((B, C), dtype=x.dtype)
            bb0 = jnp.zeros((B, C), dtype=x.dtype)
            pp0 = jnp.full((B, C), NEG_BIG, dtype=x.dtype)
            wkv, aa, bb, pp = _wkv_scan(w, u, k, v, aa0, bb0, pp0)
            rwkv = jax.nn.sigmoid(r) * wkv
            out = jnp.einsum('btc,dc->btd', rwkv, W_out)
            h = aa
            c = jnp.stack([bb, pp], axis=-1).reshape(B, 2 * C)
            return (out, h, c)
        key = jax.random.key(seed)
        k1, k2, k3 = jax.random.split(key, 3)
        B, T, C = (32, 128, 128)
        x = jax.random.normal(k1, (B, T, C), dtype=jnp.float32)
        W_rvk = jax.random.normal(k2, (3 * C, C), dtype=jnp.float32) * (1.0 / np.sqrt(C))
        W_out = jax.random.normal(k3, (C, C), dtype=jnp.float32) * (1.0 / np.sqrt(C))
        time_decay = jnp.ones((C,), dtype=jnp.float32)
        time_first = jnp.ones((C,), dtype=jnp.float32)
        return {'x': x, 'W_rvk': W_rvk, 'W_out': W_out, 'time_decay': time_decay, 'time_first': time_first}
    _L0_attn_in = _L0_attn_setup()

    def _L0_ffn_setup():
        import jax, jax.numpy as jnp
        import numpy as np
        D_MODEL = 128
        M = 64
        INNER = 16
        key = jax.random.key(seed)
        ks = jax.random.split(key, 9)

        def init(k, shape, fan_in):
            bound = 1.0 / np.sqrt(fan_in)
            return jax.random.uniform(k, shape, jnp.float32, -bound, bound)
        x = jax.random.normal(ks[0], (16, 512, D_MODEL), dtype=jnp.float32)
        Win = init(ks[1], (D_MODEL, M), D_MODEL)
        bin_ = init(ks[2], (M,), D_MODEL)
        W1 = init(ks[3], (M, INNER), 1)
        b1 = init(ks[4], (M, INNER), 1)
        W2 = init(ks[5], (M, INNER), INNER)
        b2 = init(ks[6], (M,), INNER)
        Wout = init(ks[7], (M, D_MODEL), M)
        bout = init(ks[8], (D_MODEL,), M)
        return {'x': x, 'Win': Win, 'bin_': bin_, 'W1': W1, 'b1': b1, 'W2': W2, 'b2': b2, 'Wout': Wout, 'bout': bout}
    _L0_ffn_in = _L0_ffn_setup()
    _L0_c = _w((lambda *s: np.random.randn(*s).astype(np.float32) * 0.05)(8, 128))
    _L0_wmod = _w((lambda *s: np.random.randn(*s).astype(np.float32) * 0.05)(128, 6 * 128) * 128 ** (-0.5))

    def _L1_attn_setup():
        import jax, jax.numpy as jnp
        import numpy as np
        B, N, E = (2, 256, 128)
        H = 16
        BM = 32
        BN = 32
        BUDGET = 0.2

        def _forward(x, W_Q, W_K, W_V, W_O):
            Bx, Nx, Ex = x.shape
            D = Ex // H
            Tr, Tc = (Nx // BM, Nx // BN)
            k = max(1, int(BUDGET * Tc))

            def heads(t):
                return t.reshape(Bx, Nx, H, D).transpose(0, 2, 1, 3)
            Q = heads(x @ W_Q)
            K = heads(x @ W_K)
            V = heads(x @ W_V)
            Qp = Q.reshape(Bx, H, Tr, BM, D).mean(axis=3)
            Kp = K.reshape(Bx, H, Tc, BN, D).mean(axis=3)
            avg_sc = jnp.einsum('bhid,bhjd->bhij', Qp, Kp).mean(axis=(0, 1))
            _, idx = jax.lax.top_k(avg_sc, k)
            Kb = K.reshape(Bx, H, Tc, BN, D)
            Vb = V.reshape(Bx, H, Tc, BN, D)
            Ksel = Kb[:, :, idx]
            Vsel = Vb[:, :, idx]
            Qb = Q.reshape(Bx, H, Tr, BM, D)
            scale = 1.0 / jnp.sqrt(jnp.asarray(D, jnp.float32))
            logits = jnp.einsum('bhtqd,bhtknd->bhtqkn', Qb, Ksel).reshape(Bx, H, Tr, BM, k * BN) * scale
            P = jax.nn.softmax(logits, axis=-1)
            Ob = jnp.einsum('bhtqs,bhtsd->bhtqd', P, Vsel.reshape(Bx, H, Tr, k * BN, D))
            O = Ob.reshape(Bx, H, Nx, D).transpose(0, 2, 1, 3).reshape(Bx, Nx, Ex)
            return O @ W_O
        key = jax.random.key(seed)
        ks = jax.random.split(key, 5)
        w = lambda k: jax.random.normal(k, (E, E), jnp.float32) * 0.02
        return {'x': jax.random.normal(ks[0], (B, N, E), jnp.float32), 'W_Q': w(ks[1]), 'W_K': w(ks[2]), 'W_V': w(ks[3]), 'W_O': w(ks[4])}
    _L1_attn_in = _L1_attn_setup()

    def _L1_ffn_setup():
        import jax, jax.numpy as jnp
        import numpy as np
        TOP_K = 2
        CAP_FACTOR = 1.25
        MIN_CAPACITY = 4
        key = jax.random.key(seed)
        k1, k2, k3, k4 = jax.random.split(key, 4)
        B, T, C, E = (8, 256, 128, 8)
        x = jax.random.normal(k1, (B, T, C), dtype=jnp.float32)
        w_g = jax.random.normal(k2, (E, C), dtype=jnp.float32) * 0.02
        c_fc = jax.random.normal(k3, (E, C, 4 * C), dtype=jnp.float32) * 0.02
        c_proj = jax.random.normal(k4, (E, 4 * C, C), dtype=jnp.float32) * 0.02
        return {'x': x, 'w_g': w_g, 'c_fc': c_fc, 'c_proj': c_proj}
    _L1_ffn_in = _L1_ffn_setup()
    _L1_c = _w((lambda *s: np.random.randn(*s).astype(np.float32) * 0.05)(8, 128))
    _L1_wmod = _w((lambda *s: np.random.randn(*s).astype(np.float32) * 0.05)(128, 6 * 128) * 128 ** (-0.5))

    def _L2_attn_setup():
        import jax, jax.numpy as jnp
        import numpy as np
        B, L, DIM, H, D = (4, 128, 128, 8, 32)
        key = jax.random.key(seed)
        ks = jax.random.split(key, 8)
        s = 0.02
        return dict(x=jax.random.normal(ks[0], (B, L, DIM), jnp.float32), W_in=jax.random.normal(ks[1], (DIM, DIM), jnp.float32) * s, b_in=jnp.zeros((DIM,), jnp.float32), W_qkva=jax.random.normal(ks[2], (H * D * 8, DIM), jnp.float32) * s, b_qkva=jnp.zeros((H * D * 8,), jnp.float32), W_y=jax.random.normal(ks[3], (DIM, H * D * 2), jnp.float32) * s, b_y=jnp.zeros((DIM,), jnp.float32), W_out=jax.random.normal(ks[4], (DIM, DIM), jnp.float32) * s, b_out=jnp.zeros((DIM,), jnp.float32), h0_re=jax.random.normal(ks[5], (H, D, D), jnp.float32), h0_im=jax.random.normal(ks[6], (H, D, D), jnp.float32))
    _L2_attn_in = _L2_attn_setup()

    def _L2_ffn_setup():
        import jax, jax.numpy as jnp
        import numpy as np
        D_MODEL = 128
        HIDDEN = 512
        N_ROUTING = 2
        key = jax.random.key(seed)
        ks = jax.random.split(key, 10)
        s = 0.02
        x = jax.random.normal(ks[0], (4, 512, D_MODEL), dtype=jnp.float32)
        gate_w = jax.random.normal(ks[1], (N_ROUTING, D_MODEL), dtype=jnp.float32) * s
        w1 = jax.random.normal(ks[2], (N_ROUTING, D_MODEL, HIDDEN), dtype=jnp.float32) * s
        b1 = jax.random.normal(ks[3], (N_ROUTING, HIDDEN), dtype=jnp.float32) * s
        w2 = jax.random.normal(ks[4], (N_ROUTING, HIDDEN, D_MODEL), dtype=jnp.float32) * s
        b2 = jax.random.normal(ks[5], (N_ROUTING, D_MODEL), dtype=jnp.float32) * s
        sw1 = jax.random.normal(ks[6], (D_MODEL, HIDDEN), dtype=jnp.float32) * s
        sb1 = jax.random.normal(ks[7], (HIDDEN,), dtype=jnp.float32) * s
        sw2 = jax.random.normal(ks[8], (HIDDEN, D_MODEL), dtype=jnp.float32) * s
        sb2 = jax.random.normal(ks[9], (D_MODEL,), dtype=jnp.float32) * s
        return {'x': x, 'gate_w': gate_w, 'w1': w1, 'b1': b1, 'w2': w2, 'b2': b2, 'sw1': sw1, 'sb1': sb1, 'sw2': sw2, 'sb2': sb2}
    _L2_ffn_in = _L2_ffn_setup()
    _L2_c = _w((lambda *s: np.random.randn(*s).astype(np.float32) * 0.05)(8, 128))
    _L2_wmod = _w((lambda *s: np.random.randn(*s).astype(np.float32) * 0.05)(128, 6 * 128) * 128 ** (-0.5))

    def _L3_attn_setup():
        import jax, jax.numpy as jnp
        import numpy as np
        B, T, D = (2, 256, 128)
        H = 8
        KD = 128
        VD = 32
        KEY_DIM = H * KD
        VAL_DIM = H * VD
        KS = 4
        EPS_NORM = 1e-06
        EPS_RMS = 1e-05

        def _xavier(key, shape):
            fan_in, fan_out = (shape[0], shape[1])
            lim = np.sqrt(6.0 / (fan_in + fan_out))
            return jax.random.uniform(key, shape, jnp.float32, -lim, lim)

        def _causal_dw_conv_silu(x, w):
            C = x.shape[-1]
            y = jax.lax.conv_general_dilated(jnp.swapaxes(x, 1, 2), w[:, None, :], window_strides=(1,), padding=[(KS - 1, 0)], feature_group_count=C)
            return jax.nn.silu(jnp.swapaxes(y, 1, 2))

        def _l2norm(x):
            n = jnp.sqrt(jnp.sum(x * x, axis=-1, keepdims=True))
            return x / jnp.maximum(n, EPS_NORM)

        def _gdn_forward(x, Wq, Wk, Wv, Wa, Wb, Wg, Wo, A_log, dt_bias, conv_q, conv_k, conv_v, o_norm_w):
            bsz, seq_len, _ = x.shape
            beta = jax.nn.sigmoid(x @ Wb) * 2.0
            g = -jnp.exp(A_log)[None, None, :] * jax.nn.softplus(x @ Wa + dt_bias[None, None, :])
            alpha = jnp.exp(g)
            q = _causal_dw_conv_silu(x @ Wq, conv_q).reshape(bsz, seq_len, H, KD)
            k = _causal_dw_conv_silu(x @ Wk, conv_k).reshape(bsz, seq_len, H, KD)
            v = _causal_dw_conv_silu(x @ Wv, conv_v).reshape(bsz, seq_len, H, VD)
            q = _l2norm(q)
            k = _l2norm(k)
            qT = jnp.swapaxes(q, 0, 1)
            kT = jnp.swapaxes(k, 0, 1)
            vT = jnp.swapaxes(v, 0, 1)
            aT = jnp.swapaxes(alpha, 0, 1)
            bT = jnp.swapaxes(beta, 0, 1)

            def step(state, inp):
                q_t, k_t, v_t, a_t, b_t = inp
                retained = jnp.einsum('bhvk,bhk->bhv', state, k_t)
                a4 = a_t[..., None, None]
                b4 = b_t[..., None, None]
                rk = retained[..., None] * k_t[:, :, None, :]
                vk = v_t[..., None] * k_t[:, :, None, :]
                state = a4 * (state - b4 * rk) + b4 * vk
                o_t = jnp.einsum('bhvk,bhk->bhv', state, q_t)
                return (state, o_t)
            state0 = jnp.zeros((bsz, H, VD, KD), jnp.float32)
            _, outT = jax.lax.scan(step, state0, (qT, kT, vT, aT, bT))
            out = jnp.swapaxes(outT, 0, 1)
            gate = (x @ Wg).reshape(bsz, seq_len, H, VD)
            rms = jax.lax.rsqrt(jnp.mean(out * out, axis=-1, keepdims=True) + EPS_RMS)
            out = out * rms * o_norm_w * jax.nn.silu(gate)
            out = out.reshape(bsz, seq_len, VAL_DIM)
            return out @ Wo
        key = jax.random.key(seed)
        ks = jax.random.split(key, 16)
        x = jax.random.normal(ks[0], (B, T, D), jnp.float32)
        Wq = _xavier(ks[1], (D, KEY_DIM))
        Wk = _xavier(ks[2], (D, KEY_DIM))
        Wv = _xavier(ks[3], (D, VAL_DIM))
        Wa = _xavier(ks[4], (D, H))
        Wb = _xavier(ks[5], (D, H))
        Wg = _xavier(ks[6], (D, VAL_DIM))
        Wo = _xavier(ks[7], (VAL_DIM, D))
        A_log = jnp.log(jax.random.uniform(ks[8], (H,), jnp.float32, 0.5, 16.0))
        dt = jnp.exp(jax.random.uniform(ks[9], (H,), jnp.float32, np.log(0.001), np.log(0.1)))
        dt = jnp.clip(dt, 0.0001, None)
        dt_bias = dt + jnp.log(-jnp.expm1(-dt))

        def conv_w(k, c):
            lim = np.sqrt(6.0 / (1 + KS))
            return jax.random.uniform(k, (c, KS), jnp.float32, -lim, lim)
        conv_q = conv_w(ks[10], KEY_DIM)
        conv_k = conv_w(ks[11], KEY_DIM)
        conv_v = conv_w(ks[12], VAL_DIM)
        o_norm_w = jnp.ones((VD,), jnp.float32)
        return dict(x=x, Wq=Wq, Wk=Wk, Wv=Wv, Wa=Wa, Wb=Wb, Wg=Wg, Wo=Wo, A_log=A_log, dt_bias=dt_bias, conv_q=conv_q, conv_k=conv_k, conv_v=conv_v, o_norm_w=o_norm_w)
    _L3_attn_in = _L3_attn_setup()

    def _L3_ffn_setup():
        import jax, jax.numpy as jnp
        import numpy as np
        DIM = 128

        def _reference_tuple_inner(x, W_r, W_k, W_v, mu_r, mu_k):
            B, T, C = x.shape
            x_prev = jnp.concatenate([jnp.zeros((B, 1, C), x.dtype), x[:, :-1, :]], axis=1)
            xr = mu_r * x + (1.0 - mu_r) * x_prev
            xk = mu_k * x + (1.0 - mu_k) * x_prev
            r = jax.nn.sigmoid(jnp.einsum('btc,dc->btd', xr, W_r))
            k = jnp.einsum('btc,dc->btd', xk, W_k)
            k_act = jnp.square(jax.nn.relu(k))
            out = r * jnp.einsum('btc,dc->btd', k_act, W_v)
            new_state = x[:, -1, :]
            return (out, new_state)
        key = jax.random.key(seed)
        ks = jax.random.split(key, 6)
        B, T, C = (8, 256, DIM)
        x = jax.random.normal(ks[0], (B, T, C), dtype=jnp.float32)
        s = 1.0 / np.sqrt(C)
        W_r = jax.random.uniform(ks[1], (C, C), jnp.float32, -s, s)
        W_k = jax.random.uniform(ks[2], (C, C), jnp.float32, -s, s)
        W_v = jax.random.uniform(ks[3], (C, C), jnp.float32, -s, s)
        mu_r = jax.random.uniform(ks[4], (C,), jnp.float32)
        mu_k = jax.random.uniform(ks[5], (C,), jnp.float32)
        return {'x': x, 'W_r': W_r, 'W_k': W_k, 'W_v': W_v, 'mu_r': mu_r, 'mu_k': mu_k}
    _L3_ffn_in = _L3_ffn_setup()
    _L3_c = _w((lambda *s: np.random.randn(*s).astype(np.float32) * 0.05)(8, 128))
    _L3_wmod = _w((lambda *s: np.random.randn(*s).astype(np.float32) * 0.05)(128, 6 * 128) * 128 ** (-0.5))
    _d = {'L0_attn_x': _L0_attn_in['x'], 'L0_attn_W_rvk': _L0_attn_in['W_rvk'], 'L0_attn_W_out': _L0_attn_in['W_out'], 'L0_attn_time_decay': _L0_attn_in['time_decay'], 'L0_attn_time_first': _L0_attn_in['time_first'], 'L0_ffn_Win': _L0_ffn_in['Win'], 'L0_ffn_bin_': _L0_ffn_in['bin_'], 'L0_ffn_W1': _L0_ffn_in['W1'], 'L0_ffn_b1': _L0_ffn_in['b1'], 'L0_ffn_W2': _L0_ffn_in['W2'], 'L0_ffn_b2': _L0_ffn_in['b2'], 'L0_ffn_Wout': _L0_ffn_in['Wout'], 'L0_ffn_bout': _L0_ffn_in['bout'], 'L0_c': _L0_c, 'L0_wmod': _L0_wmod, 'L1_attn_W_Q': _L1_attn_in['W_Q'], 'L1_attn_W_K': _L1_attn_in['W_K'], 'L1_attn_W_V': _L1_attn_in['W_V'], 'L1_attn_W_O': _L1_attn_in['W_O'], 'L1_ffn_w_g': _L1_ffn_in['w_g'], 'L1_ffn_c_fc': _L1_ffn_in['c_fc'], 'L1_ffn_c_proj': _L1_ffn_in['c_proj'], 'L1_c': _L1_c, 'L1_wmod': _L1_wmod, 'L2_attn_W_in': _L2_attn_in['W_in'], 'L2_attn_b_in': _L2_attn_in['b_in'], 'L2_attn_W_qkva': _L2_attn_in['W_qkva'], 'L2_attn_b_qkva': _L2_attn_in['b_qkva'], 'L2_attn_W_y': _L2_attn_in['W_y'], 'L2_attn_b_y': _L2_attn_in['b_y'], 'L2_attn_W_out': _L2_attn_in['W_out'], 'L2_attn_b_out': _L2_attn_in['b_out'], 'L2_attn_h0_re': _L2_attn_in['h0_re'], 'L2_attn_h0_im': _L2_attn_in['h0_im'], 'L2_ffn_gate_w': _L2_ffn_in['gate_w'], 'L2_ffn_w1': _L2_ffn_in['w1'], 'L2_ffn_b1': _L2_ffn_in['b1'], 'L2_ffn_w2': _L2_ffn_in['w2'], 'L2_ffn_b2': _L2_ffn_in['b2'], 'L2_ffn_sw1': _L2_ffn_in['sw1'], 'L2_ffn_sb1': _L2_ffn_in['sb1'], 'L2_ffn_sw2': _L2_ffn_in['sw2'], 'L2_ffn_sb2': _L2_ffn_in['sb2'], 'L2_c': _L2_c, 'L2_wmod': _L2_wmod, 'L3_attn_Wq': _L3_attn_in['Wq'], 'L3_attn_Wk': _L3_attn_in['Wk'], 'L3_attn_Wv': _L3_attn_in['Wv'], 'L3_attn_Wa': _L3_attn_in['Wa'], 'L3_attn_Wb': _L3_attn_in['Wb'], 'L3_attn_Wg': _L3_attn_in['Wg'], 'L3_attn_Wo': _L3_attn_in['Wo'], 'L3_attn_A_log': _L3_attn_in['A_log'], 'L3_attn_dt_bias': _L3_attn_in['dt_bias'], 'L3_attn_conv_q': _L3_attn_in['conv_q'], 'L3_attn_conv_k': _L3_attn_in['conv_k'], 'L3_attn_conv_v': _L3_attn_in['conv_v'], 'L3_attn_o_norm_w': _L3_attn_in['o_norm_w'], 'L3_ffn_W_r': _L3_ffn_in['W_r'], 'L3_ffn_W_k': _L3_ffn_in['W_k'], 'L3_ffn_W_v': _L3_ffn_in['W_v'], 'L3_ffn_mu_r': _L3_ffn_in['mu_r'], 'L3_ffn_mu_k': _L3_ffn_in['mu_k'], 'L3_c': _L3_c, 'L3_wmod': _L3_wmod}
    _x0 = _d['L0_attn_x']
    _d['L0_attn_x'] = jax.random.normal(jax.random.fold_in(jax.random.key(seed), 1), (8, 512, 128), dtype=_x0.dtype)
    del _x0
    return _d

def reference(L0_attn_x, L0_attn_W_rvk, L0_attn_W_out, L0_attn_time_decay, L0_attn_time_first, L0_ffn_Win, L0_ffn_bin_, L0_ffn_W1, L0_ffn_b1, L0_ffn_W2, L0_ffn_b2, L0_ffn_Wout, L0_ffn_bout, L0_c, L0_wmod, L1_attn_W_Q, L1_attn_W_K, L1_attn_W_V, L1_attn_W_O, L1_ffn_w_g, L1_ffn_c_fc, L1_ffn_c_proj, L1_c, L1_wmod, L2_attn_W_in, L2_attn_b_in, L2_attn_W_qkva, L2_attn_b_qkva, L2_attn_W_y, L2_attn_b_y, L2_attn_W_out, L2_attn_b_out, L2_attn_h0_re, L2_attn_h0_im, L2_ffn_gate_w, L2_ffn_w1, L2_ffn_b1, L2_ffn_w2, L2_ffn_b2, L2_ffn_sw1, L2_ffn_sb1, L2_ffn_sw2, L2_ffn_sb2, L2_c, L2_wmod, L3_attn_Wq, L3_attn_Wk, L3_attn_Wv, L3_attn_Wa, L3_attn_Wb, L3_attn_Wg, L3_attn_Wo, L3_attn_A_log, L3_attn_dt_bias, L3_attn_conv_q, L3_attn_conv_k, L3_attn_conv_v, L3_attn_o_norm_w, L3_ffn_W_r, L3_ffn_W_k, L3_ffn_W_v, L3_ffn_mu_r, L3_ffn_mu_k, L3_c, L3_wmod):

    def _L0_attn_ref(x, W_rvk, W_out, time_decay, time_first):
        import jax, jax.numpy as jnp
        import numpy as np
        NEG_BIG = -1e+38

        def _wkv_scan(w, u, k, v, aa0, bb0, pp0):
            kT = jnp.moveaxis(k, 1, 0)
            vT = jnp.moveaxis(v, 1, 0)

            def step(carry, kv):
                aa, bb, pp = carry
                kt, vt = kv
                ww = u + kt
                p = jnp.maximum(pp, ww)
                e1 = jnp.exp(pp - p)
                e2 = jnp.exp(ww - p)
                y = (e1 * aa + e2 * vt) / (e1 * bb + e2)
                ww2 = pp + w
                p2 = jnp.maximum(ww2, kt)
                e1 = jnp.exp(ww2 - p2)
                e2 = jnp.exp(kt - p2)
                return ((e1 * aa + e2 * vt, e1 * bb + e2, p2), y)
            (aa, bb, pp), yT = jax.lax.scan(step, (aa0, bb0, pp0), (kT, vT))
            return (jnp.moveaxis(yT, 0, 1), aa, bb, pp)

        def _reference_tuple_inner(x, W_rvk, W_out, time_decay, time_first):
            B, T, C = x.shape
            rvk = jnp.einsum('btc,dc->btd', x, W_rvk)
            r, v, k = jnp.split(rvk, 3, axis=-1)
            w = -jnp.exp(time_decay)
            u = time_first
            aa0 = jnp.zeros((B, C), dtype=x.dtype)
            bb0 = jnp.zeros((B, C), dtype=x.dtype)
            pp0 = jnp.full((B, C), NEG_BIG, dtype=x.dtype)
            wkv, aa, bb, pp = _wkv_scan(w, u, k, v, aa0, bb0, pp0)
            rwkv = jax.nn.sigmoid(r) * wkv
            out = jnp.einsum('btc,dc->btd', rwkv, W_out)
            h = aa
            c = jnp.stack([bb, pp], axis=-1).reshape(B, 2 * C)
            return (out, h, c)
        return _reference_tuple_inner(x, W_rvk, W_out, time_decay, time_first)[0]

    def _L0_ffn_ref(x, Win, bin_, W1, b1, W2, b2, Wout, bout):
        import jax, jax.numpy as jnp
        import numpy as np
        D_MODEL = 128
        M = 64
        INNER = 16
        s = jnp.einsum('btd,dm->btm', x, Win) + bin_
        h = jax.nn.relu(s[..., None] * W1 + b1)
        g = jnp.einsum('btmh,mh->btm', h, W2) + b2
        out = jnp.einsum('btm,md->btd', g, Wout) + bout
        return out

    def _L1_attn_ref(x, W_Q, W_K, W_V, W_O):
        import jax, jax.numpy as jnp
        import numpy as np
        B, N, E = (2, 256, 128)
        H = 16
        BM = 32
        BN = 32
        BUDGET = 0.2

        def _forward(x, W_Q, W_K, W_V, W_O):
            Bx, Nx, Ex = x.shape
            D = Ex // H
            Tr, Tc = (Nx // BM, Nx // BN)
            k = max(1, int(BUDGET * Tc))

            def heads(t):
                return t.reshape(Bx, Nx, H, D).transpose(0, 2, 1, 3)
            Q = heads(x @ W_Q)
            K = heads(x @ W_K)
            V = heads(x @ W_V)
            Qp = Q.reshape(Bx, H, Tr, BM, D).mean(axis=3)
            Kp = K.reshape(Bx, H, Tc, BN, D).mean(axis=3)
            avg_sc = jnp.einsum('bhid,bhjd->bhij', Qp, Kp).mean(axis=(0, 1))
            _, idx = jax.lax.top_k(avg_sc, k)
            Kb = K.reshape(Bx, H, Tc, BN, D)
            Vb = V.reshape(Bx, H, Tc, BN, D)
            Ksel = Kb[:, :, idx]
            Vsel = Vb[:, :, idx]
            Qb = Q.reshape(Bx, H, Tr, BM, D)
            scale = 1.0 / jnp.sqrt(jnp.asarray(D, jnp.float32))
            logits = jnp.einsum('bhtqd,bhtknd->bhtqkn', Qb, Ksel).reshape(Bx, H, Tr, BM, k * BN) * scale
            P = jax.nn.softmax(logits, axis=-1)
            Ob = jnp.einsum('bhtqs,bhtsd->bhtqd', P, Vsel.reshape(Bx, H, Tr, k * BN, D))
            O = Ob.reshape(Bx, H, Nx, D).transpose(0, 2, 1, 3).reshape(Bx, Nx, Ex)
            return O @ W_O
        return _forward(x, W_Q, W_K, W_V, W_O)

    def _L1_ffn_ref(x, w_g, c_fc, c_proj):
        import jax, jax.numpy as jnp
        import numpy as np
        TOP_K = 2
        CAP_FACTOR = 1.25
        MIN_CAPACITY = 4
        B, T, C = x.shape
        E = w_g.shape[0]
        N = B * T
        capacity = max(MIN_CAPACITY, int(CAP_FACTOR * N * TOP_K / E))
        xf = x.reshape(N, C)
        logits = xf @ w_g.T
        top_logits, top_idx = jax.lax.top_k(logits, TOP_K)
        router_probs = jax.nn.softmax(top_logits, axis=-1)
        oh = jax.nn.one_hot(top_idx, E, dtype=jnp.int32)
        oh_t = oh.transpose(1, 0, 2).reshape(TOP_K * N, E)
        pos = jnp.cumsum(oh_t, axis=0).reshape(TOP_K, N, E).transpose(1, 0, 2)
        rank = jnp.sum((pos - 1) * oh, axis=-1)
        valid = rank < capacity
        probs_masked = router_probs * valid.astype(router_probs.dtype)
        rank_c = jnp.clip(rank, 0, capacity - 1)
        contrib = xf[:, None, :] * valid[..., None].astype(xf.dtype)
        buf = jnp.zeros((E, capacity, C), dtype=xf.dtype).at[top_idx, rank_c].add(contrib)
        h = jnp.einsum('ecd,edf->ecf', buf, c_fc)
        h = jnp.square(jax.nn.relu(h))
        expert_out = jnp.einsum('ecf,efd->ecd', h, c_proj)
        gathered = expert_out[top_idx, rank_c]
        out = jnp.sum(gathered * probs_masked[..., None], axis=1)
        return out.reshape(B, T, C)

    def _L2_attn_ref(x, W_in, b_in, W_qkva, b_qkva, W_y, b_y, W_out, b_out, h0_re, h0_im):
        import jax, jax.numpy as jnp
        import numpy as np
        B, L, DIM, H, D = (4, 128, 128, 8, 32)
        b, Ls, dim = x.shape
        Hh, Dd = (h0_re.shape[0], h0_re.shape[1])
        u = jax.nn.silu(x @ W_in.T + b_in)
        qkva = (u @ W_qkva.T + b_qkva).reshape(b, Ls, Hh, Dd, 4, 2)
        c = jax.lax.complex(qkva[..., 0], qkva[..., 1])
        q, k, v, a = (c[..., 0], c[..., 1], c[..., 2], c[..., 3])
        mag2 = a.real * a.real + a.imag * a.imag
        a = a * (jax.lax.rsqrt(mag2) * jax.nn.sigmoid(jnp.log(mag2)))
        kv = jnp.einsum('blhd,blhe->blhde', k, v)
        h0 = jax.lax.complex(h0_re, h0_im)[None]
        kv = kv.at[:, 0].add(a[:, 0, ..., None] * h0)
        a_e = a[..., None]

        def comb(c1, c2):
            a1, x1 = c1
            a2, x2 = c2
            return (a1 * a2, a2 * x1 + x2)
        _, h = jax.lax.associative_scan(comb, (a_e, kv), axis=1)
        y = jnp.einsum('blhd,blhde->blhe', q, h)
        y2 = jnp.stack([y.real, y.imag], axis=-1).reshape(b, Ls, Hh * Dd * 2)
        y2 = jax.nn.silu(y2 @ W_y.T + b_y)
        return y2 @ W_out.T + b_out

    def _L2_ffn_ref(x, gate_w, w1, b1, w2, b2, sw1, sb1, sw2, sb2):
        import jax, jax.numpy as jnp
        import numpy as np
        D_MODEL = 128
        HIDDEN = 512
        N_ROUTING = 2
        B, S, D = x.shape
        xf = x.reshape(-1, D)
        gate_scores = xf @ gate_w.T
        gate_probs = jax.nn.softmax(gate_scores, axis=-1)
        top1 = jnp.argmax(gate_probs, axis=-1)
        one_hot = jax.nn.one_hot(top1, N_ROUTING, dtype=xf.dtype)
        masked = xf[None, :, :] * one_hot.T[:, :, None]
        h = jax.nn.relu(jnp.einsum('end,edh->enh', masked, w1) + b1[:, None, :])
        expert_out = jnp.einsum('enh,ehd->end', h, w2) + b2[:, None, :]
        routing_output = expert_out.sum(axis=0)
        shared = jax.nn.relu(xf @ sw1 + sb1) @ sw2 + sb2
        return (routing_output + shared).reshape(B, S, D)

    def _L3_attn_ref(x, Wq, Wk, Wv, Wa, Wb, Wg, Wo, A_log, dt_bias, conv_q, conv_k, conv_v, o_norm_w):
        import jax, jax.numpy as jnp
        import numpy as np
        B, T, D = (2, 256, 128)
        H = 8
        KD = 128
        VD = 32
        KEY_DIM = H * KD
        VAL_DIM = H * VD
        KS = 4
        EPS_NORM = 1e-06
        EPS_RMS = 1e-05

        def _xavier(key, shape):
            fan_in, fan_out = (shape[0], shape[1])
            lim = np.sqrt(6.0 / (fan_in + fan_out))
            return jax.random.uniform(key, shape, jnp.float32, -lim, lim)

        def _causal_dw_conv_silu(x, w):
            C = x.shape[-1]
            y = jax.lax.conv_general_dilated(jnp.swapaxes(x, 1, 2), w[:, None, :], window_strides=(1,), padding=[(KS - 1, 0)], feature_group_count=C)
            return jax.nn.silu(jnp.swapaxes(y, 1, 2))

        def _l2norm(x):
            n = jnp.sqrt(jnp.sum(x * x, axis=-1, keepdims=True))
            return x / jnp.maximum(n, EPS_NORM)

        def _gdn_forward(x, Wq, Wk, Wv, Wa, Wb, Wg, Wo, A_log, dt_bias, conv_q, conv_k, conv_v, o_norm_w):
            bsz, seq_len, _ = x.shape
            beta = jax.nn.sigmoid(x @ Wb) * 2.0
            g = -jnp.exp(A_log)[None, None, :] * jax.nn.softplus(x @ Wa + dt_bias[None, None, :])
            alpha = jnp.exp(g)
            q = _causal_dw_conv_silu(x @ Wq, conv_q).reshape(bsz, seq_len, H, KD)
            k = _causal_dw_conv_silu(x @ Wk, conv_k).reshape(bsz, seq_len, H, KD)
            v = _causal_dw_conv_silu(x @ Wv, conv_v).reshape(bsz, seq_len, H, VD)
            q = _l2norm(q)
            k = _l2norm(k)
            qT = jnp.swapaxes(q, 0, 1)
            kT = jnp.swapaxes(k, 0, 1)
            vT = jnp.swapaxes(v, 0, 1)
            aT = jnp.swapaxes(alpha, 0, 1)
            bT = jnp.swapaxes(beta, 0, 1)

            def step(state, inp):
                q_t, k_t, v_t, a_t, b_t = inp
                retained = jnp.einsum('bhvk,bhk->bhv', state, k_t)
                a4 = a_t[..., None, None]
                b4 = b_t[..., None, None]
                rk = retained[..., None] * k_t[:, :, None, :]
                vk = v_t[..., None] * k_t[:, :, None, :]
                state = a4 * (state - b4 * rk) + b4 * vk
                o_t = jnp.einsum('bhvk,bhk->bhv', state, q_t)
                return (state, o_t)
            state0 = jnp.zeros((bsz, H, VD, KD), jnp.float32)
            _, outT = jax.lax.scan(step, state0, (qT, kT, vT, aT, bT))
            out = jnp.swapaxes(outT, 0, 1)
            gate = (x @ Wg).reshape(bsz, seq_len, H, VD)
            rms = jax.lax.rsqrt(jnp.mean(out * out, axis=-1, keepdims=True) + EPS_RMS)
            out = out * rms * o_norm_w * jax.nn.silu(gate)
            out = out.reshape(bsz, seq_len, VAL_DIM)
            return out @ Wo
        return _gdn_forward(x, Wq, Wk, Wv, Wa, Wb, Wg, Wo, A_log, dt_bias, conv_q, conv_k, conv_v, o_norm_w)

    def _L3_ffn_ref(x, W_r, W_k, W_v, mu_r, mu_k):
        import jax, jax.numpy as jnp
        import numpy as np
        DIM = 128

        def _reference_tuple_inner(x, W_r, W_k, W_v, mu_r, mu_k):
            B, T, C = x.shape
            x_prev = jnp.concatenate([jnp.zeros((B, 1, C), x.dtype), x[:, :-1, :]], axis=1)
            xr = mu_r * x + (1.0 - mu_r) * x_prev
            xk = mu_k * x + (1.0 - mu_k) * x_prev
            r = jax.nn.sigmoid(jnp.einsum('btc,dc->btd', xr, W_r))
            k = jnp.einsum('btc,dc->btd', xk, W_k)
            k_act = jnp.square(jax.nn.relu(k))
            out = r * jnp.einsum('btc,dc->btd', k_act, W_v)
            new_state = x[:, -1, :]
            return (out, new_state)
        return _reference_tuple_inner(x, W_r, W_k, W_v, mu_r, mu_k)[0]
    x = L0_attn_x
    mod = (_silu(L0_c) @ L0_wmod).reshape(L0_c.shape[0], 6, 1, -1)
    sa, ca, ga, sb, cb, gb = (mod[:, 0], mod[:, 1], mod[:, 2], mod[:, 3], mod[:, 4], mod[:, 5])
    ga = (2 * (ga >= 0) - 1) * jnp.maximum(jnp.abs(ga), 0.25)
    gb = (2 * (gb >= 0) - 1) * jnp.maximum(jnp.abs(gb), 0.25)
    h = _layernorm(x, axis=-1) * (1 + ca) + sa
    x = x + ga * _L0_attn_ref(h, L0_attn_W_rvk, L0_attn_W_out, L0_attn_time_decay, L0_attn_time_first)
    h = _layernorm(x, axis=-1) * (1 + cb) + sb
    x = x + gb * _L0_ffn_ref(h, L0_ffn_Win, L0_ffn_bin_, L0_ffn_W1, L0_ffn_b1, L0_ffn_W2, L0_ffn_b2, L0_ffn_Wout, L0_ffn_bout)
    mod = (_silu(L1_c) @ L1_wmod).reshape(L1_c.shape[0], 6, 1, -1)
    sa, ca, ga, sb, cb, gb = (mod[:, 0], mod[:, 1], mod[:, 2], mod[:, 3], mod[:, 4], mod[:, 5])
    ga = (2 * (ga >= 0) - 1) * jnp.maximum(jnp.abs(ga), 0.25)
    gb = (2 * (gb >= 0) - 1) * jnp.maximum(jnp.abs(gb), 0.25)
    h = _layernorm(x, axis=-1) * (1 + ca) + sa
    x = x + ga * _L1_attn_ref(h, L1_attn_W_Q, L1_attn_W_K, L1_attn_W_V, L1_attn_W_O)
    h = _layernorm(x, axis=-1) * (1 + cb) + sb
    x = x + gb * _L1_ffn_ref(h, L1_ffn_w_g, L1_ffn_c_fc, L1_ffn_c_proj)
    mod = (_silu(L2_c) @ L2_wmod).reshape(L2_c.shape[0], 6, 1, -1)
    sa, ca, ga, sb, cb, gb = (mod[:, 0], mod[:, 1], mod[:, 2], mod[:, 3], mod[:, 4], mod[:, 5])
    ga = (2 * (ga >= 0) - 1) * jnp.maximum(jnp.abs(ga), 0.25)
    gb = (2 * (gb >= 0) - 1) * jnp.maximum(jnp.abs(gb), 0.25)
    h = _layernorm(x, axis=-1) * (1 + ca) + sa
    x = x + ga * _L2_attn_ref(h, L2_attn_W_in, L2_attn_b_in, L2_attn_W_qkva, L2_attn_b_qkva, L2_attn_W_y, L2_attn_b_y, L2_attn_W_out, L2_attn_b_out, L2_attn_h0_re, L2_attn_h0_im)
    h = _layernorm(x, axis=-1) * (1 + cb) + sb
    x = x + gb * _L2_ffn_ref(h, L2_ffn_gate_w, L2_ffn_w1, L2_ffn_b1, L2_ffn_w2, L2_ffn_b2, L2_ffn_sw1, L2_ffn_sb1, L2_ffn_sw2, L2_ffn_sb2)
    mod = (_silu(L3_c) @ L3_wmod).reshape(L3_c.shape[0], 6, 1, -1)
    sa, ca, ga, sb, cb, gb = (mod[:, 0], mod[:, 1], mod[:, 2], mod[:, 3], mod[:, 4], mod[:, 5])
    ga = (2 * (ga >= 0) - 1) * jnp.maximum(jnp.abs(ga), 0.25)
    gb = (2 * (gb >= 0) - 1) * jnp.maximum(jnp.abs(gb), 0.25)
    h = _layernorm(x, axis=-1) * (1 + ca) + sa
    x = x + ga * _L3_attn_ref(h, L3_attn_Wq, L3_attn_Wk, L3_attn_Wv, L3_attn_Wa, L3_attn_Wb, L3_attn_Wg, L3_attn_Wo, L3_attn_A_log, L3_attn_dt_bias, L3_attn_conv_q, L3_attn_conv_k, L3_attn_conv_v, L3_attn_o_norm_w)
    h = _layernorm(x, axis=-1) * (1 + cb) + sb
    x = x + gb * _L3_ffn_ref(h, L3_ffn_W_r, L3_ffn_W_k, L3_ffn_W_v, L3_ffn_mu_r, L3_ffn_mu_k)
    return x

_drawn_inputs = setup_inputs


def setup_inputs(seed=0):
    import zlib

    import numpy as np

    out = dict(_drawn_inputs(seed))
    spreads = {'L0_attn_time_decay': (1.0, 0.6),
     'L0_attn_time_first': (1.0, 0.6),
     'L2_attn_b_in': (0.0, 0.8),
     'L2_attn_b_qkva': (0.0, 0.8),
     'L2_attn_b_y': (0.0, 0.8),
     'L2_attn_b_out': (0.0, 0.302),
     'L3_attn_o_norm_w': (1.0, 0.2)}
    factors = {'L0_ffn_Win': 3.223,
     'L0_ffn_bin_': 8.0,
     'L0_ffn_W1': 3.175,
     'L0_ffn_bout': 2.88,
     'L1_attn_W_Q': 8.0,
     'L1_attn_W_K': 8.0,
     'L1_attn_W_V': 8.0,
     'L1_attn_W_O': 8.0,
     'L1_ffn_w_g': 8.0,
     'L1_ffn_c_fc': 8.0,
     'L1_ffn_c_proj': 8.0,
     'L1_c': 8.0,
     'L1_wmod': 8.0,
     'L2_attn_W_in': 8.0,
     'L2_attn_W_qkva': 8.0,
     'L2_attn_W_y': 8.0,
     'L2_attn_W_out': 8.0,
     'L2_attn_h0_re': 8.0,
     'L2_attn_h0_im': 8.0,
     'L2_ffn_gate_w': 4.317,
     'L2_ffn_w1': 3.687,
     'L2_ffn_b1': 8.0,
     'L2_ffn_w2': 3.023,
     'L2_ffn_b2': 7.166,
     'L2_ffn_sw1': 3.731,
     'L2_ffn_sb1': 8.0,
     'L2_ffn_sw2': 3.025,
     'L2_ffn_sb2': 8.0,
     'L3_ffn_W_r': 8.0,
     'L3_ffn_W_k': 3.023,
     'L3_ffn_W_v': 2.789,
     'L3_ffn_mu_r': 8.0,
     'L3_ffn_mu_k': 4.737}
    for name, (base, spread) in spreads.items():
        noise = np.random.default_rng([zlib.crc32(name.encode()), seed]).standard_normal(out[name].shape)
        drawn = base * np.exp(spread * noise) if base else spread * noise
        out[name] = jnp.asarray(drawn.astype(out[name].dtype))
    for name, factor in factors.items():
        out[name] = (out[name] * factor).astype(out[name].dtype)
    return out
```

```python
from contextlib import ExitStack

import numpy as np

import concourse.bass as bass
from concourse import mybir

F32 = mybir.dt.float32
U32 = mybir.dt.uint32
ALU = mybir.AluOpType
ACT = mybir.ActivationFunctionType
AX = mybir.AxisListType

C = 128
B = 8
T = 512
LN_EPS = 1e-5
NEG_BIG = -1e38
EXP_LN = "natural_log_exp_and_others"
LEAST = -37.0
SA, CA, GA, SB_, CB, GB = range(6)


class Steps:

    def __init__(self, steps, stage, counts, unit=1):
        self.steps, self.stage, self.counts, self.unit, self.n = steps, stage, counts, unit, 0

    def did(self, name=None):
        self.n += self.unit
        if name is not None:
            self.counts[self.stage, self.steps.name, name] = self.n
        return self.unit

    def at(self, name):
        return self.counts.get((self.stage, self.steps.name, name), 1)


class Kernel:

    def __init__(self, nc, counts):
        self.nc, self.counts, self.stack, self.w = nc, counts, ExitStack(), {}
        self.ps = self.stack.enter_context(nc.psum_tensor("ps", [128, 8, 512], F32))
        names = ("tensor_steps", "scalar_steps", "vector_steps", "gpsimd_steps", "dma_steps")
        self.sems = [self.stack.enter_context(nc.semaphore(n)) for n in names]

    def sb(self, name, shape, dt=F32, stack=None):
        return (stack or self.stack).enter_context(self.nc.sbuf_tensor(name, shape, dt))

    def stage(self, name):
        pe, act, dve, pool, dma = (Steps(s, name, self.counts, u) for s, u in zip(self.sems, (1, 1, 1, 1, 16)))
        return pe, act, dve, pool, dma

    def end(self):
        with self.nc.Block() as block:
            @block.vector
            def _(v):
                for s in self.sems:
                    v.sem_clear(s)


class Norm:

    def __init__(self, k, st, tag, bank_c, bank_v, x, h, mod, shift, scale, tmp):
        self.k, self.st, self.tag, self.x, self.h, self.tmp = k, st, tag, x, h, tmp
        self.pc, self.pv = k.ps[:, bank_c, :], k.ps[:, bank_v, :]
        self.shift, self.scale = mod[:, shift:shift + 1], mod[:, scale:scale + 1]

    def tensor(self, e):
        pe, act, dve, pool, _ = self.st
        k, g = self.k, self.tag
        e.matmul(self.pc, k.w["center"][:], self.x, start=True, stop=True).then_inc(pe.steps, pe.did(g + "c"))
        e.wait_ge(act.steps, act.at(g + "sq"))
        e.matmul(self.pv, k.w["mean"][:], self.tmp[:, 0, :], start=True, stop=True).then_inc(pe.steps, pe.did(g + "v"))

    def scalar(self, e):
        pe, act, dve, pool, _ = self.st
        g = self.tag
        e.wait_ge(pe.steps, pe.at(g + "c"))
        e.activation(self.tmp[:, 0, :], self.pc, ACT.Square).then_inc(act.steps, act.did(g + "sq"))
        e.wait_ge(pe.steps, pe.at(g + "v"))
        e.activation(self.tmp[:, 1, :], self.pv, ACT.Ln, bias=self.k.eps[:, 0:1]).then_inc(act.steps, act.did())
        e.wait_ge(act.steps, act.n)
        e.activation(self.tmp[:, 2, :], self.tmp[:, 1, :], ACT.Exp, scale=-0.5).then_inc(act.steps, act.did(g + "rs"))

    def vector(self, e):
        pe, act, dve, pool, _ = self.st
        g = self.tag
        e.wait_ge(act.steps, act.at(g + "rs"))
        e.tensor_tensor(self.tmp[:, 1, :], self.pc, self.tmp[:, 2, :], ALU.mult).then_inc(dve.steps, dve.did())
        e.wait_ge(dve.steps, dve.n)
        e.tensor_scalar(self.h, self.tmp[:, 1, :], self.scale, self.shift, ALU.mult, ALU.add).then_inc(dve.steps, dve.did(g + "h"))


def ts(i, n):
    return slice(i * n, (i + 1) * n)


GROUPS = {
    "all": ["center", "mean", "ident"],
    "modulation": ["cT", "wmod"],
    "layers01": ["W_rvk", "W_out0", "decay", "time_first", "Win0", "bin_0", "W1_0", "b1_0", "W2_0", "b2_0", "Wout0",
                 "bout_0", "W_Q", "W_K", "W_V", "W_O", "head_mask", "head_scale", "w_gate1", "rev8", "upto", "ones",
                 "c_fc", "c_proj"],
    "gla": ["W_in2", "b_in2", "W_qka", "b_qka", "W_v2", "b_v2", "W_y2", "b_y2", "W_out2", "b_out2", "h0", "gla_mask"],
    "delta": ["Wqk3", "Wv3", "Wg3", "Wab3", "Wo3", "A_log", "dt_bias", "conv_v", "o_norm_w", "joins", "eye32", "upto3", "ones3"],
    "mix": ["W_r3", "W_k3", "W_v3", "mu"],
    "mlp2": ["gate_w2", "w1_2", "w2_2", "b1_2", "b2_2"],
}


def place(k, a, names, stack):
    for name in names:
        k.w[name] = k.sb("w_" + name, list(a[name].shape), a[name].dtype, stack)


def load(k, a, group, stack):
    place(k, a, GROUPS[group], stack)
    pe, act, dve, pool, dma = k.stage("load_" + group)
    with k.nc.Block() as block:
        @block.sync
        def _(e):
            for name in GROUPS[group]:
                e.dma_start(k.w[name][:], a[name]).then_inc(dma.steps, dma.did("all"))
            e.wait_ge(dma.steps, dma.at("all"))
    k.end()


def load_weights(k, a):
    nc = k.nc
    place(k, a, GROUPS["all"], k.stack)
    k.X = k.sb("X", [C, B, T])
    k.eps = k.sb("eps", [C, 1])
    k.mod = k.sb("mod", [C, 4, 6, B])
    k.modb = k.sb("modb", [C, 4, 6])
    st = pe, act, dve, pool, dma = k.stage("load")
    scope = ExitStack()
    place(k, a, GROUPS["modulation"], scope)
    cT = k.sb("c_silu", [C, 4, B], stack=scope)
    with scope, nc.Block() as block:
        @block.sync
        def _(e):
            for name, ap in a.items():
                if name in GROUPS["all"] + GROUPS["modulation"]:
                    e.dma_start(k.w[name][:], ap).then_inc(dma.steps, dma.did())
            e.dma_start(k.X[:], a["x"]).then_inc(dma.steps, dma.did("all"))
            e.wait_ge(dma.steps, dma.at("all"))

        @block.scalar
        def _(e):
            e.wait_ge(dma.steps, dma.at("all"))
            e.activation(cT[:], k.w["cT"][:], ACT.Exp, scale=-1.0).then_inc(act.steps, act.did("exp"))

        @block.vector
        def _(e):
            e.memset(k.eps[:], LN_EPS).then_inc(dve.steps, dve.did())
            e.wait_ge(act.steps, act.at("exp"))
            e.tensor_scalar(cT[:], cT[:], 1.0, None, ALU.add).then_inc(dve.steps, dve.did())
            e.wait_ge(dve.steps, dve.n)
            e.reciprocal(cT[:], cT[:]).then_inc(dve.steps, dve.did())
            e.wait_ge(dve.steps, dve.n)
            e.tensor_tensor(cT[:], cT[:], k.w["cT"][:], ALU.mult).then_inc(dve.steps, dve.did("silu"))
            e.wait_ge(pe.steps, pe.at("mod"))
            m = k.mod[:].rearrange("p l s b -> p (l s b)")
            e.tensor_copy(m, k.ps[:, 0, 0:4 * 6 * B]).then_inc(dve.steps, dve.did())
            e.wait_ge(dve.steps, dve.n)
            for s in (CA, CB):
                e.tensor_scalar(k.mod[:, :, s, :], k.mod[:, :, s, :], 1.0, None, ALU.add).then_inc(dve.steps, dve.did())
            for s in (GA, GB):
                g = k.mod[:, :, s, :]
                e.tensor_scalar(cT[:], g, 0.0, 2.0, ALU.is_ge, ALU.mult).then_inc(dve.steps, dve.did())
                e.wait_ge(dve.steps, dve.n)
                e.tensor_scalar(cT[:], cT[:], -1.0, None, ALU.add).then_inc(dve.steps, dve.did())
                e.wait_ge(dve.steps, dve.n)
                e.tensor_tensor(g, g, cT[:], ALU.mult).then_inc(dve.steps, dve.did())
                e.wait_ge(dve.steps, dve.n)
                e.tensor_scalar(g, g, 0.25, None, ALU.max).then_inc(dve.steps, dve.did())
                e.wait_ge(dve.steps, dve.n)
                e.tensor_tensor(g, g, cT[:], ALU.mult).then_inc(dve.steps, dve.did())
                e.wait_ge(dve.steps, dve.n)

        @block.tensor
        def _(e):
            e.wait_ge(dve.steps, dve.at("silu"))
            for l in range(4):
                for s in range(6):
                    i = (l * 6 + s) * B
                    ins = e.matmul(k.ps[:, 0, i:i + B], k.w["wmod"][:, l, ts(s, C)], cT[:, l, :], start=True, stop=True)
            ins.then_inc(pe.steps, pe.did("mod"))
    k.end()


def wkv_mlp_prologue(k, s):
    nc = k.nc
    k.w_decay = k.sb("neg_decay", [C, 1], stack=s)
    k.w_full = k.sb("neg_decay_time", [C, T], stack=s)
    k.w2out = k.sb("w2out", [C, 8, C], stack=s)
    k.mlp0_const = k.sb("mlp0_const", [C, 1], stack=s)
    pe, act, dve, pool, dma = k.stage("wkv_prologue")
    with nc.Block() as block:
        @block.scalar
        def _(e):
            e.activation(k.w_decay[:], k.w["decay"][:], ACT.Exp).then_inc(act.steps, act.did("exp"))

        @block.tensor
        def _(e):
            e.matmul(k.ps[:, 0, 0:1], k.w["Wout0"][0:64, :], k.w["b2_0"][0:64, :], start=True, stop=True).then_inc(pe.steps, pe.did("const"))

        @block.vector
        def _(e):
            e.memset(k.w_full[:], 0.0).then_inc(dve.steps, dve.did("zero"))
            e.wait_ge(act.steps, act.at("exp"))
            e.tensor_scalar(k.w_decay[:], k.w_decay[:], -1.0, None, ALU.mult).then_inc(dve.steps, dve.did())
            e.wait_ge(dve.steps, dve.n)
            e.tensor_scalar(k.w_full[:], k.w_full[:], k.w_decay[:, 0:1], None, ALU.add).then_inc(dve.steps, dve.did())
            for j in range(8):
                e.tensor_scalar(k.w2out[:, j, :], k.w["Wout0"][:], k.w["W2_0"][:, j:j + 1], None, ALU.mult).then_inc(dve.steps, dve.did())
            e.wait_ge(pe.steps, pe.at("const"))
            e.tensor_tensor(k.mlp0_const[:], k.ps[:, 0, 0:1], k.w["bout_0"][:], ALU.add).then_inc(dve.steps, dve.did())
    k.end()


def layer0(k, q1, k1, v1, qbar, kbar):
    nc = k.nc
    with ExitStack() as s:
        xb = k.sb("l0_xb", [C, T], stack=s)
        h = k.sb("l0_h", [C, T], stack=s)
        tmp = k.sb("l0_tmp", [C, 3, T], stack=s)
        ks = k.sb("l0_k", [C, T], stack=s)
        er = k.sb("l0_er", [C, T], stack=s)
        pp = k.sb("l0_pp", [C, T + 1], stack=s)
        aa = k.sb("l0_aa", [C, T + 1], stack=s)
        bb = k.sb("l0_bb", [C, T + 1], stack=s)
        e1 = k.sb("l0_e1", [C, T], stack=s)
        e2 = k.sb("l0_e2", [C, T], stack=s)
        f1 = k.sb("l0_f1", [C, T], stack=s)
        f2 = k.sb("l0_f2", [C, T], stack=s)
        pm = k.sb("l0_pm", [C, T], stack=s)
        e2v = k.sb("l0_e2v", [C, T], stack=s)
        n1 = k.sb("l0_n1", [C, T], stack=s)
        n2 = k.sb("l0_n2", [C, T], stack=s)
        d1 = k.sb("l0_d1", [C, T], stack=s)
        y = k.sb("l0_y", [C, T], stack=s)
        hid = k.sb("l0_hid", [C, 8, T], stack=s)
        P = [k.ps[:, i, :] for i in range(8)]
        u = k.w["time_first"][:, 0:1]
        wd = k.w_decay[:, 0:1]
        with nc.Fori(0, B) as b:
            st = pe, act, dve, pool, dma = k.stage("layer0")
            m0, m1 = k.modb[:, 0, :], k.modb[:, 1, :]
            na = Norm(k, st, "a", 0, 1, xb[:], h[:], m0, SA, CA, tmp)
            nb = Norm(k, st, "b", 0, 1, xb[:], h[:], m0, SB_, CB, tmp)
            nq = Norm(k, st, "q", 0, 1, xb[:], h[:], m1, SA, CA, tmp)
            with nc.Block() as block:
                @block.tensor
                def _(e):
                    e.wait_ge(pool.steps, pool.at("xb"))
                    na.tensor(e)
                    e.wait_ge(dve.steps, dve.at("ah"))
                    for i, name in ((2, "k"), (1, "v"), (0, "r")):
                        e.matmul(P[4 - i], k.w["W_rvk"][:, ts(i, C)], h[:], start=True, stop=True).then_inc(pe.steps, pe.did(name))
                    e.wait_ge(dve.steps, dve.at("y"))
                    e.matmul(P[5], k.w["W_out0"][:], y[:], start=True, stop=True).then_inc(pe.steps, pe.did("att"))
                    e.wait_ge(dve.steps, dve.at("x1"))
                    nb.tensor(e)
                    e.wait_ge(dve.steps, dve.at("bh"))
                    e.matmul(P[6], k.w["Win0"][:], h[:], start=True, stop=True).then_inc(pe.steps, pe.did("s"))
                    for j in range(8):
                        e.wait_ge(act.steps, act.at(f"hid{j}"))
                        ins = e.matmul(P[7], k.w2out[:, j, :], hid[:, j, :], start=(j == 0), stop=(j == 7))
                    ins.then_inc(pe.steps, pe.did("mlp"))
                    e.wait_ge(dve.steps, dve.at("x2"))
                    nq.tensor(e)
                    e.wait_ge(dve.steps, dve.at("qh"))
                    for i, w in enumerate((k.w["W_Q"], k.w["W_K"], k.w["W_V"])):
                        e.matmul(P[2 + i], w[:], h[:], start=True, stop=True).then_inc(pe.steps, pe.did(f"p{i}"))

                @block.gpsimd
                def _(e):
                    e.tensor_copy(xb[:], k.X[:, bass.ds(b, 1), :].rearrange("p a t -> p (a t)")).then_inc(pool.steps, pool.did("xb"))
                    e.wait_ge(dve.steps, dve.at("pp"))
                    e.wait_ge(act.steps, act.at("k"))
                    e.tensor_tensor(e2[:], ks[:], pp[:, 1:], ALU.subtract).then_inc(pool.steps, pool.did("e2a"))
                    e.wait_ge(dve.steps, dve.at("pm"))
                    e.tensor_tensor(f1[:], pp[:, 0:T], pm[:], ALU.subtract).then_inc(pool.steps, pool.did("f1a"))
                    e.wait_ge(act.steps, act.at("f1"))
                    e.wait_ge(dve.steps, dve.at("aa"))
                    e.tensor_tensor(n1[:], f1[:], aa[:, 0:T], ALU.mult).then_inc(pool.steps, pool.did("n1"))
                    e.wait_ge(dve.steps, dve.at("bb"))
                    e.tensor_tensor(d1[:], f1[:], bb[:, 0:T], ALU.mult).then_inc(pool.steps, pool.did("d1"))

                @block.scalar
                def _(e):
                    e.preload_act_table_set(EXP_LN)
                    na.scalar(e)
                    e.wait_ge(pe.steps, pe.at("k"))
                    e.activation(ks[:], P[2], ACT.Copy).then_inc(act.steps, act.did("k"))
                    e.wait_ge(dve.steps, dve.at("er"))
                    e.activation(er[:], er[:], ACT.Exp, scale=-1.0).then_inc(act.steps, act.did())
                    e.wait_ge(dve.steps, dve.at("e1a"))
                    e.activation(e1[:], e1[:], ACT.Exp).then_inc(act.steps, act.did("e1"))
                    e.wait_ge(pool.steps, pool.at("e2a"))
                    e.activation(e2[:], e2[:], ACT.Exp).then_inc(act.steps, act.did("e2"))
                    e.wait_ge(pool.steps, pool.at("f1a"))
                    e.activation(f1[:], f1[:], ACT.Exp).then_inc(act.steps, act.did("f1"))
                    e.wait_ge(dve.steps, dve.at("f2a"))
                    e.activation(f2[:], f2[:], ACT.Exp).then_inc(act.steps, act.did("f2"))
                    e.wait_ge(dve.steps, dve.at("den"))
                    e.activation(d1[:], d1[:], ACT.Ln).then_inc(act.steps, act.did())
                    e.wait_ge(act.steps, act.n)
                    e.activation(d1[:], d1[:], ACT.Exp, scale=-1.0).then_inc(act.steps, act.did("inv"))
                    nb.scalar(e)
                    e.wait_ge(pe.steps, pe.at("s"))
                    e.activation(er[:], P[6], ACT.Identity, bias=k.w["bin_0"][:, 0:1]).then_inc(act.steps, act.did("s"))
                    e.wait_ge(act.steps, act.n)
                    for j in range(8):
                        e.activation(hid[:, j, :], er[:], ACT.Relu, bias=k.w["b1_0"][:, j:j + 1],
                                              scale=k.w["W1_0"][:, j:j + 1]).then_inc(act.steps, act.did(f"hid{j}"))
                    e.wait_ge(pe.steps, pe.at("mlp"))
                    e.activation(y[:], P[7], ACT.Identity, bias=k.mlp0_const[:, 0:1]).then_inc(act.steps, act.did("mlp"))
                    nq.scalar(e)
                    for i, dst in ((0, q1), (1, k1)):
                        e.wait_ge(pe.steps, pe.at(f"p{i}"))
                        e.activation(dst[:, bass.ds(b, 1), :].rearrange("p a t -> p (a t)"), P[2 + i], ACT.Copy).then_inc(act.steps, act.did(f"cp{i}"))

                @block.vector
                def _(e):
                    e.tensor_copy(k.modb[:], k.mod[:, :, :, bass.ds(b, 1)].rearrange("p l s a -> p l (s a)")).then_inc(dve.steps, dve.did())
                    e.memset(pp[:, 0:1], NEG_BIG).then_inc(dve.steps, dve.did())
                    e.memset(aa[:, 0:1], 0.0).then_inc(dve.steps, dve.did())
                    e.memset(bb[:, 0:1], 0.0).then_inc(dve.steps, dve.did())
                    e.wait_ge(dve.steps, dve.n)
                    na.vector(e)
                    e.wait_ge(pe.steps, pe.at("r"))
                    e.tensor_scalar(er[:], P[4], LEAST, None, ALU.max).then_inc(dve.steps, dve.did("er"))
                    e.wait_ge(act.steps, act.at("k"))
                    e.tensor_tensor_scan(pp[:, 1:], k.w_full[:], ks[:], NEG_BIG, ALU.add, ALU.max).then_inc(dve.steps, dve.did("pp"))
                    e.wait_ge(dve.steps, dve.n)
                    e.scalar_tensor_tensor(e1[:], pp[:, 0:T], wd, pp[:, 1:], ALU.add, ALU.subtract).then_inc(dve.steps, dve.did("e1a"))
                    e.scalar_tensor_tensor(pm[:], ks[:], u, pp[:, 0:T], ALU.add, ALU.max).then_inc(dve.steps, dve.did("pm"))
                    e.wait_ge(dve.steps, dve.n)
                    e.scalar_tensor_tensor(f2[:], ks[:], u, pm[:], ALU.add, ALU.subtract).then_inc(dve.steps, dve.did("f2a"))
                    e.wait_ge(act.steps, act.at("e2"))
                    e.wait_ge(pe.steps, pe.at("v"))
                    e.tensor_tensor(e2v[:], e2[:], P[3], ALU.mult).then_inc(dve.steps, dve.did())
                    e.wait_ge(dve.steps, dve.n)
                    e.tensor_tensor_scan(aa[:, 1:], e1[:], e2v[:], 0.0, ALU.mult, ALU.add).then_inc(dve.steps, dve.did("aa"))
                    e.tensor_tensor_scan(bb[:, 1:], e1[:], e2[:], 0.0, ALU.mult, ALU.add).then_inc(dve.steps, dve.did("bb"))
                    e.wait_ge(act.steps, act.at("f2"))
                    e.tensor_tensor(n2[:], f2[:], P[3], ALU.mult).then_inc(dve.steps, dve.did())
                    e.wait_ge(pool.steps, pool.at("d1"))
                    e.tensor_tensor(d1[:], d1[:], f2[:], ALU.add).then_inc(dve.steps, dve.did())
                    e.wait_ge(dve.steps, dve.n)
                    e.scalar_tensor_tensor(d1[:], er[:], 1.0, d1[:], ALU.add, ALU.mult).then_inc(dve.steps, dve.did("den"))
                    e.tensor_tensor(n1[:], n1[:], n2[:], ALU.add).then_inc(dve.steps, dve.did())
                    e.wait_ge(dve.steps, dve.n)
                    e.wait_ge(act.steps, act.at("inv"))
                    e.tensor_tensor(y[:], n1[:], d1[:], ALU.mult).then_inc(dve.steps, dve.did("y"))
                    e.wait_ge(pe.steps, pe.at("att"))
                    e.scalar_tensor_tensor(xb[:], P[5], m0[:, GA:GA + 1], xb[:], ALU.mult, ALU.add).then_inc(dve.steps, dve.did("x1"))
                    nb.vector(e)
                    e.wait_ge(act.steps, act.at("mlp"))
                    e.scalar_tensor_tensor(xb[:], y[:], m0[:, GB:GB + 1], xb[:], ALU.mult, ALU.add).then_inc(dve.steps, dve.did("x2"))
                    e.wait_ge(dve.steps, dve.n)
                    e.tensor_copy(k.X[:, bass.ds(b, 1), :].rearrange("p a t -> p (a t)"), xb[:]).then_inc(dve.steps, dve.did())
                    nq.vector(e)
                    e.wait_ge(pe.steps, pe.at("p2"))
                    e.tensor_copy(v1[:, bass.ds(b, 1), :].rearrange("p a t -> p (a t)"), P[4]).then_inc(dve.steps, dve.did())
                    for i, dst, src in ((0, qbar, q1), (1, kbar, k1)):
                        e.wait_ge(act.steps, act.at(f"cp{i}"))
                        e.tensor_reduce(dst[:, bass.ds(b, 1), :].rearrange("p a t -> p (a t)"),
                                                 src[:, bass.ds(b, 1), :].rearrange("p a (i q) -> p (a i) q", q=32),
                                                 AX.X, ALU.add).then_inc(dve.steps, dve.did())
            k.end()


def flat(ap):
    return ap.rearrange("p a t -> p (a t)")


def choose_blocks(k, qbar, kbar, idx_row):
    with ExitStack() as s:
        sc = k.sb("blk_sc", [16, 16], stack=s)
        best = k.sb("blk_best", [16, 8], stack=s)
        idx = k.sb("blk_idx", [16, 8], U32, stack=s)
        pe, act, dve, pool, dma = k.stage("choose")
        with k.nc.Block() as block:
            @block.tensor
            def _(e):
                for b in range(B):
                    ins = e.matmul(k.ps[0:16, 0, 0:16], qbar[:, b, :], kbar[:, b, :], start=(b == 0), stop=(b == B - 1))
                ins.then_inc(pe.steps, pe.did("score"))

            @block.vector
            def _(e):
                e.wait_ge(pe.steps, pe.at("score"))
                e.tensor_copy(sc[:], k.ps[0:16, 0, 0:16]).then_inc(dve.steps, dve.did())
                e.wait_ge(dve.steps, dve.n)
                e.max(best[:], sc[:]).then_inc(dve.steps, dve.did())
                e.wait_ge(dve.steps, dve.n)
                e.max_index(idx[:], best[:], sc[:]).then_inc(dve.steps, dve.did("idx"))

            @block.sync
            def _(e):
                e.wait_ge(dve.steps, dve.at("idx"))
                e.dma_start(idx_row[0:1, :].rearrange("a (t s) -> a t s", s=3), idx[:, 0:3]).then_inc(dma.steps, dma.did("row"))
                e.wait_ge(dma.steps, dma.at("row"))
        k.end()


def block_attention(k, q1, k1, v1, idx_row):
    nc = k.nc
    NK = 96
    with ExitStack() as s:
        kg = k.sb("att_kg", [C, B, NK], stack=s)
        vg = k.sb("att_vg", [C, B, NK], stack=s)
        qx = k.sb("att_qx", [C, B, 4, 32], stack=s)
        mx = k.sb("att_mx", [C, 2, 16], stack=s)
        den = k.sb("att_den", [C, 2, 16], stack=s)
        p = k.sb("att_p", [C, 2, 16, NK], stack=s)
        pt = k.sb("att_pt", [NK, 2, 16, C], stack=s)
        vt = k.sb("att_vt", [NK, 2, 4, C], stack=s)
        o = k.sb("att_o", [C, 4, 32], stack=s)
        S = k.ps[:, 0:4, 0:4 * NK]
        with nc.Fori(0, 16) as t:
            pe, act, dve, pool, dma = k.stage("attention")
            with nc.Block() as block:
                @block.gpsimd
                def _(e):
                    for i in range(3):
                        j = e.value_load(idx_row[0:1, bass.ds(t * 3 + i, 1)], min_val=0, max_val=15)
                        e.tensor_copy(vg[:, :, ts(i, 32)], v1[:, :, bass.ds(j * 32, 32)]).then_inc(pool.steps, pool.did(f"v{i}"))
                    for u in range(2):
                        e.wait_ge(act.steps, act.at(f"exp{u}"))
                        e.wait_ge(dve.steps, dve.at(f"rden{u}"))
                        e.tensor_tensor(p[:, u], p[:, u],
                                                  den[:, u].unsqueeze(2).to_broadcast([C, 16, NK]), ALU.mult).then_inc(pool.steps, pool.did(f"p{u}"))

                @block.vector
                def _(e):
                    for i in range(3):
                        j = e.value_load(idx_row[0:1, bass.ds(t * 3 + i, 1)], min_val=0, max_val=15)
                        e.tensor_copy(kg[:, :, ts(i, 32)], k1[:, :, bass.ds(j * 32, 32)]).then_inc(dve.steps, dve.did(f"k{i}"))
                    for i in range(4):
                        e.tensor_scalar(qx[:, :, i, :], q1[:, :, bass.ds(t * 32, 32)], k.w["head_scale"][:, i:i + 1],
                                                 None, ALU.mult).then_inc(dve.steps, dve.did(f"q{i}"))
                    for u in range(2):
                        e.wait_ge(pe.steps, pe.at(f"s{u}"))
                        e.tensor_reduce(mx[:, u].rearrange("p (g n) -> p g n", g=4),
                                                 S.rearrange("p g (n k) -> p g n k", k=NK), AX.X, ALU.max).then_inc(dve.steps, dve.did())
                        e.wait_ge(dve.steps, dve.n)
                        e.tensor_tensor(p[:, u].rearrange("p (g n) k -> p g n k", g=4),
                                                 S.rearrange("p g (n k) -> p g n k", k=NK),
                                                 mx[:, u].rearrange("p (g n) -> p g n", g=4).unsqueeze(3)
                                                 .to_broadcast([C, 4, 4, NK]), ALU.subtract).then_inc(dve.steps, dve.did(f"sub{u}"))
                        e.wait_ge(act.steps, act.at(f"exp{u}"))
                        e.tensor_reduce(den[:, u], p[:, u], AX.X, ALU.add).then_inc(dve.steps, dve.did())
                        e.wait_ge(dve.steps, dve.n)
                        e.reciprocal(den[:, u], den[:, u]).then_inc(dve.steps, dve.did(f"rden{u}"))
                        e.wait_ge(pe.steps, pe.at(f"vt{u}"))
                        e.tensor_copy(vt[:, u].rearrange("p n c -> p (n c)"), k.ps[0:NK, 6, :]).then_inc(dve.steps, dve.did(f"vt{u}"))
                        e.wait_ge(pe.steps, pe.at(f"o{u}"))
                        O = k.ps[:, 7, :].rearrange("p (n h q) -> p n h q", n=4, h=4)
                        e.tensor_scalar(o[:], O[:, :, 0, :], k.w["head_mask"][:, 0:1], None, ALU.mult).then_inc(dve.steps, dve.did())
                        for i in range(1, 4):
                            e.wait_ge(dve.steps, dve.n)
                            dst = o[:] if i < 3 else q1[:, 4 * u:4 * u + 4, bass.ds(t * 32, 32)]
                            e.scalar_tensor_tensor(dst, O[:, :, i, :], k.w["head_mask"][:, i:i + 1], o[:],
                                                            ALU.mult, ALU.add).then_inc(dve.steps, dve.did(f"out{u}"))
                        e.wait_ge(dve.steps, dve.n)

                @block.scalar
                def _(e):
                    e.preload_act_table_set(EXP_LN)
                    for u in range(2):
                        e.wait_ge(dve.steps, dve.at(f"sub{u}"))
                        e.activation(p[:, u].rearrange("p a k -> p (a k)"),
                                              p[:, u].rearrange("p a k -> p (a k)"), ACT.Exp).then_inc(act.steps, act.did(f"exp{u}"))
                        for r in range(4):
                            e.wait_ge(pe.steps, pe.at(f"pt{u}{r}"))
                            e.activation(pt[:, u, ts(r, 4), :].rearrange("p a c -> p (a c)"),
                                                  k.ps[0:NK, 4 + r % 2, :], ACT.Copy).then_inc(act.steps, act.did(f"pt{u}{r}"))

                @block.tensor
                def _(e):
                    for u in range(2):
                        if u == 0:
                            e.wait_ge(dve.steps, dve.at("q3"))
                        else:
                            e.wait_ge(dve.steps, dve.at("sub0"))
                        for g in range(4):
                            for n in range(4):
                                ins = e.matmul(S[:, g, ts(n, NK)], qx[ts(g, 32), 4 * u + n, :, :].rearrange("p h q -> p (h q)"),
                                               kg[ts(g, 32), 4 * u + n, :], start=True, stop=True, tile_position=(32 * g, 0))
                        ins.then_inc(pe.steps, pe.did(f"s{u}"))
                        if u == 0:
                            e.wait_ge(pool.steps, pool.at("v2"))
                        else:
                            e.wait_ge(dve.steps, dve.at("vt0"))
                        for n in range(4):
                            ins = e.transpose(k.ps[0:NK, 6, ts(n, C)], vg[:, 4 * u + n, :], k.w["ident"][:])
                        ins.then_inc(pe.steps, pe.did(f"vt{u}"))
                        e.wait_ge(pool.steps, pool.at(f"p{u}"))
                        for r in range(4):
                            if r >= 2 or u:
                                e.wait_ge(act.steps, act.at(f"pt{u}{r - 2}" if r >= 2 else f"pt{u - 1}{r + 2}"))
                            for n in range(4):
                                ins = e.transpose(k.ps[0:NK, 4 + r % 2, ts(n, C)], p[:, u, 4 * r + n, :], k.w["ident"][:])
                            ins.then_inc(pe.steps, pe.did(f"pt{u}{r}"))
                        e.wait_ge(act.steps, act.at(f"pt{u}3"))
                        e.wait_ge(dve.steps, dve.at(f"vt{u}"))
                        if u:
                            e.wait_ge(dve.steps, dve.at("out0"))
                        for n in range(4):
                            for g in range(4):
                                ins = e.matmul(k.ps[ts(g, 32), 7, ts(n, C)], vt[:, u, n, ts(g, 32)], pt[:, u, 4 * g + n, :],
                                               start=True, stop=True, tile_position=(0, 32 * g))
                        ins.then_inc(pe.steps, pe.did(f"o{u}"))
            k.end()


def attention_out(k, o1, h1, lg):
    nc = k.nc
    with ExitStack() as s:
        ob = k.sb("ao_ob", [C, T], stack=s)
        xb = k.sb("ao_xb", [C, T], stack=s)
        h = k.sb("ao_h", [C, T], stack=s)
        tmp = k.sb("ao_tmp", [C, 3, T], stack=s)
        with nc.Fori(0, B) as b:
            st = pe, act, dve, pool, dma = k.stage("attention_out")
            m = k.modb[:, 1, :]
            n = Norm(k, st, "n", 0, 1, xb[:], h[:], m, SB_, CB, tmp)
            with nc.Block() as block:
                @block.tensor
                def _(e):
                    e.wait_ge(pool.steps, pool.at("ob"))
                    e.matmul(k.ps[:, 2, :], k.w["W_O"][:], ob[:], start=True, stop=True).then_inc(pe.steps, pe.did("att"))
                    e.wait_ge(dve.steps, dve.at("x1"))
                    n.tensor(e)
                    e.wait_ge(dve.steps, dve.at("nh"))
                    for i in range(4):
                        ins = e.matmul(k.ps[:, 3, ts(i, 8)], h[:, ts(i, C)], k.w["w_gate1"][:], start=True, stop=True)
                    ins.then_inc(pe.steps, pe.did("lg"))

                @block.gpsimd
                def _(e):
                    e.tensor_copy(ob[:], flat(o1[:, bass.ds(b, 1), :])).then_inc(pool.steps, pool.did("ob"))
                    e.wait_ge(dve.steps, dve.at("nh"))
                    e.tensor_copy(flat(h1[:, bass.ds(b, 1), :]), h[:]).then_inc(pool.steps, pool.did())

                @block.scalar
                def _(e):
                    e.preload_act_table_set(EXP_LN)
                    n.scalar(e)

                @block.vector
                def _(e):
                    e.tensor_copy(k.modb[:], k.mod[:, :, :, bass.ds(b, 1)].rearrange("p l s a -> p l (s a)")).then_inc(dve.steps, dve.did())
                    e.wait_ge(dve.steps, dve.n)
                    e.wait_ge(pe.steps, pe.at("att"))
                    e.scalar_tensor_tensor(xb[:], k.ps[:, 2, :], m[:, GA:GA + 1], flat(k.X[:, bass.ds(b, 1), :]),
                                                    ALU.mult, ALU.add).then_inc(dve.steps, dve.did("x1"))
                    e.wait_ge(dve.steps, dve.n)
                    e.tensor_copy(flat(k.X[:, bass.ds(b, 1), :]), xb[:]).then_inc(dve.steps, dve.did())
                    n.vector(e)
                    e.wait_ge(pe.steps, pe.at("lg"))
                    e.tensor_copy(flat(lg[:, bass.ds(b, 1), :]), k.ps[:, 3, 0:32]).then_inc(dve.steps, dve.did())
            k.end()


def route(k, lg, gates):
    E, NT = 8, B * T // C
    CAP = int(1.25 * B * T * 2 / E)
    nc = k.nc
    with ExitStack() as s:
        l = lg[:].rearrange("p b (i x) -> p (b i) x", x=E)
        eq = k.sb("rt_eq", [C, NT, E], stack=s)
        oh = k.sb("rt_oh", [C, 2, NT, E], stack=s)
        m = k.sb("rt_m", [C, 2, NT], stack=s)
        mk = k.sb("rt_mk", [C, NT], stack=s)
        pr = k.sb("rt_pr", [C, 2, NT], stack=s)
        tot = k.sb("rt_tot", [C, 2 * NT, E], stack=s)
        cum = k.sb("rt_cum", [C, 2 * NT, E], stack=s)
        one = k.sb("rt_one", [C, 2 * NT], stack=s)
        wide = lambda ap: ap.unsqueeze(2).to_broadcast([C, NT, E])
        pe, act, dve, pool, dma = k.stage("route")
        with nc.Block() as block:
            @block.vector
            def _(e):
                e.memset(one[:], 1.0).then_inc(dve.steps, dve.did())
                for c in range(2):
                    e.tensor_reduce(m[:, c], l, AX.X, ALU.max).then_inc(dve.steps, dve.did())
                    e.wait_ge(dve.steps, dve.n)
                    e.tensor_tensor(eq[:], l, wide(m[:, c]), ALU.is_equal).then_inc(dve.steps, dve.did())
                    e.wait_ge(dve.steps, dve.n)
                    e.tensor_tensor(eq[:], eq[:], k.w["rev8"][:].unsqueeze(1).to_broadcast([C, NT, E]), ALU.mult).then_inc(dve.steps, dve.did())
                    e.wait_ge(dve.steps, dve.n)
                    e.tensor_reduce(mk[:], eq[:], AX.X, ALU.max).then_inc(dve.steps, dve.did())
                    e.wait_ge(dve.steps, dve.n)
                    e.tensor_tensor(oh[:, c], eq[:], wide(mk[:]), ALU.is_equal).then_inc(dve.steps, dve.did(f"oh{c}"))
                    e.wait_ge(dve.steps, dve.n)
                    if c == 0:
                        e.scalar_tensor_tensor(l, oh[:, 0], -1e30, l, ALU.mult, ALU.add).then_inc(dve.steps, dve.did())
                        e.wait_ge(dve.steps, dve.n)
                e.tensor_tensor(pr[:, 1], m[:, 1], m[:, 0], ALU.subtract).then_inc(dve.steps, dve.did("diff"))
                e.wait_ge(act.steps, act.at("exp"))
                e.tensor_scalar(pr[:, 0], pr[:, 1], 1.0, None, ALU.add).then_inc(dve.steps, dve.did())
                e.wait_ge(dve.steps, dve.n)
                e.reciprocal(pr[:, 0], pr[:, 0]).then_inc(dve.steps, dve.did())
                e.wait_ge(dve.steps, dve.n)
                e.tensor_tensor(pr[:, 1], pr[:, 1], pr[:, 0], ALU.mult).then_inc(dve.steps, dve.did())
                e.wait_ge(pe.steps, pe.at("cum"))
                e.tensor_copy(tot[:].rearrange("p a x -> p (a x)"), k.ps[:, 1, :]).then_inc(dve.steps, dve.did())
                e.wait_ge(dve.steps, dve.n)
                for x in range(E):
                    e.tensor_tensor_scan(cum[:, :, x], one[:], tot[:, :, x], 0.0, ALU.mult, ALU.add).then_inc(dve.steps, dve.did())
                e.wait_ge(dve.steps, dve.n)
                e.tensor_tensor(cum[:], cum[:], tot[:], ALU.subtract).then_inc(dve.steps, dve.did())
                e.wait_ge(dve.steps, dve.n)
                c2 = cum[:].rearrange("p a x -> p (a x)")
                e.tensor_tensor(c2, c2, k.ps[:, 0, :], ALU.add).then_inc(dve.steps, dve.did())
                e.wait_ge(dve.steps, dve.n)
                e.scalar_tensor_tensor(c2, c2, float(CAP), oh[:].rearrange("p c n x -> p (c n x)"), ALU.is_le, ALU.mult).then_inc(dve.steps, dve.did())
                e.wait_ge(dve.steps, dve.n)
                for c in range(2):
                    e.tensor_tensor(oh[:, c], cum[:, ts(c, NT), :], wide(pr[:, c]), ALU.mult).then_inc(dve.steps, dve.did())
                e.wait_ge(dve.steps, dve.n)
                e.tensor_tensor(gates[:], oh[:, 0], oh[:, 1], ALU.add).then_inc(dve.steps, dve.did())

            @block.scalar
            def _(e):
                e.preload_act_table_set(EXP_LN)
                e.wait_ge(dve.steps, dve.at("diff"))
                e.activation(pr[:, 1], pr[:, 1], ACT.Exp).then_inc(act.steps, act.did("exp"))

            @block.tensor
            def _(e):
                e.wait_ge(dve.steps, dve.at("oh1"))
                o = oh[:].rearrange("p c n x -> p (c n x)")
                e.matmul(k.ps[:, 0, :], k.w["upto"][:], o, start=True, stop=True)
                e.matmul(k.ps[:, 1, :], k.w["ones"][:], o, start=True, stop=True).then_inc(pe.steps, pe.did("cum"))
        k.end()


def experts(k, h1, gates):
    nc = k.nc
    E, F = 8, 4
    with ExitStack() as s:
        h = k.sb("ex_h", [C, T], stack=s)
        g = k.sb("ex_g", [C, 4, E], stack=s)
        r = k.sb("ex_r", [C, 2, F, T], stack=s)
        acc = k.sb("ex_acc", [C, 4, C], stack=s)
        with nc.Fori(0, B) as b:
            pe, act, dve, pool, dma = k.stage("experts")
            with nc.Block() as block:
                @block.gpsimd
                def _(e):
                    e.tensor_copy(h[:], flat(h1[:, bass.ds(b, 1), :])).then_inc(pool.steps, pool.did("h"))
                    for x in range(E):
                        for f in range(2, F):
                            e.wait_ge(act.steps, act.at(f"r{x}{f}"))
                            e.tensor_tensor(r[:, x % 2, f], r[:, x % 2, f], r[:, x % 2, f], ALU.mult).then_inc(pool.steps, pool.did(f"r{x}{f}"))

                @block.scalar
                def _(e):
                    for x in range(E):
                        if x >= 2:
                            e.wait_ge(pe.steps, pe.at(f"y{x - 2}"))
                        for f in range(F):
                            e.wait_ge(pe.steps, pe.at(f"u{x}{f}"))
                            e.activation(r[:, x % 2, f], k.ps[:, f, :], ACT.Relu).then_inc(act.steps, act.did(f"r{x}{f}"))

                @block.tensor
                def _(e):
                    def up(x):
                        for f in range(F):
                            if x:
                                e.wait_ge(act.steps, act.at(f"r{x - 1}{f}"))
                            e.matmul(k.ps[:, f, :], k.w["c_fc"][:, x, ts(f, C)], h[:], start=True, stop=True).then_inc(pe.steps, pe.did(f"u{x}{f}"))

                    def down(x):
                        e.wait_ge(dve.steps, dve.at(f"r{x}1"))
                        e.wait_ge(pool.steps, pool.at(f"r{x}3"))
                        if x >= 2:
                            e.wait_ge(dve.steps, dve.at(f"acc{x - 2}"))
                        for i in range(4):
                            for f in range(F):
                                ins = e.matmul(k.ps[:, 4 + x % 2, ts(i, C)], r[:, x % 2, f, ts(i, C)], k.w["c_proj"][:, x, f, :],
                                               start=(f == 0), stop=(f == F - 1))
                        ins.then_inc(pe.steps, pe.did(f"y{x}"))

                    e.wait_ge(pool.steps, pool.at("h"))
                    up(0)
                    for x in range(E):
                        if x + 1 < E:
                            up(x + 1)
                        down(x)
                    e.wait_ge(dve.steps, dve.at(f"acc{E - 1}"))
                    for i in range(4):
                        ins = e.transpose(k.ps[:, 6, ts(i, C)], acc[:, i, :], k.w["ident"][:])
                    ins.then_inc(pe.steps, pe.did("yT"))

                @block.vector
                def _(e):
                    e.tensor_copy(g[:], gates[:, bass.ds(b * 4, 4), :]).then_inc(dve.steps, dve.did())
                    e.tensor_copy(k.modb[:], k.mod[:, :, :, bass.ds(b, 1)].rearrange("p l s a -> p l (s a)")).then_inc(dve.steps, dve.did())
                    e.wait_ge(dve.steps, dve.n)

                    def gather(x):
                        e.wait_ge(pe.steps, pe.at(f"y{x}"))
                        for i in range(4):
                            y = k.ps[:, 4 + x % 2, ts(i, C)]
                            if x == 0:
                                e.tensor_scalar(acc[:, i, :], y, g[:, i, 0:1], None, ALU.mult).then_inc(dve.steps, dve.did(f"acc{x}"))
                            else:
                                e.scalar_tensor_tensor(acc[:, i, :], y, g[:, i, x:x + 1], acc[:, i, :],
                                                                ALU.mult, ALU.add).then_inc(dve.steps, dve.did(f"acc{x}"))
                    for x in range(E):
                        for f in range(2):
                            e.wait_ge(act.steps, act.at(f"r{x}{f}"))
                            e.tensor_tensor(r[:, x % 2, f], r[:, x % 2, f], r[:, x % 2, f], ALU.mult).then_inc(dve.steps, dve.did(f"r{x}{f}"))
                        if x:
                            gather(x - 1)
                            e.wait_ge(dve.steps, dve.n)
                    gather(E - 1)
                    e.wait_ge(pe.steps, pe.at("yT"))
                    xb = flat(k.X[:, bass.ds(b, 1), :])
                    e.scalar_tensor_tensor(xb, k.ps[:, 6, :], k.modb[:, 1, GB:GB + 1], xb, ALU.mult, ALU.add).then_inc(dve.steps, dve.did())
            k.end()


class Silu:

    def __init__(self, st, tag, psum, bias, out, tmp, ready):
        self.st, self.tag, self.psum, self.bias, self.out, self.tmp, self.ready = st, tag, psum, bias, out, tmp, ready

    def vector(self, e):
        pe, act, dve, pool, _ = self.st
        g, a = self.tag, self.tmp[:, 0, :]
        e.wait_ge(pe.steps, pe.at(self.ready))
        e.tensor_scalar(self.out, self.psum, self.bias, None, ALU.add).then_inc(dve.steps, dve.did())
        e.wait_ge(dve.steps, dve.n)
        e.tensor_scalar(a, self.out, LEAST, None, ALU.max).then_inc(dve.steps, dve.did(g + "z"))
        e.wait_ge(act.steps, act.at(g + "i"))
        e.tensor_tensor(self.out, self.out, a, ALU.mult).then_inc(dve.steps, dve.did(g + "o"))

    def scalar(self, e):
        pe, act, dve, pool, _ = self.st
        g, a = self.tag, self.tmp[:, 0, :]
        e.wait_ge(dve.steps, dve.at(g + "z"))
        e.activation(a, a, ACT.Exp, scale=-1.0).then_inc(act.steps, act.did())
        e.wait_ge(act.steps, act.n)
        e.activation(a, a, ACT.Ln, bias=1.0).then_inc(act.steps, act.did())
        e.wait_ge(act.steps, act.n)
        e.activation(a, a, ACT.Exp, scale=-1.0).then_inc(act.steps, act.did(g + "i"))


R, I = 1, 2
KI, KR = 0, 1
LOG_MIN = -19.0


def gla(k):
    nc = k.nc
    with ExitStack() as s:
        u = k.sb("g_u", [C, T], stack=s)
        y_first = k.sb("g_y_first", [C, 2, T], stack=s)
        mem_qk = k.sb("g_qk_Q0_K0_S2", [C, 12, T], stack=s)
        mem_unit = k.sb("g_unit_qh_y_S", [C, 6, T], stack=s)
        mem_cum = k.sb("g_cum_KT", [C, 4, T], stack=s)
        mem_U = k.sb("g_U_H", [C, 2, 3, T], stack=s)
        qk = mem_qk[:].rearrange("p (j r g) t -> p j r g t", j=3, r=2)
        unit = mem_unit[:].rearrange("p (r g) t -> p r g t", r=3)
        cum = mem_cum[:].rearrange("p (r g) t -> p r g t", r=2)
        U = lambda g: mem_U[:, g]
        m1, m2 = k.sb("g_m1", [C, 2, 2, T], stack=s), k.sb("g_m2", [C, 2, 2, T], stack=s)
        L = k.sb("g_L", [C, 2, T + 1], stack=s)
        one = k.sb("g_one", [C, 1], stack=s)
        qh = unit
        kh = k.sb("g_kh", [C, 2, 2, T], stack=s)[:]
        F, E = k.sb("g_F", [C, 4, 2, T], stack=s), k.sb("g_E", [C, 4, 2, T], stack=s)
        mem_F = F[:].rearrange("p a g t -> p (a g) t")
        tmp, h = mem_F[:, 0:3], mem_F[:, 3]
        xb, h2, o2 = (E[:, i, 1] for i in (3, 1, 2))
        Q = [mem_qk[:, 0:6].rearrange("p (r g) t -> p r g t", r=3)] + [k.sb(f"g_Q{i}", [C, 3, 2, T], stack=s) for i in (1, 2)]
        K = [mem_qk[:, 6:10].rearrange("p (r g) t -> p r g t", r=2)] + [k.sb(f"g_K{i}", [C, 2, 2, T], stack=s) for i in (1, 2)]
        products_over_blocks = lambda g: Q[1][:, 0, g, 0:198].rearrange("p (v r c) -> p v r c", v=2, r=3)
        qs, ks = m1, m2
        V = k.sb("g_V", [C, 4, 8, 96], stack=s)
        KT = lambda g: mem_cum[:].rearrange("p (r g) (i x) -> p g r i x", r=2, i=4)[:, g]
        H0 = k.sb("g_H0", [C, 2, 96], stack=s)

        def H(n, g):
            return H0[:, g] if n == 0 else mem_U[:, g].rearrange("p a t -> p (a t)")[:, 96 * (n - 1):96 * n]

        y = lambda g, pair: y_first[:, pair] if g == 0 else mem_unit[:, 2 * pair + 1]
        S = lambda g: mem_unit[:, 4 + g].rearrange("p (i h r t) -> p i h r t", i=2, h=4, r=2)
        S2 = lambda g: mem_qk[:, 10 + g, 0:256]
        P = [k.ps[:, i, :] for i in range(8)]
        halves = ((8, 1), (16, 2))
        blk = lambda ap, n: ap.rearrange("p (c x) -> p c x", x=n)
        m = k.modb[:, 2, :]

        def later(ap, n):
            return (ap, ap.rearrange("p r (c x) -> p r c x", c=2)[:, :, :, 8:16], ap[:, :, 16:32])[n]

        def half_of(ap, i, later_half):
            if i in (0, 3):
                return ap
            return blk(ap, 16 * i)[:, :, 8 * i:] if later_half else blk(ap, 16 * i)[:, :, :8 * i]

        ORDER = (("scores", 0), ("prepare", "norm"), ("gains", 0), ("prepare", "hidden"), ("scores", 1), ("prepare", "project"),
                 ("gains", 1), ("outputs", 0), ("prepare", "units"), ("scores", 2), ("prepare", "decays"), ("gains", 2),
                 ("outputs", 1), ("prepare", "running"), ("scores", 3), ("gains", 3), ("prepare", "blocks"), ("outputs", 2),
                 ("prepare", "turn"), ("outputs", 3), ("prepare", "split"), ("prepare", "keys"))

        def stage(name, scan_g, prep_b, prep_g):
            st = pe, act, dve, pool, dma = k.stage(name)
            g, sg = prep_g, scan_g
            tot = products_over_blocks(g) if g is not None else None
            n = Norm(k, st, "n", 6, 7, xb, h, m, SA, CA, tmp)
            act_u = Silu(st, "u", P[6], k.w["b_in2"][:, 0:1], u[:], tmp[:, 0:2], "z")
            products = [("c", j, ri) for j in range(3) for ri in range(2)] + [("v", i, 0) for i in range(4)]
            evacuated = lambda x: (act if products[x][0] == "c" else dve)

            def in_turn(scan, prepare):
                for what, which in ORDER:
                    if what == "prepare":
                        if prep_g is not None and (prep_g == 0 or which not in ("norm", "hidden")):
                            prepare(which)
                    elif scan_g is not None:
                        scan(what, which)

            with nc.Block() as block:
                @block.gpsimd
                def _(e):
                    def prepare(what):
                        if what == "norm":
                            e.tensor_copy(xb, flat(k.X[:, bass.ds(prep_b, 1), :])).then_inc(pool.steps, pool.did("xb"))
                        elif what == "units":
                            mag = F[:, 3, g]
                            e.wait_ge(dve.steps, dve.at("parts"))
                            e.tensor_tensor(m1[:, 0, g], qk[:, 2, 1, g], qk[:, 2, 1, g], ALU.mult).then_inc(pool.steps, pool.did("ai2"))
                            e.wait_ge(act.steps, act.at("rs"))
                            e.tensor_tensor(m2[:, 0, g], m1[:, 1, g], m1[:, 1, g], ALU.mult).then_inc(pool.steps, pool.did())
                            e.wait_ge(pool.steps, pool.n)
                            e.tensor_tensor(m2[:, 0, g], m2[:, 0, g], mag, ALU.mult).then_inc(pool.steps, pool.did())
                            e.wait_ge(pool.steps, pool.n)
                            e.tensor_scalar(m2[:, 0, g], m2[:, 0, g], -0.5, 1.5, ALU.mult, ALU.add).then_inc(pool.steps, pool.did())
                            e.wait_ge(pool.steps, pool.n)
                            e.tensor_tensor(m1[:, 1, g], m1[:, 1, g], m2[:, 0, g], ALU.mult).then_inc(pool.steps, pool.did("rs"))
                        elif what == "split":
                            e.wait_ge(dve.steps, dve.at("kh"))
                            e.wait_ge(act.steps, act.at("f2"))
                            for i in range(3):
                                for p_ in range(2):
                                    e.tensor_tensor(half_of(K[i][:, p_, g], i, False), half_of(kh[:, p_, g], i, False), half_of(E[:, i, g], i, False),
                                                    ALU.mult).then_inc(pool.steps, pool.did())

                    in_turn(lambda what, i: None, prepare)

                @block.tensor
                def _(e):
                    def scan(what, i):
                        odd = i % 2
                        if what == "scores":
                            if i >= 2:
                                e.wait_ge(dve.steps, dve.at(f"s{i - 2}"))
                                e.wait_ge(dve.steps, dve.at(f"h{i - 2}"))
                            for turn in range(4):
                                if turn:
                                    ins.then_inc(pe.steps, pe.did())
                                    e.wait_ge(pe.steps, pe.n)
                                for part, j, n_ in ((part, j, n_) for part in range(2) for j in range(4) for n_ in range(3)):
                                    h4 = (turn + n_ // 2) % 4
                                    t, r = slice(i * C + 32 * j, i * C + 32 * j + 32), ts(h4, 32)
                                    keys, planes = (K[n_][r, KR, sg, t], slice(1, 3)) if part == 0 else (K[n_][r, KI, sg, t], slice(0, 2))
                                    col = 64 * h4 + (256 if n_ == 1 else 0)
                                    scored = P[2 * odd + n_ // 2][ts(j, 32), col:col + 64].rearrange("p (r x) -> p r x", r=2)
                                    ins = e.matmul(later(scored, n_), keys, later(Q[n_][r, planes, sg, t], n_),
                                                   start=(turn == 0 and part == 0 and n_ != 1), stop=(part == 1),
                                                   tile_position=(32 * h4, 32 * j), skip_group_check=True)
                            ins.then_inc(pe.steps, pe.did(f"s{i}"))
                            e.wait_ge(pe.steps, pe.n)
                        elif what == "gains":
                            for j in range(4):
                                if j:
                                    ins.then_inc(pe.steps, pe.did())
                                    e.wait_ge(pe.steps, pe.n)
                                rows = ts(j, 32)
                                for part, h4 in ((part, h4) for part in range(2) for h4 in range(4)):
                                    ins = e.matmul(P[2 * odd + 1][ts(h4, 32), 256 + j * 64:320 + j * 64], KT(sg)[rows, (KR, KI)[part], i, ts(h4, 32)],
                                                   V[rows, i, 4 * sg + h4, (slice(32, 96), slice(0, 64))[part]], start=(part == 0), stop=(part == 1),
                                                   tile_position=(32 * j, 32 * h4))
                            ins.then_inc(pe.steps, pe.did(f"g{i}"))
                        else:
                            e.wait_ge(dve.steps, dve.at(f"s{i}"))
                            e.wait_ge(dve.steps, dve.at(f"h{i}"))
                            if i:
                                e.wait_ge(pe.steps, pe.at(f"y{i - 1}"))
                            for turn in range(4):
                                for part, second, bank in ((part, second, bank) for part in range(2) for second in range(2) for bank in range(2)):
                                    j, h4 = (turn + bank) % 4, 2 * bank + second
                                    rows, t = ts(j, 32), slice(i * C + 32 * j, i * C + 32 * j + 32)
                                    ins = e.matmul(P[4 + bank][ts(second, 64), t], V[rows, i, 4 * sg + h4, (slice(32, 96), slice(0, 64))[part]],
                                                   S(sg)[rows, i % 2, h4, part, :], start=(turn == 0 and part == 0), stop=False,
                                                   tile_position=(32 * j, 64 * second), skip_group_check=True)
                                ins.then_inc(pe.steps, pe.did())
                                e.wait_ge(pe.steps, pe.n)
                            for j, part, h4 in ((j, part, h4) for j in range(4) for part in range(2) for h4 in (0, 2, 1, 3)):
                                t = slice(i * C + 32 * j, i * C + 32 * j + 32)
                                ins = e.matmul(P[4 + h4 // 2][ts(h4 % 2, 64), t], H(4 * i + j, sg)[ts(h4, 32), (slice(32, 96), slice(0, 64))[part]],
                                               qs[ts(h4, 32), part, sg, t], start=False, stop=(part == 1),
                                               tile_position=(32 * h4, 64 * (h4 % 2)), skip_group_check=True)
                            ins.then_inc(pe.steps, pe.did(f"y{i}"))

                    def prepare(what):
                        if what == "norm":
                            e.wait_ge(pool.steps, pool.at("xb"))
                            n.tensor(e)
                        elif what == "hidden":
                            e.wait_ge(dve.steps, dve.at("nh"))
                            e.matmul(P[6], k.w["W_in2"][:], h, start=True, stop=True).then_inc(pe.steps, pe.did("z"))
                        elif what == "project":
                            if g == 0:
                                e.wait_ge(dve.steps, dve.at("uo"))
                            for x, (kind, j, ri) in enumerate(products):
                                if x >= 2:
                                    e.wait_ge(evacuated(x - 2).steps, evacuated(x - 2).at(f"p{x - 2}"))
                                if kind == "c":
                                    ins = e.matmul(P[6 + x % 2], k.w["W_qka"][:, j, ri, g, :], u[:], start=True, stop=True)
                                else:
                                    ins = e.matmul(P[6 + x % 2][:, 0:256], u[:, ts(j, C)], k.w["W_v2"][:, ts(g, 256)], start=True, stop=True)
                                ins.then_inc(pe.steps, pe.did(f"p{x}"))
                        elif what == "keys":
                            e.wait_ge(dve.steps, dve.at("ks"))
                            for r in range(2):
                                for i in range(4):
                                    ins = e.transpose(P[6 + r][:, ts(i, C)], ks[:, r, g, ts(i, C)], k.w["ident"][:])
                                ins.then_inc(pe.steps, pe.did(f"kt{r}"))

                    in_turn(scan, prepare)

                @block.scalar
                def _(e):
                    def prepare(what):
                        if what == "norm":
                            n.scalar(e)
                        elif what == "hidden":
                            act_u.scalar(e)
                        elif what == "project":
                            for x, (kind, j, ri) in enumerate(products):
                                if kind == "c":
                                    e.wait_ge(pe.steps, pe.at(f"p{x}"))
                                    e.activation(qk[:, j, ri, g], P[6 + x % 2], ACT.Identity, bias=k.w["b_qka"][:, j, ri, g:g + 1]).then_inc(act.steps, act.did(f"p{x}"))
                        elif what == "units":
                            lg, mag = E[:, 3, g], F[:, 3, g]
                            e.wait_ge(dve.steps, dve.at("mag"))
                            e.activation(lg, mag, ACT.Ln).then_inc(act.steps, act.did("ln"))
                            e.wait_ge(act.steps, act.n)
                            e.activation(F[:, 0, g], mag, ACT.Ln, bias=1.0).then_inc(act.steps, act.did("ln1"))
                            e.activation(m1[:, 1, g], lg, ACT.Exp, scale=-0.5).then_inc(act.steps, act.did("rs"))
                        elif what == "decays":
                            e.wait_ge(dve.steps, dve.at("d0"))
                            e.activation(E[:, 0, g], F[:, 0, g], ACT.Exp, scale=-1.0).then_inc(act.steps, act.did())
                            e.wait_ge(act.steps, act.n)
                            e.activation(F[:, 0, g], F[:, 0, g], ACT.Exp).then_inc(act.steps, act.did("f0"))
                            for i in (1, 2, 3):
                                e.wait_ge(dve.steps, dve.at(f"d{i}"))
                                e.activation(half_of(F[:, i, g], i, True), half_of(F[:, i, g], i, True), ACT.Exp).then_inc(act.steps, act.did())
                                e.activation(half_of(E[:, i, g], i, False), half_of(E[:, i, g], i, False), ACT.Exp).then_inc(act.steps, act.did(f"f{i}"))
                        elif what == "keys":
                            for r in range(2):
                                e.wait_ge(pe.steps, pe.at(f"kt{r}"))
                                e.activation(KT(g)[:, r], P[6 + r].rearrange("p (i x) -> p i x", i=4), ACT.Copy).then_inc(act.steps, act.did())

                    e.preload_act_table_set(EXP_LN)
                    in_turn(lambda what, i: None, prepare)
                    if sg is not None:
                        e.wait_ge(pe.steps, pe.at("y3"))
                        e.activation(y(sg, 1), P[5], ACT.Copy).then_inc(act.steps, act.did())

                @block.vector
                def _(e):
                    def sums(i):
                        e.wait_ge(pe.steps, pe.at(f"s{i}"))
                        if i >= 2:
                            e.wait_ge(pe.steps, pe.at(f"y{i - 2}"))
                        whole = lambda ap: ap.rearrange("p (a x) -> p a x", a=8)
                        s_ = whole(S(sg)[:, i % 2].rearrange("p h r t -> p (h r t)"))
                        t_ = whole(S2(sg))
                        msk = lambda n_: k.w["gla_mask"][:, n_:n_ + 1, :].to_broadcast([C, 8, 32])
                        bank = P[2 * (i % 2)]
                        e.tensor_tensor(s_, whole(bank[:, 0:256]), msk(0), ALU.mult).then_inc(dve.steps, dve.did())
                        e.tensor_tensor(later(t_, 1), later(whole(bank[:, 256:512]), 1), later(msk(1), 1), ALU.mult).then_inc(dve.steps, dve.did())
                        e.wait_ge(dve.steps, dve.n)
                        e.tensor_tensor(later(s_, 1), later(s_, 1), later(t_, 1), ALU.add).then_inc(dve.steps, dve.did())
                        e.wait_ge(dve.steps, dve.n)
                        e.wait_ge(pe.steps, pe.at(f"g{i}"))
                        e.tensor_tensor(later(s_, 2), later(s_, 2), later(whole(P[2 * (i % 2) + 1][:, 0:256]), 2), ALU.add).then_inc(dve.steps, dve.did(f"s{i}"))

                    def states(i):
                        e.wait_ge(pe.steps, pe.at(f"g{i}"))
                        for j in range(4):
                            c_ = 4 * i + j
                            new, end = H(c_ + 1, sg), 32 * c_ + 31
                            e.scalar_tensor_tensor(new[:, 32:96], H(c_, sg)[:, 32:96], F[:, 3, sg, end:end + 1],
                                                   P[2 * (i % 2) + 1][:, 256 + j * 64:320 + j * 64], ALU.mult, ALU.add).then_inc(dve.steps, dve.did())
                            e.wait_ge(dve.steps, dve.n)
                            e.tensor_scalar(new[:, 0:32], new[:, 64:96], -1.0, None, ALU.mult).then_inc(dve.steps, dve.did(f"h{i}"))

                    def scan(what, i):
                        if what == "scores" and i:
                            sums(i - 1)
                        elif what == "gains" and i:
                            states(i - 1)
                        elif what == "outputs" and i == 2:
                            sums(3)
                            states(3)

                    def prepare(what):
                        if what == "norm":
                            e.tensor_copy(k.modb[:], k.mod[:, :, :, bass.ds(prep_b, 1)].rearrange("p l s a -> p l (s a)")).then_inc(dve.steps, dve.did())
                            e.wait_ge(dve.steps, dve.n)
                            n.vector(e)
                        elif what == "hidden":
                            act_u.vector(e)
                        elif what == "project":
                            for x, (kind, i, _) in enumerate(products):
                                if kind == "v":
                                    e.wait_ge(pe.steps, pe.at(f"p{x}"))
                                    e.tensor_tensor(V[:, i, ts(g, 4), 32:96], P[6 + x % 2][:, 0:256].rearrange("p (h x) -> p h x", h=4),
                                                    k.w["b_v2"][:, ts(g, 256)].rearrange("p (h x) -> p h x", h=4), ALU.add).then_inc(dve.steps, dve.did(f"p{x}"))
                            e.wait_ge(dve.steps, dve.n)
                            e.tensor_scalar(V[:, :, ts(g, 4), 0:32], V[:, :, ts(g, 4), 64:96], -1.0, None, ALU.mult).then_inc(dve.steps, dve.did())
                            e.wait_ge(act.steps, act.at("p5"))
                            e.tensor_tensor(F[:, 3, g], qk[:, 2, 0, g], qk[:, 2, 0, g], ALU.mult).then_inc(dve.steps, dve.did("parts"))
                        elif what == "units":
                            lg, mag = E[:, 3, g], F[:, 3, g]
                            e.wait_ge(pool.steps, pool.at("ai2"))
                            e.wait_ge(dve.steps, dve.at("parts"))
                            e.tensor_tensor(mag, mag, m1[:, 0, g], ALU.add).then_inc(dve.steps, dve.did())
                            e.wait_ge(dve.steps, dve.n)
                            e.tensor_scalar(mag, mag, 1e-18, None, ALU.max).then_inc(dve.steps, dve.did("mag"))
                            e.wait_ge(act.steps, act.at("rs"))
                            e.tensor_tensor(lg, lg, F[:, 0, g], ALU.subtract).then_inc(dve.steps, dve.did("lg"))
                        elif what == "decays":
                            lg = E[:, 3, g]
                            e.wait_ge(act.steps, act.at("rs"))
                            e.wait_ge(dve.steps, dve.at("lg"))
                            e.tensor_scalar(lg, lg, LOG_MIN, None, ALU.max).then_inc(dve.steps, dve.did())
                            e.wait_ge(pool.steps, pool.at("rs"))
                            for plane in (R, I):
                                e.tensor_tensor(unit[:, plane, g], qk[:, 2, plane - 1, g], m1[:, 1, g], ALU.mult).then_inc(dve.steps, dve.did())
                            e.wait_ge(dve.steps, dve.n)
                            e.tensor_scalar(unit[:, 0, g], unit[:, I, g], -1.0, None, ALU.mult).then_inc(dve.steps, dve.did())
                            e.tensor_tensor_scan(L[:, g, 1:], one[:].to_broadcast([C, T]), lg, 0.0, ALU.mult, ALU.add).then_inc(dve.steps, dve.did())
                            e.wait_ge(dve.steps, dve.n)
                            Lt = L[:, g, 1:]
                            l8 = blk(Lt, 8)
                            e.tensor_tensor(blk(F[:, 0, g], 8), l8, l8[:, :, 3:4].to_broadcast([C, 64, 8]), ALU.subtract).then_inc(dve.steps, dve.did("d0"))
                            for half, i in halves:
                                l2 = blk(Lt, 2 * half)
                                mid = l2[:, :, half - 1:half].to_broadcast([C, T // (2 * half), half])
                                e.tensor_tensor(half_of(F[:, i, g], i, True), l2[:, :, half:], mid, ALU.subtract).then_inc(dve.steps, dve.did())
                                e.tensor_tensor(half_of(E[:, i, g], i, False), mid, l2[:, :, :half], ALU.subtract).then_inc(dve.steps, dve.did(f"d{i}"))
                            l32 = blk(Lt, 32)
                            before = blk(L[:, g, 0:T], 32)[:, :, 0:1].to_broadcast([C, 16, 32])
                            e.tensor_tensor(blk(F[:, 3, g], 32), l32, before, ALU.subtract).then_inc(dve.steps, dve.did())
                            e.tensor_tensor(blk(E[:, 3, g], 32), l32[:, :, 31:32].to_broadcast([C, 16, 32]), l32, ALU.subtract).then_inc(dve.steps, dve.did("d3"))
                        elif what == "running":
                            cb = cum[:, :, g].rearrange("p r (c x) -> p r c x", x=16)
                            ub = unit[:, :, g].rearrange("p r (c x) -> p r c x", x=16)
                            A1 = m1[:, 0, g, 0:64].rearrange("p (r c) -> p r c", r=2)
                            A2 = m2[:, 0, g, 0:64].rearrange("p (r c) -> p r c", r=2)
                            e.tensor_copy(cb[:, :, :, 0], ub[:, 1:3, :, 0]).then_inc(dve.steps, dve.did())
                            for x in range(1, 16):
                                e.wait_ge(dve.steps, dve.n)
                                e.tensor_tensor(A1, cb[:, 0:1, :, x - 1].to_broadcast([C, 2, 32]), ub[:, 1:3, :, x], ALU.mult).then_inc(dve.steps, dve.did())
                                e.tensor_tensor(A2, cb[:, 1:2, :, x - 1].to_broadcast([C, 2, 32]), ub[:, 0:2, :, x], ALU.mult).then_inc(dve.steps, dve.did())
                                e.wait_ge(dve.steps, dve.n)
                                e.tensor_tensor(cb[:, :, :, x], A1, A2, ALU.add).then_inc(dve.steps, dve.did())
                        elif what == "blocks":
                            e.memset(tot[:, :, 0::2, 0:1], 0.0).then_inc(dve.steps, dve.did())
                            e.memset(tot[:, :, 1, 0:1], 1.0).then_inc(dve.steps, dve.did())
                            e.wait_ge(dve.steps, dve.n)
                            last = cum[:, :, g].rearrange("p r (c x) -> p r c x", x=16)[:, :, :, 15]
                            e.tensor_copy(tot[:, 0, 1:3, 1:33], last).then_inc(dve.steps, dve.did())
                            e.wait_ge(dve.steps, dve.n)
                            e.tensor_scalar(tot[:, 0, 0, 1:33], tot[:, 0, 2, 1:33], -1.0, None, ALU.mult).then_inc(dve.steps, dve.did())
                            e.wait_ge(dve.steps, dve.n)
                            src, d = 0, 1
                            while d < 32:
                                c_ = 32 - d
                                B1 = m1[:, 0, g, 0:2 * c_].rearrange("p (r c) -> p r c", r=2)
                                B2 = m2[:, 0, g, 0:2 * c_].rearrange("p (r c) -> p r c", r=2)
                                old, new = tot[:, src], tot[:, 1 - src]
                                e.tensor_tensor(B1, old[:, 1:2, 1:1 + c_].to_broadcast([C, 2, c_]), old[:, 1:3, 1 + d:33], ALU.mult).then_inc(dve.steps, dve.did())
                                e.tensor_tensor(B2, old[:, 2:3, 1:1 + c_].to_broadcast([C, 2, c_]), old[:, 0:2, 1 + d:33], ALU.mult).then_inc(dve.steps, dve.did())
                                e.tensor_copy(new[:, :, 1:1 + d], old[:, :, 1:1 + d]).then_inc(dve.steps, dve.did())
                                e.wait_ge(dve.steps, dve.n)
                                e.tensor_tensor(new[:, 1:3, 1 + d:33], B1, B2, ALU.add).then_inc(dve.steps, dve.did())
                                e.wait_ge(dve.steps, dve.n)
                                e.tensor_scalar(new[:, 0, 1 + d:33], new[:, 2, 1 + d:33], -1.0, None, ALU.mult).then_inc(dve.steps, dve.did())
                                e.wait_ge(dve.steps, dve.n)
                                src, d = 1 - src, 2 * d
                        elif what == "turn":
                            w = lambda ap: ap.rearrange("p r (c x) -> p r c x", x=16)
                            pre = lambda lo: tot[:, 1, lo:lo + 2, 0:32].unsqueeze(3).to_broadcast([C, 2, 32, 16])
                            e.tensor_tensor(w(m1[:, :, g]), w(cum[:, 0:1, g].to_broadcast([C, 2, T])), pre(1), ALU.mult).then_inc(dve.steps, dve.did())
                            e.tensor_tensor(w(m2[:, :, g]), w(cum[:, 1:2, g].to_broadcast([C, 2, T])), pre(0), ALU.mult).then_inc(dve.steps, dve.did())
                            e.wait_ge(dve.steps, dve.n)
                            e.tensor_tensor(U(g)[:, 1:3], m1[:, :, g], m2[:, :, g], ALU.add).then_inc(dve.steps, dve.did())
                            e.wait_ge(dve.steps, dve.n)
                            e.tensor_scalar(U(g)[:, 0], U(g)[:, 2], -1.0, None, ALU.mult).then_inc(dve.steps, dve.did())
                            e.wait_ge(dve.steps, dve.n)
                            for j, out, (p1, p2), name_ in ((0, qh[:, 1:3, g], (1, 0), "qh"), (1, kh[:, :, g], (0, 1), "kh")):
                                wide = lambda ri: qk[:, j, ri:ri + 1, g].to_broadcast([C, 2, T])
                                e.tensor_tensor(m1[:, :, g], wide(0), U(g)[:, p1:p1 + 2], ALU.mult).then_inc(dve.steps, dve.did())
                                e.tensor_tensor(m2[:, :, g], wide(1), U(g)[:, p2:p2 + 2], ALU.mult).then_inc(dve.steps, dve.did())
                                e.wait_ge(dve.steps, dve.n)
                                e.tensor_tensor(out, m1[:, :, g], m2[:, :, g], ALU.add).then_inc(dve.steps, dve.did(name_))
                                e.wait_ge(dve.steps, dve.n)
                            e.tensor_scalar(qh[:, 0, g], qh[:, 2, g], -1.0, None, ALU.mult).then_inc(dve.steps, dve.did())
                            e.wait_ge(dve.steps, dve.n)
                        elif what == "split":
                            e.wait_ge(act.steps, act.at("f3"))
                            for p_ in range(2):
                                e.tensor_tensor(ks[:, p_, g], kh[:, p_, g], E[:, 3, g], ALU.mult).then_inc(dve.steps, dve.did("ks"))
                            for i in range(3):
                                for p_ in range(3):
                                    e.tensor_tensor(half_of(Q[i][:, p_, g], i, True), half_of(qh[:, p_, g], i, True), half_of(F[:, i, g], i, True),
                                                    ALU.mult).then_inc(dve.steps, dve.did())
                            for p_ in range(2):
                                e.tensor_tensor(qs[:, p_, g], qh[:, 1 + p_, g], F[:, 3, g], ALU.mult).then_inc(dve.steps, dve.did())

                    in_turn(scan, prepare)
                    if sg is not None:
                        e.wait_ge(pe.steps, pe.at("y3"))
                        e.tensor_copy(y(sg, 0), P[4]).then_inc(dve.steps, dve.did())
            k.end()

        def out(name, b):
            st = pe, act, dve, pool, dma = k.stage(name)
            act_y = Silu(st, "y", P[0], k.w["b_y2"][:, 0:1], h2, tmp[:, 0:2], "z")
            with nc.Block() as block:
                @block.tensor
                def _(e):
                    for i in range(4):
                        ins = e.matmul(P[0], k.w["W_y2"][:, i, :], y(i // 2, i % 2), start=(i == 0), stop=(i == 3))
                    ins.then_inc(pe.steps, pe.did("z"))
                    e.wait_ge(dve.steps, dve.at("yo"))
                    e.matmul(P[1], k.w["W_out2"][:], h2, start=True, stop=True).then_inc(pe.steps, pe.did("o"))

                @block.scalar
                def _(e):
                    e.preload_act_table_set(EXP_LN)
                    act_y.scalar(e)
                    e.wait_ge(pe.steps, pe.at("o"))
                    e.activation(o2, P[1], ACT.Identity, bias=k.w["b_out2"][:, 0:1]).then_inc(act.steps, act.did("o"))

                @block.vector
                def _(e):
                    e.tensor_copy(k.modb[:], k.mod[:, :, :, bass.ds(b, 1)].rearrange("p l s a -> p l (s a)")).then_inc(dve.steps, dve.did())
                    act_y.vector(e)
                    e.wait_ge(act.steps, act.at("o"))
                    x = flat(k.X[:, bass.ds(b, 1), :])
                    e.scalar_tensor_tensor(x, o2, m[:, GA:GA + 1], x, ALU.mult, ALU.add).then_inc(dve.steps, dve.did())
            k.end()

        pe, act, dve, pool, dma = k.stage("gla_start")
        with nc.Block() as block:
            @block.vector
            def _(e):
                for t in (one, L):
                    e.memset(t[:], 1.0 if t is one else 0.0).then_inc(dve.steps, dve.did())
                for t in (K[1], K[2]):
                    e.memset(t[:], 0.0).then_inc(dve.steps, dve.did())
                e.tensor_copy(H0[:, :, 32:96], k.w["h0"][:]).then_inc(dve.steps, dve.did())
                e.tensor_scalar(H0[:, :, 0:32], k.w["h0"][:, :, 32:64], -1.0, None, ALU.mult).then_inc(dve.steps, dve.did())
        k.end()
        stage("gla_first", None, 0, 0)
        with nc.Fori(0, B - 1) as b:
            stage("gla_scan0", 0, b, 1)
            stage("gla_scan1", 1, b + 1, 0)
            out("gla_out", b)
        stage("gla_scan0_last", 0, B - 1, 1)
        stage("gla_scan1_last", 1, None, None)
        out("gla_out_last", B - 1)


def routed_mlp(k):
    nc = k.nc
    with ExitStack() as s:
        xb, h = k.sb("m_xb", [C, T], stack=s), k.sb("m_h", [C, T], stack=s)
        tmp = k.sb("m_tmp", [C, 3, T], stack=s)
        masked = k.sb("m_masked", [C, 2, T], stack=s)
        r = k.sb("m_r", [C, 4, T], stack=s)
        dw = k.sb("m_dw", [C, 1], stack=s)
        gate = k.sb("m_gate", [C, C], stack=s)
        bias = k.sb("m_bias", [C, 1], stack=s)
        P = [k.ps[:, i, :] for i in range(8)]
        pe, act, dve, pool, dma = k.stage("mlp2_start")
        with nc.Block() as block:
            @block.vector
            def _(e):
                e.tensor_tensor(dw[:], k.w["gate_w2"][:, 1:2], k.w["gate_w2"][:, 0:1], ALU.subtract).then_inc(dve.steps, dve.did())
                e.tensor_reduce(bias[:], k.w["b2_2"][:], AX.X, ALU.add).then_inc(dve.steps, dve.did())
                e.wait_ge(dve.steps, dve.n)
                e.tensor_copy(gate[:], dw[:, 0:1].to_broadcast([C, C])).then_inc(dve.steps, dve.did())
        k.end()
        with nc.Fori(0, B) as b:
            st = pe, act, dve, pool, dma = k.stage("mlp2")
            m = k.modb[:, 2, :]
            n = Norm(k, st, "n", 0, 1, xb[:], h[:], m, SB_, CB, tmp)
            order = [(p_, f) for p_ in (2, 0, 1) for f in range(4)]
            with nc.Block() as block:
                @block.gpsimd
                def _(e):
                    e.tensor_copy(xb[:], flat(k.X[:, bass.ds(b, 1), :])).then_inc(pool.steps, pool.did("xb"))

                @block.tensor
                def _(e):
                    def down(i):
                        p_, f = order[i]
                        e.wait_ge(act.steps, act.at(f"r{i}"))
                        e.matmul(P[7], k.w["w2_2"][:, p_, f, :], r[:, i % 4, :], start=(i == 0), stop=(i == 11)).then_inc(pe.steps, pe.did(f"d{i}"))

                    e.wait_ge(pool.steps, pool.at("xb"))
                    n.tensor(e)
                    e.wait_ge(dve.steps, dve.at("nh"))
                    e.matmul(P[2], gate[:], h[:], start=True, stop=True).then_inc(pe.steps, pe.did("score"))
                    for i, (p_, f) in enumerate(order):
                        if i >= 4:
                            e.wait_ge(act.steps, act.at(f"r{i - 4}"))
                        if p_ < 2:
                            e.wait_ge(dve.steps, dve.at(f"m{p_}"))
                        x = h[:] if p_ == 2 else masked[:, p_, :]
                        e.matmul(P[3 + i % 4], k.w["w1_2"][:, p_, ts(f, C)], x, start=True, stop=True).then_inc(pe.steps, pe.did(f"u{i}"))
                        if i >= 2:
                            down(i - 2)
                    down(10)
                    down(11)

                @block.scalar
                def _(e):
                    e.preload_act_table_set(EXP_LN)
                    n.scalar(e)
                    for i, (p_, f) in enumerate(order):
                        e.wait_ge(pe.steps, pe.at(f"u{i}"))
                        if i >= 4:
                            e.wait_ge(pe.steps, pe.at(f"d{i - 4}"))
                        e.activation(r[:, i % 4, :], P[3 + i % 4], ACT.Relu, bias=k.w["b1_2"][:, p_, f:f + 1]).then_inc(act.steps, act.did(f"r{i}"))
                    e.wait_ge(pe.steps, pe.at("d11"))
                    e.activation(h[:], P[7], ACT.Identity, bias=bias[:, 0:1]).then_inc(act.steps, act.did("o"))

                @block.vector
                def _(e):
                    e.tensor_copy(k.modb[:], k.mod[:, :, :, bass.ds(b, 1)].rearrange("p l s a -> p l (s a)")).then_inc(dve.steps, dve.did())
                    e.wait_ge(dve.steps, dve.n)
                    n.vector(e)
                    e.wait_ge(pe.steps, pe.at("score"))
                    e.wait_ge(dve.steps, dve.n)
                    for x, op in ((0, ALU.is_le), (1, ALU.is_gt)):
                        e.scalar_tensor_tensor(masked[:, x, :], P[2], 0.0, h[:], op, ALU.mult).then_inc(dve.steps, dve.did(f"m{x}"))
                    e.wait_ge(act.steps, act.at("o"))
                    e.scalar_tensor_tensor(flat(k.X[:, bass.ds(b, 1), :]), h[:], m[:, GB:GB + 1], xb[:], ALU.mult, ALU.add).then_inc(dve.steps, dve.did())
            k.end()


def delta_rule(k):
    nc = k.nc
    TAPS, NH, NT = 4, 8, 4
    with ExitStack() as s:
        w_qk = k.sb("d_w_qk", [C, TAPS, 2, 8 * C], stack=s)
        w_v = k.sb("d_w_v", [C, TAPS, 256], stack=s)
        neg_a = k.sb("d_neg_a", [C, NH], stack=s)
        xb = k.sb("d_xb", [C, T], stack=s)
        hp = k.sb("d_hp", [C, T + 3], stack=s)
        QK = k.sb("d_QK", [C, 2, NH, T], stack=s)
        KT = k.sb("d_KT", [C, NT, NH, C], stack=s)
        V = k.sb("d_V", [C, NT, 256], stack=s)
        G = k.sb("d_gate", [C, NT, 256], stack=s)
        O = k.sb("d_O", [C, NT, NH, 32], stack=s)
        sq = k.sb("d_sq", [C, 2, 2, T], stack=s)
        small = {n: k.sb("d_" + n, [C, NT, NH], stack=s) for n in
                 ("beta", "z", "g", "t", "gc", "gam", "end", "ga", "qn", "kn", "gtot", "n2", "ss", "sp", "eq", "ek")}
        ssq = k.sb("d_ssq", [C, 2, NT, NH], stack=s)
        S = k.sb("d_S", [C, NH, 32], stack=s)
        D = k.sb("d_D", [C, 2, 4, C], stack=s)
        A, Pm = (k.sb("d_" + n, [C, 6, 4, C], stack=s) for n in ("A", "P"))
        M = k.sb("d_M", [C, 4, 5, 4, 32], stack=s)
        A32, Y = (k.sb("d_" + n, [C, 4, 4, 32], stack=s) for n in ("A32", "Y"))
        F, X, W = (k.sb("d_" + n, [C, 2, 4, 32], stack=s) for n in ("F", "X", "W"))
        rv, zz, ze, o1 = (k.sb("d_" + n, [C, 2, 4, 32], stack=s) for n in ("r", "zz", "ze", "o1"))
        tmp3 = k.sb("d_tmp3", [C, 3, T], stack=s)
        P = [k.ps[:, i, :] for i in range(8)]
        m = k.modb[:, 3, :]

        pe, act, dve, pool, dma = k.stage("delta_start")
        with nc.Block() as block:
            @block.scalar
            def _(e):
                e.activation(neg_a[:], k.w["A_log"][:], ACT.Exp).then_inc(act.steps, act.did("a"))

            @block.vector
            def _(e):
                e.memset(hp[:, 0:3], 0.0).then_inc(dve.steps, dve.did())
                for j in range(TAPS):
                    e.tensor_tensor(w_v[:, j], k.w["Wv3"][:], k.w["conv_v"][:, j], ALU.mult).then_inc(dve.steps, dve.did())
                e.wait_ge(act.steps, act.at("a"))
                e.tensor_scalar(neg_a[:], neg_a[:], -1.0, None, ALU.mult).then_inc(dve.steps, dve.did())
        k.end()
        taps = QK[:].rearrange("p c h t -> p (c h t)")[:, 0:TAPS * 8 * C].rearrange("p (j f) -> p j f", j=TAPS)
        for n in range(2):
            pe, act, dve, pool, dma = k.stage(f"delta_taps{n}")
            with nc.Block() as block:
                @block.sync
                def _(e):
                    src = k.dram["conv_qk"][n].rearrange("(a j) f -> a j f", a=1)
                    e.dma_start(taps, src.to_broadcast([C, TAPS, 8 * C])).then_inc(dma.steps, dma.did("taps"))

                @block.vector
                def _(e):
                    e.wait_ge(dma.steps, dma.at("taps"))
                    for j in range(TAPS):
                        e.tensor_tensor(w_qk[:, j, n], k.w["Wqk3"][:, n], taps[:, j], ALU.mult).then_inc(dve.steps, dve.did())
            k.end()

        with nc.Fori(0, B) as b:
            st = pe, act, dve, pool, dma = k.stage("delta_project")
            n = Norm(k, st, "n", 0, 1, xb[:], hp[:, 3:], m, SA, CA, tmp3)
            def silu_tables(e):
                e.preload_act_table_set("silu_and_others")
            with nc.Block() as block:
                @block.gpsimd
                def _(e):
                    e.tensor_copy(xb[:], flat(k.X[:, bass.ds(b, 1), :])).then_inc(pool.steps, pool.did("xb"))
                    e.memset(S[:], 0.0).then_inc(pool.steps, pool.did())
                    for h in range(NH):
                        if h >= 2:
                            e.wait_ge(pe.steps, pe.at(f"ss{h - 2}"))
                        for c in range(2):
                            e.wait_ge(act.steps, act.at(f"qk{c}{h}"))
                            e.tensor_tensor(sq[:, h % 2, c], QK[:, c, h], QK[:, c, h], ALU.mult).then_inc(pool.steps, pool.did(f"sq{h}"))

                @block.tensor
                def _(e):
                    def sums(h):
                        e.wait_ge(pool.steps, pool.at(f"sq{h}"))
                        for c in range(2):
                            for i in range(NT):
                                ins = e.matmul(P[2][:, c * 32 + i * 8 + h:c * 32 + i * 8 + h + 1], sq[:, h % 2, c, ts(i, C)],
                                               k.w["ones3"][:, 0:1], start=True, stop=True)
                        ins.then_inc(pe.steps, pe.did(f"ss{h}"))

                    e.wait_ge(pool.steps, pool.at("xb"))
                    n.tensor(e)
                    e.wait_ge(dve.steps, dve.at("nh"))
                    for i in range(NT):
                        e.matmul(P[3][:, ts(i, 16)], hp[:, 3 + i * C:3 + i * C + C], k.w["Wab3"][:], start=True, stop=True)
                    for i in range(NT):
                        for j in range(TAPS):
                            ins = e.matmul(P[4 + i][:, 0:256], hp[:, j + i * C:j + i * C + C], w_v[:, j], start=(j == 0),
                                           stop=(j == TAPS - 1))
                        ins = e.matmul(P[4 + i][:, 256:512], hp[:, 3 + i * C:3 + i * C + C], k.w["Wg3"][:], start=True, stop=True)
                    ins.then_inc(pe.steps, pe.did("vg"))
                    for h in range(NH):
                        for c in range(2):
                            i = 2 * h + c
                            bank = P[4 + i % 4]
                            (e.wait_ge(act.steps, act.at("v")) if i < 4 else e.wait_ge(act.steps, act.at(f"qk{c}{h - 2}")))
                            for j in range(TAPS):
                                ins = e.matmul(bank, w_qk[:, j, c, ts(h, C)], hp[:, j:j + T], start=(j == 0), stop=(j == TAPS - 1))
                            ins.then_inc(pe.steps, pe.did(f"qk{c}{h}"))
                        if h >= 2:
                            sums(h - 2)
                    sums(NH - 2)
                    sums(NH - 1)

                @block.scalar
                def _(e):
                    e.preload_act_table_set(EXP_LN)
                    n.scalar(e)
                    e.wait_ge(pe.steps, pe.at("vg"))
                    for i in range(NT):
                        e.activation(V[:, i], P[4 + i][:, 0:256], ACT.Silu).then_inc(act.steps, act.did())
                        e.activation(G[:, i], P[4 + i][:, 256:512], ACT.Silu).then_inc(act.steps, act.did("v"))
                    for h in range(NH):
                        for c in range(2):
                            e.wait_ge(pe.steps, pe.at(f"qk{c}{h}"))
                            e.activation(QK[:, c, h], P[4 + (2 * h + c) % 4], ACT.Silu).then_inc(act.steps, act.did(f"qk{c}{h}"))

                @block.vector
                def _(e):
                    e.tensor_copy(k.modb[:], k.mod[:, :, :, bass.ds(b, 1)].rearrange("p l s a -> p l (s a)")).then_inc(dve.steps, dve.did())
                    e.wait_ge(dve.steps, dve.n)
                    n.vector(e)
                    e.wait_ge(pe.steps, pe.at("vg"))
                    ab = P[3][:, 0:64].rearrange("p (i x) -> p i x", i=NT)
                    e.tensor_tensor(small["z"][:], ab[:, :, 0:8], k.w["dt_bias"][:].unsqueeze(1).to_broadcast([C, NT, NH]), ALU.add).then_inc(dve.steps, dve.did())
                    e.tensor_scalar(small["beta"][:], ab[:, :, 8:16], LEAST, None, ALU.max).then_inc(dve.steps, dve.did())
                    e.wait_ge(pe.steps, pe.at("ss7"))
                    e.tensor_scalar(ssq[:].rearrange("p c i h -> p (c i h)"), P[2][:, 0:64], 1e-12, None, ALU.max).then_inc(dve.steps, dve.did())
            k.end()

            st = pe, act, dve, pool, dma = k.stage("delta_scalars")
            q = small
            with nc.Block() as block:
                @block.vector
                def _(e):
                    e.tensor_scalar(q["t"][:], q["z"][:], -1.0, None, ALU.mult).then_inc(dve.steps, dve.did())
                    e.wait_ge(dve.steps, dve.n)
                    e.tensor_tensor(q["t"][:], q["t"][:], q["z"][:], ALU.min).then_inc(dve.steps, dve.did("negabs"))
                    e.tensor_scalar(q["z"][:], q["z"][:], 0.0, None, ALU.max).then_inc(dve.steps, dve.did())
                    e.wait_ge(act.steps, act.at("sp"))
                    e.wait_ge(dve.steps, dve.n)
                    e.tensor_tensor(q["g"][:], q["z"][:], q["sp"][:], ALU.add).then_inc(dve.steps, dve.did())
                    e.wait_ge(dve.steps, dve.n)
                    e.tensor_tensor(q["g"][:], q["g"][:], neg_a[:].unsqueeze(1).to_broadcast([C, NT, NH]), ALU.mult).then_inc(dve.steps, dve.did("g"))
                    e.wait_ge(pe.steps, pe.at("cum"))
                    f = lambda t: t[:].rearrange("p i h -> p (i h)")
                    e.tensor_copy(f(q["gc"]), P[0][:, 0:32]).then_inc(dve.steps, dve.did())
                    e.tensor_copy(f(q["gtot"]), P[0][:, 32:64]).then_inc(dve.steps, dve.did())
                    e.wait_ge(dve.steps, dve.n)
                    e.tensor_tensor(q["end"][:], q["gtot"][:], q["gc"][:], ALU.subtract).then_inc(dve.steps, dve.did("gc"))
                    e.wait_ge(act.steps, act.at("norms"))
                    e.scalar_tensor_tensor(q["gam"][:], q["n2"][:], 2.0, q["beta"][:], ALU.mult, ALU.mult).then_inc(dve.steps, dve.did())
                    v4 = V[:].rearrange("p i (h x) -> p i h x", h=NH)
                    e.tensor_tensor(v4, v4, q["kn"][:].unsqueeze(3).to_broadcast([C, NT, NH, 32]), ALU.mult).then_inc(dve.steps, dve.did())
                    for r in range(8):
                        if r % 2:
                            e.wait_ge(pe.steps, pe.at(f"kt{r}"))
                            e.tensor_copy(KT[:, r // 2, ts(r % 2, 4)].rearrange("p h x -> p (h x)"), P[1 + r % 7]).then_inc(dve.steps, dve.did(f"kt{r}"))

                @block.scalar
                def _(e):
                    e.preload_act_table_set(EXP_LN)
                    e.activation(q["beta"][:], q["beta"][:], ACT.Exp, scale=-1.0).then_inc(act.steps, act.did())
                    e.wait_ge(act.steps, act.n)
                    e.activation(q["beta"][:], q["beta"][:], ACT.Ln, bias=1.0).then_inc(act.steps, act.did())
                    e.wait_ge(act.steps, act.n)
                    e.activation(q["beta"][:], q["beta"][:], ACT.Exp, scale=-1.0).then_inc(act.steps, act.did())
                    e.wait_ge(dve.steps, dve.at("negabs"))
                    e.activation(q["t"][:], q["t"][:], ACT.Exp).then_inc(act.steps, act.did())
                    e.wait_ge(act.steps, act.n)
                    e.activation(q["sp"][:], q["t"][:], ACT.Ln, bias=1.0).then_inc(act.steps, act.did("sp"))
                    e.activation(ssq[:], ssq[:], ACT.Ln).then_inc(act.steps, act.did())
                    e.wait_ge(act.steps, act.n)
                    e.activation(q["qn"][:], ssq[:, 0], ACT.Exp, scale=-0.5).then_inc(act.steps, act.did())
                    e.activation(q["n2"][:], ssq[:, 1], ACT.Exp, scale=-1.0).then_inc(act.steps, act.did())
                    e.activation(q["kn"][:], ssq[:, 1], ACT.Exp, scale=0.5).then_inc(act.steps, act.did("norms"))
                    e.wait_ge(dve.steps, dve.at("gc"))
                    e.activation(q["ga"][:], q["gc"][:], ACT.Exp).then_inc(act.steps, act.did())
                    e.activation(q["end"][:], q["end"][:], ACT.Exp).then_inc(act.steps, act.did())
                    e.activation(q["gtot"][:], q["gtot"][:], ACT.Exp).then_inc(act.steps, act.did())
                    for r in range(0, 8, 2):
                        e.wait_ge(pe.steps, pe.at(f"kt{r}"))
                        e.activation(KT[:, r // 2, ts(r % 2, 4)].rearrange("p h x -> p (h x)"), P[1 + r % 7], ACT.Copy).then_inc(act.steps, act.did(f"kt{r}"))

                @block.tensor
                def _(e):
                    def turn(r):
                        for h in range(4):
                            ins = e.transpose(P[1 + r % 7][:, ts(h, C)], QK[:, 1, (r % 2) * 4 + h, ts(r // 2, C)], k.w["ident"][:])
                        ins.then_inc(pe.steps, pe.did(f"kt{r}"))

                    for r in range(7):
                        turn(r)
                    e.wait_ge(dve.steps, dve.at("g"))
                    gg = q["g"][:].rearrange("p i h -> p (i h)")
                    e.matmul(P[0][:, 0:32], k.w["upto3"][:], gg, start=True, stop=True)
                    e.matmul(P[0][:, 32:64], k.w["ones3"][:], gg, start=True, stop=True).then_inc(pe.steps, pe.did("cum"))
                    e.wait_ge(act.steps, act.at("kt0"))
                    turn(7)
            k.end()

            st = pe, act, dve, pool, dma = k.stage("delta_tiles")
            f4 = lambda ap: ap.rearrange("p h t -> p (h t)")
            v4 = lambda ap: ap.rearrange("p (h t) -> p h t", h=4)
            p32 = lambda bank: v4(P[bank][:, 0:128])
            p_inv = lambda step, u: p32(4 * u + (1 if step == "y" else 0))
            INVERT = [("x", 0)] + [(step, l) for l in range(1, 5) for step in "fxy" if (step, l) != ("x", 4)]
            SOLVE = [("state", 0), ("solve", 0)] + [(step, j) for j in range(1, 4) for step in ("before", "solve")] + [("finish", 0)]
            MAKE = {0: (0, 0), 1: (1, 0), 3: (0, 1), 4: (1, 1), 5: (0, 2), 6: (1, 2)}

            def in_turn(make, invert, solve):
                for turn in MAKE:
                    make(*MAKE[turn])
                for i in range(NT + 1):
                    for turn, (step, l) in enumerate(INVERT):
                        if i and turn < len(SOLVE):
                            for u in range(2):
                                solve(2 * (i - 1) + u, *SOLVE[turn])
                        if i + 1 < NT and turn in MAKE:
                            u, part = MAKE[turn]
                            make(2 * (i + 1) + u, part)
                        if i < NT:
                            for u in range(2):
                                invert(2 * i + u, step, l)

            with nc.Block() as block:
                @block.tensor
                def _(e):
                    def make(n, part):
                        i, u = n // 2, n % 2
                        t = ts(i, C)
                        if part == 0:
                            if n >= 2:
                                e.wait_ge(dve.steps, dve.at(f"A{n - 2}"))
                            for h in range(4):
                                H = 4 * u + h
                                ins = e.matmul(P[4 * u + 2][:, ts(h, C)], q["g"][:, i, H:H + 1].to_broadcast([C, C]), k.w["upto3"][:], start=True, stop=True)
                            ins.then_inc(pe.steps, pe.did(f"gb{n}"))
                        else:
                            e.wait_ge(dve.steps, dve.at((f"d{n}", f"P{n}")[part - 1]))
                            for h in range(4):
                                H = 4 * u + h
                                ins = e.matmul(P[4 * u + 2][:, ts(h, C)], QK[:, 1, H, t], QK[:, part - 1, H, t], start=True, stop=True)
                            ins.then_inc(pe.steps, pe.did((f"kq{n}", f"kk{n}")[part - 1]))

                    def products(step, stationary, moving, u):
                        for h in range(4):
                            for j in range(4):
                                rows = ts(j, 32)
                                ins = e.matmul(p_inv(step, u)[rows, h], stationary[rows, h], moving(rows, h), start=True, stop=True,
                                               tile_position=(32 * j, 32 * j))
                        return ins

                    def invert(n, step, l):
                        u = n % 2
                        if l == 0:
                            e.wait_ge(pool.steps, pool.at(f"c0{n}"))
                            products("x", M[:, n % 4, 0], lambda rows, h: k.w["eye32"][rows], u).then_inc(pe.steps, pe.did(f"x0{n}"))
                        elif step == "f":
                            if l == 1:
                                e.wait_ge(pool.steps, pool.at(f"c1{n}"))
                            e.wait_ge(dve.steps, dve.at(f"x{l - 1}{n}"))
                            products("f", M[:, n % 4, l], lambda rows, h: X[rows, u, h], u).then_inc(pe.steps, pe.did(f"f{l}{n}"))
                        elif step == "x":
                            e.wait_ge(act.steps, act.at(f"f{l}{n}"))
                            e.wait_ge(dve.steps, dve.at(f"y{l - 1}{n}"))
                            products("x", Y[:, n % 4], lambda rows, h: F[rows, u, h], u).then_inc(pe.steps, pe.did(f"x{l}{n}"))
                        else:
                            e.wait_ge(act.steps, act.at(f"f{l}{n}"))
                            e.wait_ge(dve.steps, dve.at(f"y{l - 1}{n}"))
                            products("y", F[:, u], lambda rows, h: Y[rows, n % 4, h], u).then_inc(pe.steps, pe.did(f"y{l}{n}"))

                    def solve(n, step, j):
                        i, u, rows = n // 2, n % 2, ts(j, 32)
                        if step == "state":
                            if n >= 2:
                                e.wait_ge(dve.steps, dve.at(f"out{n - 2}"))
                            for bank_half, c in ((0, 1), (1, 0)):
                                for h in range(4):
                                    H = 4 * u + h
                                    ins = e.matmul(P[4 * u + 3][:, bank_half * 128 + 32 * h:bank_half * 128 + 32 * h + 32], QK[:, c, H, ts(i, C)],
                                                   S[:, H], start=True, stop=True)
                            ins.then_inc(pe.steps, pe.did(f"s{n}"))
                        elif step == "before":
                            e.wait_ge(dve.steps, dve.at(f"w{j - 1}{n}"))
                            for h in range(4):
                                ins = e.matmul(P[4 * u + 3][rows, ts(h, 32)], A[:, n % 6, h, rows], W[:, u, h], start=True, stop=True,
                                               tile_position=(0, 32 * j))
                            ins.then_inc(pe.steps, pe.did(f"b{j}{n}"))
                        elif step == "solve":
                            e.wait_ge(dve.steps, dve.at(f"y4{n}"))
                            e.wait_ge(dve.steps, dve.at(f"r{j}{n}"))
                            for h in range(4):
                                ins = e.matmul(P[4 * u + 3][rows, 256 + 32 * h:288 + 32 * h], Y[rows, n % 4, h], rv[rows, u, h], start=True,
                                               stop=True, tile_position=(32 * j, 32 * j))
                            ins.then_inc(pe.steps, pe.did(f"w{j}{n}"))
                        else:
                            e.wait_ge(dve.steps, dve.at(f"z{n}"))
                            for h in range(4):
                                ins = e.matmul(P[4 * u + 3][:, 384 + 32 * h:416 + 32 * h], Pm[:, n % 6, h], zz[:, u, h], start=True, stop=True)
                            for h in range(4):
                                ins = e.matmul(P[4 * u + 3][:, 256 + 32 * h:288 + 32 * h], KT[:, i, 4 * u + h], ze[:, u, h], start=True, stop=True)
                            ins.then_inc(pe.steps, pe.did(f"o{n}"))

                    in_turn(make, invert, solve)

                @block.gpsimd
                def _(e):
                    def make(n, part):
                        u = n % 2
                        if part == 0:
                            e.wait_ge(act.steps, act.at(f"d{n}"))
                            e.tensor_tensor(D[:, u], D[:, u], k.w["upto3"][:].unsqueeze(1).to_broadcast([C, 4, C]), ALU.mult).then_inc(pool.steps, pool.did(f"d{n}"))
                        elif part == 2:
                            e.wait_ge(act.steps, act.at(f"a{n}"))
                            for l, levels in enumerate((slice(0, 1), slice(1, 5))):
                                many = levels.stop - levels.start
                                e.tensor_tensor(M[:, n % 4, levels], A32[:, n % 4].unsqueeze(1).to_broadcast([C, many, 4, 32]),
                                                k.w["joins"][:, levels].unsqueeze(2).to_broadcast([C, many, 4, 32]), ALU.mult).then_inc(pool.steps, pool.did(f"c{l}{n}"))

                    in_turn(make, lambda n, step, l: None, lambda n, step, j: None)

                @block.scalar
                def _(e):
                    def make(n, part):
                        u = n % 2
                        if part == 0:
                            e.wait_ge(dve.steps, dve.at(f"d{n}"))
                            e.activation(D[:, u], D[:, u], ACT.Exp).then_inc(act.steps, act.did(f"d{n}"))
                        elif part == 2:
                            e.wait_ge(dve.steps, dve.at(f"A{n}"))
                            for j in range(4):
                                e.activation(A32[ts(j, 32), n % 4], A[ts(j, 32), n % 6, :, ts(j, 32)], ACT.Copy).then_inc(act.steps, act.did(f"a{n}"))

                    def invert(n, step, l):
                        if step == "f":
                            e.wait_ge(pe.steps, pe.at(f"f{l}{n}"))
                            e.activation(F[:, n % 2], p_inv("f", n % 2), ACT.Copy).then_inc(act.steps, act.did(f"f{l}{n}"))

                    e.preload_act_table_set(EXP_LN)
                    in_turn(make, invert, lambda n, step, j: None)

                @block.vector
                def _(e):
                    wide = lambda name, i, u, w: q[name][:, i, 4 * u:4 * u + 4].unsqueeze(2).to_broadcast([C, 4, w])
                    eye32 = k.w["eye32"][:].unsqueeze(1).to_broadcast([C, 4, 32])

                    def make(n, part):
                        i, u = n // 2, n % 2
                        if part == 0:
                            e.wait_ge(pe.steps, pe.at(f"gb{n}"))
                            for h in range(4):
                                e.tensor_scalar(D[:, u, h], P[4 * u + 2][:, ts(h, C)], q["gc"][:, i, 4 * u + h:4 * u + h + 1], 0.0,
                                                ALU.subtract, ALU.min).then_inc(dve.steps, dve.did(f"d{n}"))
                        elif part == 1:
                            e.wait_ge(pe.steps, pe.at(f"kq{n}"))
                            e.wait_ge(pool.steps, pool.at(f"d{n}"))
                            e.tensor_tensor(Pm[:, n % 6], v4(P[4 * u + 2]), D[:, u], ALU.mult).then_inc(dve.steps, dve.did(f"P{n}"))
                            e.tensor_tensor(D[:, u], D[:, u], wide("gam", i, u, C), ALU.mult).then_inc(dve.steps, dve.did(f"dg{n}"))
                        else:
                            e.wait_ge(pe.steps, pe.at(f"kk{n}"))
                            e.wait_ge(dve.steps, dve.at(f"dg{n}"))
                            e.tensor_tensor(A[:, n % 6], v4(P[4 * u + 2]), D[:, u], ALU.mult).then_inc(dve.steps, dve.did(f"A{n}"))

                    def invert(n, step, l):
                        u = n % 2
                        if l == 0:
                            e.wait_ge(pe.steps, pe.at(f"x0{n}"))
                            e.tensor_tensor(X[:, u], eye32, p_inv("x", u), ALU.subtract).then_inc(dve.steps, dve.did(f"x0{n}"))
                            e.tensor_tensor(Y[:, n % 4], eye32, M[:, n % 4, 0], ALU.subtract).then_inc(dve.steps, dve.did(f"y0{n}"))
                        elif step == "x":
                            e.wait_ge(pe.steps, pe.at(f"x{l}{n}"))
                            e.tensor_tensor(X[:, u], X[:, u], p_inv("x", u), ALU.subtract).then_inc(dve.steps, dve.did(f"x{l}{n}"))
                        elif step == "y":
                            e.wait_ge(pe.steps, pe.at(f"y{l}{n}"))
                            e.tensor_tensor(Y[:, n % 4], Y[:, n % 4], p_inv("y", u), ALU.subtract).then_inc(dve.steps, dve.did(f"y{l}{n}"))

                    def solve(n, step, j):
                        i, u, rows = n // 2, n % 2, ts(j, 32)
                        s_u = S[:, ts(u, 4)]
                        if step == "state":
                            e.memset(W[:, u], 0.0).then_inc(dve.steps, dve.did())
                            e.wait_ge(pe.steps, pe.at(f"s{n}"))
                            e.tensor_tensor(rv[:, u], v4(P[4 * u + 3][:, 0:128]), wide("ga", i, u, 32), ALU.mult).then_inc(dve.steps, dve.did())
                            e.tensor_tensor(o1[:, u], v4(P[4 * u + 3][:, 128:256]), wide("ga", i, u, 32), ALU.mult).then_inc(dve.steps, dve.did())
                            e.wait_ge(dve.steps, dve.n)
                            e.tensor_tensor(rv[:, u], v4(V[:, i, ts(u, 128)]), rv[:, u], ALU.subtract).then_inc(dve.steps, dve.did(f"r0{n}"))
                            e.tensor_tensor(s_u, s_u, wide("gtot", i, u, 32), ALU.mult).then_inc(dve.steps, dve.did())
                        elif step == "before":
                            e.wait_ge(pe.steps, pe.at(f"b{j}{n}"))
                            e.tensor_tensor(rv[rows, u], rv[rows, u], p32(4 * u + 3)[rows], ALU.subtract).then_inc(dve.steps, dve.did(f"r{j}{n}"))
                        elif step == "solve":
                            e.wait_ge(pe.steps, pe.at(f"w{j}{n}"))
                            e.tensor_copy(W[rows, u], v4(P[4 * u + 3][rows, 256:384])).then_inc(dve.steps, dve.did(f"w{j}{n}"))
                            if j == 3:
                                e.wait_ge(dve.steps, dve.n)
                                e.tensor_tensor(zz[:, u], W[:, u], wide("gam", i, u, 32), ALU.mult).then_inc(dve.steps, dve.did())
                                e.wait_ge(dve.steps, dve.n)
                                e.tensor_tensor(ze[:, u], zz[:, u], wide("end", i, u, 32), ALU.mult).then_inc(dve.steps, dve.did(f"z{n}"))
                        else:
                            e.wait_ge(pe.steps, pe.at(f"o{n}"))
                            e.tensor_tensor(s_u, s_u, v4(P[4 * u + 3][:, 256:384]), ALU.add).then_inc(dve.steps, dve.did())
                            e.tensor_tensor(o1[:, u], o1[:, u], v4(P[4 * u + 3][:, 384:512]), ALU.add).then_inc(dve.steps, dve.did())
                            e.wait_ge(dve.steps, dve.n)
                            e.tensor_tensor(O[:, i, ts(u, 4)], o1[:, u], wide("qn", i, u, 32), ALU.mult).then_inc(dve.steps, dve.did(f"out{n}"))

                    in_turn(make, invert, solve)
            k.end()

            st = pe, act, dve, pool, dma = k.stage("delta_out")
            O2 = sq[:].rearrange("p a c t -> p (a c t)")[:, 0:1024]
            OT = sq[:].rearrange("p a c t -> p (a c) t")
            o3 = O[:].rearrange("p i h x -> p (i h) x")
            flat_s = lambda n: q[n][:].rearrange("p i h -> p (i h)")
            with nc.Block() as block:
                @block.vector
                def _(e):
                    e.tensor_tensor(O2, O[:].rearrange("p i h x -> p (i h x)"), O[:].rearrange("p i h x -> p (i h x)"), ALU.mult).then_inc(dve.steps, dve.did())
                    e.wait_ge(dve.steps, dve.n)
                    e.tensor_reduce(flat_s("t"), O2.rearrange("p (a x) -> p a x", x=32), AX.X, ALU.add).then_inc(dve.steps, dve.did())
                    e.wait_ge(dve.steps, dve.n)
                    e.tensor_scalar(flat_s("t"), flat_s("t"), 1.0 / 32, 1e-5, ALU.mult, ALU.add).then_inc(dve.steps, dve.did("ms"))
                    e.tensor_tensor(G[:].rearrange("p i (h x) -> p (i h) x", x=32), G[:].rearrange("p i (h x) -> p (i h) x", x=32),
                                             k.w["o_norm_w"][:].unsqueeze(1).to_broadcast([C, 32, 32]), ALU.mult).then_inc(dve.steps, dve.did())
                    e.wait_ge(act.steps, act.at("rms"))
                    e.wait_ge(dve.steps, dve.n)
                    e.tensor_tensor(o3, o3, flat_s("t").unsqueeze(2).to_broadcast([C, 32, 32]), ALU.mult).then_inc(dve.steps, dve.did())
                    e.wait_ge(dve.steps, dve.n)
                    e.tensor_tensor(O[:].rearrange("p i h x -> p (i h x)"), O[:].rearrange("p i h x -> p (i h x)"),
                                             G[:].rearrange("p i x -> p (i x)"), ALU.mult).then_inc(dve.steps, dve.did("o"))
                    e.wait_ge(pe.steps, pe.at("oT"))
                    e.tensor_copy(OT[:, 0], P[0]).then_inc(dve.steps, dve.did("oT"))
                    e.wait_ge(pe.steps, pe.at("att"))
                    e.scalar_tensor_tensor(flat(k.X[:, bass.ds(b, 1), :]), P[2], m[:, GA:GA + 1], xb[:], ALU.mult, ALU.add).then_inc(dve.steps, dve.did())

                @block.scalar
                def _(e):
                    e.preload_act_table_set(EXP_LN)
                    e.wait_ge(dve.steps, dve.at("ms"))
                    e.activation(flat_s("t"), flat_s("t"), ACT.Ln).then_inc(act.steps, act.did())
                    e.wait_ge(act.steps, act.n)
                    e.activation(flat_s("t"), flat_s("t"), ACT.Exp, scale=-0.5).then_inc(act.steps, act.did("rms"))
                    e.wait_ge(pe.steps, pe.at("oT"))
                    e.activation(OT[:, 1], P[1], ACT.Copy).then_inc(act.steps, act.did("oT"))

                @block.tensor
                def _(e):
                    e.wait_ge(dve.steps, dve.at("o"))
                    for u in range(2):
                        for i in range(NT):
                            ins = e.transpose(P[u][:, ts(i, C)], O[:, i, ts(u, 4)].rearrange("p h x -> p (h x)"), k.w["ident"][:])
                    ins.then_inc(pe.steps, pe.did("oT"))
                    for u, w_ in ((0, dve), (1, act)):
                        e.wait_ge(w_.steps, w_.at("oT"))
                        ins = e.matmul(P[2], k.w["Wo3"][:, u, :], OT[:, u], start=(u == 0), stop=(u == 1))
                    ins.then_inc(pe.steps, pe.did("att"))
            k.end()


def channel_mix(k):
    nc = k.nc
    with ExitStack() as s:
        xb, dl, xr, xk, kk, rr, tmp1 = (k.sb("c_" + n, [C, T], stack=s) for n in ("xb", "dl", "xr", "xk", "kk", "rr", "t1"))
        hp = k.sb("c_hp", [C, T + 1], stack=s)
        tmp = k.sb("c_tmp", [C, 3, T], stack=s)
        P = [k.ps[:, i, :] for i in range(8)]
        m = k.modb[:, 3, :]
        with nc.Fori(0, B) as b:
            st = pe, act, dve, pool, dma = k.stage("mix")
            n = Norm(k, st, "n", 0, 1, xb[:], hp[:, 1:], m, SB_, CB, tmp)
            with nc.Block() as block:
                @block.gpsimd
                def _(e):
                    e.tensor_copy(xb[:], flat(k.X[:, bass.ds(b, 1), :])).then_inc(pool.steps, pool.did("xb"))
                    e.wait_ge(act.steps, act.at("k"))
                    e.tensor_tensor(kk[:], kk[:], kk[:], ALU.mult).then_inc(pool.steps, pool.did("k2"))

                @block.tensor
                def _(e):
                    e.wait_ge(pool.steps, pool.at("xb"))
                    n.tensor(e)
                    e.wait_ge(dve.steps, dve.at("xr"))
                    e.matmul(P[2], k.w["W_r3"][:], xr[:], start=True, stop=True).then_inc(pe.steps, pe.did("r"))
                    e.wait_ge(dve.steps, dve.at("xk"))
                    e.matmul(P[3], k.w["W_k3"][:], xk[:], start=True, stop=True).then_inc(pe.steps, pe.did("k"))
                    e.wait_ge(pool.steps, pool.at("k2"))
                    e.matmul(P[4], k.w["W_v3"][:], kk[:], start=True, stop=True).then_inc(pe.steps, pe.did("v"))

                @block.scalar
                def _(e):
                    e.preload_act_table_set(EXP_LN)
                    n.scalar(e)
                    e.wait_ge(dve.steps, dve.at("r"))
                    e.activation(rr[:], rr[:], ACT.Exp, scale=-1.0).then_inc(act.steps, act.did())
                    e.wait_ge(act.steps, act.n)
                    e.activation(rr[:], rr[:], ACT.Ln, bias=1.0).then_inc(act.steps, act.did())
                    e.wait_ge(act.steps, act.n)
                    e.activation(rr[:], rr[:], ACT.Exp, scale=-1.0).then_inc(act.steps, act.did("r"))
                    e.wait_ge(pe.steps, pe.at("k"))
                    e.activation(kk[:], P[3], ACT.Relu).then_inc(act.steps, act.did("k"))

                @block.vector
                def _(e):
                    e.memset(hp[:, 0:1], 0.0).then_inc(dve.steps, dve.did())
                    e.tensor_copy(k.modb[:], k.mod[:, :, :, bass.ds(b, 1)].rearrange("p l s a -> p l (s a)")).then_inc(dve.steps, dve.did())
                    e.wait_ge(dve.steps, dve.n)
                    n.vector(e)
                    e.wait_ge(dve.steps, dve.n)
                    e.tensor_tensor(dl[:], hp[:, 1:], hp[:, 0:T], ALU.subtract).then_inc(dve.steps, dve.did())
                    e.wait_ge(dve.steps, dve.n)
                    e.scalar_tensor_tensor(xr[:], dl[:], k.w["mu"][:, 0:1], hp[:, 0:T], ALU.mult, ALU.add).then_inc(dve.steps, dve.did("xr"))
                    e.scalar_tensor_tensor(xk[:], dl[:], k.w["mu"][:, 1:2], hp[:, 0:T], ALU.mult, ALU.add).then_inc(dve.steps, dve.did("xk"))
                    e.wait_ge(pe.steps, pe.at("r"))
                    e.tensor_scalar(rr[:], P[2], LEAST, None, ALU.max).then_inc(dve.steps, dve.did("r"))
                    e.wait_ge(act.steps, act.at("r"))
                    e.wait_ge(pe.steps, pe.at("v"))
                    e.tensor_tensor(rr[:], rr[:], P[4], ALU.mult).then_inc(dve.steps, dve.did())
                    e.wait_ge(dve.steps, dve.n)
                    e.scalar_tensor_tensor(flat(k.X[:, bass.ds(b, 1), :]), rr[:], m[:, GB:GB + 1], xb[:], ALU.mult, ALU.add).then_inc(dve.steps, dve.did())
            k.end()


def build(nc, a, counts, upto=99, first=0):
    k = Kernel(nc, counts)
    k.dram = a
    with k.stack:
        load_weights(k, a)
        if first <= 0:
            with ExitStack() as s:
                load(k, a, "layers01", s)
                wkv_mlp_prologue(k, s)
                q1 = k.sb("q1", [C, B, T], stack=s)
                k1 = k.sb("k1", [C, B, T], stack=s)
                v1 = k.sb("v1", [C, B, T], stack=s)
                qbar = k.sb("qbar", [C, B, 16], stack=s)
                kbar = k.sb("kbar", [C, B, 16], stack=s)
                idx_row = k.sb("idx_row", [1, 48], U32, stack=s)
                lg = k.sb("router_logits", [C, B, 32], stack=s)
                gates = k.sb("gates", [C, 32, 8], stack=s)
                layer0(k, q1, k1, v1, qbar, kbar)
                if upto >= 1:
                    choose_blocks(k, qbar, kbar, idx_row)
                    block_attention(k, q1, k1, v1, idx_row)
                    attention_out(k, q1, k1, lg)
                if upto >= 2:
                    route(k, lg, gates)
                    experts(k, k1, gates)
        if first <= 3 <= upto:
            with ExitStack() as s:
                load(k, a, "gla", s)
                gla(k)
        if first <= 4 <= upto:
            with ExitStack() as s:
                load(k, a, "mlp2", s)
                routed_mlp(k)
        if first <= 5 <= upto:
            with ExitStack() as s:
                load(k, a, "delta", s)
                delta_rule(k)
        if first <= 6 <= upto:
            with ExitStack() as s:
                load(k, a, "mix", s)
                channel_mix(k)
        pe, act, dve, pool, dma = k.stage("store")
        with nc.Block() as block:
            @block.sync
            def _(e):
                e.dma_start(a["out"], k.X[:]).then_inc(dma.steps, dma.did("out"))
                e.wait_ge(dma.steps, dma.at("out"))


def layouts(i):
    c = np.ascontiguousarray
    i = {n: np.asarray(v) for n, v in i.items()}
    o = {}
    o["x"] = c(i["L0_attn_x"].transpose(2, 0, 1))
    o["center"] = (np.eye(C) - 1.0 / C).astype(np.float32)
    o["mean"] = np.full((C, C), 1.0 / C, np.float32)
    o["ident"] = np.eye(C, dtype=np.float32)
    o["cT"] = c(np.stack([i[f"L{l}_c"].T for l in range(4)], 1))
    o["wmod"] = c(np.stack([i[f"L{l}_wmod"] for l in range(4)], 1))
    o["W_rvk"] = c(i["L0_attn_W_rvk"].T)
    o["W_out0"] = c(i["L0_attn_W_out"].T)
    o["decay"] = c(i["L0_attn_time_decay"][:, None])
    o["time_first"] = c(i["L0_attn_time_first"][:, None])
    two = lambda v: c(np.concatenate([v, v], 0))
    halves = lambda v: c(v.reshape(64, 8, 2).transpose(2, 0, 1).reshape(128, 8))
    o["Win0"] = c(np.concatenate([i["L0_ffn_Win"]] * 2, 1))
    o["bin_0"] = two(i["L0_ffn_bin_"][:, None])
    o["W1_0"], o["b1_0"], o["W2_0"] = halves(i["L0_ffn_W1"]), halves(i["L0_ffn_b1"]), halves(i["L0_ffn_W2"])
    o["b2_0"] = two(i["L0_ffn_b2"][:, None])
    o["Wout0"] = two(i["L0_ffn_Wout"])
    o["bout_0"] = c(i["L0_ffn_bout"][:, None])
    for n in "QKV":
        o[f"W_{n}"] = c(i[f"L1_attn_W_{n}"])
    o["W_O"] = c(i["L1_attn_W_O"])
    head = (np.arange(C)[:, None] % 32 // 8 == np.arange(4)[None]).astype(np.float32)
    o["head_mask"] = head
    o["head_scale"] = head * np.float32(1 / np.sqrt(8))
    o["w_gate1"] = c(i["L1_ffn_w_g"].T)
    o["rev8"] = np.broadcast_to(np.arange(8, 0, -1, dtype=np.float32), (C, 8)).copy()
    o["upto"] = np.triu(np.ones((C, C), np.float32))
    o["ones"] = np.ones((C, C), np.float32)
    o["c_fc"] = c(i["L1_ffn_c_fc"].transpose(1, 0, 2))
    o["c_proj"] = c(i["L1_ffn_c_proj"].reshape(8, 4, C, C).transpose(2, 0, 1, 3))
    o["W_in2"] = c(i["L2_attn_W_in"].T)
    o["b_in2"] = c(i["L2_attn_b_in"][:, None])
    wq = i["L2_attn_W_qkva"].reshape(2, 4, 32, 4, 2, C)
    bq = i["L2_attn_b_qkva"].reshape(2, 4, 32, 4, 2)
    sel = [0, 1, 3]
    o["W_qka"] = c(wq[:, :, :, sel].transpose(5, 3, 4, 0, 1, 2).reshape(C, 3, 2, 2, C))
    o["b_qka"] = c(bq[:, :, :, sel].transpose(1, 2, 3, 4, 0).reshape(C, 3, 2, 2))
    o["W_v2"] = c(wq[:, :, :, 2].transpose(4, 0, 1, 3, 2).reshape(C, 512))
    o["b_v2"] = c(np.broadcast_to(bq[:, :, :, 2].transpose(0, 1, 3, 2).reshape(1, 512), (C, 512)))
    o["W_y2"] = c(i["L2_attn_W_y"].reshape(C, 4, 2, 32, 2).transpose(2, 4, 3, 1, 0).reshape(C, 4, C))
    o["b_y2"] = c(i["L2_attn_b_y"][:, None])
    o["W_out2"] = c(i["L2_attn_W_out"].T)
    o["b_out2"] = c(i["L2_attn_b_out"][:, None])
    h0 = np.stack([i["L2_attn_h0_re"], i["L2_attn_h0_im"]], 2)
    o["h0"] = c(h0.reshape(2, 4, 32, 64).transpose(1, 2, 0, 3).reshape(C, 2, 64))
    s_, t_ = np.arange(C)[:, None] % 32, np.arange(32)[None]
    same8 = (s_ // 8 == t_ // 8) & (s_ <= t_)
    half8 = (s_ // 16 == t_ // 16) & (s_ // 8 < t_ // 8)
    o["gla_mask"] = c(np.stack([same8, half8], 1).astype(np.float32))
    o["gate_w2"] = c(i["L2_ffn_gate_w"].T)
    o["w1_2"] = c(np.stack([*i["L2_ffn_w1"], i["L2_ffn_sw1"]], 1))
    o["w2_2"] = c(np.stack([*i["L2_ffn_w2"], i["L2_ffn_sw2"]], 0).reshape(3, 4, C, C).transpose(2, 0, 1, 3))
    o["b1_2"] = c(np.stack([*i["L2_ffn_b1"], i["L2_ffn_sb1"]], 0).reshape(3, 4, C).transpose(2, 0, 1))
    o["b2_2"] = c(np.stack([*i["L2_ffn_b2"], i["L2_ffn_sb2"]], 1))
    rows = lambda v: c(np.broadcast_to(v[None], (C,) + v.shape))
    o["Wqk3"] = c(np.stack([i["L3_attn_Wq"], i["L3_attn_Wk"]], 1))
    o["conv_qk"] = c(np.stack([i["L3_attn_conv_q"].T, i["L3_attn_conv_k"].T], 0))
    o["Wv3"] = c(i["L3_attn_Wv"])
    o["conv_v"] = rows(c(i["L3_attn_conv_v"].T))
    o["Wg3"] = c(i["L3_attn_Wg"])
    o["Wab3"] = c(np.concatenate([i["L3_attn_Wa"], i["L3_attn_Wb"]], 1))
    o["Wo3"] = c(i["L3_attn_Wo"].reshape(2, C, C).transpose(1, 0, 2))
    for n in ("A_log", "dt_bias", "o_norm_w"):
        o[n] = rows(i["L3_attn_" + n])
    s_, t_ = np.arange(C)[:, None], np.arange(C)[None]
    joins = np.stack([(s_ // (2 * n) == t_ // (2 * n)) & (s_ // n < t_ // n) for n in (1, 2, 4, 8, 16)], 1)
    o["joins"] = np.tile(joins[0:32, :, 0:32].astype(np.float32), (4, 1, 1))
    o["eye32"] = np.tile(np.eye(32, dtype=np.float32), (4, 1))
    o["upto3"], o["ones3"] = o["upto"].copy(), o["ones"].copy()
    for n in "rkv":
        o[f"W_{n}3"] = c(i[f"L3_ffn_W_{n}"].T)
    o["mu"] = c(np.stack([i["L3_ffn_mu_r"], i["L3_ffn_mu_k"]], 1))
    return o


def kernel(**inputs):
    import concourse.bacc as _bacc
    from concourse.bass_utils import run_bass_kernel_spmd as _run

    counts, arrays = {}, layouts(inputs)

    def program():
        nc = _bacc.Bacc("TRN2", target_bir_lowering=False, num_devices=1)
        a = {n: nc.dram_tensor(f"in_{n}_dram", v.shape, mybir.dt.from_np(v.dtype), kind="ExternalInput").ap()
             for n, v in arrays.items()}
        a["out"] = nc.dram_tensor("out_0_dram", (C, B, T), F32, kind="ExternalOutput").ap()
        build(nc, a, counts)
        return nc

    program()
    result = _run(program(), [{f"in_{n}_dram": v for n, v in arrays.items()}], core_ids=[0])
    return np.ascontiguousarray(result.results[0]["out_0_dram"].transpose(1, 2, 0))
```

```python
from contextlib import ExitStack

import numpy as np

import concourse.bass as bass
from concourse import mybir

F32 = mybir.dt.float32
U32 = mybir.dt.uint32
ALU = mybir.AluOpType
ACT = mybir.ActivationFunctionType
AX = mybir.AxisListType

C = 128
B = 8
T = 512
LN_EPS = 1e-5
NEG_BIG = -1e38
EXP_LN = "natural_log_exp_and_others"
LEAST = -37.0
SA, CA, GA, SB_, CB, GB = range(6)


class Steps:

    def __init__(self, steps, stage, counts, unit=1):
        self.steps, self.stage, self.counts, self.unit, self.n = steps, stage, counts, unit, 0

    def did(self, name=None):
        self.n += self.unit
        if name is not None:
            self.counts[self.stage, self.steps.name, name] = self.n
        return self.unit

    def at(self, name):
        return self.counts.get((self.stage, self.steps.name, name), 1)


class Kernel:

    def __init__(self, nc, counts):
        self.nc, self.counts, self.stack, self.w = nc, counts, ExitStack(), {}
        self.ps = self.stack.enter_context(nc.psum_tensor("ps", [128, 8, 512], F32))
        names = ("tensor_steps", "scalar_steps", "vector_steps", "gpsimd_steps", "dma_steps")
        self.sems = [self.stack.enter_context(nc.semaphore(n)) for n in names]

    def sb(self, name, shape, dt=F32, stack=None):
        return (stack or self.stack).enter_context(self.nc.sbuf_tensor(name, shape, dt))

    def stage(self, name):
        pe, act, dve, pool, dma = (Steps(s, name, self.counts, u) for s, u in zip(self.sems, (1, 1, 1, 1, 16)))
        return pe, act, dve, pool, dma

    def end(self):
        with self.nc.Block() as block:
            @block.vector
            def _(v):
                for s in self.sems:
                    v.sem_clear(s)


class Norm:

    def __init__(self, k, st, tag, bank_c, bank_v, x, h, mod, shift, scale, tmp):
        self.k, self.st, self.tag, self.x, self.h, self.tmp = k, st, tag, x, h, tmp
        self.pc, self.pv = k.ps[:, bank_c, :], k.ps[:, bank_v, :]
        self.shift, self.scale = mod[:, shift:shift + 1], mod[:, scale:scale + 1]

    def tensor(self, e):
        pe, act, dve, pool, _ = self.st
        k, g = self.k, self.tag
        e.matmul(self.pc, k.w["center"][:], self.x, start=True, stop=True).then_inc(pe.steps, pe.did(g + "c"))
        e.wait_ge(act.steps, act.at(g + "sq"))
        e.matmul(self.pv, k.w["mean"][:], self.tmp[:, 0, :], start=True, stop=True).then_inc(pe.steps, pe.did(g + "v"))

    def scalar(self, e):
        pe, act, dve, pool, _ = self.st
        g = self.tag
        e.wait_ge(pe.steps, pe.at(g + "c"))
        e.activation(self.tmp[:, 0, :], self.pc, ACT.Square).then_inc(act.steps, act.did(g + "sq"))
        e.wait_ge(pe.steps, pe.at(g + "v"))
        e.activation(self.tmp[:, 1, :], self.pv, ACT.Ln, bias=self.k.eps[:, 0:1]).then_inc(act.steps, act.did())
        e.wait_ge(act.steps, act.n)
        e.activation(self.tmp[:, 2, :], self.tmp[:, 1, :], ACT.Exp, scale=-0.5).then_inc(act.steps, act.did(g + "rs"))

    def vector(self, e):
        pe, act, dve, pool, _ = self.st
        g = self.tag
        e.wait_ge(act.steps, act.at(g + "rs"))
        e.tensor_tensor(self.tmp[:, 1, :], self.pc, self.tmp[:, 2, :], ALU.mult).then_inc(dve.steps, dve.did())
        e.wait_ge(dve.steps, dve.n)
        e.tensor_scalar(self.h, self.tmp[:, 1, :], self.scale, self.shift, ALU.mult, ALU.add).then_inc(dve.steps, dve.did(g + "h"))


def ts(i, n):
    return slice(i * n, (i + 1) * n)


GROUPS = {
    "all": ["center", "mean", "ident"],
    "modulation": ["cT", "wmod"],
    "layers01": ["W_rvk", "W_out0", "decay", "time_first", "Win0", "bin_0", "W1_0", "b1_0", "W2_0", "b2_0", "Wout0",
                 "bout_0", "W_Q", "W_K", "W_V", "W_O", "head_mask", "head_scale", "w_gate1", "rev8", "upto", "ones",
                 "c_fc", "c_proj"],
    "gla": ["W_in2", "b_in2", "W_qka", "b_qka", "W_v2", "b_v2", "W_y2", "b_y2", "W_out2", "b_out2", "h0", "gla_mask"],
    "delta": ["Wqk3", "Wv3", "Wg3", "Wab3", "Wo3", "A_log", "dt_bias", "conv_v", "o_norm_w", "joins", "eye32", "upto3", "ones3"],
    "mix": ["W_r3", "W_k3", "W_v3", "mu"],
    "mlp2": ["gate_w2", "w1_2", "w2_2", "b1_2", "b2_2"],
}


def place(k, a, names, stack):
    for name in names:
        k.w[name] = k.sb("w_" + name, list(a[name].shape), a[name].dtype, stack)


def load(k, a, group, stack):
    place(k, a, GROUPS[group], stack)
    pe, act, dve, pool, dma = k.stage("load_" + group)
    with k.nc.Block() as block:
        @block.sync
        def _(e):
            for name in GROUPS[group]:
                e.dma_start(k.w[name][:], a[name]).then_inc(dma.steps, dma.did("all"))
            e.wait_ge(dma.steps, dma.at("all"))
    k.end()


def load_weights(k, a):
    nc = k.nc
    place(k, a, GROUPS["all"], k.stack)
    k.X = k.sb("X", [C, B, T])
    k.eps = k.sb("eps", [C, 1])
    k.mod = k.sb("mod", [C, 4, 6, B])
    k.modb = k.sb("modb", [C, 4, 6])
    st = pe, act, dve, pool, dma = k.stage("load")
    scope = ExitStack()
    place(k, a, GROUPS["modulation"], scope)
    cT = k.sb("c_silu", [C, 4, B], stack=scope)
    with scope, nc.Block() as block:
        @block.sync
        def _(e):
            for name, ap in a.items():
                if name in GROUPS["all"] + GROUPS["modulation"]:
                    e.dma_start(k.w[name][:], ap).then_inc(dma.steps, dma.did())
            e.dma_start(k.X[:], a["x"]).then_inc(dma.steps, dma.did("all"))
            e.wait_ge(dma.steps, dma.at("all"))

        @block.scalar
        def _(e):
            e.wait_ge(dma.steps, dma.at("all"))
            e.activation(cT[:], k.w["cT"][:], ACT.Exp, scale=-1.0).then_inc(act.steps, act.did("exp"))

        @block.vector
        def _(e):
            e.memset(k.eps[:], LN_EPS).then_inc(dve.steps, dve.did())
            e.wait_ge(act.steps, act.at("exp"))
            e.tensor_scalar(cT[:], cT[:], 1.0, None, ALU.add).then_inc(dve.steps, dve.did())
            e.wait_ge(dve.steps, dve.n)
            e.reciprocal(cT[:], cT[:]).then_inc(dve.steps, dve.did())
            e.wait_ge(dve.steps, dve.n)
            e.tensor_tensor(cT[:], cT[:], k.w["cT"][:], ALU.mult).then_inc(dve.steps, dve.did("silu"))
            e.wait_ge(pe.steps, pe.at("mod"))
            m = k.mod[:].rearrange("p l s b -> p (l s b)")
            e.tensor_copy(m, k.ps[:, 0, 0:4 * 6 * B]).then_inc(dve.steps, dve.did())
            e.wait_ge(dve.steps, dve.n)
            for s in (CA, CB):
                e.tensor_scalar(k.mod[:, :, s, :], k.mod[:, :, s, :], 1.0, None, ALU.add).then_inc(dve.steps, dve.did())
            for s in (GA, GB):
                g = k.mod[:, :, s, :]
                e.tensor_scalar(cT[:], g, 0.0, 2.0, ALU.is_ge, ALU.mult).then_inc(dve.steps, dve.did())
                e.wait_ge(dve.steps, dve.n)
                e.tensor_scalar(cT[:], cT[:], -1.0, None, ALU.add).then_inc(dve.steps, dve.did())
                e.wait_ge(dve.steps, dve.n)
                e.tensor_tensor(g, g, cT[:], ALU.mult).then_inc(dve.steps, dve.did())
                e.wait_ge(dve.steps, dve.n)
                e.tensor_scalar(g, g, 0.25, None, ALU.max).then_inc(dve.steps, dve.did())
                e.wait_ge(dve.steps, dve.n)
                e.tensor_tensor(g, g, cT[:], ALU.mult).then_inc(dve.steps, dve.did())
                e.wait_ge(dve.steps, dve.n)

        @block.tensor
        def _(e):
            e.wait_ge(dve.steps, dve.at("silu"))
            for l in range(4):
                for s in range(6):
                    i = (l * 6 + s) * B
                    ins = e.matmul(k.ps[:, 0, i:i + B], k.w["wmod"][:, l, ts(s, C)], cT[:, l, :], start=True, stop=True)
            ins.then_inc(pe.steps, pe.did("mod"))
    k.end()


def wkv_mlp_prologue(k, s):
    nc = k.nc
    k.w_decay = k.sb("neg_decay", [C, 1], stack=s)
    k.w_full = k.sb("neg_decay_time", [C, T], stack=s)
    k.w2out = k.sb("w2out", [C, 8, C], stack=s)
    k.mlp0_const = k.sb("mlp0_const", [C, 1], stack=s)
    pe, act, dve, pool, dma = k.stage("wkv_prologue")
    with nc.Block() as block:
        @block.scalar
        def _(e):
            e.activation(k.w_decay[:], k.w["decay"][:], ACT.Exp).then_inc(act.steps, act.did("exp"))

        @block.tensor
        def _(e):
            e.matmul(k.ps[:, 0, 0:1], k.w["Wout0"][0:64, :], k.w["b2_0"][0:64, :], start=True, stop=True).then_inc(pe.steps, pe.did("const"))

        @block.vector
        def _(e):
            e.memset(k.w_full[:], 0.0).then_inc(dve.steps, dve.did("zero"))
            e.wait_ge(act.steps, act.at("exp"))
            e.tensor_scalar(k.w_decay[:], k.w_decay[:], -1.0, None, ALU.mult).then_inc(dve.steps, dve.did())
            e.wait_ge(dve.steps, dve.n)
            e.tensor_scalar(k.w_full[:], k.w_full[:], k.w_decay[:, 0:1], None, ALU.add).then_inc(dve.steps, dve.did())
            for j in range(8):
                e.tensor_scalar(k.w2out[:, j, :], k.w["Wout0"][:], k.w["W2_0"][:, j:j + 1], None, ALU.mult).then_inc(dve.steps, dve.did())
            e.wait_ge(pe.steps, pe.at("const"))
            e.tensor_tensor(k.mlp0_const[:], k.ps[:, 0, 0:1], k.w["bout_0"][:], ALU.add).then_inc(dve.steps, dve.did())
    k.end()


def layer0(k, q1, k1, v1, qbar, kbar):
    nc = k.nc
    with ExitStack() as s:
        xb = k.sb("l0_xb", [C, T], stack=s)
        h = k.sb("l0_h", [C, T], stack=s)
        tmp = k.sb("l0_tmp", [C, 3, T], stack=s)
        ks = k.sb("l0_k", [C, T], stack=s)
        er = k.sb("l0_er", [C, T], stack=s)
        pp = k.sb("l0_pp", [C, T + 1], stack=s)
        aa = k.sb("l0_aa", [C, T + 1], stack=s)
        bb = k.sb("l0_bb", [C, T + 1], stack=s)
        e1 = k.sb("l0_e1", [C, T], stack=s)
        e2 = k.sb("l0_e2", [C, T], stack=s)
        f1 = k.sb("l0_f1", [C, T], stack=s)
        f2 = k.sb("l0_f2", [C, T], stack=s)
        pm = k.sb("l0_pm", [C, T], stack=s)
        e2v = k.sb("l0_e2v", [C, T], stack=s)
        n1 = k.sb("l0_n1", [C, T], stack=s)
        n2 = k.sb("l0_n2", [C, T], stack=s)
        d1 = k.sb("l0_d1", [C, T], stack=s)
        y = k.sb("l0_y", [C, T], stack=s)
        hid = k.sb("l0_hid", [C, 8, T], stack=s)
        P = [k.ps[:, i, :] for i in range(8)]
        u = k.w["time_first"][:, 0:1]
        wd = k.w_decay[:, 0:1]
        with nc.Fori(0, B) as b:
            st = pe, act, dve, pool, dma = k.stage("layer0")
            m0, m1 = k.modb[:, 0, :], k.modb[:, 1, :]
            na = Norm(k, st, "a", 0, 1, xb[:], h[:], m0, SA, CA, tmp)
            nb = Norm(k, st, "b", 0, 1, xb[:], h[:], m0, SB_, CB, tmp)
            nq = Norm(k, st, "q", 0, 1, xb[:], h[:], m1, SA, CA, tmp)
            with nc.Block() as block:
                @block.tensor
                def _(e):
                    e.wait_ge(pool.steps, pool.at("xb"))
                    na.tensor(e)
                    e.wait_ge(dve.steps, dve.at("ah"))
                    for i, name in ((2, "k"), (1, "v"), (0, "r")):
                        e.matmul(P[4 - i], k.w["W_rvk"][:, ts(i, C)], h[:], start=True, stop=True).then_inc(pe.steps, pe.did(name))
                    e.wait_ge(dve.steps, dve.at("y"))
                    e.matmul(P[5], k.w["W_out0"][:], y[:], start=True, stop=True).then_inc(pe.steps, pe.did("att"))
                    e.wait_ge(dve.steps, dve.at("x1"))
                    nb.tensor(e)
                    e.wait_ge(dve.steps, dve.at("bh"))
                    e.matmul(P[6], k.w["Win0"][:], h[:], start=True, stop=True).then_inc(pe.steps, pe.did("s"))
                    for j in range(8):
                        e.wait_ge(act.steps, act.at(f"hid{j}"))
                        ins = e.matmul(P[7], k.w2out[:, j, :], hid[:, j, :], start=(j == 0), stop=(j == 7))
                    ins.then_inc(pe.steps, pe.did("mlp"))
                    e.wait_ge(dve.steps, dve.at("x2"))
                    nq.tensor(e)
                    e.wait_ge(dve.steps, dve.at("qh"))
                    for i, w in enumerate((k.w["W_Q"], k.w["W_K"], k.w["W_V"])):
                        e.matmul(P[2 + i], w[:], h[:], start=True, stop=True).then_inc(pe.steps, pe.did(f"p{i}"))

                @block.gpsimd
                def _(e):
                    e.tensor_copy(xb[:], k.X[:, bass.ds(b, 1), :].rearrange("p a t -> p (a t)")).then_inc(pool.steps, pool.did("xb"))
                    e.wait_ge(dve.steps, dve.at("pp"))
                    e.wait_ge(act.steps, act.at("k"))
                    e.tensor_tensor(e2[:], ks[:], pp[:, 1:], ALU.subtract).then_inc(pool.steps, pool.did("e2a"))
                    e.wait_ge(dve.steps, dve.at("pm"))
                    e.tensor_tensor(f1[:], pp[:, 0:T], pm[:], ALU.subtract).then_inc(pool.steps, pool.did("f1a"))
                    e.wait_ge(act.steps, act.at("f1"))
                    e.wait_ge(dve.steps, dve.at("aa"))
                    e.tensor_tensor(n1[:], f1[:], aa[:, 0:T], ALU.mult).then_inc(pool.steps, pool.did("n1"))
                    e.wait_ge(dve.steps, dve.at("bb"))
                    e.tensor_tensor(d1[:], f1[:], bb[:, 0:T], ALU.mult).then_inc(pool.steps, pool.did("d1"))

                @block.scalar
                def _(e):
                    e.preload_act_table_set(EXP_LN)
                    na.scalar(e)
                    e.wait_ge(pe.steps, pe.at("k"))
                    e.activation(ks[:], P[2], ACT.Copy).then_inc(act.steps, act.did("k"))
                    e.wait_ge(dve.steps, dve.at("er"))
                    e.activation(er[:], er[:], ACT.Exp, scale=-1.0).then_inc(act.steps, act.did())
                    e.wait_ge(dve.steps, dve.at("e1a"))
                    e.activation(e1[:], e1[:], ACT.Exp).then_inc(act.steps, act.did("e1"))
                    e.wait_ge(pool.steps, pool.at("e2a"))
                    e.activation(e2[:], e2[:], ACT.Exp).then_inc(act.steps, act.did("e2"))
                    e.wait_ge(pool.steps, pool.at("f1a"))
                    e.activation(f1[:], f1[:], ACT.Exp).then_inc(act.steps, act.did("f1"))
                    e.wait_ge(dve.steps, dve.at("f2a"))
                    e.activation(f2[:], f2[:], ACT.Exp).then_inc(act.steps, act.did("f2"))
                    e.wait_ge(dve.steps, dve.at("den"))
                    e.activation(d1[:], d1[:], ACT.Ln).then_inc(act.steps, act.did())
                    e.wait_ge(act.steps, act.n)
                    e.activation(d1[:], d1[:], ACT.Exp, scale=-1.0).then_inc(act.steps, act.did("inv"))
                    nb.scalar(e)
                    e.wait_ge(pe.steps, pe.at("s"))
                    e.activation(er[:], P[6], ACT.Identity, bias=k.w["bin_0"][:, 0:1]).then_inc(act.steps, act.did("s"))
                    e.wait_ge(act.steps, act.n)
                    for j in range(8):
                        e.activation(hid[:, j, :], er[:], ACT.Relu, bias=k.w["b1_0"][:, j:j + 1],
                                              scale=k.w["W1_0"][:, j:j + 1]).then_inc(act.steps, act.did(f"hid{j}"))
                    e.wait_ge(pe.steps, pe.at("mlp"))
                    e.activation(y[:], P[7], ACT.Identity, bias=k.mlp0_const[:, 0:1]).then_inc(act.steps, act.did("mlp"))
                    nq.scalar(e)
                    for i, dst in ((0, q1), (1, k1)):
                        e.wait_ge(pe.steps, pe.at(f"p{i}"))
                        e.activation(dst[:, bass.ds(b, 1), :].rearrange("p a t -> p (a t)"), P[2 + i], ACT.Copy).then_inc(act.steps, act.did(f"cp{i}"))

                @block.vector
                def _(e):
                    e.tensor_copy(k.modb[:], k.mod[:, :, :, bass.ds(b, 1)].rearrange("p l s a -> p l (s a)")).then_inc(dve.steps, dve.did())
                    e.memset(pp[:, 0:1], NEG_BIG).then_inc(dve.steps, dve.did())
                    e.memset(aa[:, 0:1], 0.0).then_inc(dve.steps, dve.did())
                    e.memset(bb[:, 0:1], 0.0).then_inc(dve.steps, dve.did())
                    e.wait_ge(dve.steps, dve.n)
                    na.vector(e)
                    e.wait_ge(pe.steps, pe.at("r"))
                    e.tensor_scalar(er[:], P[4], LEAST, None, ALU.max).then_inc(dve.steps, dve.did("er"))
                    e.wait_ge(act.steps, act.at("k"))
                    e.tensor_tensor_scan(pp[:, 1:], k.w_full[:], ks[:], NEG_BIG, ALU.add, ALU.max).then_inc(dve.steps, dve.did("pp"))
                    e.wait_ge(dve.steps, dve.n)
                    e.scalar_tensor_tensor(e1[:], pp[:, 0:T], wd, pp[:, 1:], ALU.add, ALU.subtract).then_inc(dve.steps, dve.did("e1a"))
                    e.scalar_tensor_tensor(pm[:], ks[:], u, pp[:, 0:T], ALU.add, ALU.max).then_inc(dve.steps, dve.did("pm"))
                    e.wait_ge(dve.steps, dve.n)
                    e.scalar_tensor_tensor(f2[:], ks[:], u, pm[:], ALU.add, ALU.subtract).then_inc(dve.steps, dve.did("f2a"))
                    e.wait_ge(act.steps, act.at("e2"))
                    e.wait_ge(pe.steps, pe.at("v"))
                    e.tensor_tensor(e2v[:], e2[:], P[3], ALU.mult).then_inc(dve.steps, dve.did())
                    e.wait_ge(dve.steps, dve.n)
                    e.tensor_tensor_scan(aa[:, 1:], e1[:], e2v[:], 0.0, ALU.mult, ALU.add).then_inc(dve.steps, dve.did("aa"))
                    e.tensor_tensor_scan(bb[:, 1:], e1[:], e2[:], 0.0, ALU.mult, ALU.add).then_inc(dve.steps, dve.did("bb"))
                    e.wait_ge(act.steps, act.at("f2"))
                    e.tensor_tensor(n2[:], f2[:], P[3], ALU.mult).then_inc(dve.steps, dve.did())
                    e.wait_ge(pool.steps, pool.at("d1"))
                    e.tensor_tensor(d1[:], d1[:], f2[:], ALU.add).then_inc(dve.steps, dve.did())
                    e.wait_ge(dve.steps, dve.n)
                    e.scalar_tensor_tensor(d1[:], er[:], 1.0, d1[:], ALU.add, ALU.mult).then_inc(dve.steps, dve.did("den"))
                    e.tensor_tensor(n1[:], n1[:], n2[:], ALU.add).then_inc(dve.steps, dve.did())
                    e.wait_ge(dve.steps, dve.n)
                    e.wait_ge(act.steps, act.at("inv"))
                    e.tensor_tensor(y[:], n1[:], d1[:], ALU.mult).then_inc(dve.steps, dve.did("y"))
                    e.wait_ge(pe.steps, pe.at("att"))
                    e.scalar_tensor_tensor(xb[:], P[5], m0[:, GA:GA + 1], xb[:], ALU.mult, ALU.add).then_inc(dve.steps, dve.did("x1"))
                    nb.vector(e)
                    e.wait_ge(act.steps, act.at("mlp"))
                    e.scalar_tensor_tensor(xb[:], y[:], m0[:, GB:GB + 1], xb[:], ALU.mult, ALU.add).then_inc(dve.steps, dve.did("x2"))
                    e.wait_ge(dve.steps, dve.n)
                    e.tensor_copy(k.X[:, bass.ds(b, 1), :].rearrange("p a t -> p (a t)"), xb[:]).then_inc(dve.steps, dve.did())
                    nq.vector(e)
                    e.wait_ge(pe.steps, pe.at("p2"))
                    e.tensor_copy(v1[:, bass.ds(b, 1), :].rearrange("p a t -> p (a t)"), P[4]).then_inc(dve.steps, dve.did())
                    for i, dst, src in ((0, qbar, q1), (1, kbar, k1)):
                        e.wait_ge(act.steps, act.at(f"cp{i}"))
                        e.tensor_reduce(dst[:, bass.ds(b, 1), :].rearrange("p a t -> p (a t)"),
                                                 src[:, bass.ds(b, 1), :].rearrange("p a (i q) -> p (a i) q", q=32),
                                                 AX.X, ALU.add).then_inc(dve.steps, dve.did())
            k.end()


def flat(ap):
    return ap.rearrange("p a t -> p (a t)")


def choose_blocks(k, qbar, kbar, idx_row):
    with ExitStack() as s:
        sc = k.sb("blk_sc", [16, 16], stack=s)
        best = k.sb("blk_best", [16, 8], stack=s)
        idx = k.sb("blk_idx", [16, 8], U32, stack=s)
        pe, act, dve, pool, dma = k.stage("choose")
        with k.nc.Block() as block:
            @block.tensor
            def _(e):
                for b in range(B):
                    ins = e.matmul(k.ps[0:16, 0, 0:16], qbar[:, b, :], kbar[:, b, :], start=(b == 0), stop=(b == B - 1))
                ins.then_inc(pe.steps, pe.did("score"))

            @block.vector
            def _(e):
                e.wait_ge(pe.steps, pe.at("score"))
                e.tensor_copy(sc[:], k.ps[0:16, 0, 0:16]).then_inc(dve.steps, dve.did())
                e.wait_ge(dve.steps, dve.n)
                e.max(best[:], sc[:]).then_inc(dve.steps, dve.did())
                e.wait_ge(dve.steps, dve.n)
                e.max_index(idx[:], best[:], sc[:]).then_inc(dve.steps, dve.did("idx"))

            @block.sync
            def _(e):
                e.wait_ge(dve.steps, dve.at("idx"))
                e.dma_start(idx_row[0:1, :].rearrange("a (t s) -> a t s", s=3), idx[:, 0:3]).then_inc(dma.steps, dma.did("row"))
                e.wait_ge(dma.steps, dma.at("row"))
        k.end()


def block_attention(k, q1, k1, v1, idx_row):
    nc = k.nc
    NK = 96
    with ExitStack() as s:
        kg = k.sb("att_kg", [C, B, NK], stack=s)
        vg = k.sb("att_vg", [C, B, NK], stack=s)
        qx = k.sb("att_qx", [C, B, 4, 32], stack=s)
        mx = k.sb("att_mx", [C, 2, 16], stack=s)
        den = k.sb("att_den", [C, 2, 16], stack=s)
        p = k.sb("att_p", [C, 2, 16, NK], stack=s)
        pt = k.sb("att_pt", [NK, 2, 16, C], stack=s)
        vt = k.sb("att_vt", [NK, 2, 4, C], stack=s)
        o = k.sb("att_o", [C, 4, 32], stack=s)
        scored = lambda u: k.ps[:, 4 * u:4 * u + 4, 0:4 * NK]
        S_VT, S_PT, S_O = 0, 1, 3
        with nc.Fori(0, 16) as t:
            pe, act, dve, pool, dma = k.stage("attention")
            with nc.Block() as block:
                @block.gpsimd
                def _(e):
                    for i in range(3):
                        j = e.value_load(idx_row[0:1, bass.ds(t * 3 + i, 1)], min_val=0, max_val=15)
                        e.tensor_copy(vg[:, :, ts(i, 32)], v1[:, :, bass.ds(j * 32, 32)]).then_inc(pool.steps, pool.did(f"v{i}"))
                    for u in range(2):
                        e.wait_ge(act.steps, act.at(f"exp{u}"))
                        e.wait_ge(dve.steps, dve.at(f"rden{u}"))
                        e.tensor_tensor(p[:, u], p[:, u],
                                                  den[:, u].unsqueeze(2).to_broadcast([C, 16, NK]), ALU.mult).then_inc(pool.steps, pool.did(f"p{u}"))

                @block.vector
                def _(e):
                    for i in range(3):
                        j = e.value_load(idx_row[0:1, bass.ds(t * 3 + i, 1)], min_val=0, max_val=15)
                        e.tensor_copy(kg[:, :, ts(i, 32)], k1[:, :, bass.ds(j * 32, 32)]).then_inc(dve.steps, dve.did(f"k{i}"))
                    for i in range(4):
                        e.tensor_scalar(qx[:, :, i, :], q1[:, :, bass.ds(t * 32, 32)], k.w["head_scale"][:, i:i + 1],
                                                 None, ALU.mult).then_inc(dve.steps, dve.did(f"q{i}"))
                    for u in range(2):
                        e.wait_ge(pe.steps, pe.at(f"s{u}"))
                        e.tensor_reduce(mx[:, u].rearrange("p (g n) -> p g n", g=4),
                                                 scored(u).rearrange("p g (n k) -> p g n k", k=NK), AX.X, ALU.max).then_inc(dve.steps, dve.did())
                        e.wait_ge(dve.steps, dve.n)
                        e.tensor_tensor(p[:, u].rearrange("p (g n) k -> p g n k", g=4),
                                                 scored(u).rearrange("p g (n k) -> p g n k", k=NK),
                                                 mx[:, u].rearrange("p (g n) -> p g n", g=4).unsqueeze(3)
                                                 .to_broadcast([C, 4, 4, NK]), ALU.subtract).then_inc(dve.steps, dve.did(f"sub{u}"))
                    for u in range(2):
                        e.wait_ge(act.steps, act.at(f"exp{u}"))
                        e.tensor_reduce(den[:, u], p[:, u], AX.X, ALU.add).then_inc(dve.steps, dve.did())
                        e.wait_ge(dve.steps, dve.n)
                        e.reciprocal(den[:, u], den[:, u]).then_inc(dve.steps, dve.did(f"rden{u}"))
                        if u == 0:
                            e.wait_ge(pe.steps, pe.at("vt0"))
                            e.tensor_copy(vt[:, 0].rearrange("p n c -> p (n c)"), k.ps[0:NK, S_VT, :]).then_inc(dve.steps, dve.did("vt0"))
                    for u in range(2):
                        if u:
                            e.wait_ge(pe.steps, pe.at("vt1"))
                            e.tensor_copy(vt[:, 1].rearrange("p n c -> p (n c)"), k.ps[0:NK, S_VT, :]).then_inc(dve.steps, dve.did("vt1"))
                        e.wait_ge(pe.steps, pe.at(f"o{u}"))
                        O = k.ps[:, S_O, :].rearrange("p (n h q) -> p n h q", n=4, h=4)
                        e.tensor_scalar(o[:], O[:, :, 0, :], k.w["head_mask"][:, 0:1], None, ALU.mult).then_inc(dve.steps, dve.did())
                        for i in range(1, 4):
                            e.wait_ge(dve.steps, dve.n)
                            dst = o[:] if i < 3 else q1[:, 4 * u:4 * u + 4, bass.ds(t * 32, 32)]
                            e.scalar_tensor_tensor(dst, O[:, :, i, :], k.w["head_mask"][:, i:i + 1], o[:],
                                                            ALU.mult, ALU.add).then_inc(dve.steps, dve.did(f"out{u}"))
                        e.wait_ge(dve.steps, dve.n)

                @block.scalar
                def _(e):
                    e.preload_act_table_set(EXP_LN)
                    for u in range(2):
                        e.wait_ge(dve.steps, dve.at(f"sub{u}"))
                        e.activation(p[:, u].rearrange("p a k -> p (a k)"),
                                              p[:, u].rearrange("p a k -> p (a k)"), ACT.Exp).then_inc(act.steps, act.did(f"exp{u}"))
                    for u in range(2):
                        for r in range(4):
                            e.wait_ge(pe.steps, pe.at(f"pt{u}{r}"))
                            e.activation(pt[:, u, ts(r, 4), :].rearrange("p a c -> p (a c)"),
                                                  k.ps[0:NK, S_PT + r % 2, :], ACT.Copy).then_inc(act.steps, act.did(f"pt{u}{r}"))

                @block.tensor
                def _(e):
                    def values_by_time(u):
                        if u == 0:
                            e.wait_ge(pool.steps, pool.at("v2"))
                            e.wait_ge(dve.steps, dve.at("sub0"))
                        else:
                            e.wait_ge(dve.steps, dve.at("vt0"))
                        for n in range(4):
                            ins = e.transpose(k.ps[0:NK, S_VT, ts(n, C)], vg[:, 4 * u + n, :], k.w["ident"][:])
                        ins.then_inc(pe.steps, pe.did(f"vt{u}"))

                    for u in range(2):
                        if u == 0:
                            e.wait_ge(dve.steps, dve.at("q3"))
                        for g in range(4):
                            for n in range(4):
                                ins = e.matmul(scored(u)[:, g, ts(n, NK)], qx[ts(g, 32), 4 * u + n, :, :].rearrange("p h q -> p (h q)"),
                                               kg[ts(g, 32), 4 * u + n, :], start=True, stop=True, tile_position=(32 * g, 0))
                        ins.then_inc(pe.steps, pe.did(f"s{u}"))
                    for u in range(2):
                        values_by_time(u)
                        e.wait_ge(pool.steps, pool.at(f"p{u}"))
                        for r in range(4):
                            if r >= 2 or u:
                                e.wait_ge(act.steps, act.at(f"pt{u}{r - 2}" if r >= 2 else f"pt{u - 1}{r + 2}"))
                            for n in range(4):
                                ins = e.transpose(k.ps[0:NK, S_PT + r % 2, ts(n, C)], p[:, u, 4 * r + n, :], k.w["ident"][:])
                            ins.then_inc(pe.steps, pe.did(f"pt{u}{r}"))
                        e.wait_ge(act.steps, act.at(f"pt{u}3"))
                        e.wait_ge(dve.steps, dve.at(f"vt{u}"))
                        if u:
                            e.wait_ge(dve.steps, dve.at("out0"))
                        for n in range(4):
                            for g in range(4):
                                ins = e.matmul(k.ps[ts(g, 32), S_O, ts(n, C)], vt[:, u, n, ts(g, 32)], pt[:, u, 4 * g + n, :],
                                               start=True, stop=True, tile_position=(0, 32 * g))
                        ins.then_inc(pe.steps, pe.did(f"o{u}"))
            k.end()


def attention_out(k, o1, h1, lg):
    nc = k.nc
    with ExitStack() as s:
        ob = k.sb("ao_ob", [C, T], stack=s)
        xb = k.sb("ao_xb", [C, T], stack=s)
        h = k.sb("ao_h", [C, T], stack=s)
        tmp = k.sb("ao_tmp", [C, 3, T], stack=s)
        with nc.Fori(0, B) as b:
            st = pe, act, dve, pool, dma = k.stage("attention_out")
            m = k.modb[:, 1, :]
            n = Norm(k, st, "n", 0, 1, xb[:], h[:], m, SB_, CB, tmp)
            with nc.Block() as block:
                @block.tensor
                def _(e):
                    e.wait_ge(pool.steps, pool.at("ob"))
                    e.matmul(k.ps[:, 2, :], k.w["W_O"][:], ob[:], start=True, stop=True).then_inc(pe.steps, pe.did("att"))
                    e.wait_ge(dve.steps, dve.at("x1"))
                    n.tensor(e)
                    e.wait_ge(dve.steps, dve.at("nh"))
                    for i in range(4):
                        ins = e.matmul(k.ps[:, 3, ts(i, 8)], h[:, ts(i, C)], k.w["w_gate1"][:], start=True, stop=True)
                    ins.then_inc(pe.steps, pe.did("lg"))

                @block.gpsimd
                def _(e):
                    e.tensor_copy(ob[:], flat(o1[:, bass.ds(b, 1), :])).then_inc(pool.steps, pool.did("ob"))
                    e.wait_ge(dve.steps, dve.at("nh"))
                    e.tensor_copy(flat(h1[:, bass.ds(b, 1), :]), h[:]).then_inc(pool.steps, pool.did())

                @block.scalar
                def _(e):
                    e.preload_act_table_set(EXP_LN)
                    n.scalar(e)

                @block.vector
                def _(e):
                    e.tensor_copy(k.modb[:], k.mod[:, :, :, bass.ds(b, 1)].rearrange("p l s a -> p l (s a)")).then_inc(dve.steps, dve.did())
                    e.wait_ge(dve.steps, dve.n)
                    e.wait_ge(pe.steps, pe.at("att"))
                    e.scalar_tensor_tensor(xb[:], k.ps[:, 2, :], m[:, GA:GA + 1], flat(k.X[:, bass.ds(b, 1), :]),
                                                    ALU.mult, ALU.add).then_inc(dve.steps, dve.did("x1"))
                    e.wait_ge(dve.steps, dve.n)
                    e.tensor_copy(flat(k.X[:, bass.ds(b, 1), :]), xb[:]).then_inc(dve.steps, dve.did())
                    n.vector(e)
                    e.wait_ge(pe.steps, pe.at("lg"))
                    e.tensor_copy(flat(lg[:, bass.ds(b, 1), :]), k.ps[:, 3, 0:32]).then_inc(dve.steps, dve.did())
            k.end()


def route(k, lg, gates):
    E, NT = 8, B * T // C
    CAP = int(1.25 * B * T * 2 / E)
    nc = k.nc
    with ExitStack() as s:
        l = lg[:].rearrange("p b (i x) -> p (b i) x", x=E)
        eq = k.sb("rt_eq", [C, NT, E], stack=s)
        oh = k.sb("rt_oh", [C, 2, NT, E], stack=s)
        m = k.sb("rt_m", [C, 2, NT], stack=s)
        mk = k.sb("rt_mk", [C, NT], stack=s)
        pr = k.sb("rt_pr", [C, 2, NT], stack=s)
        tot = k.sb("rt_tot", [C, 2 * NT, E], stack=s)
        cum = k.sb("rt_cum", [C, 2 * NT, E], stack=s)
        one = k.sb("rt_one", [C, 2 * NT], stack=s)
        wide = lambda ap: ap.unsqueeze(2).to_broadcast([C, NT, E])
        pe, act, dve, pool, dma = k.stage("route")
        with nc.Block() as block:
            @block.vector
            def _(e):
                e.memset(one[:], 1.0).then_inc(dve.steps, dve.did())
                for c in range(2):
                    e.tensor_reduce(m[:, c], l, AX.X, ALU.max).then_inc(dve.steps, dve.did())
                    e.wait_ge(dve.steps, dve.n)
                    e.tensor_tensor(eq[:], l, wide(m[:, c]), ALU.is_equal).then_inc(dve.steps, dve.did())
                    e.wait_ge(dve.steps, dve.n)
                    e.tensor_tensor(eq[:], eq[:], k.w["rev8"][:].unsqueeze(1).to_broadcast([C, NT, E]), ALU.mult).then_inc(dve.steps, dve.did())
                    e.wait_ge(dve.steps, dve.n)
                    e.tensor_reduce(mk[:], eq[:], AX.X, ALU.max).then_inc(dve.steps, dve.did())
                    e.wait_ge(dve.steps, dve.n)
                    e.tensor_tensor(oh[:, c], eq[:], wide(mk[:]), ALU.is_equal).then_inc(dve.steps, dve.did(f"oh{c}"))
                    e.wait_ge(dve.steps, dve.n)
                    if c == 0:
                        e.scalar_tensor_tensor(l, oh[:, 0], -1e30, l, ALU.mult, ALU.add).then_inc(dve.steps, dve.did())
                        e.wait_ge(dve.steps, dve.n)
                e.tensor_tensor(pr[:, 1], m[:, 1], m[:, 0], ALU.subtract).then_inc(dve.steps, dve.did("diff"))
                e.wait_ge(act.steps, act.at("exp"))
                e.tensor_scalar(pr[:, 0], pr[:, 1], 1.0, None, ALU.add).then_inc(dve.steps, dve.did())
                e.wait_ge(dve.steps, dve.n)
                e.reciprocal(pr[:, 0], pr[:, 0]).then_inc(dve.steps, dve.did())
                e.wait_ge(dve.steps, dve.n)
                e.tensor_tensor(pr[:, 1], pr[:, 1], pr[:, 0], ALU.mult).then_inc(dve.steps, dve.did())
                e.wait_ge(pe.steps, pe.at("cum"))
                e.tensor_copy(tot[:].rearrange("p a x -> p (a x)"), k.ps[:, 1, :]).then_inc(dve.steps, dve.did())
                e.wait_ge(dve.steps, dve.n)
                for x in range(E):
                    e.tensor_tensor_scan(cum[:, :, x], one[:], tot[:, :, x], 0.0, ALU.mult, ALU.add).then_inc(dve.steps, dve.did())
                e.wait_ge(dve.steps, dve.n)
                e.tensor_tensor(cum[:], cum[:], tot[:], ALU.subtract).then_inc(dve.steps, dve.did())
                e.wait_ge(dve.steps, dve.n)
                c2 = cum[:].rearrange("p a x -> p (a x)")
                e.tensor_tensor(c2, c2, k.ps[:, 0, :], ALU.add).then_inc(dve.steps, dve.did())
                e.wait_ge(dve.steps, dve.n)
                e.scalar_tensor_tensor(c2, c2, float(CAP), oh[:].rearrange("p c n x -> p (c n x)"), ALU.is_le, ALU.mult).then_inc(dve.steps, dve.did())
                e.wait_ge(dve.steps, dve.n)
                for c in range(2):
                    e.tensor_tensor(oh[:, c], cum[:, ts(c, NT), :], wide(pr[:, c]), ALU.mult).then_inc(dve.steps, dve.did())
                e.wait_ge(dve.steps, dve.n)
                e.tensor_tensor(gates[:], oh[:, 0], oh[:, 1], ALU.add).then_inc(dve.steps, dve.did())

            @block.scalar
            def _(e):
                e.preload_act_table_set(EXP_LN)
                e.wait_ge(dve.steps, dve.at("diff"))
                e.activation(pr[:, 1], pr[:, 1], ACT.Exp).then_inc(act.steps, act.did("exp"))

            @block.tensor
            def _(e):
                e.wait_ge(dve.steps, dve.at("oh1"))
                o = oh[:].rearrange("p c n x -> p (c n x)")
                e.matmul(k.ps[:, 0, :], k.w["upto"][:], o, start=True, stop=True)
                e.matmul(k.ps[:, 1, :], k.w["ones"][:], o, start=True, stop=True).then_inc(pe.steps, pe.did("cum"))
        k.end()


def experts(k, h1, gates):
    nc = k.nc
    E, F = 8, 4
    with ExitStack() as s:
        h = k.sb("ex_h", [C, T], stack=s)
        g = k.sb("ex_g", [C, 4, E], stack=s)
        r = k.sb("ex_r", [C, 2, F, T], stack=s)
        acc = k.sb("ex_acc", [C, 4, C], stack=s)
        with nc.Fori(0, B) as b:
            pe, act, dve, pool, dma = k.stage("experts")
            with nc.Block() as block:
                @block.gpsimd
                def _(e):
                    e.tensor_copy(h[:], flat(h1[:, bass.ds(b, 1), :])).then_inc(pool.steps, pool.did("h"))
                    for x in range(E):
                        for f in range(2, F):
                            e.wait_ge(act.steps, act.at(f"r{x}{f}"))
                            e.tensor_tensor(r[:, x % 2, f], r[:, x % 2, f], r[:, x % 2, f], ALU.mult).then_inc(pool.steps, pool.did(f"r{x}{f}"))

                @block.scalar
                def _(e):
                    for x in range(E):
                        if x >= 2:
                            e.wait_ge(pe.steps, pe.at(f"y{x - 2}"))
                        for f in range(F):
                            e.wait_ge(pe.steps, pe.at(f"u{x}{f}"))
                            e.activation(r[:, x % 2, f], k.ps[:, f, :], ACT.Relu).then_inc(act.steps, act.did(f"r{x}{f}"))

                @block.tensor
                def _(e):
                    def up(x):
                        for f in range(F):
                            if x:
                                e.wait_ge(act.steps, act.at(f"r{x - 1}{f}"))
                            e.matmul(k.ps[:, f, :], k.w["c_fc"][:, x, ts(f, C)], h[:], start=True, stop=True).then_inc(pe.steps, pe.did(f"u{x}{f}"))

                    def down(x):
                        e.wait_ge(dve.steps, dve.at(f"r{x}1"))
                        e.wait_ge(pool.steps, pool.at(f"r{x}3"))
                        if x >= 2:
                            e.wait_ge(dve.steps, dve.at(f"acc{x - 2}"))
                        for i in range(4):
                            for f in range(F):
                                ins = e.matmul(k.ps[:, 4 + x % 2, ts(i, C)], r[:, x % 2, f, ts(i, C)], k.w["c_proj"][:, x, f, :],
                                               start=(f == 0), stop=(f == F - 1))
                        ins.then_inc(pe.steps, pe.did(f"y{x}"))

                    e.wait_ge(pool.steps, pool.at("h"))
                    up(0)
                    for x in range(E):
                        if x + 1 < E:
                            up(x + 1)
                        down(x)
                    e.wait_ge(dve.steps, dve.at(f"acc{E - 1}"))
                    for i in range(4):
                        ins = e.transpose(k.ps[:, 6, ts(i, C)], acc[:, i, :], k.w["ident"][:])
                    ins.then_inc(pe.steps, pe.did("yT"))

                @block.vector
                def _(e):
                    e.tensor_copy(g[:], gates[:, bass.ds(b * 4, 4), :]).then_inc(dve.steps, dve.did())
                    e.tensor_copy(k.modb[:], k.mod[:, :, :, bass.ds(b, 1)].rearrange("p l s a -> p l (s a)")).then_inc(dve.steps, dve.did())
                    e.wait_ge(dve.steps, dve.n)

                    def gather(x):
                        e.wait_ge(pe.steps, pe.at(f"y{x}"))
                        for i in range(4):
                            y = k.ps[:, 4 + x % 2, ts(i, C)]
                            if x == 0:
                                e.tensor_scalar(acc[:, i, :], y, g[:, i, 0:1], None, ALU.mult).then_inc(dve.steps, dve.did(f"acc{x}"))
                            else:
                                e.scalar_tensor_tensor(acc[:, i, :], y, g[:, i, x:x + 1], acc[:, i, :],
                                                                ALU.mult, ALU.add).then_inc(dve.steps, dve.did(f"acc{x}"))
                    for x in range(E):
                        for f in range(2):
                            e.wait_ge(act.steps, act.at(f"r{x}{f}"))
                            e.tensor_tensor(r[:, x % 2, f], r[:, x % 2, f], r[:, x % 2, f], ALU.mult).then_inc(dve.steps, dve.did(f"r{x}{f}"))
                        if x:
                            gather(x - 1)
                            e.wait_ge(dve.steps, dve.n)
                    gather(E - 1)
                    e.wait_ge(pe.steps, pe.at("yT"))
                    xb = flat(k.X[:, bass.ds(b, 1), :])
                    e.scalar_tensor_tensor(xb, k.ps[:, 6, :], k.modb[:, 1, GB:GB + 1], xb, ALU.mult, ALU.add).then_inc(dve.steps, dve.did())
            k.end()


class Silu:

    def __init__(self, st, tag, psum, bias, out, tmp, ready):
        self.st, self.tag, self.psum, self.bias, self.out, self.tmp, self.ready = st, tag, psum, bias, out, tmp, ready

    def vector(self, e):
        pe, act, dve, pool, _ = self.st
        g, a = self.tag, self.tmp[:, 0, :]
        e.wait_ge(pe.steps, pe.at(self.ready))
        e.tensor_scalar(self.out, self.psum, self.bias, None, ALU.add).then_inc(dve.steps, dve.did())
        e.wait_ge(dve.steps, dve.n)
        e.tensor_scalar(a, self.out, LEAST, None, ALU.max).then_inc(dve.steps, dve.did(g + "z"))
        e.wait_ge(act.steps, act.at(g + "i"))
        e.tensor_tensor(self.out, self.out, a, ALU.mult).then_inc(dve.steps, dve.did(g + "o"))

    def scalar(self, e):
        pe, act, dve, pool, _ = self.st
        g, a = self.tag, self.tmp[:, 0, :]
        e.wait_ge(dve.steps, dve.at(g + "z"))
        e.activation(a, a, ACT.Exp, scale=-1.0).then_inc(act.steps, act.did())
        e.wait_ge(act.steps, act.n)
        e.activation(a, a, ACT.Ln, bias=1.0).then_inc(act.steps, act.did())
        e.wait_ge(act.steps, act.n)
        e.activation(a, a, ACT.Exp, scale=-1.0).then_inc(act.steps, act.did(g + "i"))


R, I = 1, 2
KI, KR = 0, 1
LOG_MIN = -19.0


def gla(k):
    nc = k.nc
    with ExitStack() as s:
        u = k.sb("g_u", [C, T], stack=s)
        y_first = k.sb("g_y_first", [C, 2, T], stack=s)
        mem_qk = k.sb("g_qk_Q0_K0_S2", [C, 12, T], stack=s)
        mem_unit = k.sb("g_unit_qh_y_S", [C, 6, T], stack=s)
        mem_cum = k.sb("g_cum_KT", [C, 4, T], stack=s)
        mem_U = k.sb("g_U_H", [C, 2, 3, T], stack=s)
        qk = mem_qk[:].rearrange("p (j r g) t -> p j r g t", j=3, r=2)
        unit = mem_unit[:].rearrange("p (r g) t -> p r g t", r=3)
        cum = mem_cum[:].rearrange("p (r g) t -> p r g t", r=2)
        U = lambda g: mem_U[:, g]
        m1, m2 = k.sb("g_m1", [C, 2, 2, T], stack=s), k.sb("g_m2", [C, 2, 2, T], stack=s)
        L = k.sb("g_L", [C, 2, T + 1], stack=s)
        one = k.sb("g_one", [C, 1], stack=s)
        qh = unit
        kh = k.sb("g_kh", [C, 2, 2, T], stack=s)[:]
        F, E = k.sb("g_F", [C, 4, 2, T], stack=s), k.sb("g_E", [C, 4, 2, T], stack=s)
        mem_F = F[:].rearrange("p a g t -> p (a g) t")
        tmp, h = mem_F[:, 0:3], mem_F[:, 3]
        xb, h2, o2 = (E[:, i, 1] for i in (3, 1, 2))
        Q = [mem_qk[:, 0:6].rearrange("p (r g) t -> p r g t", r=3)] + [k.sb(f"g_Q{i}", [C, 3, 2, T], stack=s) for i in (1, 2)]
        K = [mem_qk[:, 6:10].rearrange("p (r g) t -> p r g t", r=2)] + [k.sb(f"g_K{i}", [C, 2, 2, T], stack=s) for i in (1, 2)]
        products_over_blocks = lambda g: Q[1][:, 0, g, 0:198].rearrange("p (v r c) -> p v r c", v=2, r=3)
        qs, ks = m1, m2
        V = k.sb("g_V", [C, 4, 8, 96], stack=s)
        KT = lambda g: mem_cum[:].rearrange("p (r g) (i x) -> p g r i x", r=2, i=4)[:, g]
        H0 = k.sb("g_H0", [C, 2, 96], stack=s)

        def H(n, g):
            return H0[:, g] if n == 0 else mem_U[:, g].rearrange("p a t -> p (a t)")[:, 96 * (n - 1):96 * n]

        y = lambda g, pair: y_first[:, pair] if g == 0 else mem_unit[:, 2 * pair + 1]
        S = lambda g: mem_unit[:, 4 + g].rearrange("p (i h r t) -> p i h r t", i=2, h=4, r=2)
        S2 = lambda g: mem_qk[:, 10 + g, 0:256]
        P = [k.ps[:, i, :] for i in range(8)]
        halves = ((8, 1), (16, 2))
        blk = lambda ap, n: ap.rearrange("p (c x) -> p c x", x=n)
        m = k.modb[:, 2, :]

        def later(ap, n):
            return (ap, ap.rearrange("p r (c x) -> p r c x", c=2)[:, :, :, 8:16], ap[:, :, 16:32])[n]

        def half_of(ap, i, later_half):
            if i in (0, 3):
                return ap
            return blk(ap, 16 * i)[:, :, 8 * i:] if later_half else blk(ap, 16 * i)[:, :, :8 * i]

        ORDER = (("scores", 0), ("prepare", "norm"), ("gains", 0), ("prepare", "hidden"), ("scores", 1), ("prepare", "project"),
                 ("gains", 1), ("outputs", 0), ("prepare", "units"), ("scores", 2), ("prepare", "decays"), ("gains", 2),
                 ("outputs", 1), ("prepare", "running"), ("scores", 3), ("gains", 3), ("prepare", "blocks"), ("outputs", 2),
                 ("prepare", "turn"), ("outputs", 3), ("prepare", "split"), ("prepare", "keys"))

        def stage(name, scan_g, prep_b, prep_g):
            st = pe, act, dve, pool, dma = k.stage(name)
            g, sg = prep_g, scan_g
            tot = products_over_blocks(g) if g is not None else None
            n = Norm(k, st, "n", 6, 7, xb, h, m, SA, CA, tmp)
            act_u = Silu(st, "u", P[6], k.w["b_in2"][:, 0:1], u[:], tmp[:, 0:2], "z")
            products = [("c", j, ri) for j in range(3) for ri in range(2)] + [("v", i, 0) for i in range(4)]
            evacuated = lambda x: (act if products[x][0] == "c" else dve)

            def in_turn(scan, prepare):
                for what, which in ORDER:
                    if what == "prepare":
                        if prep_g is not None and (prep_g == 0 or which not in ("norm", "hidden")):
                            prepare(which)
                    elif scan_g is not None:
                        scan(what, which)

            with nc.Block() as block:
                @block.gpsimd
                def _(e):
                    def prepare(what):
                        if what == "norm":
                            e.tensor_copy(xb, flat(k.X[:, bass.ds(prep_b, 1), :])).then_inc(pool.steps, pool.did("xb"))
                        elif what == "units":
                            mag = F[:, 3, g]
                            e.wait_ge(dve.steps, dve.at("parts"))
                            e.tensor_tensor(m1[:, 0, g], qk[:, 2, 1, g], qk[:, 2, 1, g], ALU.mult).then_inc(pool.steps, pool.did("ai2"))
                            e.wait_ge(act.steps, act.at("rs"))
                            e.tensor_tensor(m2[:, 0, g], m1[:, 1, g], m1[:, 1, g], ALU.mult).then_inc(pool.steps, pool.did())
                            e.wait_ge(pool.steps, pool.n)
                            e.tensor_tensor(m2[:, 0, g], m2[:, 0, g], mag, ALU.mult).then_inc(pool.steps, pool.did())
                            e.wait_ge(pool.steps, pool.n)
                            e.tensor_scalar(m2[:, 0, g], m2[:, 0, g], -0.5, 1.5, ALU.mult, ALU.add).then_inc(pool.steps, pool.did())
                            e.wait_ge(pool.steps, pool.n)
                            e.tensor_tensor(m1[:, 1, g], m1[:, 1, g], m2[:, 0, g], ALU.mult).then_inc(pool.steps, pool.did("rs"))
                        elif what == "split":
                            e.wait_ge(dve.steps, dve.at("kh"))
                            e.wait_ge(act.steps, act.at("f2"))
                            for i in range(3):
                                for p_ in range(2):
                                    e.tensor_tensor(half_of(K[i][:, p_, g], i, False), half_of(kh[:, p_, g], i, False), half_of(E[:, i, g], i, False),
                                                    ALU.mult).then_inc(pool.steps, pool.did())

                    in_turn(lambda what, i: None, prepare)

                @block.tensor
                def _(e):
                    def scan(what, i):
                        odd = i % 2
                        if what == "scores":
                            if i >= 2:
                                e.wait_ge(dve.steps, dve.at(f"s{i - 2}"))
                                e.wait_ge(dve.steps, dve.at(f"h{i - 2}"))
                            for turn in range(4):
                                if turn:
                                    ins.then_inc(pe.steps, pe.did())
                                    e.wait_ge(pe.steps, pe.n)
                                for part, j, n_ in ((part, j, n_) for part in range(2) for j in range(4) for n_ in range(3)):
                                    h4 = (turn + n_ // 2) % 4
                                    t, r = slice(i * C + 32 * j, i * C + 32 * j + 32), ts(h4, 32)
                                    keys, planes = (K[n_][r, KR, sg, t], slice(1, 3)) if part == 0 else (K[n_][r, KI, sg, t], slice(0, 2))
                                    col = 64 * h4 + (256 if n_ == 1 else 0)
                                    scored = P[2 * odd + n_ // 2][ts(j, 32), col:col + 64].rearrange("p (r x) -> p r x", r=2)
                                    ins = e.matmul(later(scored, n_), keys, later(Q[n_][r, planes, sg, t], n_),
                                                   start=(turn == 0 and part == 0 and n_ != 1), stop=(part == 1),
                                                   tile_position=(32 * h4, 32 * j), skip_group_check=True)
                            ins.then_inc(pe.steps, pe.did(f"s{i}"))
                            e.wait_ge(pe.steps, pe.n)
                        elif what == "gains":
                            for j in range(4):
                                if j:
                                    ins.then_inc(pe.steps, pe.did())
                                    e.wait_ge(pe.steps, pe.n)
                                rows = ts(j, 32)
                                for part, h4 in ((part, h4) for part in range(2) for h4 in range(4)):
                                    ins = e.matmul(P[2 * odd + 1][ts(h4, 32), 256 + j * 64:320 + j * 64], KT(sg)[rows, (KR, KI)[part], i, ts(h4, 32)],
                                                   V[rows, i, 4 * sg + h4, (slice(32, 96), slice(0, 64))[part]], start=(part == 0), stop=(part == 1),
                                                   tile_position=(32 * j, 32 * h4))
                            ins.then_inc(pe.steps, pe.did(f"g{i}"))
                        else:
                            e.wait_ge(dve.steps, dve.at(f"s{i}"))
                            e.wait_ge(dve.steps, dve.at(f"h{i}"))
                            if i:
                                e.wait_ge(pe.steps, pe.at(f"y{i - 1}"))
                            for turn in range(4):
                                for part, second, bank in ((part, second, bank) for part in range(2) for second in range(2) for bank in range(2)):
                                    j, h4 = (turn + bank) % 4, 2 * bank + second
                                    rows, t = ts(j, 32), slice(i * C + 32 * j, i * C + 32 * j + 32)
                                    ins = e.matmul(P[4 + bank][ts(second, 64), t], V[rows, i, 4 * sg + h4, (slice(32, 96), slice(0, 64))[part]],
                                                   S(sg)[rows, i % 2, h4, part, :], start=(turn == 0 and part == 0), stop=False,
                                                   tile_position=(32 * j, 64 * second), skip_group_check=True)
                                ins.then_inc(pe.steps, pe.did())
                                e.wait_ge(pe.steps, pe.n)
                            for j, part, h4 in ((j, part, h4) for j in range(4) for part in range(2) for h4 in (0, 2, 1, 3)):
                                t = slice(i * C + 32 * j, i * C + 32 * j + 32)
                                ins = e.matmul(P[4 + h4 // 2][ts(h4 % 2, 64), t], H(4 * i + j, sg)[ts(h4, 32), (slice(32, 96), slice(0, 64))[part]],
                                               qs[ts(h4, 32), part, sg, t], start=False, stop=(part == 1),
                                               tile_position=(32 * h4, 64 * (h4 % 2)), skip_group_check=True)
                            ins.then_inc(pe.steps, pe.did(f"y{i}"))

                    def prepare(what):
                        if what == "norm":
                            e.wait_ge(pool.steps, pool.at("xb"))
                            n.tensor(e)
                        elif what == "hidden":
                            e.wait_ge(dve.steps, dve.at("nh"))
                            e.matmul(P[6], k.w["W_in2"][:], h, start=True, stop=True).then_inc(pe.steps, pe.did("z"))
                        elif what == "project":
                            if g == 0:
                                e.wait_ge(dve.steps, dve.at("uo"))
                            for x, (kind, j, ri) in enumerate(products):
                                if x >= 2:
                                    e.wait_ge(evacuated(x - 2).steps, evacuated(x - 2).at(f"p{x - 2}"))
                                if kind == "c":
                                    ins = e.matmul(P[6 + x % 2], k.w["W_qka"][:, j, ri, g, :], u[:], start=True, stop=True)
                                else:
                                    ins = e.matmul(P[6 + x % 2][:, 0:256], u[:, ts(j, C)], k.w["W_v2"][:, ts(g, 256)], start=True, stop=True)
                                ins.then_inc(pe.steps, pe.did(f"p{x}"))
                        elif what == "keys":
                            e.wait_ge(dve.steps, dve.at("ks"))
                            for r in range(2):
                                for i in range(4):
                                    ins = e.transpose(P[6 + r][:, ts(i, C)], ks[:, r, g, ts(i, C)], k.w["ident"][:])
                                ins.then_inc(pe.steps, pe.did(f"kt{r}"))

                    in_turn(scan, prepare)

                @block.scalar
                def _(e):
                    def prepare(what):
                        if what == "norm":
                            n.scalar(e)
                        elif what == "hidden":
                            act_u.scalar(e)
                        elif what == "project":
                            for x, (kind, j, ri) in enumerate(products):
                                if kind == "c":
                                    e.wait_ge(pe.steps, pe.at(f"p{x}"))
                                    e.activation(qk[:, j, ri, g], P[6 + x % 2], ACT.Identity, bias=k.w["b_qka"][:, j, ri, g:g + 1]).then_inc(act.steps, act.did(f"p{x}"))
                        elif what == "units":
                            lg, mag = E[:, 3, g], F[:, 3, g]
                            e.wait_ge(dve.steps, dve.at("mag"))
                            e.activation(lg, mag, ACT.Ln).then_inc(act.steps, act.did("ln"))
                            e.wait_ge(act.steps, act.n)
                            e.activation(F[:, 0, g], mag, ACT.Ln, bias=1.0).then_inc(act.steps, act.did("ln1"))
                            e.activation(m1[:, 1, g], lg, ACT.Exp, scale=-0.5).then_inc(act.steps, act.did("rs"))
                        elif what == "decays":
                            e.wait_ge(dve.steps, dve.at("d0"))
                            e.activation(E[:, 0, g], F[:, 0, g], ACT.Exp, scale=-1.0).then_inc(act.steps, act.did())
                            e.wait_ge(act.steps, act.n)
                            e.activation(F[:, 0, g], F[:, 0, g], ACT.Exp).then_inc(act.steps, act.did("f0"))
                            for i in (1, 2, 3):
                                e.wait_ge(dve.steps, dve.at(f"d{i}"))
                                e.activation(half_of(F[:, i, g], i, True), half_of(F[:, i, g], i, True), ACT.Exp).then_inc(act.steps, act.did())
                                e.activation(half_of(E[:, i, g], i, False), half_of(E[:, i, g], i, False), ACT.Exp).then_inc(act.steps, act.did(f"f{i}"))
                        elif what == "keys":
                            for r in range(2):
                                e.wait_ge(pe.steps, pe.at(f"kt{r}"))
                                e.activation(KT(g)[:, r], P[6 + r].rearrange("p (i x) -> p i x", i=4), ACT.Copy).then_inc(act.steps, act.did())

                    e.preload_act_table_set(EXP_LN)
                    in_turn(lambda what, i: None, prepare)
                    if sg is not None:
                        e.wait_ge(pe.steps, pe.at("y3"))
                        e.activation(y(sg, 1), P[5], ACT.Copy).then_inc(act.steps, act.did())

                @block.vector
                def _(e):
                    def sums(i):
                        e.wait_ge(pe.steps, pe.at(f"s{i}"))
                        if i >= 2:
                            e.wait_ge(pe.steps, pe.at(f"y{i - 2}"))
                        whole = lambda ap: ap.rearrange("p (a x) -> p a x", a=8)
                        s_ = whole(S(sg)[:, i % 2].rearrange("p h r t -> p (h r t)"))
                        t_ = whole(S2(sg))
                        msk = lambda n_: k.w["gla_mask"][:, n_:n_ + 1, :].to_broadcast([C, 8, 32])
                        bank = P[2 * (i % 2)]
                        e.tensor_tensor(s_, whole(bank[:, 0:256]), msk(0), ALU.mult).then_inc(dve.steps, dve.did())
                        e.tensor_tensor(later(t_, 1), later(whole(bank[:, 256:512]), 1), later(msk(1), 1), ALU.mult).then_inc(dve.steps, dve.did())
                        e.wait_ge(dve.steps, dve.n)
                        e.tensor_tensor(later(s_, 1), later(s_, 1), later(t_, 1), ALU.add).then_inc(dve.steps, dve.did())
                        e.wait_ge(dve.steps, dve.n)
                        e.wait_ge(pe.steps, pe.at(f"g{i}"))
                        e.tensor_tensor(later(s_, 2), later(s_, 2), later(whole(P[2 * (i % 2) + 1][:, 0:256]), 2), ALU.add).then_inc(dve.steps, dve.did(f"s{i}"))

                    def states(i):
                        e.wait_ge(pe.steps, pe.at(f"g{i}"))
                        for j in range(4):
                            c_ = 4 * i + j
                            new, end = H(c_ + 1, sg), 32 * c_ + 31
                            e.scalar_tensor_tensor(new[:, 32:96], H(c_, sg)[:, 32:96], F[:, 3, sg, end:end + 1],
                                                   P[2 * (i % 2) + 1][:, 256 + j * 64:320 + j * 64], ALU.mult, ALU.add).then_inc(dve.steps, dve.did())
                            e.wait_ge(dve.steps, dve.n)
                            e.tensor_scalar(new[:, 0:32], new[:, 64:96], -1.0, None, ALU.mult).then_inc(dve.steps, dve.did(f"h{i}"))

                    def scan(what, i):
                        if what == "scores" and i:
                            sums(i - 1)
                        elif what == "gains" and i:
                            states(i - 1)
                        elif what == "outputs" and i == 2:
                            sums(3)
                            states(3)

                    def prepare(what):
                        if what == "norm":
                            e.tensor_copy(k.modb[:], k.mod[:, :, :, bass.ds(prep_b, 1)].rearrange("p l s a -> p l (s a)")).then_inc(dve.steps, dve.did())
                            e.wait_ge(dve.steps, dve.n)
                            n.vector(e)
                        elif what == "hidden":
                            act_u.vector(e)
                        elif what == "project":
                            for x, (kind, i, _) in enumerate(products):
                                if kind == "v":
                                    e.wait_ge(pe.steps, pe.at(f"p{x}"))
                                    e.tensor_tensor(V[:, i, ts(g, 4), 32:96], P[6 + x % 2][:, 0:256].rearrange("p (h x) -> p h x", h=4),
                                                    k.w["b_v2"][:, ts(g, 256)].rearrange("p (h x) -> p h x", h=4), ALU.add).then_inc(dve.steps, dve.did(f"p{x}"))
                            e.wait_ge(dve.steps, dve.n)
                            e.tensor_scalar(V[:, :, ts(g, 4), 0:32], V[:, :, ts(g, 4), 64:96], -1.0, None, ALU.mult).then_inc(dve.steps, dve.did())
                            e.wait_ge(act.steps, act.at("p5"))
                            e.tensor_tensor(F[:, 3, g], qk[:, 2, 0, g], qk[:, 2, 0, g], ALU.mult).then_inc(dve.steps, dve.did("parts"))
                        elif what == "units":
                            lg, mag = E[:, 3, g], F[:, 3, g]
                            e.wait_ge(pool.steps, pool.at("ai2"))
                            e.wait_ge(dve.steps, dve.at("parts"))
                            e.tensor_tensor(mag, mag, m1[:, 0, g], ALU.add).then_inc(dve.steps, dve.did())
                            e.wait_ge(dve.steps, dve.n)
                            e.tensor_scalar(mag, mag, 1e-18, None, ALU.max).then_inc(dve.steps, dve.did("mag"))
                            e.wait_ge(act.steps, act.at("rs"))
                            e.tensor_tensor(lg, lg, F[:, 0, g], ALU.subtract).then_inc(dve.steps, dve.did("lg"))
                        elif what == "decays":
                            lg = E[:, 3, g]
                            e.wait_ge(act.steps, act.at("rs"))
                            e.wait_ge(dve.steps, dve.at("lg"))
                            e.tensor_scalar(lg, lg, LOG_MIN, None, ALU.max).then_inc(dve.steps, dve.did())
                            e.wait_ge(pool.steps, pool.at("rs"))
                            for plane in (R, I):
                                e.tensor_tensor(unit[:, plane, g], qk[:, 2, plane - 1, g], m1[:, 1, g], ALU.mult).then_inc(dve.steps, dve.did())
                            e.wait_ge(dve.steps, dve.n)
                            e.tensor_scalar(unit[:, 0, g], unit[:, I, g], -1.0, None, ALU.mult).then_inc(dve.steps, dve.did())
                            e.tensor_tensor_scan(L[:, g, 1:], one[:].to_broadcast([C, T]), lg, 0.0, ALU.mult, ALU.add).then_inc(dve.steps, dve.did())
                            e.wait_ge(dve.steps, dve.n)
                            Lt = L[:, g, 1:]
                            l8 = blk(Lt, 8)
                            e.tensor_tensor(blk(F[:, 0, g], 8), l8, l8[:, :, 3:4].to_broadcast([C, 64, 8]), ALU.subtract).then_inc(dve.steps, dve.did("d0"))
                            for half, i in halves:
                                l2 = blk(Lt, 2 * half)
                                mid = l2[:, :, half - 1:half].to_broadcast([C, T // (2 * half), half])
                                e.tensor_tensor(half_of(F[:, i, g], i, True), l2[:, :, half:], mid, ALU.subtract).then_inc(dve.steps, dve.did())
                                e.tensor_tensor(half_of(E[:, i, g], i, False), mid, l2[:, :, :half], ALU.subtract).then_inc(dve.steps, dve.did(f"d{i}"))
                            l32 = blk(Lt, 32)
                            before = blk(L[:, g, 0:T], 32)[:, :, 0:1].to_broadcast([C, 16, 32])
                            e.tensor_tensor(blk(F[:, 3, g], 32), l32, before, ALU.subtract).then_inc(dve.steps, dve.did())
                            e.tensor_tensor(blk(E[:, 3, g], 32), l32[:, :, 31:32].to_broadcast([C, 16, 32]), l32, ALU.subtract).then_inc(dve.steps, dve.did("d3"))
                        elif what == "running":
                            cb = cum[:, :, g].rearrange("p r (c x) -> p r c x", x=16)
                            ub = unit[:, :, g].rearrange("p r (c x) -> p r c x", x=16)
                            A1 = m1[:, 0, g, 0:64].rearrange("p (r c) -> p r c", r=2)
                            A2 = m2[:, 0, g, 0:64].rearrange("p (r c) -> p r c", r=2)
                            e.tensor_copy(cb[:, :, :, 0], ub[:, 1:3, :, 0]).then_inc(dve.steps, dve.did())
                            for x in range(1, 16):
                                e.wait_ge(dve.steps, dve.n)
                                e.tensor_tensor(A1, cb[:, 0:1, :, x - 1].to_broadcast([C, 2, 32]), ub[:, 1:3, :, x], ALU.mult).then_inc(dve.steps, dve.did())
                                e.tensor_tensor(A2, cb[:, 1:2, :, x - 1].to_broadcast([C, 2, 32]), ub[:, 0:2, :, x], ALU.mult).then_inc(dve.steps, dve.did())
                                e.wait_ge(dve.steps, dve.n)
                                e.tensor_tensor(cb[:, :, :, x], A1, A2, ALU.add).then_inc(dve.steps, dve.did())
                        elif what == "blocks":
                            e.memset(tot[:, :, 0::2, 0:1], 0.0).then_inc(dve.steps, dve.did())
                            e.memset(tot[:, :, 1, 0:1], 1.0).then_inc(dve.steps, dve.did())
                            e.wait_ge(dve.steps, dve.n)
                            last = cum[:, :, g].rearrange("p r (c x) -> p r c x", x=16)[:, :, :, 15]
                            e.tensor_copy(tot[:, 0, 1:3, 1:33], last).then_inc(dve.steps, dve.did())
                            e.wait_ge(dve.steps, dve.n)
                            e.tensor_scalar(tot[:, 0, 0, 1:33], tot[:, 0, 2, 1:33], -1.0, None, ALU.mult).then_inc(dve.steps, dve.did())
                            e.wait_ge(dve.steps, dve.n)
                            src, d = 0, 1
                            while d < 32:
                                c_ = 32 - d
                                B1 = m1[:, 0, g, 0:2 * c_].rearrange("p (r c) -> p r c", r=2)
                                B2 = m2[:, 0, g, 0:2 * c_].rearrange("p (r c) -> p r c", r=2)
                                old, new = tot[:, src], tot[:, 1 - src]
                                e.tensor_tensor(B1, old[:, 1:2, 1:1 + c_].to_broadcast([C, 2, c_]), old[:, 1:3, 1 + d:33], ALU.mult).then_inc(dve.steps, dve.did())
                                e.tensor_tensor(B2, old[:, 2:3, 1:1 + c_].to_broadcast([C, 2, c_]), old[:, 0:2, 1 + d:33], ALU.mult).then_inc(dve.steps, dve.did())
                                e.tensor_copy(new[:, :, 1:1 + d], old[:, :, 1:1 + d]).then_inc(dve.steps, dve.did())
                                e.wait_ge(dve.steps, dve.n)
                                e.tensor_tensor(new[:, 1:3, 1 + d:33], B1, B2, ALU.add).then_inc(dve.steps, dve.did())
                                e.wait_ge(dve.steps, dve.n)
                                e.tensor_scalar(new[:, 0, 1 + d:33], new[:, 2, 1 + d:33], -1.0, None, ALU.mult).then_inc(dve.steps, dve.did())
                                e.wait_ge(dve.steps, dve.n)
                                src, d = 1 - src, 2 * d
                        elif what == "turn":
                            w = lambda ap: ap.rearrange("p r (c x) -> p r c x", x=16)
                            pre = lambda lo: tot[:, 1, lo:lo + 2, 0:32].unsqueeze(3).to_broadcast([C, 2, 32, 16])
                            e.tensor_tensor(w(m1[:, :, g]), w(cum[:, 0:1, g].to_broadcast([C, 2, T])), pre(1), ALU.mult).then_inc(dve.steps, dve.did())
                            e.tensor_tensor(w(m2[:, :, g]), w(cum[:, 1:2, g].to_broadcast([C, 2, T])), pre(0), ALU.mult).then_inc(dve.steps, dve.did())
                            e.wait_ge(dve.steps, dve.n)
                            e.tensor_tensor(U(g)[:, 1:3], m1[:, :, g], m2[:, :, g], ALU.add).then_inc(dve.steps, dve.did())
                            e.wait_ge(dve.steps, dve.n)
                            e.tensor_scalar(U(g)[:, 0], U(g)[:, 2], -1.0, None, ALU.mult).then_inc(dve.steps, dve.did())
                            e.wait_ge(dve.steps, dve.n)
                            for j, out, (p1, p2), name_ in ((0, qh[:, 1:3, g], (1, 0), "qh"), (1, kh[:, :, g], (0, 1), "kh")):
                                wide = lambda ri: qk[:, j, ri:ri + 1, g].to_broadcast([C, 2, T])
                                e.tensor_tensor(m1[:, :, g], wide(0), U(g)[:, p1:p1 + 2], ALU.mult).then_inc(dve.steps, dve.did())
                                e.tensor_tensor(m2[:, :, g], wide(1), U(g)[:, p2:p2 + 2], ALU.mult).then_inc(dve.steps, dve.did())
                                e.wait_ge(dve.steps, dve.n)
                                e.tensor_tensor(out, m1[:, :, g], m2[:, :, g], ALU.add).then_inc(dve.steps, dve.did(name_))
                                e.wait_ge(dve.steps, dve.n)
                            e.tensor_scalar(qh[:, 0, g], qh[:, 2, g], -1.0, None, ALU.mult).then_inc(dve.steps, dve.did())
                            e.wait_ge(dve.steps, dve.n)
                        elif what == "split":
                            e.wait_ge(act.steps, act.at("f3"))
                            for p_ in range(2):
                                e.tensor_tensor(ks[:, p_, g], kh[:, p_, g], E[:, 3, g], ALU.mult).then_inc(dve.steps, dve.did("ks"))
                            for i in range(3):
                                for p_ in range(3):
                                    e.tensor_tensor(half_of(Q[i][:, p_, g], i, True), half_of(qh[:, p_, g], i, True), half_of(F[:, i, g], i, True),
                                                    ALU.mult).then_inc(dve.steps, dve.did())
                            for p_ in range(2):
                                e.tensor_tensor(qs[:, p_, g], qh[:, 1 + p_, g], F[:, 3, g], ALU.mult).then_inc(dve.steps, dve.did())

                    in_turn(scan, prepare)
                    if sg is not None:
                        e.wait_ge(pe.steps, pe.at("y3"))
                        e.tensor_copy(y(sg, 0), P[4]).then_inc(dve.steps, dve.did())
            k.end()

        def out(name, b):
            st = pe, act, dve, pool, dma = k.stage(name)
            act_y = Silu(st, "y", P[0], k.w["b_y2"][:, 0:1], h2, tmp[:, 0:2], "z")
            with nc.Block() as block:
                @block.tensor
                def _(e):
                    for i in range(4):
                        ins = e.matmul(P[0], k.w["W_y2"][:, i, :], y(i // 2, i % 2), start=(i == 0), stop=(i == 3))
                    ins.then_inc(pe.steps, pe.did("z"))
                    e.wait_ge(dve.steps, dve.at("yo"))
                    e.matmul(P[1], k.w["W_out2"][:], h2, start=True, stop=True).then_inc(pe.steps, pe.did("o"))

                @block.scalar
                def _(e):
                    e.preload_act_table_set(EXP_LN)
                    act_y.scalar(e)
                    e.wait_ge(pe.steps, pe.at("o"))
                    e.activation(o2, P[1], ACT.Identity, bias=k.w["b_out2"][:, 0:1]).then_inc(act.steps, act.did("o"))

                @block.vector
                def _(e):
                    e.tensor_copy(k.modb[:], k.mod[:, :, :, bass.ds(b, 1)].rearrange("p l s a -> p l (s a)")).then_inc(dve.steps, dve.did())
                    act_y.vector(e)
                    e.wait_ge(act.steps, act.at("o"))
                    x = flat(k.X[:, bass.ds(b, 1), :])
                    e.scalar_tensor_tensor(x, o2, m[:, GA:GA + 1], x, ALU.mult, ALU.add).then_inc(dve.steps, dve.did())
            k.end()

        pe, act, dve, pool, dma = k.stage("gla_start")
        with nc.Block() as block:
            @block.vector
            def _(e):
                for t in (one, L):
                    e.memset(t[:], 1.0 if t is one else 0.0).then_inc(dve.steps, dve.did())
                for t in (K[1], K[2]):
                    e.memset(t[:], 0.0).then_inc(dve.steps, dve.did())
                e.tensor_copy(H0[:, :, 32:96], k.w["h0"][:]).then_inc(dve.steps, dve.did())
                e.tensor_scalar(H0[:, :, 0:32], k.w["h0"][:, :, 32:64], -1.0, None, ALU.mult).then_inc(dve.steps, dve.did())
        k.end()
        stage("gla_first", None, 0, 0)
        with nc.Fori(0, B - 1) as b:
            stage("gla_scan0", 0, b, 1)
            stage("gla_scan1", 1, b + 1, 0)
            out("gla_out", b)
        stage("gla_scan0_last", 0, B - 1, 1)
        stage("gla_scan1_last", 1, None, None)
        out("gla_out_last", B - 1)


def routed_mlp(k):
    nc = k.nc
    with ExitStack() as s:
        lanes = lambda name, shape: [k.sb(f"m_{name}{l}", shape, stack=s) for l in range(2)]
        xb, h, tmp, masked, modb = (lanes(name, shape) for name, shape in
                                    (("xb", [C, T]), ("h", [C, T]), ("tmp", [C, 3, T]), ("masked", [C, 2, T]), ("modb", [C, 4, 6])))
        r = k.sb("m_r", [C, 4, T], stack=s)
        dw = k.sb("m_dw", [C, 1], stack=s)
        gate = k.sb("m_gate", [C, C], stack=s)
        bias = k.sb("m_bias", [C, 1], stack=s)
        P = [k.ps[:, i, :] for i in range(8)]
        pe, act, dve, pool, dma = k.stage("mlp2_start")
        with nc.Block() as block:
            @block.vector
            def _(e):
                e.tensor_tensor(dw[:], k.w["gate_w2"][:, 1:2], k.w["gate_w2"][:, 0:1], ALU.subtract).then_inc(dve.steps, dve.did())
                e.tensor_reduce(bias[:], k.w["b2_2"][:], AX.X, ALU.add).then_inc(dve.steps, dve.did())
                e.wait_ge(dve.steps, dve.n)
                e.tensor_copy(gate[:], dw[:, 0:1].to_broadcast([C, C])).then_inc(dve.steps, dve.did())
        k.end()
        with nc.Fori(0, B // 2) as pair:
            st = pe, act, dve, pool, dma = k.stage("mlp2")
            batch = lambda l: bass.ds(pair * 2 + l, 1)
            m = [modb[l][:, 2, :] for l in range(2)]
            n = [Norm(k, st, f"n{l}", 3 * l, 3 * l + 1, xb[l][:], h[l][:], m[l], SB_, CB, tmp[l]) for l in range(2)]
            scores, total = (lambda l: P[3 * l + 2]), (lambda l: P[6 + l])
            hidden = lambda i: P[(0, 1, 3, 4)[i % 4]]
            order = [(l, p_, f) for l in range(2) for p_ in (2, 0, 1) for f in range(4)]
            with nc.Block() as block:
                @block.gpsimd
                def _(e):
                    for l in range(2):
                        e.tensor_copy(xb[l][:], flat(k.X[:, batch(l), :])).then_inc(pool.steps, pool.did(f"xb{l}"))

                @block.tensor
                def _(e):
                    def down(i):
                        l, p_, f = order[i]
                        e.wait_ge(act.steps, act.at(f"r{i}"))
                        e.matmul(total(l), k.w["w2_2"][:, p_, f, :], r[:, i % 4, :], start=(i % 12 == 0), stop=(i % 12 == 11)).then_inc(pe.steps, pe.did(f"d{i}"))

                    for l in range(2):
                        e.wait_ge(pool.steps, pool.at(f"xb{l}"))
                        n[l].tensor(e)
                    for l in range(2):
                        e.wait_ge(dve.steps, dve.at(f"n{l}h"))
                        e.matmul(scores(l), gate[:], h[l][:], start=True, stop=True).then_inc(pe.steps, pe.did(f"score{l}"))
                    for i, (l, p_, f) in enumerate(order):
                        if i >= 4:
                            e.wait_ge(act.steps, act.at(f"r{i - 4}"))
                        if p_ < 2:
                            e.wait_ge(dve.steps, dve.at(f"m{l}{p_}"))
                        x = h[l][:] if p_ == 2 else masked[l][:, p_, :]
                        e.matmul(hidden(i), k.w["w1_2"][:, p_, ts(f, C)], x, start=True, stop=True).then_inc(pe.steps, pe.did(f"u{i}"))
                        if i >= 2:
                            down(i - 2)
                    down(22)
                    down(23)

                @block.scalar
                def _(e):
                    e.preload_act_table_set(EXP_LN)
                    for l in range(2):
                        n[l].scalar(e)
                    for i, (l, p_, f) in enumerate(order):
                        e.wait_ge(pe.steps, pe.at(f"u{i}"))
                        if i >= 4:
                            e.wait_ge(pe.steps, pe.at(f"d{i - 4}"))
                        e.activation(r[:, i % 4, :], hidden(i), ACT.Relu, bias=k.w["b1_2"][:, p_, f:f + 1]).then_inc(act.steps, act.did(f"r{i}"))

                @block.vector
                def _(e):
                    for l in range(2):
                        e.tensor_copy(modb[l][:], k.mod[:, :, :, batch(l)].rearrange("p l s a -> p l (s a)")).then_inc(dve.steps, dve.did())
                    e.wait_ge(dve.steps, dve.n)
                    for l in range(2):
                        n[l].vector(e)
                    for l in range(2):
                        e.wait_ge(pe.steps, pe.at(f"score{l}"))
                        e.wait_ge(dve.steps, dve.at(f"n{l}h"))
                        for x, op in ((0, ALU.is_le), (1, ALU.is_gt)):
                            e.scalar_tensor_tensor(masked[l][:, x, :], scores(l), 0.0, h[l][:], op, ALU.mult).then_inc(dve.steps, dve.did(f"m{l}{x}"))
                    for l in range(2):
                        e.wait_ge(pe.steps, pe.at(f"d{12 * l + 11}"))
                        e.tensor_scalar(h[l][:], total(l), bias[:, 0:1], None, ALU.add).then_inc(dve.steps, dve.did())
                        e.wait_ge(dve.steps, dve.n)
                        e.scalar_tensor_tensor(flat(k.X[:, batch(l), :]), h[l][:], m[l][:, GB:GB + 1], xb[l][:], ALU.mult, ALU.add).then_inc(dve.steps, dve.did())
            k.end()


def delta_rule(k):
    nc = k.nc
    TAPS, NH, NT = 4, 8, 4
    with ExitStack() as s:
        w_qk = k.sb("d_w_qk", [C, TAPS, 2, 8 * C], stack=s)
        w_v = k.sb("d_w_v", [C, TAPS, 256], stack=s)
        neg_a = k.sb("d_neg_a", [C, NH], stack=s)
        xb = k.sb("d_xb", [C, T], stack=s)
        hp = k.sb("d_hp", [C, T + 3], stack=s)
        QK = k.sb("d_QK", [C, 2, NH, T], stack=s)
        KT = k.sb("d_KT", [C, NT, NH, C], stack=s)
        VG = k.sb("d_values_gates", [C, 2, NT, 256], stack=s)
        V, G = VG[:, 0], VG[:, 1]
        O = k.sb("d_O", [C, NT, NH, 32], stack=s)
        sq = k.sb("d_sq", [C, 2, 2, T], stack=s)
        small = {n: k.sb("d_" + n, [C, NT, NH], stack=s) for n in
                 ("beta", "z", "g", "t", "gc", "gam", "end", "ga", "qn", "kn", "gtot", "n2", "ss", "sp", "eq", "ek")}
        ssq = k.sb("d_ssq", [C, 2, NT, NH], stack=s)
        S = k.sb("d_S", [C, NH, 32], stack=s)
        D = k.sb("d_D", [C, 2, 4, C], stack=s)
        A, Pm = (k.sb("d_" + n, [C, 6, 4, C], stack=s) for n in ("A", "P"))
        M = k.sb("d_M", [C, 4, 5, 4, 32], stack=s)
        A32, Y = (k.sb("d_" + n, [C, 4, 4, 32], stack=s) for n in ("A32", "Y"))
        F, X, W = (k.sb("d_" + n, [C, 2, 4, 32], stack=s) for n in ("F", "X", "W"))
        rv, zz, ze, o1 = (k.sb("d_" + n, [C, 2, 4, 32], stack=s) for n in ("r", "zz", "ze", "o1"))
        P = [k.ps[:, i, :] for i in range(8)]
        m = k.modb[:, 3, :]

        pe, act, dve, pool, dma = k.stage("delta_start")
        with nc.Block() as block:
            @block.scalar
            def _(e):
                e.activation(neg_a[:], k.w["A_log"][:], ACT.Exp).then_inc(act.steps, act.did("a"))

            @block.vector
            def _(e):
                e.memset(hp[:, 0:3], 0.0).then_inc(dve.steps, dve.did())
                for j in range(TAPS):
                    e.tensor_tensor(w_v[:, j], k.w["Wv3"][:], k.w["conv_v"][:, j], ALU.mult).then_inc(dve.steps, dve.did())
                e.wait_ge(act.steps, act.at("a"))
                e.tensor_scalar(neg_a[:], neg_a[:], -1.0, None, ALU.mult).then_inc(dve.steps, dve.did())
        k.end()
        taps = QK[:].rearrange("p c h t -> p (c h t)")[:, 0:TAPS * 8 * C].rearrange("p (j f) -> p j f", j=TAPS)
        for n in range(2):
            pe, act, dve, pool, dma = k.stage(f"delta_taps{n}")
            with nc.Block() as block:
                @block.sync
                def _(e):
                    src = k.dram["conv_qk"][n].rearrange("(a j) f -> a j f", a=1)
                    e.dma_start(taps, src.to_broadcast([C, TAPS, 8 * C])).then_inc(dma.steps, dma.did("taps"))

                @block.vector
                def _(e):
                    e.wait_ge(dma.steps, dma.at("taps"))
                    for j in range(TAPS):
                        e.tensor_tensor(w_qk[:, j, n], k.w["Wqk3"][:, n], taps[:, j], ALU.mult).then_inc(dve.steps, dve.did())
            k.end()

        f4 = lambda ap: ap.rearrange("p h t -> p (h t)")
        v4 = lambda ap: ap.rearrange("p (h t) -> p h t", h=4)
        p32 = lambda bank: v4(P[bank][:, 0:128])
        p_inv = lambda step, u: p32(4 * u + (1 if step == "y" else 0))
        INVERT = [("x", 0)] + [(step, l) for l in range(1, 5) for step in "fxy" if (step, l) != ("x", 4)]
        SOLVE = [("state", 0), ("solve", 0)] + [(step, j) for j in range(1, 4) for step in ("before", "solve")] + [("finish", 0)]
        MAKE = {0: 0, 3: 1, 6: 2}
        TURNS = (NT + 1) * len(INVERT)
        PIECES = [("norm", 0), ("small", 0), ("gate", 0), ("values", 0), ("gate", 1), ("values", 1), ("gate", 2), ("values", 2), ("gate", 3),
                  ("gate", 4), ("finish", 0), ("values", 3), ("finish", 1), ("finish", 2)]
        for run in range(4, 12):
            PIECES += [("first_taps", run - 4), ("last_taps", run - 4), ("finish", run - 1)]
            PIECES += [("squares", run - 7)] if run >= 7 else []
        PIECES += [("finish", 11), ("squares", 5), ("squares", 6), ("squares", 7)]
        PIECES += [("norms", 0), ("norms", 1), ("norms", 2)] + [("keys", i) for i in range(NT)]

        def stage(name, sg, pb, g):
            st = pe, act, dve, pool, dma = k.stage(name)
            q = small
            norm_tmp = A[:].rearrange("p (a x) h t -> p x a (h t)", x=2)[:, 0]
            norm = Norm(k, st, "n", 0, 1, xb[:], hp[:, 3:], m, SA, CA, norm_tmp)
            hs = slice(4 * (g or 0), 4 * (g or 0) + 4)
            four = lambda name_: q[name_][:, :, hs]
            run_bank = lambda run: P[4 * g + (0, 1, 3)[run % 3]]
            few = P[4 * g + 2] if g is not None else None
            made = lambda x: VG[:, :, x, ts(g, 128)] if x < 4 else QK[:, x % 2, 4 * g + (x - 4) // 2]
            products = lambda x: run_bank(x)[:, 0:256].rearrange("p (v x) -> p v x", v=2) if x < 4 else run_bank(x)
            pieces = [] if g is None else PIECES[0 if g == 0 else 1:]

            def in_turn(make, invert, solve, prepare):
                begun = 0
                if sg is not None:
                    for part in range(3):
                        make(sg, part)
                        if begun < len(pieces):
                            prepare(*pieces[begun])
                            begun += 1
                    for i in range(NT + 1):
                        for turn, (step, l) in enumerate(INVERT):
                            if i and turn < len(SOLVE):
                                solve(2 * (i - 1) + sg, *SOLVE[turn])
                            if i + 1 < NT and turn in MAKE:
                                make(2 * (i + 1) + sg, MAKE[turn])
                            if i < NT:
                                invert(2 * i + sg, step, l)
                            while begun < len(pieces) and begun * (TURNS - 18) <= len(pieces) * (i * len(INVERT) + turn):
                                prepare(*pieces[begun])
                                begun += 1
                for piece in pieces[begun:]:
                    prepare(*piece)

            with nc.Block() as block:
                @block.tensor
                def _(e):
                    def make(n, part):
                        i, u = n // 2, n % 2
                        t = ts(i, C)
                        if part == 0:
                            if n >= 2:
                                e.wait_ge(dve.steps, dve.at(f"A{n - 2}"))
                            for h in range(4):
                                H = 4 * u + h
                                ins = e.matmul(P[4 * u + 2][:, ts(h, C)], q["g"][:, i, H:H + 1].to_broadcast([C, C]), k.w["upto3"][:], start=True, stop=True)
                            ins.then_inc(pe.steps, pe.did(f"gb{n}"))
                        else:
                            e.wait_ge(dve.steps, dve.at((f"d{n}", f"P{n}")[part - 1]))
                            for h in range(4):
                                H = 4 * u + h
                                ins = e.matmul(P[4 * u + 2][:, ts(h, C)], QK[:, 1, H, t], QK[:, part - 1, H, t], start=True, stop=True)
                            ins.then_inc(pe.steps, pe.did((f"kq{n}", f"kk{n}")[part - 1]))

                    def products(step, stationary, moving, u):
                        for h in range(4):
                            for j in range(4):
                                rows = ts(j, 32)
                                ins = e.matmul(p_inv(step, u)[rows, h], stationary[rows, h], moving(rows, h), start=True, stop=True,
                                               tile_position=(32 * j, 32 * j))
                        return ins

                    def invert(n, step, l):
                        u = n % 2
                        if l == 0:
                            e.wait_ge(pool.steps, pool.at(f"c0{n}"))
                            products("x", M[:, n % 4, 0], lambda rows, h: k.w["eye32"][rows], u).then_inc(pe.steps, pe.did(f"x0{n}"))
                        elif step == "f":
                            if l == 1:
                                e.wait_ge(pool.steps, pool.at(f"c1{n}"))
                            e.wait_ge(dve.steps, dve.at(f"x{l - 1}{n}"))
                            products("f", M[:, n % 4, l], lambda rows, h: X[rows, u, h], u).then_inc(pe.steps, pe.did(f"f{l}{n}"))
                        elif step == "x":
                            e.wait_ge(act.steps, act.at(f"f{l}{n}"))
                            e.wait_ge(dve.steps, dve.at(f"y{l - 1}{n}"))
                            products("x", Y[:, n % 4], lambda rows, h: F[rows, u, h], u).then_inc(pe.steps, pe.did(f"x{l}{n}"))
                        else:
                            e.wait_ge(act.steps, act.at(f"f{l}{n}"))
                            e.wait_ge(dve.steps, dve.at(f"y{l - 1}{n}"))
                            products("y", F[:, u], lambda rows, h: Y[rows, n % 4, h], u).then_inc(pe.steps, pe.did(f"y{l}{n}"))

                    def solve(n, step, j):
                        i, u, rows = n // 2, n % 2, ts(j, 32)
                        if step == "state":
                            if n >= 2:
                                e.wait_ge(dve.steps, dve.at(f"out{n - 2}"))
                            for bank_half, c in ((0, 1), (1, 0)):
                                for h in range(4):
                                    H = 4 * u + h
                                    ins = e.matmul(P[4 * u + 3][:, bank_half * 128 + 32 * h:bank_half * 128 + 32 * h + 32], QK[:, c, H, ts(i, C)],
                                                   S[:, H], start=True, stop=True)
                            ins.then_inc(pe.steps, pe.did(f"s{n}"))
                        elif step == "before":
                            e.wait_ge(dve.steps, dve.at(f"w{j - 1}{n}"))
                            for h in range(4):
                                ins = e.matmul(P[4 * u + 3][rows, ts(h, 32)], A[:, n % 6, h, rows], W[:, u, h], start=True, stop=True,
                                               tile_position=(0, 32 * j))
                            ins.then_inc(pe.steps, pe.did(f"b{j}{n}"))
                        elif step == "solve":
                            e.wait_ge(dve.steps, dve.at(f"y4{n}"))
                            e.wait_ge(dve.steps, dve.at(f"r{j}{n}"))
                            for h in range(4):
                                ins = e.matmul(P[4 * u + 3][rows, 256 + 32 * h:288 + 32 * h], Y[rows, n % 4, h], rv[rows, u, h], start=True,
                                               stop=True, tile_position=(32 * j, 32 * j))
                            ins.then_inc(pe.steps, pe.did(f"w{j}{n}"))
                        else:
                            e.wait_ge(dve.steps, dve.at(f"z{n}"))
                            for h in range(4):
                                ins = e.matmul(P[4 * u + 3][:, 384 + 32 * h:416 + 32 * h], Pm[:, n % 6, h], zz[:, u, h], start=True, stop=True)
                            for h in range(4):
                                ins = e.matmul(P[4 * u + 3][:, 256 + 32 * h:288 + 32 * h], KT[:, i, 4 * u + h], ze[:, u, h], start=True, stop=True)
                            ins.then_inc(pe.steps, pe.did(f"o{n}"))

                    def prepare(what, x):
                        def free(run):
                            if run >= 3:
                                e.wait_ge(act.steps, act.at(f"p_run{run - 3}"))

                        if what == "norm":
                            e.wait_ge(pool.steps, pool.at("p_xb"))
                            norm.tensor(e)
                        elif what == "small":
                            if g == 0:
                                e.wait_ge(dve.steps, dve.at("nh"))
                            for i in range(NT):
                                ins = e.matmul(few[:, ts(i, 16)], hp[:, 3 + i * C:3 + i * C + C], k.w["Wab3"][:], start=True, stop=True)
                            ins.then_inc(pe.steps, pe.did("p_ab"))
                        elif what == "values":
                            free(x)
                            cols = ts(g, 128)
                            for j in range(TAPS):
                                e.matmul(run_bank(x)[:, 0:128], hp[:, j + x * C:j + x * C + C], w_v[:, j, cols], start=(j == 0), stop=(j == TAPS - 1))
                            e.matmul(run_bank(x)[:, 128:256], hp[:, 3 + x * C:3 + x * C + C], k.w["Wg3"][:, cols], start=True,
                                     stop=True).then_inc(pe.steps, pe.did(f"p_run{x}"))
                        elif what in ("first_taps", "last_taps"):
                            run, c, H = 4 + x, x % 2, 4 * g + x // 2
                            if what == "first_taps":
                                free(run)
                            for j in ((0, 1) if what == "first_taps" else (2, 3)):
                                ins = e.matmul(run_bank(run), w_qk[:, j, c, ts(H, C)], hp[:, j:j + T], start=(j == 0), stop=(j == TAPS - 1))
                            if what == "last_taps":
                                ins.then_inc(pe.steps, pe.did(f"p_run{run}"))
                        elif what == "squares":
                            e.wait_ge(pool.steps, pool.at(f"p_sq{x}"))
                            if x == 0:
                                e.wait_ge(dve.steps, dve.at("p_gc"))
                            for i in range(NT):
                                col = (x % 2) * 16 + i * 4 + x // 2
                                ins = e.matmul(few[:, col:col + 1], squares(x)[:, ts(i, C)], k.w["ones3"][:, 0:1], start=True, stop=True)
                            ins.then_inc(pe.steps, pe.did(f"p_ss{x}"))
                        elif what == "gate" and x == 2:
                            e.wait_ge(dve.steps, dve.at("p_g"))
                            e.matmul(few[:, 64:80], k.w["upto3"][:], four("g"), start=True, stop=True)
                            e.matmul(few[:, 80:96], k.w["ones3"][:], four("g"), start=True, stop=True).then_inc(pe.steps, pe.did("p_cum"))
                        elif what == "keys":
                            free(12 + x)
                            for h in range(4):
                                ins = e.transpose(run_bank(12 + x)[:, ts(h, C)], QK[:, 1, 4 * g + h, ts(x, C)], k.w["ident"][:])
                            ins.then_inc(pe.steps, pe.did(f"p_run{12 + x}"))

                    in_turn(make, invert, solve, prepare)

                @block.gpsimd
                def _(e):
                    def make(n, part):
                        u = n % 2
                        if part == 0:
                            e.wait_ge(act.steps, act.at(f"d{n}"))
                            e.tensor_tensor(D[:, u], D[:, u], k.w["upto3"][:].unsqueeze(1).to_broadcast([C, 4, C]), ALU.mult).then_inc(pool.steps, pool.did(f"d{n}"))
                        elif part == 2:
                            e.wait_ge(act.steps, act.at(f"a{n}"))
                            for l, levels in enumerate((slice(0, 1), slice(1, 5))):
                                many = levels.stop - levels.start
                                e.tensor_tensor(M[:, n % 4, levels], A32[:, n % 4].unsqueeze(1).to_broadcast([C, many, 4, 32]),
                                                k.w["joins"][:, levels].unsqueeze(2).to_broadcast([C, many, 4, 32]), ALU.mult).then_inc(pool.steps, pool.did(f"c{l}{n}"))

                    def prepare(what, x):
                        if what == "norm":
                            e.tensor_copy(xb[:], flat(k.X[:, bass.ds(pb, 1), :])).then_inc(pool.steps, pool.did("p_xb"))
                        elif what == "small":
                            e.memset(S[:, hs], 0.0).then_inc(pool.steps, pool.did())
                        elif what == "finish" and x >= 4:
                            y = x - 4
                            if y >= 4:
                                e.wait_ge(pe.steps, pe.at(f"p_ss{y - 4}"))
                            e.wait_ge(act.steps, act.at(f"p_run{x}"))
                            e.tensor_tensor(squares(y), made(x), made(x), ALU.mult).then_inc(pool.steps, pool.did(f"p_sq{y}"))

                    in_turn(make, lambda n, step, l: None, lambda n, step, j: None, prepare)

                @block.scalar
                def _(e):
                    def make(n, part):
                        u = n % 2
                        if part == 0:
                            e.wait_ge(dve.steps, dve.at(f"d{n}"))
                            e.activation(D[:, u], D[:, u], ACT.Exp).then_inc(act.steps, act.did(f"d{n}"))
                        elif part == 2:
                            e.wait_ge(dve.steps, dve.at(f"A{n}"))
                            for j in range(4):
                                e.activation(A32[ts(j, 32), n % 4], A[ts(j, 32), n % 6, :, ts(j, 32)], ACT.Copy).then_inc(act.steps, act.did(f"a{n}"))

                    def invert(n, step, l):
                        if step == "f":
                            e.wait_ge(pe.steps, pe.at(f"f{l}{n}"))
                            e.activation(F[:, n % 2], p_inv("f", n % 2), ACT.Copy).then_inc(act.steps, act.did(f"f{l}{n}"))

                    def prepare(what, x):
                        if what == "norm":
                            norm.scalar(e)
                        elif what == "finish":
                            e.wait_ge(pe.steps, pe.at(f"p_run{x}"))
                            e.activation(made(x), products(x), ACT.Silu).then_inc(act.steps, act.did(f"p_run{x}"))
                        elif what == "gate" and x == 0:
                            e.wait_ge(dve.steps, dve.at("p_negabs"))
                            e.activation(four("beta"), four("beta"), ACT.Exp, scale=-1.0).then_inc(act.steps, act.did())
                            e.activation(four("t"), four("t"), ACT.Exp).then_inc(act.steps, act.did())
                            e.wait_ge(act.steps, act.n)
                            e.activation(four("beta"), four("beta"), ACT.Ln, bias=1.0).then_inc(act.steps, act.did())
                            e.activation(four("sp"), four("t"), ACT.Ln, bias=1.0).then_inc(act.steps, act.did("p_sp"))
                            e.wait_ge(act.steps, act.n)
                            e.activation(four("beta"), four("beta"), ACT.Exp, scale=-1.0).then_inc(act.steps, act.did("p_beta"))
                        elif what == "gate" and x == 4:
                            e.wait_ge(dve.steps, dve.at("p_gc"))
                            e.activation(four("ga"), four("gc"), ACT.Exp).then_inc(act.steps, act.did())
                            e.activation(four("end"), four("end"), ACT.Exp).then_inc(act.steps, act.did())
                            e.activation(four("gtot"), four("gtot"), ACT.Exp).then_inc(act.steps, act.did())
                        elif what == "norms" and x == 1:
                            e.wait_ge(dve.steps, dve.at("p_ssq"))
                            e.activation(ssq[:, :, :, hs], ssq[:, :, :, hs], ACT.Ln).then_inc(act.steps, act.did())
                            e.wait_ge(act.steps, act.n)
                            e.activation(four("qn"), ssq[:, 0, :, hs], ACT.Exp, scale=-0.5).then_inc(act.steps, act.did())
                            e.activation(four("n2"), ssq[:, 1, :, hs], ACT.Exp, scale=-1.0).then_inc(act.steps, act.did())
                            e.activation(four("kn"), ssq[:, 1, :, hs], ACT.Exp, scale=0.5).then_inc(act.steps, act.did("p_norms"))
                        elif what == "keys":
                            e.wait_ge(pe.steps, pe.at(f"p_run{12 + x}"))
                            e.activation(KT[:, x, hs].rearrange("p h x -> p (h x)"), run_bank(12 + x), ACT.Copy).then_inc(act.steps, act.did(f"p_run{12 + x}"))

                    e.preload_act_table_set(EXP_LN)
                    in_turn(make, invert, lambda n, step, j: None, prepare)
                    if sg is not None:
                        ms = q["t"][:, :, ts(sg, 4)]
                        e.preload_act_table_set(EXP_LN)
                        e.wait_ge(dve.steps, dve.at("ms"))
                        e.activation(ms, ms, ACT.Ln).then_inc(act.steps, act.did())
                        e.wait_ge(act.steps, act.n)
                        e.activation(ms, ms, ACT.Exp, scale=-0.5).then_inc(act.steps, act.did("rms"))

                @block.vector
                def _(e):
                    wide = lambda name, i, u, w: q[name][:, i, 4 * u:4 * u + 4].unsqueeze(2).to_broadcast([C, 4, w])
                    eye32 = k.w["eye32"][:].unsqueeze(1).to_broadcast([C, 4, 32])

                    def make(n, part):
                        i, u = n // 2, n % 2
                        if part == 0:
                            e.wait_ge(pe.steps, pe.at(f"gb{n}"))
                            for h in range(4):
                                e.tensor_scalar(D[:, u, h], P[4 * u + 2][:, ts(h, C)], q["gc"][:, i, 4 * u + h:4 * u + h + 1], 0.0,
                                                ALU.subtract, ALU.min).then_inc(dve.steps, dve.did(f"d{n}"))
                        elif part == 1:
                            e.wait_ge(pe.steps, pe.at(f"kq{n}"))
                            e.wait_ge(pool.steps, pool.at(f"d{n}"))
                            e.tensor_tensor(Pm[:, n % 6], v4(P[4 * u + 2]), D[:, u], ALU.mult).then_inc(dve.steps, dve.did(f"P{n}"))
                            e.tensor_tensor(D[:, u], D[:, u], wide("gam", i, u, C), ALU.mult).then_inc(dve.steps, dve.did(f"dg{n}"))
                        else:
                            e.wait_ge(pe.steps, pe.at(f"kk{n}"))
                            e.wait_ge(dve.steps, dve.at(f"dg{n}"))
                            e.tensor_tensor(A[:, n % 6], v4(P[4 * u + 2]), D[:, u], ALU.mult).then_inc(dve.steps, dve.did(f"A{n}"))

                    def invert(n, step, l):
                        u = n % 2
                        if l == 0:
                            e.wait_ge(pe.steps, pe.at(f"x0{n}"))
                            e.tensor_tensor(X[:, u], eye32, p_inv("x", u), ALU.subtract).then_inc(dve.steps, dve.did(f"x0{n}"))
                            e.tensor_tensor(Y[:, n % 4], eye32, M[:, n % 4, 0], ALU.subtract).then_inc(dve.steps, dve.did(f"y0{n}"))
                        elif step == "x":
                            e.wait_ge(pe.steps, pe.at(f"x{l}{n}"))
                            e.tensor_tensor(X[:, u], X[:, u], p_inv("x", u), ALU.subtract).then_inc(dve.steps, dve.did(f"x{l}{n}"))
                        elif step == "y":
                            e.wait_ge(pe.steps, pe.at(f"y{l}{n}"))
                            e.tensor_tensor(Y[:, n % 4], Y[:, n % 4], p_inv("y", u), ALU.subtract).then_inc(dve.steps, dve.did(f"y{l}{n}"))

                    def solve(n, step, j):
                        i, u, rows = n // 2, n % 2, ts(j, 32)
                        s_u = S[:, ts(u, 4)]
                        if step == "state":
                            e.memset(W[:, u], 0.0).then_inc(dve.steps, dve.did())
                            e.wait_ge(pe.steps, pe.at(f"s{n}"))
                            e.tensor_tensor(rv[:, u], v4(P[4 * u + 3][:, 0:128]), wide("ga", i, u, 32), ALU.mult).then_inc(dve.steps, dve.did())
                            e.tensor_tensor(o1[:, u], v4(P[4 * u + 3][:, 128:256]), wide("ga", i, u, 32), ALU.mult).then_inc(dve.steps, dve.did())
                            e.wait_ge(dve.steps, dve.n)
                            e.tensor_tensor(rv[:, u], v4(V[:, i, ts(u, 128)]), rv[:, u], ALU.subtract).then_inc(dve.steps, dve.did(f"r0{n}"))
                            e.tensor_tensor(s_u, s_u, wide("gtot", i, u, 32), ALU.mult).then_inc(dve.steps, dve.did())
                        elif step == "before":
                            e.wait_ge(pe.steps, pe.at(f"b{j}{n}"))
                            e.tensor_tensor(rv[rows, u], rv[rows, u], p32(4 * u + 3)[rows], ALU.subtract).then_inc(dve.steps, dve.did(f"r{j}{n}"))
                        elif step == "solve":
                            e.wait_ge(pe.steps, pe.at(f"w{j}{n}"))
                            e.tensor_copy(W[rows, u], v4(P[4 * u + 3][rows, 256:384])).then_inc(dve.steps, dve.did(f"w{j}{n}"))
                            if j == 3:
                                e.wait_ge(dve.steps, dve.n)
                                e.tensor_tensor(zz[:, u], W[:, u], wide("gam", i, u, 32), ALU.mult).then_inc(dve.steps, dve.did())
                                e.wait_ge(dve.steps, dve.n)
                                e.tensor_tensor(ze[:, u], zz[:, u], wide("end", i, u, 32), ALU.mult).then_inc(dve.steps, dve.did(f"z{n}"))
                        else:
                            e.wait_ge(pe.steps, pe.at(f"o{n}"))
                            e.tensor_tensor(s_u, s_u, v4(P[4 * u + 3][:, 256:384]), ALU.add).then_inc(dve.steps, dve.did())
                            e.tensor_tensor(o1[:, u], o1[:, u], v4(P[4 * u + 3][:, 384:512]), ALU.add).then_inc(dve.steps, dve.did())
                            e.wait_ge(dve.steps, dve.n)
                            e.tensor_tensor(O[:, i, ts(u, 4)], o1[:, u], wide("qn", i, u, 32), ALU.mult).then_inc(dve.steps, dve.did(f"out{n}"))

                    def prepare(what, x):
                        if what == "norm":
                            e.tensor_copy(k.modb[:], k.mod[:, :, :, bass.ds(pb, 1)].rearrange("p l s a -> p l (s a)")).then_inc(dve.steps, dve.did())
                            e.wait_ge(dve.steps, dve.n)
                            norm.vector(e)
                        elif what == "gate" and x == 0:
                            e.wait_ge(pe.steps, pe.at("p_ab"))
                            ab = few[:, 0:64].rearrange("p (i x) -> p i x", i=NT)
                            e.tensor_tensor(four("z"), ab[:, :, hs], k.w["dt_bias"][:, hs].unsqueeze(1).to_broadcast([C, NT, 4]), ALU.add).then_inc(dve.steps, dve.did())
                            e.tensor_scalar(four("beta"), ab[:, :, 8 + 4 * g:12 + 4 * g], LEAST, None, ALU.max).then_inc(dve.steps, dve.did())
                            e.wait_ge(dve.steps, dve.n)
                            e.tensor_scalar(four("t"), four("z"), -1.0, None, ALU.mult).then_inc(dve.steps, dve.did())
                            e.wait_ge(dve.steps, dve.n)
                            e.tensor_tensor(four("t"), four("t"), four("z"), ALU.min).then_inc(dve.steps, dve.did("p_negabs"))
                            e.tensor_scalar(four("z"), four("z"), 0.0, None, ALU.max).then_inc(dve.steps, dve.did("p_z"))
                        elif what == "gate" and x == 1:
                            e.wait_ge(act.steps, act.at("p_sp"))
                            e.wait_ge(dve.steps, dve.at("p_z"))
                            e.tensor_tensor(four("g"), four("z"), four("sp"), ALU.add).then_inc(dve.steps, dve.did())
                            e.wait_ge(dve.steps, dve.n)
                            e.tensor_tensor(four("g"), four("g"), neg_a[:, hs].unsqueeze(1).to_broadcast([C, NT, 4]), ALU.mult).then_inc(dve.steps, dve.did("p_g"))
                        elif what == "gate" and x == 3:
                            e.wait_ge(pe.steps, pe.at("p_cum"))
                            sums = lambda at: few[:, at:at + 16].rearrange("p (i h) -> p i h", i=NT)
                            e.tensor_copy(four("gc"), sums(64)).then_inc(dve.steps, dve.did())
                            e.tensor_copy(four("gtot"), sums(80)).then_inc(dve.steps, dve.did())
                            e.wait_ge(dve.steps, dve.n)
                            e.tensor_tensor(four("end"), four("gtot"), four("gc"), ALU.subtract).then_inc(dve.steps, dve.did("p_gc"))
                        elif what == "norms" and x == 0:
                            e.wait_ge(pe.steps, pe.at("p_ss7"))
                            for c in range(2):
                                e.tensor_scalar(ssq[:, c, :, hs], few[:, ts(c, 16)].rearrange("p (i h) -> p i h", i=NT), 1e-12, None, ALU.max).then_inc(dve.steps, dve.did("p_ssq"))
                        elif what == "norms" and x == 2:
                            e.wait_ge(act.steps, act.at("p_norms"))
                            e.scalar_tensor_tensor(four("gam"), four("n2"), 2.0, four("beta"), ALU.mult, ALU.mult).then_inc(dve.steps, dve.did())
                            vals = V.rearrange("p i (h x) -> p i h x", h=NH)[:, :, hs]
                            e.tensor_tensor(vals, vals, four("kn").unsqueeze(3).to_broadcast([C, NT, 4, 32]), ALU.mult).then_inc(dve.steps, dve.did())

                    in_turn(make, invert, solve, prepare)
                    if sg is not None:
                        ms, og = q["t"][:, :, ts(sg, 4)], O[:, :, ts(sg, 4)]
                        gate = G.rearrange("p i (h x) -> p i h x", h=NH)[:, :, ts(sg, 4)]
                        o2 = f4(D[:, sg]).rearrange("p (i h x) -> p i h x", i=NT, h=4)
                        e.wait_ge(dve.steps, dve.n)
                        e.tensor_tensor(o2, og, og, ALU.mult).then_inc(dve.steps, dve.did())
                        e.wait_ge(dve.steps, dve.n)
                        e.tensor_reduce(ms, o2, AX.X, ALU.add).then_inc(dve.steps, dve.did())
                        e.wait_ge(dve.steps, dve.n)
                        e.tensor_scalar(ms, ms, 1.0 / 32, 1e-5, ALU.mult, ALU.add).then_inc(dve.steps, dve.did("ms"))
                        for i in range(NT):
                            e.tensor_tensor(gate[:, i], gate[:, i], k.w["o_norm_w"][:].unsqueeze(1).to_broadcast([C, 4, 32]), ALU.mult).then_inc(dve.steps, dve.did())
                        e.wait_ge(dve.steps, dve.n)
                        e.tensor_tensor(og, og, gate, ALU.mult).then_inc(dve.steps, dve.did())
                        e.wait_ge(act.steps, act.at("rms"))
                        e.wait_ge(dve.steps, dve.n)
                        e.tensor_tensor(og, og, ms.unsqueeze(3).to_broadcast([C, NT, 4, 32]), ALU.mult).then_inc(dve.steps, dve.did())
            k.end()

        def out(name, b):
            st = pe, act, dve, pool, dma = k.stage(name)
            OT = sq[:].rearrange("p a c t -> p (a c) t")
            with nc.Block() as block:
                @block.vector
                def _(e):
                    e.tensor_copy(k.modb[:], k.mod[:, :, :, bass.ds(b, 1)].rearrange("p l s a -> p l (s a)")).then_inc(dve.steps, dve.did())
                    e.wait_ge(pe.steps, pe.at("oT0"))
                    e.tensor_copy(OT[:, 0], P[0]).then_inc(dve.steps, dve.did("oT"))
                    e.wait_ge(pe.steps, pe.at("att"))
                    x = flat(k.X[:, bass.ds(b, 1), :])
                    e.scalar_tensor_tensor(x, P[2], m[:, GA:GA + 1], x, ALU.mult, ALU.add).then_inc(dve.steps, dve.did())

                @block.scalar
                def _(e):
                    e.wait_ge(pe.steps, pe.at("oT1"))
                    e.activation(OT[:, 1], P[1], ACT.Copy).then_inc(act.steps, act.did("oT"))

                @block.tensor
                def _(e):
                    for u in range(2):
                        for i in range(NT):
                            ins = e.transpose(P[u][:, ts(i, C)], O[:, i, ts(u, 4)].rearrange("p h x -> p (h x)"), k.w["ident"][:])
                        ins.then_inc(pe.steps, pe.did(f"oT{u}"))
                    for u, copied in ((0, dve), (1, act)):
                        e.wait_ge(copied.steps, copied.at("oT"))
                        ins = e.matmul(P[2], k.w["Wo3"][:, u, :], OT[:, u], start=(u == 0), stop=(u == 1))
                    ins.then_inc(pe.steps, pe.did("att"))
            k.end()

        squares = lambda x: sq[:, x % 4 // 2, x % 2]
        stage("delta_first", None, 0, 0)
        with nc.Fori(0, B - 1) as b:
            stage("delta_group0", 0, b, 1)
            stage("delta_group1", 1, b + 1, 0)
            out("delta_out", b)
        stage("delta_group0_last", 0, B - 1, 1)
        stage("delta_group1_last", 1, None, None)
        out("delta_out_last", B - 1)


def channel_mix(k):
    nc = k.nc
    with ExitStack() as s:
        lanes = lambda name, shape: [k.sb(f"c_{name}{l}", shape, stack=s) for l in range(2)]
        xb, dl, xr, xk, kk, rr = (lanes(n, [C, T]) for n in ("xb", "dl", "xr", "xk", "kk", "rr"))
        hp, tmp, modb = lanes("hp", [C, T + 1]), lanes("tmp", [C, 3, T]), lanes("modb", [C, 4, 6])
        bank = lambda l, i: k.ps[:, 4 * l + i, :]
        m = [modb[l][:, 3, :] for l in range(2)]
        with nc.Fori(0, B // 2) as pair:
            st = pe, act, dve, pool, dma = k.stage("mix")
            batch = lambda l: bass.ds(pair * 2 + l, 1)
            n = [Norm(k, st, f"n{l}", 4 * l, 4 * l + 1, xb[l][:], hp[l][:, 1:], m[l], SB_, CB, tmp[l]) for l in range(2)]
            with nc.Block() as block:
                @block.gpsimd
                def _(e):
                    for l in range(2):
                        e.tensor_copy(xb[l][:], flat(k.X[:, batch(l), :])).then_inc(pool.steps, pool.did(f"xb{l}"))
                    for l in range(2):
                        e.wait_ge(act.steps, act.at(f"k{l}"))
                        e.tensor_tensor(kk[l][:], kk[l][:], kk[l][:], ALU.mult).then_inc(pool.steps, pool.did(f"k2{l}"))

                @block.tensor
                def _(e):
                    for l in range(2):
                        e.wait_ge(pool.steps, pool.at(f"xb{l}"))
                        n[l].tensor(e)
                    for l in range(2):
                        e.wait_ge(dve.steps, dve.at(f"xr{l}"))
                        e.matmul(bank(l, 2), k.w["W_r3"][:], xr[l][:], start=True, stop=True).then_inc(pe.steps, pe.did(f"r{l}"))
                        e.wait_ge(dve.steps, dve.at(f"xk{l}"))
                        e.matmul(bank(l, 3), k.w["W_k3"][:], xk[l][:], start=True, stop=True).then_inc(pe.steps, pe.did(f"k{l}"))
                    for l in range(2):
                        e.wait_ge(pool.steps, pool.at(f"k2{l}"))
                        e.matmul(bank(l, 0), k.w["W_v3"][:], kk[l][:], start=True, stop=True).then_inc(pe.steps, pe.did(f"v{l}"))

                @block.scalar
                def _(e):
                    e.preload_act_table_set(EXP_LN)
                    for l in range(2):
                        n[l].scalar(e)
                    for l in range(2):
                        e.wait_ge(pe.steps, pe.at(f"k{l}"))
                        e.activation(kk[l][:], bank(l, 3), ACT.Relu).then_inc(act.steps, act.did(f"k{l}"))
                        e.wait_ge(dve.steps, dve.at(f"r{l}"))
                        e.activation(rr[l][:], rr[l][:], ACT.Exp, scale=-1.0).then_inc(act.steps, act.did())
                        e.wait_ge(act.steps, act.n)
                        e.activation(rr[l][:], rr[l][:], ACT.Ln, bias=1.0).then_inc(act.steps, act.did())
                        e.wait_ge(act.steps, act.n)
                        e.activation(rr[l][:], rr[l][:], ACT.Exp, scale=-1.0).then_inc(act.steps, act.did(f"r{l}"))

                @block.vector
                def _(e):
                    for l in range(2):
                        e.memset(hp[l][:, 0:1], 0.0).then_inc(dve.steps, dve.did())
                        e.tensor_copy(modb[l][:], k.mod[:, :, :, batch(l)].rearrange("p l s a -> p l (s a)")).then_inc(dve.steps, dve.did())
                    e.wait_ge(dve.steps, dve.n)
                    for l in range(2):
                        n[l].vector(e)
                        e.wait_ge(dve.steps, dve.n)
                        e.tensor_tensor(dl[l][:], hp[l][:, 1:], hp[l][:, 0:T], ALU.subtract).then_inc(dve.steps, dve.did())
                        e.wait_ge(dve.steps, dve.n)
                        for x, dst in (("xr", xr), ("xk", xk)):
                            mu = k.w["mu"][:, 0:1] if x == "xr" else k.w["mu"][:, 1:2]
                            e.scalar_tensor_tensor(dst[l][:], dl[l][:], mu, hp[l][:, 0:T], ALU.mult, ALU.add).then_inc(dve.steps, dve.did(f"{x}{l}"))
                    for l in range(2):
                        e.wait_ge(pe.steps, pe.at(f"r{l}"))
                        e.tensor_scalar(rr[l][:], bank(l, 2), LEAST, None, ALU.max).then_inc(dve.steps, dve.did(f"r{l}"))
                    for l in range(2):
                        e.wait_ge(act.steps, act.at(f"r{l}"))
                        e.wait_ge(pe.steps, pe.at(f"v{l}"))
                        e.tensor_tensor(rr[l][:], rr[l][:], bank(l, 0), ALU.mult).then_inc(dve.steps, dve.did())
                        e.wait_ge(dve.steps, dve.n)
                        e.scalar_tensor_tensor(flat(k.X[:, batch(l), :]), rr[l][:], m[l][:, GB:GB + 1], xb[l][:], ALU.mult, ALU.add).then_inc(dve.steps, dve.did())
            k.end()


def build(nc, a, counts, upto=99, first=0):
    k = Kernel(nc, counts)
    k.dram = a
    with k.stack:
        load_weights(k, a)
        if first <= 0:
            with ExitStack() as s:
                load(k, a, "layers01", s)
                wkv_mlp_prologue(k, s)
                q1 = k.sb("q1", [C, B, T], stack=s)
                k1 = k.sb("k1", [C, B, T], stack=s)
                v1 = k.sb("v1", [C, B, T], stack=s)
                qbar = k.sb("qbar", [C, B, 16], stack=s)
                kbar = k.sb("kbar", [C, B, 16], stack=s)
                idx_row = k.sb("idx_row", [1, 48], U32, stack=s)
                lg = k.sb("router_logits", [C, B, 32], stack=s)
                gates = k.sb("gates", [C, 32, 8], stack=s)
                layer0(k, q1, k1, v1, qbar, kbar)
                if upto >= 1:
                    choose_blocks(k, qbar, kbar, idx_row)
                    block_attention(k, q1, k1, v1, idx_row)
                    attention_out(k, q1, k1, lg)
                if upto >= 2:
                    route(k, lg, gates)
                    experts(k, k1, gates)
        if first <= 3 <= upto:
            with ExitStack() as s:
                load(k, a, "gla", s)
                gla(k)
        if first <= 4 <= upto:
            with ExitStack() as s:
                load(k, a, "mlp2", s)
                routed_mlp(k)
        if first <= 5 <= upto:
            with ExitStack() as s:
                load(k, a, "delta", s)
                delta_rule(k)
        if first <= 6 <= upto:
            with ExitStack() as s:
                load(k, a, "mix", s)
                channel_mix(k)
        pe, act, dve, pool, dma = k.stage("store")
        with nc.Block() as block:
            @block.sync
            def _(e):
                e.dma_start(a["out"], k.X[:]).then_inc(dma.steps, dma.did("out"))
                e.wait_ge(dma.steps, dma.at("out"))


def layouts(i):
    c = np.ascontiguousarray
    i = {n: np.asarray(v) for n, v in i.items()}
    o = {}
    o["x"] = c(i["L0_attn_x"].transpose(2, 0, 1))
    o["center"] = (np.eye(C) - 1.0 / C).astype(np.float32)
    o["mean"] = np.full((C, C), 1.0 / C, np.float32)
    o["ident"] = np.eye(C, dtype=np.float32)
    o["cT"] = c(np.stack([i[f"L{l}_c"].T for l in range(4)], 1))
    o["wmod"] = c(np.stack([i[f"L{l}_wmod"] for l in range(4)], 1))
    o["W_rvk"] = c(i["L0_attn_W_rvk"].T)
    o["W_out0"] = c(i["L0_attn_W_out"].T)
    o["decay"] = c(i["L0_attn_time_decay"][:, None])
    o["time_first"] = c(i["L0_attn_time_first"][:, None])
    two = lambda v: c(np.concatenate([v, v], 0))
    halves = lambda v: c(v.reshape(64, 8, 2).transpose(2, 0, 1).reshape(128, 8))
    o["Win0"] = c(np.concatenate([i["L0_ffn_Win"]] * 2, 1))
    o["bin_0"] = two(i["L0_ffn_bin_"][:, None])
    o["W1_0"], o["b1_0"], o["W2_0"] = halves(i["L0_ffn_W1"]), halves(i["L0_ffn_b1"]), halves(i["L0_ffn_W2"])
    o["b2_0"] = two(i["L0_ffn_b2"][:, None])
    o["Wout0"] = two(i["L0_ffn_Wout"])
    o["bout_0"] = c(i["L0_ffn_bout"][:, None])
    for n in "QKV":
        o[f"W_{n}"] = c(i[f"L1_attn_W_{n}"])
    o["W_O"] = c(i["L1_attn_W_O"])
    head = (np.arange(C)[:, None] % 32 // 8 == np.arange(4)[None]).astype(np.float32)
    o["head_mask"] = head
    o["head_scale"] = head * np.float32(1 / np.sqrt(8))
    o["w_gate1"] = c(i["L1_ffn_w_g"].T)
    o["rev8"] = np.broadcast_to(np.arange(8, 0, -1, dtype=np.float32), (C, 8)).copy()
    o["upto"] = np.triu(np.ones((C, C), np.float32))
    o["ones"] = np.ones((C, C), np.float32)
    o["c_fc"] = c(i["L1_ffn_c_fc"].transpose(1, 0, 2))
    o["c_proj"] = c(i["L1_ffn_c_proj"].reshape(8, 4, C, C).transpose(2, 0, 1, 3))
    o["W_in2"] = c(i["L2_attn_W_in"].T)
    o["b_in2"] = c(i["L2_attn_b_in"][:, None])
    wq = i["L2_attn_W_qkva"].reshape(2, 4, 32, 4, 2, C)
    bq = i["L2_attn_b_qkva"].reshape(2, 4, 32, 4, 2)
    sel = [0, 1, 3]
    o["W_qka"] = c(wq[:, :, :, sel].transpose(5, 3, 4, 0, 1, 2).reshape(C, 3, 2, 2, C))
    o["b_qka"] = c(bq[:, :, :, sel].transpose(1, 2, 3, 4, 0).reshape(C, 3, 2, 2))
    o["W_v2"] = c(wq[:, :, :, 2].transpose(4, 0, 1, 3, 2).reshape(C, 512))
    o["b_v2"] = c(np.broadcast_to(bq[:, :, :, 2].transpose(0, 1, 3, 2).reshape(1, 512), (C, 512)))
    o["W_y2"] = c(i["L2_attn_W_y"].reshape(C, 4, 2, 32, 2).transpose(2, 4, 3, 1, 0).reshape(C, 4, C))
    o["b_y2"] = c(i["L2_attn_b_y"][:, None])
    o["W_out2"] = c(i["L2_attn_W_out"].T)
    o["b_out2"] = c(i["L2_attn_b_out"][:, None])
    h0 = np.stack([i["L2_attn_h0_re"], i["L2_attn_h0_im"]], 2)
    o["h0"] = c(h0.reshape(2, 4, 32, 64).transpose(1, 2, 0, 3).reshape(C, 2, 64))
    s_, t_ = np.arange(C)[:, None] % 32, np.arange(32)[None]
    same8 = (s_ // 8 == t_ // 8) & (s_ <= t_)
    half8 = (s_ // 16 == t_ // 16) & (s_ // 8 < t_ // 8)
    o["gla_mask"] = c(np.stack([same8, half8], 1).astype(np.float32))
    o["gate_w2"] = c(i["L2_ffn_gate_w"].T)
    o["w1_2"] = c(np.stack([*i["L2_ffn_w1"], i["L2_ffn_sw1"]], 1))
    o["w2_2"] = c(np.stack([*i["L2_ffn_w2"], i["L2_ffn_sw2"]], 0).reshape(3, 4, C, C).transpose(2, 0, 1, 3))
    o["b1_2"] = c(np.stack([*i["L2_ffn_b1"], i["L2_ffn_sb1"]], 0).reshape(3, 4, C).transpose(2, 0, 1))
    o["b2_2"] = c(np.stack([*i["L2_ffn_b2"], i["L2_ffn_sb2"]], 1))
    rows = lambda v: c(np.broadcast_to(v[None], (C,) + v.shape))
    o["Wqk3"] = c(np.stack([i["L3_attn_Wq"], i["L3_attn_Wk"]], 1))
    o["conv_qk"] = c(np.stack([i["L3_attn_conv_q"].T, i["L3_attn_conv_k"].T], 0))
    o["Wv3"] = c(i["L3_attn_Wv"])
    o["conv_v"] = rows(c(i["L3_attn_conv_v"].T))
    o["Wg3"] = c(i["L3_attn_Wg"])
    o["Wab3"] = c(np.concatenate([i["L3_attn_Wa"], i["L3_attn_Wb"]], 1))
    o["Wo3"] = c(i["L3_attn_Wo"].reshape(2, C, C).transpose(1, 0, 2))
    for n in ("A_log", "dt_bias", "o_norm_w"):
        o[n] = rows(i["L3_attn_" + n])
    s_, t_ = np.arange(C)[:, None], np.arange(C)[None]
    joins = np.stack([(s_ // (2 * n) == t_ // (2 * n)) & (s_ // n < t_ // n) for n in (1, 2, 4, 8, 16)], 1)
    o["joins"] = np.tile(joins[0:32, :, 0:32].astype(np.float32), (4, 1, 1))
    o["eye32"] = np.tile(np.eye(32, dtype=np.float32), (4, 1))
    o["upto3"], o["ones3"] = o["upto"].copy(), o["ones"].copy()
    for n in "rkv":
        o[f"W_{n}3"] = c(i[f"L3_ffn_W_{n}"].T)
    o["mu"] = c(np.stack([i["L3_ffn_mu_r"], i["L3_ffn_mu_k"]], 1))
    return o


def kernel(**inputs):
    import concourse.bacc as _bacc
    from concourse.bass_utils import run_bass_kernel_spmd as _run

    counts, arrays = {}, layouts(inputs)

    def program():
        nc = _bacc.Bacc("TRN2", target_bir_lowering=False, num_devices=1)
        a = {n: nc.dram_tensor(f"in_{n}_dram", v.shape, mybir.dt.from_np(v.dtype), kind="ExternalInput").ap()
             for n, v in arrays.items()}
        a["out"] = nc.dram_tensor("out_0_dram", (C, B, T), F32, kind="ExternalOutput").ap()
        build(nc, a, counts)
        return nc

    program()
    result = _run(program(), [{f"in_{n}_dram": v for n, v in arrays.items()}], core_ids=[0])
    return np.ascontiguousarray(result.results[0]["out_0_dram"].transpose(1, 2, 0))
```

```python
from contextlib import ExitStack

import numpy as np

import concourse.bass as bass
from concourse import mybir

F32 = mybir.dt.float32
U32 = mybir.dt.uint32
ALU = mybir.AluOpType
ACT = mybir.ActivationFunctionType
AX = mybir.AxisListType

C = 128
B = 8
T = 512
LN_EPS = 1e-5
NEG_BIG = -1e38
EXP_LN = "natural_log_exp_and_others"
LEAST = -37.0
SA, CA, GA, SB_, CB, GB = range(6)


class Steps:

    def __init__(self, steps, stage, counts, unit=1):
        self.steps, self.stage, self.counts, self.unit, self.n = steps, stage, counts, unit, 0

    def did(self, name=None):
        self.n += self.unit
        if name is not None:
            self.counts[self.stage, self.steps.name, name] = self.n
        return self.unit

    def at(self, name):
        return self.counts.get((self.stage, self.steps.name, name), 1)


class Kernel:

    def __init__(self, nc, counts):
        self.nc, self.counts, self.stack, self.w = nc, counts, ExitStack(), {}
        self.ps = self.stack.enter_context(nc.psum_tensor("ps", [128, 8, 512], F32))
        names = ("tensor_steps", "scalar_steps", "vector_steps", "gpsimd_steps", "dma_steps")
        self.sems = [self.stack.enter_context(nc.semaphore(n)) for n in names]

    def sb(self, name, shape, dt=F32, stack=None):
        return (stack or self.stack).enter_context(self.nc.sbuf_tensor(name, shape, dt))

    def stage(self, name):
        pe, act, dve, pool, dma = (Steps(s, name, self.counts, u) for s, u in zip(self.sems, (1, 1, 1, 1, 16)))
        return pe, act, dve, pool, dma

    def end(self):
        with self.nc.Block() as block:
            @block.vector
            def _(v):
                for s in self.sems:
                    v.sem_clear(s)


class Norm:

    def __init__(self, k, st, tag, bank_c, bank_v, x, h, mod, shift, scale, tmp):
        self.k, self.st, self.tag, self.x, self.h, self.tmp = k, st, tag, x, h, tmp
        self.pc, self.pv = k.ps[:, bank_c, :], k.ps[:, bank_v, :]
        self.shift, self.scale = mod[:, shift:shift + 1], mod[:, scale:scale + 1]

    def tensor(self, e):
        pe, act, dve, pool, _ = self.st
        k, g = self.k, self.tag
        e.matmul(self.pc, k.w["center"][:], self.x, start=True, stop=True).then_inc(pe.steps, pe.did(g + "c"))
        e.wait_ge(act.steps, act.at(g + "sq"))
        e.matmul(self.pv, k.w["mean"][:], self.tmp[:, 0, :], start=True, stop=True).then_inc(pe.steps, pe.did(g + "v"))

    def scalar(self, e):
        pe, act, dve, pool, _ = self.st
        g = self.tag
        e.wait_ge(pe.steps, pe.at(g + "c"))
        e.activation(self.tmp[:, 0, :], self.pc, ACT.Square).then_inc(act.steps, act.did(g + "sq"))
        e.wait_ge(pe.steps, pe.at(g + "v"))
        e.activation(self.tmp[:, 1, :], self.pv, ACT.Ln, bias=self.k.eps[:, 0:1]).then_inc(act.steps, act.did())
        e.wait_ge(act.steps, act.n)
        e.activation(self.tmp[:, 2, :], self.tmp[:, 1, :], ACT.Exp, scale=-0.5).then_inc(act.steps, act.did(g + "rs"))

    def vector(self, e):
        pe, act, dve, pool, _ = self.st
        g = self.tag
        e.wait_ge(act.steps, act.at(g + "rs"))
        e.tensor_tensor(self.tmp[:, 1, :], self.pc, self.tmp[:, 2, :], ALU.mult).then_inc(dve.steps, dve.did())
        e.wait_ge(dve.steps, dve.n)
        e.tensor_scalar(self.h, self.tmp[:, 1, :], self.scale, self.shift, ALU.mult, ALU.add).then_inc(dve.steps, dve.did(g + "h"))


def ts(i, n):
    return slice(i * n, (i + 1) * n)


GROUPS = {
    "all": ["center", "mean", "ident"],
    "modulation": ["cT", "wmod"],
    "layers01": ["W_rvk", "W_out0", "decay", "time_first", "Win0", "bin_0", "W1_0", "b1_0", "W2_0", "b2_0", "Wout0",
                 "bout_0", "W_Q", "W_K", "W_V", "W_O", "head_mask", "head_scale", "w_gate1", "rev8", "upto", "ones",
                 "c_fc", "c_proj"],
    "gla": ["W_in2", "b_in2", "W_qka", "b_qka", "W_v2", "b_v2", "W_y2", "b_y2", "W_out2", "b_out2", "h0", "gla_mask"],
    "delta": ["Wqk3", "Wv3", "Wg3", "Wab3", "Wo3", "A_log", "dt_bias", "conv_v", "o_norm_w", "joins", "eye32", "upto3", "ones3"],
    "mix": ["W_r3", "W_k3", "W_v3", "mu"],
    "mlp2": ["gate_w2", "w1_2", "w2_2", "b1_2", "b2_2"],
}


def place(k, a, names, stack):
    for name in names:
        k.w[name] = k.sb("w_" + name, list(a[name].shape), a[name].dtype, stack)


def load(k, a, group, stack):
    place(k, a, GROUPS[group], stack)
    pe, act, dve, pool, dma = k.stage("load_" + group)
    with k.nc.Block() as block:
        @block.sync
        def _(e):
            for name in GROUPS[group]:
                e.dma_start(k.w[name][:], a[name]).then_inc(dma.steps, dma.did("all"))
            e.wait_ge(dma.steps, dma.at("all"))
    k.end()


def load_weights(k, a):
    nc = k.nc
    place(k, a, GROUPS["all"], k.stack)
    k.X = k.sb("X", [C, B, T])
    k.eps = k.sb("eps", [C, 1])
    k.mod = k.sb("mod", [C, 4, 6, B])
    k.modb = k.sb("modb", [C, 4, 6])
    st = pe, act, dve, pool, dma = k.stage("load")
    scope = ExitStack()
    place(k, a, GROUPS["modulation"], scope)
    cT = k.sb("c_silu", [C, 4, B], stack=scope)
    with scope, nc.Block() as block:
        @block.sync
        def _(e):
            for name, ap in a.items():
                if name in GROUPS["all"] + GROUPS["modulation"]:
                    e.dma_start(k.w[name][:], ap).then_inc(dma.steps, dma.did())
            e.dma_start(k.X[:], a["x"]).then_inc(dma.steps, dma.did("all"))
            e.wait_ge(dma.steps, dma.at("all"))

        @block.scalar
        def _(e):
            e.wait_ge(dma.steps, dma.at("all"))
            e.activation(cT[:], k.w["cT"][:], ACT.Exp, scale=-1.0).then_inc(act.steps, act.did("exp"))

        @block.vector
        def _(e):
            e.memset(k.eps[:], LN_EPS).then_inc(dve.steps, dve.did())
            e.wait_ge(act.steps, act.at("exp"))
            e.tensor_scalar(cT[:], cT[:], 1.0, None, ALU.add).then_inc(dve.steps, dve.did())
            e.wait_ge(dve.steps, dve.n)
            e.reciprocal(cT[:], cT[:]).then_inc(dve.steps, dve.did())
            e.wait_ge(dve.steps, dve.n)
            e.tensor_tensor(cT[:], cT[:], k.w["cT"][:], ALU.mult).then_inc(dve.steps, dve.did("silu"))
            e.wait_ge(pe.steps, pe.at("mod"))
            m = k.mod[:].rearrange("p l s b -> p (l s b)")
            e.tensor_copy(m, k.ps[:, 0, 0:4 * 6 * B]).then_inc(dve.steps, dve.did())
            e.wait_ge(dve.steps, dve.n)
            for s in (CA, CB):
                e.tensor_scalar(k.mod[:, :, s, :], k.mod[:, :, s, :], 1.0, None, ALU.add).then_inc(dve.steps, dve.did())
            for s in (GA, GB):
                g = k.mod[:, :, s, :]
                e.tensor_scalar(cT[:], g, 0.0, 2.0, ALU.is_ge, ALU.mult).then_inc(dve.steps, dve.did())
                e.wait_ge(dve.steps, dve.n)
                e.tensor_scalar(cT[:], cT[:], -1.0, None, ALU.add).then_inc(dve.steps, dve.did())
                e.wait_ge(dve.steps, dve.n)
                e.tensor_tensor(g, g, cT[:], ALU.mult).then_inc(dve.steps, dve.did())
                e.wait_ge(dve.steps, dve.n)
                e.tensor_scalar(g, g, 0.25, None, ALU.max).then_inc(dve.steps, dve.did())
                e.wait_ge(dve.steps, dve.n)
                e.tensor_tensor(g, g, cT[:], ALU.mult).then_inc(dve.steps, dve.did())
                e.wait_ge(dve.steps, dve.n)

        @block.tensor
        def _(e):
            e.wait_ge(dve.steps, dve.at("silu"))
            for l in range(4):
                for s in range(6):
                    i = (l * 6 + s) * B
                    ins = e.matmul(k.ps[:, 0, i:i + B], k.w["wmod"][:, l, ts(s, C)], cT[:, l, :], start=True, stop=True)
            ins.then_inc(pe.steps, pe.did("mod"))
    k.end()


def wkv_mlp_prologue(k, s):
    nc = k.nc
    k.w_decay = k.sb("neg_decay", [C, 1], stack=s)
    k.w_full = k.sb("neg_decay_time", [C, T], stack=s)
    k.w2out = k.sb("w2out", [C, 8, C], stack=s)
    k.mlp0_const = k.sb("mlp0_const", [C, 1], stack=s)
    pe, act, dve, pool, dma = k.stage("wkv_prologue")
    with nc.Block() as block:
        @block.scalar
        def _(e):
            e.activation(k.w_decay[:], k.w["decay"][:], ACT.Exp).then_inc(act.steps, act.did("exp"))

        @block.tensor
        def _(e):
            e.matmul(k.ps[:, 0, 0:1], k.w["Wout0"][0:64, :], k.w["b2_0"][0:64, :], start=True, stop=True).then_inc(pe.steps, pe.did("const"))

        @block.vector
        def _(e):
            e.memset(k.w_full[:], 0.0).then_inc(dve.steps, dve.did("zero"))
            e.wait_ge(act.steps, act.at("exp"))
            e.tensor_scalar(k.w_decay[:], k.w_decay[:], -1.0, None, ALU.mult).then_inc(dve.steps, dve.did())
            e.wait_ge(dve.steps, dve.n)
            e.tensor_scalar(k.w_full[:], k.w_full[:], k.w_decay[:, 0:1], None, ALU.add).then_inc(dve.steps, dve.did())
            for j in range(8):
                e.tensor_scalar(k.w2out[:, j, :], k.w["Wout0"][:], k.w["W2_0"][:, j:j + 1], None, ALU.mult).then_inc(dve.steps, dve.did())
            e.wait_ge(pe.steps, pe.at("const"))
            e.tensor_tensor(k.mlp0_const[:], k.ps[:, 0, 0:1], k.w["bout_0"][:], ALU.add).then_inc(dve.steps, dve.did())
    k.end()


def layer0(k, q1, k1, v1, qbar, kbar):
    nc = k.nc
    with ExitStack() as s:
        lanes = lambda name, shape: [k.sb(f"l0_{name}{l}", shape, stack=s) for l in range(2)]
        xb, h, ks, er, e1, e2, f1, f2, pm, n1, d1, y = (lanes(name, [C, T]) for name in (
            "xb", "h", "k", "er", "e1", "e2", "f1", "f2", "pm", "n1", "d1", "y"))
        pp, aa, bb = (lanes(name, [C, T + 1]) for name in ("pp", "aa", "bb"))
        tmp, modb = lanes("tmp", [C, 3, T]), lanes("modb", [C, 4, 6])
        e2v, n2 = ([tmp[l][:, i, :] for l in range(2)] for i in range(2))
        hid = k.sb("l0_hid", [C, 8, T], stack=s)
        bank = lambda l, i: k.ps[:, 4 * l + i, :]
        u = k.w["time_first"][:, 0:1]
        wd = k.w_decay[:, 0:1]
        with nc.Fori(0, B // 2) as pair:
            st = pe, act, dve, pool, dma = k.stage("layer0")
            batch = lambda l: bass.ds(pair * 2 + l, 1)
            m0, m1 = ([modb[l][:, layer, :] for l in range(2)] for layer in (0, 1))
            na, nb, nq = ([Norm(k, st, f"{tag}{l}", 4 * l, 4 * l + 1, xb[l][:], h[l][:], mod[l], shift, scale, tmp[l]) for l in range(2)]
                          for tag, mod, shift, scale in (("a", m0, SA, CA), ("b", m0, SB_, CB), ("q", m1, SA, CA)))
            with nc.Block() as block:
                @block.tensor
                def _(e):
                    for l in range(2):
                        e.wait_ge(pool.steps, pool.at(f"xb{l}"))
                        na[l].tensor(e)
                    for l in range(2):
                        e.wait_ge(dve.steps, dve.at(f"a{l}h"))
                        for i, name in ((2, "k"), (1, "v"), (0, "r")):
                            e.matmul(bank(l, (0, 3, 2)[i]), k.w["W_rvk"][:, ts(i, C)], h[l][:], start=True, stop=True).then_inc(pe.steps, pe.did(f"{name}{l}"))
                    for l in range(2):
                        e.wait_ge(dve.steps, dve.at(f"y{l}"))
                        e.matmul(bank(l, 1), k.w["W_out0"][:], y[l][:], start=True, stop=True).then_inc(pe.steps, pe.did(f"att{l}"))
                    for l in range(2):
                        e.wait_ge(dve.steps, dve.at(f"x1{l}"))
                        nb[l].tensor(e)
                    for l in range(2):
                        e.wait_ge(dve.steps, dve.at(f"b{l}h"))
                        e.matmul(bank(l, 2), k.w["Win0"][:], h[l][:], start=True, stop=True).then_inc(pe.steps, pe.did(f"s{l}"))
                    for l in range(2):
                        for j in range(8):
                            e.wait_ge(act.steps, act.at(f"hid{j}_{l}"))
                            ins = e.matmul(bank(l, 3), k.w2out[:, j, :], hid[:, j, :], start=(j == 0), stop=(j == 7))
                            if l == 0 and j < 7:
                                ins.then_inc(pe.steps, pe.did(f"read{j}"))
                        ins.then_inc(pe.steps, pe.did(f"mlp{l}"))
                    for l in range(2):
                        e.wait_ge(dve.steps, dve.at(f"x2{l}"))
                        nq[l].tensor(e)
                    for l in range(2):
                        e.wait_ge(dve.steps, dve.at(f"q{l}h"))
                        for i, w in enumerate((k.w["W_Q"], k.w["W_K"], k.w["W_V"])):
                            e.matmul(bank(l, (2, 3, 0)[i]), w[:], h[l][:], start=True, stop=True).then_inc(pe.steps, pe.did(f"p{i}_{l}"))

                @block.gpsimd
                def _(e):
                    for l in range(2):
                        e.tensor_copy(xb[l][:], k.X[:, batch(l), :].rearrange("p a t -> p (a t)")).then_inc(pool.steps, pool.did(f"xb{l}"))
                    for l in range(2):
                        e.wait_ge(dve.steps, dve.at(f"pp{l}"))
                        e.wait_ge(act.steps, act.at(f"k{l}"))
                        e.tensor_tensor(e2[l][:], ks[l][:], pp[l][:, 1:], ALU.subtract).then_inc(pool.steps, pool.did(f"e2a{l}"))
                        e.wait_ge(dve.steps, dve.at(f"pm{l}"))
                        e.tensor_tensor(f1[l][:], pp[l][:, 0:T], pm[l][:], ALU.subtract).then_inc(pool.steps, pool.did(f"f1a{l}"))
                    for l in range(2):
                        e.wait_ge(act.steps, act.at(f"f1{l}"))
                        e.wait_ge(dve.steps, dve.at(f"aa{l}"))
                        e.tensor_tensor(n1[l][:], f1[l][:], aa[l][:, 0:T], ALU.mult).then_inc(pool.steps, pool.did(f"n1{l}"))
                        e.wait_ge(dve.steps, dve.at(f"bb{l}"))
                        e.tensor_tensor(d1[l][:], f1[l][:], bb[l][:, 0:T], ALU.mult).then_inc(pool.steps, pool.did(f"d1{l}"))

                @block.scalar
                def _(e):
                    e.preload_act_table_set(EXP_LN)
                    for l in range(2):
                        na[l].scalar(e)
                    for l in range(2):
                        e.wait_ge(pe.steps, pe.at(f"k{l}"))
                        e.activation(ks[l][:], bank(l, 2), ACT.Copy).then_inc(act.steps, act.did(f"k{l}"))
                        e.wait_ge(dve.steps, dve.at(f"er{l}"))
                        e.activation(er[l][:], er[l][:], ACT.Exp, scale=-1.0).then_inc(act.steps, act.did())
                    for l in range(2):
                        e.wait_ge(dve.steps, dve.at(f"e1a{l}"))
                        e.activation(e1[l][:], e1[l][:], ACT.Exp).then_inc(act.steps, act.did(f"e1{l}"))
                        e.wait_ge(pool.steps, pool.at(f"e2a{l}"))
                        e.activation(e2[l][:], e2[l][:], ACT.Exp).then_inc(act.steps, act.did(f"e2{l}"))
                        e.wait_ge(pool.steps, pool.at(f"f1a{l}"))
                        e.activation(f1[l][:], f1[l][:], ACT.Exp).then_inc(act.steps, act.did(f"f1{l}"))
                        e.wait_ge(dve.steps, dve.at(f"f2a{l}"))
                        e.activation(f2[l][:], f2[l][:], ACT.Exp).then_inc(act.steps, act.did(f"f2{l}"))
                    for l in range(2):
                        e.wait_ge(dve.steps, dve.at(f"den{l}"))
                        e.activation(d1[l][:], d1[l][:], ACT.Ln).then_inc(act.steps, act.did())
                        e.wait_ge(act.steps, act.n)
                        e.activation(d1[l][:], d1[l][:], ACT.Exp, scale=-1.0).then_inc(act.steps, act.did(f"inv{l}"))
                    for l in range(2):
                        nb[l].scalar(e)
                    for l in range(2):
                        e.wait_ge(pe.steps, pe.at(f"s{l}"))
                        e.activation(er[l][:], bank(l, 2), ACT.Identity, bias=k.w["bin_0"][:, 0:1]).then_inc(act.steps, act.did(f"s{l}"))
                        e.wait_ge(act.steps, act.n)
                        for j in range(8):
                            if l:
                                e.wait_ge(pe.steps, pe.at(f"read{j}" if j < 7 else "mlp0"))
                            e.activation(hid[:, j, :], er[l][:], ACT.Relu, bias=k.w["b1_0"][:, j:j + 1],
                                                  scale=k.w["W1_0"][:, j:j + 1]).then_inc(act.steps, act.did(f"hid{j}_{l}"))
                    for l in range(2):
                        e.wait_ge(pe.steps, pe.at(f"mlp{l}"))
                        e.activation(y[l][:], bank(l, 3), ACT.Identity, bias=k.mlp0_const[:, 0:1]).then_inc(act.steps, act.did(f"mlp{l}"))
                    for l in range(2):
                        nq[l].scalar(e)
                    for l in range(2):
                        for i, dst in ((0, q1), (1, k1)):
                            e.wait_ge(pe.steps, pe.at(f"p{i}_{l}"))
                            e.activation(dst[:, batch(l), :].rearrange("p a t -> p (a t)"), bank(l, (2, 3, 0)[i]), ACT.Copy).then_inc(act.steps, act.did(f"cp{i}_{l}"))

                @block.vector
                def _(e):
                    for l in range(2):
                        e.tensor_copy(modb[l][:], k.mod[:, :, :, batch(l)].rearrange("p l s a -> p l (s a)")).then_inc(dve.steps, dve.did())
                        e.memset(pp[l][:, 0:1], NEG_BIG).then_inc(dve.steps, dve.did())
                        e.memset(aa[l][:, 0:1], 0.0).then_inc(dve.steps, dve.did())
                        e.memset(bb[l][:, 0:1], 0.0).then_inc(dve.steps, dve.did())
                        e.wait_ge(dve.steps, dve.n)
                    for l in range(2):
                        na[l].vector(e)
                    for l in range(2):
                        e.wait_ge(pe.steps, pe.at(f"r{l}"))
                        e.tensor_scalar(er[l][:], bank(l, 0), LEAST, None, ALU.max).then_inc(dve.steps, dve.did(f"er{l}"))
                        e.wait_ge(act.steps, act.at(f"k{l}"))
                        e.tensor_tensor_scan(pp[l][:, 1:], k.w_full[:], ks[l][:], NEG_BIG, ALU.add, ALU.max).then_inc(dve.steps, dve.did(f"pp{l}"))
                        e.wait_ge(dve.steps, dve.n)
                        e.scalar_tensor_tensor(e1[l][:], pp[l][:, 0:T], wd, pp[l][:, 1:], ALU.add, ALU.subtract).then_inc(dve.steps, dve.did(f"e1a{l}"))
                        e.scalar_tensor_tensor(pm[l][:], ks[l][:], u, pp[l][:, 0:T], ALU.add, ALU.max).then_inc(dve.steps, dve.did(f"pm{l}"))
                        e.wait_ge(dve.steps, dve.n)
                        e.scalar_tensor_tensor(f2[l][:], ks[l][:], u, pm[l][:], ALU.add, ALU.subtract).then_inc(dve.steps, dve.did(f"f2a{l}"))
                    for l in range(2):
                        e.wait_ge(act.steps, act.at(f"e2{l}"))
                        e.wait_ge(pe.steps, pe.at(f"v{l}"))
                        e.tensor_tensor(e2v[l][:], e2[l][:], bank(l, 3), ALU.mult).then_inc(dve.steps, dve.did())
                        e.wait_ge(dve.steps, dve.n)
                        e.tensor_tensor_scan(aa[l][:, 1:], e1[l][:], e2v[l][:], 0.0, ALU.mult, ALU.add).then_inc(dve.steps, dve.did(f"aa{l}"))
                        e.tensor_tensor_scan(bb[l][:, 1:], e1[l][:], e2[l][:], 0.0, ALU.mult, ALU.add).then_inc(dve.steps, dve.did(f"bb{l}"))
                    for l in range(2):
                        e.wait_ge(act.steps, act.at(f"f2{l}"))
                        e.tensor_tensor(n2[l][:], f2[l][:], bank(l, 3), ALU.mult).then_inc(dve.steps, dve.did())
                        e.wait_ge(pool.steps, pool.at(f"d1{l}"))
                        e.tensor_tensor(d1[l][:], d1[l][:], f2[l][:], ALU.add).then_inc(dve.steps, dve.did())
                        e.wait_ge(dve.steps, dve.n)
                        e.scalar_tensor_tensor(d1[l][:], er[l][:], 1.0, d1[l][:], ALU.add, ALU.mult).then_inc(dve.steps, dve.did(f"den{l}"))
                        e.tensor_tensor(n1[l][:], n1[l][:], n2[l][:], ALU.add).then_inc(dve.steps, dve.did())
                        e.wait_ge(dve.steps, dve.n)
                    for l in range(2):
                        e.wait_ge(act.steps, act.at(f"inv{l}"))
                        e.tensor_tensor(y[l][:], n1[l][:], d1[l][:], ALU.mult).then_inc(dve.steps, dve.did(f"y{l}"))
                    for l in range(2):
                        e.wait_ge(pe.steps, pe.at(f"att{l}"))
                        e.scalar_tensor_tensor(xb[l][:], bank(l, 1), m0[l][:, GA:GA + 1], xb[l][:], ALU.mult, ALU.add).then_inc(dve.steps, dve.did(f"x1{l}"))
                    for l in range(2):
                        nb[l].vector(e)
                    for l in range(2):
                        e.wait_ge(act.steps, act.at(f"mlp{l}"))
                        e.scalar_tensor_tensor(xb[l][:], y[l][:], m0[l][:, GB:GB + 1], xb[l][:], ALU.mult, ALU.add).then_inc(dve.steps, dve.did(f"x2{l}"))
                        e.wait_ge(dve.steps, dve.n)
                        e.tensor_copy(k.X[:, batch(l), :].rearrange("p a t -> p (a t)"), xb[l][:]).then_inc(dve.steps, dve.did())
                    for l in range(2):
                        nq[l].vector(e)
                    for l in range(2):
                        e.wait_ge(pe.steps, pe.at(f"p2_{l}"))
                        e.tensor_copy(v1[:, batch(l), :].rearrange("p a t -> p (a t)"), bank(l, 0)).then_inc(dve.steps, dve.did())
                        for i, dst, src in ((0, qbar, q1), (1, kbar, k1)):
                            e.wait_ge(act.steps, act.at(f"cp{i}_{l}"))
                            e.tensor_reduce(dst[:, batch(l), :].rearrange("p a t -> p (a t)"),
                                                     src[:, batch(l), :].rearrange("p a (i q) -> p (a i) q", q=32),
                                                     AX.X, ALU.add).then_inc(dve.steps, dve.did())
            k.end()


def flat(ap):
    return ap.rearrange("p a t -> p (a t)")


def choose_blocks(k, qbar, kbar, idx_row):
    with ExitStack() as s:
        sc = k.sb("blk_sc", [16, 16], stack=s)
        best = k.sb("blk_best", [16, 8], stack=s)
        idx = k.sb("blk_idx", [16, 8], U32, stack=s)
        pe, act, dve, pool, dma = k.stage("choose")
        with k.nc.Block() as block:
            @block.tensor
            def _(e):
                for b in range(B):
                    ins = e.matmul(k.ps[0:16, 0, 0:16], qbar[:, b, :], kbar[:, b, :], start=(b == 0), stop=(b == B - 1))
                ins.then_inc(pe.steps, pe.did("score"))

            @block.vector
            def _(e):
                e.wait_ge(pe.steps, pe.at("score"))
                e.tensor_copy(sc[:], k.ps[0:16, 0, 0:16]).then_inc(dve.steps, dve.did())
                e.wait_ge(dve.steps, dve.n)
                e.max(best[:], sc[:]).then_inc(dve.steps, dve.did())
                e.wait_ge(dve.steps, dve.n)
                e.max_index(idx[:], best[:], sc[:]).then_inc(dve.steps, dve.did("idx"))

            @block.sync
            def _(e):
                e.wait_ge(dve.steps, dve.at("idx"))
                e.dma_start(idx_row[0:1, :].rearrange("a (t s) -> a t s", s=3), idx[:, 0:3]).then_inc(dma.steps, dma.did("row"))
                e.wait_ge(dma.steps, dma.at("row"))
        k.end()


def block_attention(k, q1, k1, v1, idx_row):
    nc = k.nc
    NK, BLOCKS = 96, 4
    UNITS = 2 * BLOCKS
    with ExitStack() as s:
        kg = k.sb("att_kg", [C, BLOCKS, B, NK], stack=s)
        vg = k.sb("att_vg", [C, BLOCKS, B, NK], stack=s)
        qx = k.sb("att_qx", [C, BLOCKS, B, 4, 32], stack=s)
        mx = k.sb("att_mx", [C, 2, 16], stack=s)
        den = k.sb("att_den", [C, 2, 16], stack=s)
        p = k.sb("att_p", [C, 2, 16, NK], stack=s)
        pt = k.sb("att_pt", [NK, 2, 16, C], stack=s)
        vt = k.sb("att_vt", [NK, 2, 4, C], stack=s)
        o = k.sb("att_o", [C, 4, 32], stack=s)
        scored = k.ps[:, 0:4, 0:4 * NK].rearrange("p g (n k) -> p g n k", k=NK)
        BANK_VT, BANK_PT, BANK_O = 4, 5, 7
        place_of = lambda n: (n // 2, n % 2)
        with nc.Fori(0, T // 32 // BLOCKS) as group:
            pe, act, dve, pool, dma = k.stage("attention")
            block_at = lambda q: group * BLOCKS + q
            with nc.Block() as block:
                @block.gpsimd
                def _(e):
                    def gather(q):
                        for i in range(3):
                            j = e.value_load(idx_row[0:1, bass.ds(block_at(q) * 3 + i, 1)], min_val=0, max_val=15)
                            e.tensor_copy(vg[:, q, :, ts(i, 32)], v1[:, :, bass.ds(j * 32, 32)]).then_inc(pool.steps, pool.did(f"v{q}"))

                    gather(0)
                    for n in range(UNITS):
                        if n % 2 and n + 1 < UNITS:
                            gather((n + 1) // 2)
                        e.wait_ge(act.steps, act.at(f"exp{n}"))
                        e.wait_ge(dve.steps, dve.at(f"rden{n}"))
                        for r in range(1, 4):
                            w = p[:, n % 2, ts(r, 4)]
                            e.tensor_tensor(w, w, den[:, n % 2, ts(r, 4)].unsqueeze(2).to_broadcast([C, 4, NK]),
                                            ALU.mult).then_inc(pool.steps, pool.did(f"p{n}{r}"))

                @block.vector
                def _(e):
                    def gather(q):
                        for i in range(3):
                            j = e.value_load(idx_row[0:1, bass.ds(block_at(q) * 3 + i, 1)], min_val=0, max_val=15)
                            e.tensor_copy(kg[:, q, :, ts(i, 32)], k1[:, :, bass.ds(j * 32, 32)]).then_inc(dve.steps, dve.did())
                        for i in range(4):
                            e.tensor_scalar(qx[:, q, :, i, :], q1[:, :, bass.ds(block_at(q) * 32, 32)], k.w["head_scale"][:, i:i + 1],
                                            None, ALU.mult).then_inc(dve.steps, dve.did(f"q{q}"))

                    def below_maximum(n):
                        e.wait_ge(pe.steps, pe.at(f"s{n}"))
                        m4 = mx[:, n % 2].rearrange("p (g n) -> p g n", g=4)
                        e.tensor_reduce(m4, scored, AX.X, ALU.max).then_inc(dve.steps, dve.did())
                        e.wait_ge(dve.steps, dve.n)
                        if n >= 2:
                            e.wait_ge(pe.steps, pe.at(f"pt{n - 2}3"))
                        e.tensor_tensor(p[:, n % 2].rearrange("p (g n) k -> p g n k", g=4), scored,
                                        m4.unsqueeze(3).to_broadcast([C, 4, 4, NK]), ALU.subtract).then_inc(dve.steps, dve.did(f"sub{n}"))

                    def denominator(n):
                        e.wait_ge(act.steps, act.at(f"exp{n}"))
                        e.tensor_reduce(den[:, n % 2], p[:, n % 2], AX.X, ALU.add).then_inc(dve.steps, dve.did())
                        e.wait_ge(dve.steps, dve.n)
                        e.reciprocal(den[:, n % 2], den[:, n % 2]).then_inc(dve.steps, dve.did(f"rden{n}"))
                        e.wait_ge(dve.steps, dve.n)
                        w = p[:, n % 2, 0:4]
                        e.tensor_tensor(w, w, den[:, n % 2, 0:4].unsqueeze(2).to_broadcast([C, 4, NK]),
                                        ALU.mult).then_inc(dve.steps, dve.did(f"p{n}"))

                    def keep_values(n):
                        e.wait_ge(pe.steps, pe.at(f"vt{n}"))
                        e.tensor_copy(vt[:, n % 2].rearrange("p n c -> p (n c)"), k.ps[0:NK, BANK_VT, :]).then_inc(dve.steps, dve.did(f"vt{n}"))

                    def pick_heads(n):
                        q, u = place_of(n)
                        e.wait_ge(pe.steps, pe.at(f"o{n}"))
                        O = k.ps[:, BANK_O, :].rearrange("p (n h q) -> p n h q", n=4, h=4)
                        e.tensor_scalar(o[:], O[:, :, 0, :], k.w["head_mask"][:, 0:1], None, ALU.mult).then_inc(dve.steps, dve.did())
                        for i in range(1, 4):
                            e.wait_ge(dve.steps, dve.n)
                            dst = o[:] if i < 3 else q1[:, 4 * u:4 * u + 4, bass.ds(block_at(q) * 32, 32)]
                            e.scalar_tensor_tensor(dst, O[:, :, i, :], k.w["head_mask"][:, i:i + 1], o[:],
                                                   ALU.mult, ALU.add).then_inc(dve.steps, dve.did(f"out{n}"))
                        e.wait_ge(dve.steps, dve.n)

                    gather(0)
                    for n in range(UNITS):
                        below_maximum(n)
                        if n % 2 == 0 and n + 2 < UNITS:
                            gather(n // 2 + 1)
                        denominator(n)
                        if n:
                            pick_heads(n - 1)
                        keep_values(n)
                    pick_heads(UNITS - 1)

                @block.scalar
                def _(e):
                    def exponentials(n):
                        w = p[:, n % 2].rearrange("p a k -> p (a k)")
                        e.wait_ge(dve.steps, dve.at(f"sub{n}"))
                        e.activation(w, w, ACT.Exp).then_inc(act.steps, act.did(f"exp{n}"))

                    e.preload_act_table_set(EXP_LN)
                    exponentials(0)
                    for n in range(UNITS):
                        for r in range(4):
                            e.wait_ge(pe.steps, pe.at(f"pt{n}{r}"))
                            e.activation(pt[:, n % 2, ts(r, 4), :].rearrange("p a c -> p (a c)"),
                                         k.ps[0:NK, BANK_PT + r % 2, :], ACT.Copy).then_inc(act.steps, act.did(f"pt{n}{r}"))
                        if n + 1 < UNITS:
                            exponentials(n + 1)

                @block.tensor
                def _(e):
                    def values_by_time(n):
                        q, u = place_of(n)
                        e.wait_ge(pool.steps, pool.at(f"v{q}"))
                        if n:
                            e.wait_ge(dve.steps, dve.at(f"vt{n - 1}"))
                        for b in range(4):
                            ins = e.transpose(k.ps[0:NK, BANK_VT, ts(b, C)], vg[:, q, 4 * u + b, :], k.w["ident"][:])
                        ins.then_inc(pe.steps, pe.did(f"vt{n}"))

                    def scores(n):
                        q, u = place_of(n)
                        e.wait_ge(dve.steps, dve.at(f"q{q}"))
                        if n:
                            e.wait_ge(dve.steps, dve.at(f"sub{n - 1}"))
                        for g in range(4):
                            for b in range(4):
                                ins = e.matmul(scored[:, g, b], qx[ts(g, 32), q, 4 * u + b, :, :].rearrange("p h q -> p (h q)"),
                                               kg[ts(g, 32), q, 4 * u + b, :], start=True, stop=True, tile_position=(32 * g, 0))
                        ins.then_inc(pe.steps, pe.did(f"s{n}"))

                    scores(0)
                    for n in range(UNITS):
                        values_by_time(n)
                        if n + 1 < UNITS:
                            scores(n + 1)
                        for r in range(4):
                            if r:
                                e.wait_ge(pool.steps, pool.at(f"p{n}{r}"))
                            else:
                                e.wait_ge(dve.steps, dve.at(f"p{n}"))
                            if r >= 2 or n:
                                e.wait_ge(act.steps, act.at(f"pt{n}{r - 2}" if r >= 2 else f"pt{n - 1}{r + 2}"))
                            for b in range(4):
                                ins = e.transpose(k.ps[0:NK, BANK_PT + r % 2, ts(b, C)], p[:, n % 2, 4 * r + b, :], k.w["ident"][:])
                            ins.then_inc(pe.steps, pe.did(f"pt{n}{r}"))
                        e.wait_ge(act.steps, act.at(f"pt{n}3"))
                        e.wait_ge(dve.steps, dve.at(f"vt{n}"))
                        if n:
                            e.wait_ge(dve.steps, dve.at(f"out{n - 1}"))
                        for b in range(4):
                            for g in range(4):
                                ins = e.matmul(k.ps[ts(g, 32), BANK_O, ts(b, C)], vt[:, n % 2, b, ts(g, 32)], pt[:, n % 2, 4 * g + b, :],
                                               start=True, stop=True, tile_position=(0, 32 * g))
                        ins.then_inc(pe.steps, pe.did(f"o{n}"))
            k.end()


def attention_out(k, o1, h1, lg):
    nc = k.nc
    LANES = 4
    with ExitStack() as s:
        lanes = lambda name, shape: [k.sb(f"ao_{name}{l}", shape, stack=s) for l in range(LANES)]
        ob, xb, h, tmp, modb = lanes("ob", [C, T]), lanes("xb", [C, T]), lanes("h", [C, T]), lanes("tmp", [C, 3, T]), lanes("modb", [C, 4, 6])
        bank = lambda l, i: k.ps[:, 2 * l + i, :]
        with nc.Fori(0, B // LANES) as four:
            st = pe, act, dve, pool, dma = k.stage("attention_out")
            batch = lambda l: bass.ds(four * LANES + l, 1)
            m = [modb[l][:, 1, :] for l in range(LANES)]
            n = [Norm(k, st, f"n{l}", 2 * l, 2 * l + 1, xb[l][:], h[l][:], m[l], SB_, CB, tmp[l]) for l in range(LANES)]
            with nc.Block() as block:
                @block.tensor
                def _(e):
                    for l in range(LANES):
                        e.wait_ge(pool.steps, pool.at(f"ob{l}"))
                        e.matmul(bank(l, 1), k.w["W_O"][:], ob[l][:], start=True, stop=True).then_inc(pe.steps, pe.did(f"att{l}"))
                    for l in range(LANES):
                        e.wait_ge(dve.steps, dve.at(f"x1{l}"))
                        n[l].tensor(e)
                    for l in range(LANES):
                        e.wait_ge(dve.steps, dve.at(f"n{l}h"))
                        for i in range(4):
                            ins = e.matmul(bank(l, 0)[:, ts(i, 8)], h[l][:, ts(i, C)], k.w["w_gate1"][:], start=True, stop=True)
                        ins.then_inc(pe.steps, pe.did(f"lg{l}"))

                @block.gpsimd
                def _(e):
                    for l in range(LANES):
                        e.tensor_copy(ob[l][:], flat(o1[:, batch(l), :])).then_inc(pool.steps, pool.did(f"ob{l}"))
                    for l in range(LANES):
                        e.wait_ge(dve.steps, dve.at(f"n{l}h"))
                        e.tensor_copy(flat(h1[:, batch(l), :]), h[l][:]).then_inc(pool.steps, pool.did())

                @block.scalar
                def _(e):
                    e.preload_act_table_set(EXP_LN)
                    for l in range(LANES):
                        n[l].scalar(e)
                        e.activation(flat(k.X[:, batch(l), :]), xb[l][:], ACT.Copy).then_inc(act.steps, act.did())

                @block.vector
                def _(e):
                    for l in range(LANES):
                        e.tensor_copy(modb[l][:], k.mod[:, :, :, batch(l)].rearrange("p l s a -> p l (s a)")).then_inc(dve.steps, dve.did())
                    e.wait_ge(dve.steps, dve.n)
                    for l in range(LANES):
                        e.wait_ge(pe.steps, pe.at(f"att{l}"))
                        e.scalar_tensor_tensor(xb[l][:], bank(l, 1), m[l][:, GA:GA + 1], flat(k.X[:, batch(l), :]),
                                               ALU.mult, ALU.add).then_inc(dve.steps, dve.did(f"x1{l}"))
                    for l in range(LANES):
                        n[l].vector(e)
                    for l in range(LANES):
                        e.wait_ge(pe.steps, pe.at(f"lg{l}"))
                        e.tensor_copy(flat(lg[:, batch(l), :]), bank(l, 0)[:, 0:32]).then_inc(dve.steps, dve.did())
            k.end()


def route(k, lg, gates):
    E, NT = 8, B * T // C
    CAP = int(1.25 * B * T * 2 / E)
    nc = k.nc
    with ExitStack() as s:
        l = lg[:].rearrange("p b (i x) -> p (b i) x", x=E)
        eq = k.sb("rt_eq", [C, NT, E], stack=s)
        oh = k.sb("rt_oh", [C, 2, NT, E], stack=s)
        m = k.sb("rt_m", [C, 2, NT], stack=s)
        mk = k.sb("rt_mk", [C, NT], stack=s)
        pr = k.sb("rt_pr", [C, 2, NT], stack=s)
        tot = k.sb("rt_tot", [C, 2 * NT, E], stack=s)
        cum = k.sb("rt_cum", [C, 2 * NT, E], stack=s)
        one = k.sb("rt_one", [C, 2 * NT], stack=s)
        wide = lambda ap: ap.unsqueeze(2).to_broadcast([C, NT, E])
        pe, act, dve, pool, dma = k.stage("route")
        with nc.Block() as block:
            @block.vector
            def _(e):
                e.memset(one[:], 1.0).then_inc(dve.steps, dve.did())
                for c in range(2):
                    e.tensor_reduce(m[:, c], l, AX.X, ALU.max).then_inc(dve.steps, dve.did())
                    e.wait_ge(dve.steps, dve.n)
                    e.tensor_tensor(eq[:], l, wide(m[:, c]), ALU.is_equal).then_inc(dve.steps, dve.did())
                    e.wait_ge(dve.steps, dve.n)
                    e.tensor_tensor(eq[:], eq[:], k.w["rev8"][:].unsqueeze(1).to_broadcast([C, NT, E]), ALU.mult).then_inc(dve.steps, dve.did())
                    e.wait_ge(dve.steps, dve.n)
                    e.tensor_reduce(mk[:], eq[:], AX.X, ALU.max).then_inc(dve.steps, dve.did())
                    e.wait_ge(dve.steps, dve.n)
                    e.tensor_tensor(oh[:, c], eq[:], wide(mk[:]), ALU.is_equal).then_inc(dve.steps, dve.did(f"oh{c}"))
                    e.wait_ge(dve.steps, dve.n)
                    if c == 0:
                        e.scalar_tensor_tensor(l, oh[:, 0], -1e30, l, ALU.mult, ALU.add).then_inc(dve.steps, dve.did())
                        e.wait_ge(dve.steps, dve.n)
                e.tensor_tensor(pr[:, 1], m[:, 1], m[:, 0], ALU.subtract).then_inc(dve.steps, dve.did("diff"))
                e.wait_ge(act.steps, act.at("exp"))
                e.tensor_scalar(pr[:, 0], pr[:, 1], 1.0, None, ALU.add).then_inc(dve.steps, dve.did())
                e.wait_ge(dve.steps, dve.n)
                e.reciprocal(pr[:, 0], pr[:, 0]).then_inc(dve.steps, dve.did())
                e.wait_ge(dve.steps, dve.n)
                e.tensor_tensor(pr[:, 1], pr[:, 1], pr[:, 0], ALU.mult).then_inc(dve.steps, dve.did())
                e.wait_ge(pe.steps, pe.at("cum"))
                e.tensor_copy(tot[:].rearrange("p a x -> p (a x)"), k.ps[:, 1, :]).then_inc(dve.steps, dve.did())
                e.wait_ge(dve.steps, dve.n)
                for x in range(E):
                    e.tensor_tensor_scan(cum[:, :, x], one[:], tot[:, :, x], 0.0, ALU.mult, ALU.add).then_inc(dve.steps, dve.did())
                e.wait_ge(dve.steps, dve.n)
                e.tensor_tensor(cum[:], cum[:], tot[:], ALU.subtract).then_inc(dve.steps, dve.did())
                e.wait_ge(dve.steps, dve.n)
                c2 = cum[:].rearrange("p a x -> p (a x)")
                e.tensor_tensor(c2, c2, k.ps[:, 0, :], ALU.add).then_inc(dve.steps, dve.did())
                e.wait_ge(dve.steps, dve.n)
                e.scalar_tensor_tensor(c2, c2, float(CAP), oh[:].rearrange("p c n x -> p (c n x)"), ALU.is_le, ALU.mult).then_inc(dve.steps, dve.did())
                e.wait_ge(dve.steps, dve.n)
                for c in range(2):
                    e.tensor_tensor(oh[:, c], cum[:, ts(c, NT), :], wide(pr[:, c]), ALU.mult).then_inc(dve.steps, dve.did())
                e.wait_ge(dve.steps, dve.n)
                e.tensor_tensor(gates[:], oh[:, 0], oh[:, 1], ALU.add).then_inc(dve.steps, dve.did())

            @block.scalar
            def _(e):
                e.preload_act_table_set(EXP_LN)
                e.wait_ge(dve.steps, dve.at("diff"))
                e.activation(pr[:, 1], pr[:, 1], ACT.Exp).then_inc(act.steps, act.did("exp"))

            @block.tensor
            def _(e):
                e.wait_ge(dve.steps, dve.at("oh1"))
                o = oh[:].rearrange("p c n x -> p (c n x)")
                e.matmul(k.ps[:, 0, :], k.w["upto"][:], o, start=True, stop=True)
                e.matmul(k.ps[:, 1, :], k.w["ones"][:], o, start=True, stop=True).then_inc(pe.steps, pe.did("cum"))
        k.end()


def experts(k, h1, gates):
    nc = k.nc
    E, F = 8, 4
    with ExitStack() as s:
        h = k.sb("ex_h", [C, T], stack=s)
        g = k.sb("ex_g", [C, 4, E], stack=s)
        r = k.sb("ex_r", [C, 2, F, T], stack=s)
        acc = k.sb("ex_acc", [C, 4, C], stack=s)
        with nc.Fori(0, B) as b:
            pe, act, dve, pool, dma = k.stage("experts")
            with nc.Block() as block:
                @block.gpsimd
                def _(e):
                    e.tensor_copy(h[:], flat(h1[:, bass.ds(b, 1), :])).then_inc(pool.steps, pool.did("h"))
                    for x in range(E):
                        for f in range(2, F):
                            e.wait_ge(act.steps, act.at(f"r{x}{f}"))
                            e.tensor_tensor(r[:, x % 2, f], r[:, x % 2, f], r[:, x % 2, f], ALU.mult).then_inc(pool.steps, pool.did(f"r{x}{f}"))

                @block.scalar
                def _(e):
                    for x in range(E):
                        if x >= 2:
                            e.wait_ge(pe.steps, pe.at(f"y{x - 2}"))
                        for f in range(F):
                            e.wait_ge(pe.steps, pe.at(f"u{x}{f}"))
                            e.activation(r[:, x % 2, f], k.ps[:, f, :], ACT.Relu).then_inc(act.steps, act.did(f"r{x}{f}"))

                @block.tensor
                def _(e):
                    def up(x):
                        for f in range(F):
                            if x:
                                e.wait_ge(act.steps, act.at(f"r{x - 1}{f}"))
                            e.matmul(k.ps[:, f, :], k.w["c_fc"][:, x, ts(f, C)], h[:], start=True, stop=True).then_inc(pe.steps, pe.did(f"u{x}{f}"))

                    def down(x):
                        e.wait_ge(dve.steps, dve.at(f"r{x}1"))
                        e.wait_ge(pool.steps, pool.at(f"r{x}3"))
                        if x >= 2:
                            e.wait_ge(dve.steps, dve.at(f"acc{x - 2}"))
                        for i in range(4):
                            for f in range(F):
                                ins = e.matmul(k.ps[:, 4 + x % 2, ts(i, C)], r[:, x % 2, f, ts(i, C)], k.w["c_proj"][:, x, f, :],
                                               start=(f == 0), stop=(f == F - 1))
                        ins.then_inc(pe.steps, pe.did(f"y{x}"))

                    e.wait_ge(pool.steps, pool.at("h"))
                    up(0)
                    for x in range(E):
                        if x + 1 < E:
                            up(x + 1)
                        down(x)
                    e.wait_ge(dve.steps, dve.at(f"acc{E - 1}"))
                    for i in range(4):
                        ins = e.transpose(k.ps[:, 6, ts(i, C)], acc[:, i, :], k.w["ident"][:])
                    ins.then_inc(pe.steps, pe.did("yT"))

                @block.vector
                def _(e):
                    e.tensor_copy(g[:], gates[:, bass.ds(b * 4, 4), :]).then_inc(dve.steps, dve.did())
                    e.tensor_copy(k.modb[:], k.mod[:, :, :, bass.ds(b, 1)].rearrange("p l s a -> p l (s a)")).then_inc(dve.steps, dve.did())
                    e.wait_ge(dve.steps, dve.n)

                    def gather(x):
                        e.wait_ge(pe.steps, pe.at(f"y{x}"))
                        for i in range(4):
                            y = k.ps[:, 4 + x % 2, ts(i, C)]
                            if x == 0:
                                e.tensor_scalar(acc[:, i, :], y, g[:, i, 0:1], None, ALU.mult).then_inc(dve.steps, dve.did(f"acc{x}"))
                            else:
                                e.scalar_tensor_tensor(acc[:, i, :], y, g[:, i, x:x + 1], acc[:, i, :],
                                                                ALU.mult, ALU.add).then_inc(dve.steps, dve.did(f"acc{x}"))
                    for x in range(E):
                        for f in range(2):
                            e.wait_ge(act.steps, act.at(f"r{x}{f}"))
                            e.tensor_tensor(r[:, x % 2, f], r[:, x % 2, f], r[:, x % 2, f], ALU.mult).then_inc(dve.steps, dve.did(f"r{x}{f}"))
                        if x:
                            gather(x - 1)
                            e.wait_ge(dve.steps, dve.n)
                    gather(E - 1)
                    e.wait_ge(pe.steps, pe.at("yT"))
                    xb = flat(k.X[:, bass.ds(b, 1), :])
                    e.scalar_tensor_tensor(xb, k.ps[:, 6, :], k.modb[:, 1, GB:GB + 1], xb, ALU.mult, ALU.add).then_inc(dve.steps, dve.did())
            k.end()


class Silu:

    def __init__(self, st, tag, psum, bias, out, tmp, ready):
        self.st, self.tag, self.psum, self.bias, self.out, self.tmp, self.ready = st, tag, psum, bias, out, tmp, ready

    def vector(self, e):
        pe, act, dve, pool, _ = self.st
        g, a = self.tag, self.tmp[:, 0, :]
        e.wait_ge(pe.steps, pe.at(self.ready))
        e.tensor_scalar(self.out, self.psum, self.bias, None, ALU.add).then_inc(dve.steps, dve.did())
        e.wait_ge(dve.steps, dve.n)
        e.tensor_scalar(a, self.out, LEAST, None, ALU.max).then_inc(dve.steps, dve.did(g + "z"))
        e.wait_ge(act.steps, act.at(g + "i"))
        e.tensor_tensor(self.out, self.out, a, ALU.mult).then_inc(dve.steps, dve.did(g + "o"))

    def scalar(self, e):
        pe, act, dve, pool, _ = self.st
        g, a = self.tag, self.tmp[:, 0, :]
        e.wait_ge(dve.steps, dve.at(g + "z"))
        e.activation(a, a, ACT.Exp, scale=-1.0).then_inc(act.steps, act.did())
        e.wait_ge(act.steps, act.n)
        e.activation(a, a, ACT.Ln, bias=1.0).then_inc(act.steps, act.did())
        e.wait_ge(act.steps, act.n)
        e.activation(a, a, ACT.Exp, scale=-1.0).then_inc(act.steps, act.did(g + "i"))


R, I = 1, 2
KI, KR = 0, 1
LOG_MIN = -19.0


def gla(k):
    nc = k.nc
    with ExitStack() as s:
        u = k.sb("g_u", [C, T], stack=s)
        y_first = k.sb("g_y_first", [C, 2, T], stack=s)
        mem_qk = k.sb("g_qk_Q0_K0_S2", [C, 12, T], stack=s)
        mem_unit = k.sb("g_unit_qh_y_S", [C, 6, T], stack=s)
        mem_cum = k.sb("g_cum_KT", [C, 4, T], stack=s)
        mem_U = k.sb("g_U_H", [C, 2, 3, T], stack=s)
        qk = mem_qk[:].rearrange("p (j r g) t -> p j r g t", j=3, r=2)
        unit = mem_unit[:].rearrange("p (r g) t -> p r g t", r=3)
        cum = mem_cum[:].rearrange("p (r g) t -> p r g t", r=2)
        U = lambda g: mem_U[:, g]
        m1, m2 = k.sb("g_m1", [C, 2, 2, T], stack=s), k.sb("g_m2", [C, 2, 2, T], stack=s)
        L = k.sb("g_L", [C, 2, T + 1], stack=s)
        one = k.sb("g_one", [C, 1], stack=s)
        qh = unit
        kh = k.sb("g_kh", [C, 2, 2, T], stack=s)[:]
        F, E = k.sb("g_F", [C, 4, 2, T], stack=s), k.sb("g_E", [C, 4, 2, T], stack=s)
        mem_F = F[:].rearrange("p a g t -> p (a g) t")
        tmp, h = mem_F[:, 0:3], mem_F[:, 3]
        xb, h2, o2 = (E[:, i, 1] for i in (3, 1, 2))
        Q = [mem_qk[:, 0:6].rearrange("p (r g) t -> p r g t", r=3)] + [k.sb(f"g_Q{i}", [C, 3, 2, T], stack=s) for i in (1, 2)]
        K = [mem_qk[:, 6:10].rearrange("p (r g) t -> p r g t", r=2)] + [k.sb(f"g_K{i}", [C, 2, 2, T], stack=s) for i in (1, 2)]
        products_over_blocks = lambda g: Q[1][:, 0, g, 0:198].rearrange("p (v r c) -> p v r c", v=2, r=3)
        qs, ks = m1, m2
        V = k.sb("g_V", [C, 4, 8, 96], stack=s)
        KT = lambda g: mem_cum[:].rearrange("p (r g) (i x) -> p g r i x", r=2, i=4)[:, g]
        H0 = k.sb("g_H0", [C, 2, 96], stack=s)

        def H(n, g):
            return H0[:, g] if n == 0 else mem_U[:, g].rearrange("p a t -> p (a t)")[:, 96 * (n - 1):96 * n]

        y = lambda g, pair: y_first[:, pair] if g == 0 else mem_unit[:, 2 * pair + 1]
        S = lambda g: mem_unit[:, 4 + g].rearrange("p (i h r t) -> p i h r t", i=2, h=4, r=2)
        S2 = lambda g: mem_qk[:, 10 + g, 0:256]
        P = [k.ps[:, i, :] for i in range(8)]
        halves = ((8, 1), (16, 2))
        blk = lambda ap, n: ap.rearrange("p (c x) -> p c x", x=n)
        m = k.modb[:, 2, :]

        def later(ap, n):
            return (ap, ap.rearrange("p r (c x) -> p r c x", c=2)[:, :, :, 8:16], ap[:, :, 16:32])[n]

        def half_of(ap, i, later_half):
            if i in (0, 3):
                return ap
            return blk(ap, 16 * i)[:, :, 8 * i:] if later_half else blk(ap, 16 * i)[:, :, :8 * i]

        ORDER = (("scores", 0), ("prepare", "norm"), ("gains", 0), ("prepare", "hidden"), ("scores", 1), ("prepare", "project"),
                 ("gains", 1), ("outputs", 0), ("prepare", "units"), ("scores", 2), ("prepare", "decays"), ("gains", 2),
                 ("outputs", 1), ("prepare", "running"), ("scores", 3), ("gains", 3), ("prepare", "blocks"), ("outputs", 2),
                 ("prepare", "turn"), ("outputs", 3), ("prepare", "split"), ("prepare", "keys"))

        def stage(name, scan_g, prep_b, prep_g):
            st = pe, act, dve, pool, dma = k.stage(name)
            g, sg = prep_g, scan_g
            tot = products_over_blocks(g) if g is not None else None
            n = Norm(k, st, "n", 6, 7, xb, h, m, SA, CA, tmp)
            act_u = Silu(st, "u", P[6], k.w["b_in2"][:, 0:1], u[:], tmp[:, 0:2], "z")
            products = [("c", j, ri) for j in range(3) for ri in range(2)] + [("v", i, 0) for i in range(4)]
            evacuated = lambda x: (act if products[x][0] == "c" else dve)

            def in_turn(scan, prepare):
                for what, which in ORDER:
                    if what == "prepare":
                        if prep_g is not None and (prep_g == 0 or which not in ("norm", "hidden")):
                            prepare(which)
                    elif scan_g is not None:
                        scan(what, which)

            with nc.Block() as block:
                @block.gpsimd
                def _(e):
                    def prepare(what):
                        if what == "norm":
                            e.tensor_copy(xb, flat(k.X[:, bass.ds(prep_b, 1), :])).then_inc(pool.steps, pool.did("xb"))
                        elif what == "units":
                            mag = F[:, 3, g]
                            e.wait_ge(dve.steps, dve.at("parts"))
                            e.tensor_tensor(m1[:, 0, g], qk[:, 2, 1, g], qk[:, 2, 1, g], ALU.mult).then_inc(pool.steps, pool.did("ai2"))
                            e.wait_ge(act.steps, act.at("rs"))
                            e.tensor_tensor(m2[:, 0, g], m1[:, 1, g], m1[:, 1, g], ALU.mult).then_inc(pool.steps, pool.did())
                            e.wait_ge(pool.steps, pool.n)
                            e.tensor_tensor(m2[:, 0, g], m2[:, 0, g], mag, ALU.mult).then_inc(pool.steps, pool.did())
                            e.wait_ge(pool.steps, pool.n)
                            e.tensor_scalar(m2[:, 0, g], m2[:, 0, g], -0.5, 1.5, ALU.mult, ALU.add).then_inc(pool.steps, pool.did())
                            e.wait_ge(pool.steps, pool.n)
                            e.tensor_tensor(m1[:, 1, g], m1[:, 1, g], m2[:, 0, g], ALU.mult).then_inc(pool.steps, pool.did("rs"))
                        elif what == "split":
                            e.wait_ge(dve.steps, dve.at("kh"))
                            e.wait_ge(act.steps, act.at("f2"))
                            for i in range(3):
                                for p_ in range(2):
                                    e.tensor_tensor(half_of(K[i][:, p_, g], i, False), half_of(kh[:, p_, g], i, False), half_of(E[:, i, g], i, False),
                                                    ALU.mult).then_inc(pool.steps, pool.did())

                    in_turn(lambda what, i: None, prepare)

                @block.tensor
                def _(e):
                    def scan(what, i):
                        odd = i % 2
                        if what == "scores":
                            if i >= 2:
                                e.wait_ge(dve.steps, dve.at(f"s{i - 2}"))
                                e.wait_ge(dve.steps, dve.at(f"h{i - 2}"))
                            for turn in range(4):
                                if turn:
                                    ins.then_inc(pe.steps, pe.did())
                                    e.wait_ge(pe.steps, pe.n)
                                for part, j, n_ in ((part, j, n_) for part in range(2) for j in range(4) for n_ in range(3)):
                                    h4 = (turn + n_ // 2) % 4
                                    t, r = slice(i * C + 32 * j, i * C + 32 * j + 32), ts(h4, 32)
                                    keys, planes = (K[n_][r, KR, sg, t], slice(1, 3)) if part == 0 else (K[n_][r, KI, sg, t], slice(0, 2))
                                    col = 64 * h4 + (256 if n_ == 1 else 0)
                                    scored = P[2 * odd + n_ // 2][ts(j, 32), col:col + 64].rearrange("p (r x) -> p r x", r=2)
                                    ins = e.matmul(later(scored, n_), keys, later(Q[n_][r, planes, sg, t], n_),
                                                   start=(turn == 0 and part == 0 and n_ != 1), stop=(part == 1),
                                                   tile_position=(32 * h4, 32 * j), skip_group_check=True)
                            ins.then_inc(pe.steps, pe.did(f"s{i}"))
                            e.wait_ge(pe.steps, pe.n)
                        elif what == "gains":
                            for j in range(4):
                                if j:
                                    ins.then_inc(pe.steps, pe.did())
                                    e.wait_ge(pe.steps, pe.n)
                                rows = ts(j, 32)
                                for part, h4 in ((part, h4) for part in range(2) for h4 in range(4)):
                                    ins = e.matmul(P[2 * odd + 1][ts(h4, 32), 256 + j * 64:320 + j * 64], KT(sg)[rows, (KR, KI)[part], i, ts(h4, 32)],
                                                   V[rows, i, 4 * sg + h4, (slice(32, 96), slice(0, 64))[part]], start=(part == 0), stop=(part == 1),
                                                   tile_position=(32 * j, 32 * h4))
                            ins.then_inc(pe.steps, pe.did(f"g{i}"))
                        else:
                            e.wait_ge(dve.steps, dve.at(f"s{i}"))
                            e.wait_ge(dve.steps, dve.at(f"h{i}"))
                            if i:
                                e.wait_ge(pe.steps, pe.at(f"y{i - 1}"))
                            for turn in range(4):
                                for part, second, bank in ((part, second, bank) for part in range(2) for second in range(2) for bank in range(2)):
                                    j, h4 = (turn + bank) % 4, 2 * bank + second
                                    rows, t = ts(j, 32), slice(i * C + 32 * j, i * C + 32 * j + 32)
                                    ins = e.matmul(P[4 + bank][ts(second, 64), t], V[rows, i, 4 * sg + h4, (slice(32, 96), slice(0, 64))[part]],
                                                   S(sg)[rows, i % 2, h4, part, :], start=(turn == 0 and part == 0), stop=False,
                                                   tile_position=(32 * j, 64 * second), skip_group_check=True)
                                ins.then_inc(pe.steps, pe.did())
                                e.wait_ge(pe.steps, pe.n)
                            for j, part, h4 in ((j, part, h4) for j in range(4) for part in range(2) for h4 in (0, 2, 1, 3)):
                                t = slice(i * C + 32 * j, i * C + 32 * j + 32)
                                ins = e.matmul(P[4 + h4 // 2][ts(h4 % 2, 64), t], H(4 * i + j, sg)[ts(h4, 32), (slice(32, 96), slice(0, 64))[part]],
                                               qs[ts(h4, 32), part, sg, t], start=False, stop=(part == 1),
                                               tile_position=(32 * h4, 64 * (h4 % 2)), skip_group_check=True)
                            ins.then_inc(pe.steps, pe.did(f"y{i}"))

                    def prepare(what):
                        if what == "norm":
                            e.wait_ge(pool.steps, pool.at("xb"))
                            n.tensor(e)
                        elif what == "hidden":
                            e.wait_ge(dve.steps, dve.at("nh"))
                            e.matmul(P[6], k.w["W_in2"][:], h, start=True, stop=True).then_inc(pe.steps, pe.did("z"))
                        elif what == "project":
                            if g == 0:
                                e.wait_ge(dve.steps, dve.at("uo"))
                            for x, (kind, j, ri) in enumerate(products):
                                if x >= 2:
                                    e.wait_ge(evacuated(x - 2).steps, evacuated(x - 2).at(f"p{x - 2}"))
                                if kind == "c":
                                    ins = e.matmul(P[6 + x % 2], k.w["W_qka"][:, j, ri, g, :], u[:], start=True, stop=True)
                                else:
                                    ins = e.matmul(P[6 + x % 2][:, 0:256], u[:, ts(j, C)], k.w["W_v2"][:, ts(g, 256)], start=True, stop=True)
                                ins.then_inc(pe.steps, pe.did(f"p{x}"))
                        elif what == "keys":
                            e.wait_ge(dve.steps, dve.at("ks"))
                            for r in range(2):
                                for i in range(4):
                                    ins = e.transpose(P[6 + r][:, ts(i, C)], ks[:, r, g, ts(i, C)], k.w["ident"][:])
                                ins.then_inc(pe.steps, pe.did(f"kt{r}"))

                    in_turn(scan, prepare)

                @block.scalar
                def _(e):
                    def prepare(what):
                        if what == "norm":
                            n.scalar(e)
                        elif what == "hidden":
                            act_u.scalar(e)
                        elif what == "project":
                            for x, (kind, j, ri) in enumerate(products):
                                if kind == "c":
                                    e.wait_ge(pe.steps, pe.at(f"p{x}"))
                                    e.activation(qk[:, j, ri, g], P[6 + x % 2], ACT.Identity, bias=k.w["b_qka"][:, j, ri, g:g + 1]).then_inc(act.steps, act.did(f"p{x}"))
                        elif what == "units":
                            lg, mag = E[:, 3, g], F[:, 3, g]
                            e.wait_ge(dve.steps, dve.at("mag"))
                            e.activation(lg, mag, ACT.Ln).then_inc(act.steps, act.did("ln"))
                            e.wait_ge(act.steps, act.n)
                            e.activation(F[:, 0, g], mag, ACT.Ln, bias=1.0).then_inc(act.steps, act.did("ln1"))
                            e.activation(m1[:, 1, g], lg, ACT.Exp, scale=-0.5).then_inc(act.steps, act.did("rs"))
                        elif what == "decays":
                            e.wait_ge(dve.steps, dve.at("d0"))
                            e.activation(E[:, 0, g], F[:, 0, g], ACT.Exp, scale=-1.0).then_inc(act.steps, act.did())
                            e.wait_ge(act.steps, act.n)
                            e.activation(F[:, 0, g], F[:, 0, g], ACT.Exp).then_inc(act.steps, act.did("f0"))
                            for i in (1, 2, 3):
                                e.wait_ge(dve.steps, dve.at(f"d{i}"))
                                e.activation(half_of(F[:, i, g], i, True), half_of(F[:, i, g], i, True), ACT.Exp).then_inc(act.steps, act.did())
                                e.activation(half_of(E[:, i, g], i, False), half_of(E[:, i, g], i, False), ACT.Exp).then_inc(act.steps, act.did(f"f{i}"))
                        elif what == "keys":
                            for r in range(2):
                                e.wait_ge(pe.steps, pe.at(f"kt{r}"))
                                e.activation(KT(g)[:, r], P[6 + r].rearrange("p (i x) -> p i x", i=4), ACT.Copy).then_inc(act.steps, act.did())

                    e.preload_act_table_set(EXP_LN)
                    in_turn(lambda what, i: None, prepare)
                    if sg is not None:
                        e.wait_ge(pe.steps, pe.at("y3"))
                        e.activation(y(sg, 1), P[5], ACT.Copy).then_inc(act.steps, act.did())

                @block.vector
                def _(e):
                    def sums(i):
                        e.wait_ge(pe.steps, pe.at(f"s{i}"))
                        if i >= 2:
                            e.wait_ge(pe.steps, pe.at(f"y{i - 2}"))
                        whole = lambda ap: ap.rearrange("p (a x) -> p a x", a=8)
                        s_ = whole(S(sg)[:, i % 2].rearrange("p h r t -> p (h r t)"))
                        t_ = whole(S2(sg))
                        msk = lambda n_: k.w["gla_mask"][:, n_:n_ + 1, :].to_broadcast([C, 8, 32])
                        bank = P[2 * (i % 2)]
                        e.tensor_tensor(s_, whole(bank[:, 0:256]), msk(0), ALU.mult).then_inc(dve.steps, dve.did())
                        e.tensor_tensor(later(t_, 1), later(whole(bank[:, 256:512]), 1), later(msk(1), 1), ALU.mult).then_inc(dve.steps, dve.did())
                        e.wait_ge(dve.steps, dve.n)
                        e.tensor_tensor(later(s_, 1), later(s_, 1), later(t_, 1), ALU.add).then_inc(dve.steps, dve.did())
                        e.wait_ge(dve.steps, dve.n)
                        e.wait_ge(pe.steps, pe.at(f"g{i}"))
                        e.tensor_tensor(later(s_, 2), later(s_, 2), later(whole(P[2 * (i % 2) + 1][:, 0:256]), 2), ALU.add).then_inc(dve.steps, dve.did(f"s{i}"))

                    def states(i):
                        e.wait_ge(pe.steps, pe.at(f"g{i}"))
                        for j in range(4):
                            c_ = 4 * i + j
                            new, end = H(c_ + 1, sg), 32 * c_ + 31
                            e.scalar_tensor_tensor(new[:, 32:96], H(c_, sg)[:, 32:96], F[:, 3, sg, end:end + 1],
                                                   P[2 * (i % 2) + 1][:, 256 + j * 64:320 + j * 64], ALU.mult, ALU.add).then_inc(dve.steps, dve.did())
                            e.wait_ge(dve.steps, dve.n)
                            e.tensor_scalar(new[:, 0:32], new[:, 64:96], -1.0, None, ALU.mult).then_inc(dve.steps, dve.did(f"h{i}"))

                    def scan(what, i):
                        if what == "scores" and i:
                            sums(i - 1)
                        elif what == "gains" and i:
                            states(i - 1)
                        elif what == "outputs" and i == 2:
                            sums(3)
                            states(3)

                    def prepare(what):
                        if what == "norm":
                            e.tensor_copy(k.modb[:], k.mod[:, :, :, bass.ds(prep_b, 1)].rearrange("p l s a -> p l (s a)")).then_inc(dve.steps, dve.did())
                            e.wait_ge(dve.steps, dve.n)
                            n.vector(e)
                        elif what == "hidden":
                            act_u.vector(e)
                        elif what == "project":
                            for x, (kind, i, _) in enumerate(products):
                                if kind == "v":
                                    e.wait_ge(pe.steps, pe.at(f"p{x}"))
                                    e.tensor_tensor(V[:, i, ts(g, 4), 32:96], P[6 + x % 2][:, 0:256].rearrange("p (h x) -> p h x", h=4),
                                                    k.w["b_v2"][:, ts(g, 256)].rearrange("p (h x) -> p h x", h=4), ALU.add).then_inc(dve.steps, dve.did(f"p{x}"))
                            e.wait_ge(dve.steps, dve.n)
                            e.tensor_scalar(V[:, :, ts(g, 4), 0:32], V[:, :, ts(g, 4), 64:96], -1.0, None, ALU.mult).then_inc(dve.steps, dve.did())
                            e.wait_ge(act.steps, act.at("p5"))
                            e.tensor_tensor(F[:, 3, g], qk[:, 2, 0, g], qk[:, 2, 0, g], ALU.mult).then_inc(dve.steps, dve.did("parts"))
                        elif what == "units":
                            lg, mag = E[:, 3, g], F[:, 3, g]
                            e.wait_ge(pool.steps, pool.at("ai2"))
                            e.wait_ge(dve.steps, dve.at("parts"))
                            e.tensor_tensor(mag, mag, m1[:, 0, g], ALU.add).then_inc(dve.steps, dve.did())
                            e.wait_ge(dve.steps, dve.n)
                            e.tensor_scalar(mag, mag, 1e-18, None, ALU.max).then_inc(dve.steps, dve.did("mag"))
                            e.wait_ge(act.steps, act.at("rs"))
                            e.tensor_tensor(lg, lg, F[:, 0, g], ALU.subtract).then_inc(dve.steps, dve.did("lg"))
                        elif what == "decays":
                            lg = E[:, 3, g]
                            e.wait_ge(act.steps, act.at("rs"))
                            e.wait_ge(dve.steps, dve.at("lg"))
                            e.tensor_scalar(lg, lg, LOG_MIN, None, ALU.max).then_inc(dve.steps, dve.did())
                            e.wait_ge(pool.steps, pool.at("rs"))
                            for plane in (R, I):
                                e.tensor_tensor(unit[:, plane, g], qk[:, 2, plane - 1, g], m1[:, 1, g], ALU.mult).then_inc(dve.steps, dve.did())
                            e.wait_ge(dve.steps, dve.n)
                            e.tensor_scalar(unit[:, 0, g], unit[:, I, g], -1.0, None, ALU.mult).then_inc(dve.steps, dve.did())
                            e.tensor_tensor_scan(L[:, g, 1:], one[:].to_broadcast([C, T]), lg, 0.0, ALU.mult, ALU.add).then_inc(dve.steps, dve.did())
                            e.wait_ge(dve.steps, dve.n)
                            Lt = L[:, g, 1:]
                            l8 = blk(Lt, 8)
                            e.tensor_tensor(blk(F[:, 0, g], 8), l8, l8[:, :, 3:4].to_broadcast([C, 64, 8]), ALU.subtract).then_inc(dve.steps, dve.did("d0"))
                            for half, i in halves:
                                l2 = blk(Lt, 2 * half)
                                mid = l2[:, :, half - 1:half].to_broadcast([C, T // (2 * half), half])
                                e.tensor_tensor(half_of(F[:, i, g], i, True), l2[:, :, half:], mid, ALU.subtract).then_inc(dve.steps, dve.did())
                                e.tensor_tensor(half_of(E[:, i, g], i, False), mid, l2[:, :, :half], ALU.subtract).then_inc(dve.steps, dve.did(f"d{i}"))
                            l32 = blk(Lt, 32)
                            before = blk(L[:, g, 0:T], 32)[:, :, 0:1].to_broadcast([C, 16, 32])
                            e.tensor_tensor(blk(F[:, 3, g], 32), l32, before, ALU.subtract).then_inc(dve.steps, dve.did())
                            e.tensor_tensor(blk(E[:, 3, g], 32), l32[:, :, 31:32].to_broadcast([C, 16, 32]), l32, ALU.subtract).then_inc(dve.steps, dve.did("d3"))
                        elif what == "running":
                            cb = cum[:, :, g].rearrange("p r (c x) -> p r c x", x=16)
                            ub = unit[:, :, g].rearrange("p r (c x) -> p r c x", x=16)
                            A1 = m1[:, 0, g, 0:64].rearrange("p (r c) -> p r c", r=2)
                            A2 = m2[:, 0, g, 0:64].rearrange("p (r c) -> p r c", r=2)
                            e.tensor_copy(cb[:, :, :, 0], ub[:, 1:3, :, 0]).then_inc(dve.steps, dve.did())
                            for x in range(1, 16):
                                e.wait_ge(dve.steps, dve.n)
                                e.tensor_tensor(A1, cb[:, 0:1, :, x - 1].to_broadcast([C, 2, 32]), ub[:, 1:3, :, x], ALU.mult).then_inc(dve.steps, dve.did())
                                e.tensor_tensor(A2, cb[:, 1:2, :, x - 1].to_broadcast([C, 2, 32]), ub[:, 0:2, :, x], ALU.mult).then_inc(dve.steps, dve.did())
                                e.wait_ge(dve.steps, dve.n)
                                e.tensor_tensor(cb[:, :, :, x], A1, A2, ALU.add).then_inc(dve.steps, dve.did())
                        elif what == "blocks":
                            e.memset(tot[:, :, 0::2, 0:1], 0.0).then_inc(dve.steps, dve.did())
                            e.memset(tot[:, :, 1, 0:1], 1.0).then_inc(dve.steps, dve.did())
                            e.wait_ge(dve.steps, dve.n)
                            last = cum[:, :, g].rearrange("p r (c x) -> p r c x", x=16)[:, :, :, 15]
                            e.tensor_copy(tot[:, 0, 1:3, 1:33], last).then_inc(dve.steps, dve.did())
                            e.wait_ge(dve.steps, dve.n)
                            e.tensor_scalar(tot[:, 0, 0, 1:33], tot[:, 0, 2, 1:33], -1.0, None, ALU.mult).then_inc(dve.steps, dve.did())
                            e.wait_ge(dve.steps, dve.n)
                            src, d = 0, 1
                            while d < 32:
                                c_ = 32 - d
                                B1 = m1[:, 0, g, 0:2 * c_].rearrange("p (r c) -> p r c", r=2)
                                B2 = m2[:, 0, g, 0:2 * c_].rearrange("p (r c) -> p r c", r=2)
                                old, new = tot[:, src], tot[:, 1 - src]
                                e.tensor_tensor(B1, old[:, 1:2, 1:1 + c_].to_broadcast([C, 2, c_]), old[:, 1:3, 1 + d:33], ALU.mult).then_inc(dve.steps, dve.did())
                                e.tensor_tensor(B2, old[:, 2:3, 1:1 + c_].to_broadcast([C, 2, c_]), old[:, 0:2, 1 + d:33], ALU.mult).then_inc(dve.steps, dve.did())
                                e.tensor_copy(new[:, :, 1:1 + d], old[:, :, 1:1 + d]).then_inc(dve.steps, dve.did())
                                e.wait_ge(dve.steps, dve.n)
                                e.tensor_tensor(new[:, 1:3, 1 + d:33], B1, B2, ALU.add).then_inc(dve.steps, dve.did())
                                e.wait_ge(dve.steps, dve.n)
                                e.tensor_scalar(new[:, 0, 1 + d:33], new[:, 2, 1 + d:33], -1.0, None, ALU.mult).then_inc(dve.steps, dve.did())
                                e.wait_ge(dve.steps, dve.n)
                                src, d = 1 - src, 2 * d
                        elif what == "turn":
                            w = lambda ap: ap.rearrange("p r (c x) -> p r c x", x=16)
                            pre = lambda lo: tot[:, 1, lo:lo + 2, 0:32].unsqueeze(3).to_broadcast([C, 2, 32, 16])
                            e.tensor_tensor(w(m1[:, :, g]), w(cum[:, 0:1, g].to_broadcast([C, 2, T])), pre(1), ALU.mult).then_inc(dve.steps, dve.did())
                            e.tensor_tensor(w(m2[:, :, g]), w(cum[:, 1:2, g].to_broadcast([C, 2, T])), pre(0), ALU.mult).then_inc(dve.steps, dve.did())
                            e.wait_ge(dve.steps, dve.n)
                            e.tensor_tensor(U(g)[:, 1:3], m1[:, :, g], m2[:, :, g], ALU.add).then_inc(dve.steps, dve.did())
                            e.wait_ge(dve.steps, dve.n)
                            e.tensor_scalar(U(g)[:, 0], U(g)[:, 2], -1.0, None, ALU.mult).then_inc(dve.steps, dve.did())
                            e.wait_ge(dve.steps, dve.n)
                            for j, out, (p1, p2), name_ in ((0, qh[:, 1:3, g], (1, 0), "qh"), (1, kh[:, :, g], (0, 1), "kh")):
                                wide = lambda ri: qk[:, j, ri:ri + 1, g].to_broadcast([C, 2, T])
                                e.tensor_tensor(m1[:, :, g], wide(0), U(g)[:, p1:p1 + 2], ALU.mult).then_inc(dve.steps, dve.did())
                                e.tensor_tensor(m2[:, :, g], wide(1), U(g)[:, p2:p2 + 2], ALU.mult).then_inc(dve.steps, dve.did())
                                e.wait_ge(dve.steps, dve.n)
                                e.tensor_tensor(out, m1[:, :, g], m2[:, :, g], ALU.add).then_inc(dve.steps, dve.did(name_))
                                e.wait_ge(dve.steps, dve.n)
                            e.tensor_scalar(qh[:, 0, g], qh[:, 2, g], -1.0, None, ALU.mult).then_inc(dve.steps, dve.did())
                            e.wait_ge(dve.steps, dve.n)
                        elif what == "split":
                            e.wait_ge(act.steps, act.at("f3"))
                            for p_ in range(2):
                                e.tensor_tensor(ks[:, p_, g], kh[:, p_, g], E[:, 3, g], ALU.mult).then_inc(dve.steps, dve.did("ks"))
                            for i in range(3):
                                for p_ in range(3):
                                    e.tensor_tensor(half_of(Q[i][:, p_, g], i, True), half_of(qh[:, p_, g], i, True), half_of(F[:, i, g], i, True),
                                                    ALU.mult).then_inc(dve.steps, dve.did())
                            for p_ in range(2):
                                e.tensor_tensor(qs[:, p_, g], qh[:, 1 + p_, g], F[:, 3, g], ALU.mult).then_inc(dve.steps, dve.did())

                    in_turn(scan, prepare)
                    if sg is not None:
                        e.wait_ge(pe.steps, pe.at("y3"))
                        e.tensor_copy(y(sg, 0), P[4]).then_inc(dve.steps, dve.did())
            k.end()

        def out(name, b):
            st = pe, act, dve, pool, dma = k.stage(name)
            act_y = Silu(st, "y", P[0], k.w["b_y2"][:, 0:1], h2, tmp[:, 0:2], "z")
            with nc.Block() as block:
                @block.tensor
                def _(e):
                    for i in range(4):
                        ins = e.matmul(P[0], k.w["W_y2"][:, i, :], y(i // 2, i % 2), start=(i == 0), stop=(i == 3))
                    ins.then_inc(pe.steps, pe.did("z"))
                    e.wait_ge(dve.steps, dve.at("yo"))
                    e.matmul(P[1], k.w["W_out2"][:], h2, start=True, stop=True).then_inc(pe.steps, pe.did("o"))

                @block.scalar
                def _(e):
                    e.preload_act_table_set(EXP_LN)
                    act_y.scalar(e)
                    e.wait_ge(pe.steps, pe.at("o"))
                    e.activation(o2, P[1], ACT.Identity, bias=k.w["b_out2"][:, 0:1]).then_inc(act.steps, act.did("o"))

                @block.vector
                def _(e):
                    e.tensor_copy(k.modb[:], k.mod[:, :, :, bass.ds(b, 1)].rearrange("p l s a -> p l (s a)")).then_inc(dve.steps, dve.did())
                    act_y.vector(e)
                    e.wait_ge(act.steps, act.at("o"))
                    x = flat(k.X[:, bass.ds(b, 1), :])
                    e.scalar_tensor_tensor(x, o2, m[:, GA:GA + 1], x, ALU.mult, ALU.add).then_inc(dve.steps, dve.did())
            k.end()

        pe, act, dve, pool, dma = k.stage("gla_start")
        with nc.Block() as block:
            @block.vector
            def _(e):
                for t in (one, L):
                    e.memset(t[:], 1.0 if t is one else 0.0).then_inc(dve.steps, dve.did())
                for t in (K[1], K[2]):
                    e.memset(t[:], 0.0).then_inc(dve.steps, dve.did())
                e.tensor_copy(H0[:, :, 32:96], k.w["h0"][:]).then_inc(dve.steps, dve.did())
                e.tensor_scalar(H0[:, :, 0:32], k.w["h0"][:, :, 32:64], -1.0, None, ALU.mult).then_inc(dve.steps, dve.did())
        k.end()
        stage("gla_first", None, 0, 0)
        with nc.Fori(0, B - 1) as b:
            stage("gla_scan0", 0, b, 1)
            stage("gla_scan1", 1, b + 1, 0)
            out("gla_out", b)
        stage("gla_scan0_last", 0, B - 1, 1)
        stage("gla_scan1_last", 1, None, None)
        out("gla_out_last", B - 1)


def routed_mlp(k):
    nc = k.nc
    with ExitStack() as s:
        lanes = lambda name, shape: [k.sb(f"m_{name}{l}", shape, stack=s) for l in range(2)]
        xb, h, tmp, masked, modb = (lanes(name, shape) for name, shape in
                                    (("xb", [C, T]), ("h", [C, T]), ("tmp", [C, 3, T]), ("masked", [C, 2, T]), ("modb", [C, 4, 6])))
        r = k.sb("m_r", [C, 4, T], stack=s)
        dw = k.sb("m_dw", [C, 1], stack=s)
        gate = k.sb("m_gate", [C, C], stack=s)
        bias = k.sb("m_bias", [C, 1], stack=s)
        P = [k.ps[:, i, :] for i in range(8)]
        pe, act, dve, pool, dma = k.stage("mlp2_start")
        with nc.Block() as block:
            @block.vector
            def _(e):
                e.tensor_tensor(dw[:], k.w["gate_w2"][:, 1:2], k.w["gate_w2"][:, 0:1], ALU.subtract).then_inc(dve.steps, dve.did())
                e.tensor_reduce(bias[:], k.w["b2_2"][:], AX.X, ALU.add).then_inc(dve.steps, dve.did())
                e.wait_ge(dve.steps, dve.n)
                e.tensor_copy(gate[:], dw[:, 0:1].to_broadcast([C, C])).then_inc(dve.steps, dve.did())
        k.end()
        with nc.Fori(0, B // 2) as pair:
            st = pe, act, dve, pool, dma = k.stage("mlp2")
            batch = lambda l: bass.ds(pair * 2 + l, 1)
            m = [modb[l][:, 2, :] for l in range(2)]
            n = [Norm(k, st, f"n{l}", 3 * l, 3 * l + 1, xb[l][:], h[l][:], m[l], SB_, CB, tmp[l]) for l in range(2)]
            scores, total = (lambda l: P[3 * l + 2]), (lambda l: P[6 + l])
            hidden = lambda i: P[(0, 1, 3, 4)[i % 4]]
            order = [(l, p_, f) for l in range(2) for p_ in (2, 0, 1) for f in range(4)]
            with nc.Block() as block:
                @block.gpsimd
                def _(e):
                    for l in range(2):
                        e.tensor_copy(xb[l][:], flat(k.X[:, batch(l), :])).then_inc(pool.steps, pool.did(f"xb{l}"))

                @block.tensor
                def _(e):
                    def down(i):
                        l, p_, f = order[i]
                        e.wait_ge(act.steps, act.at(f"r{i}"))
                        e.matmul(total(l), k.w["w2_2"][:, p_, f, :], r[:, i % 4, :], start=(i % 12 == 0), stop=(i % 12 == 11)).then_inc(pe.steps, pe.did(f"d{i}"))

                    for l in range(2):
                        e.wait_ge(pool.steps, pool.at(f"xb{l}"))
                        n[l].tensor(e)
                    for l in range(2):
                        e.wait_ge(dve.steps, dve.at(f"n{l}h"))
                        e.matmul(scores(l), gate[:], h[l][:], start=True, stop=True).then_inc(pe.steps, pe.did(f"score{l}"))
                    for i, (l, p_, f) in enumerate(order):
                        if i >= 4:
                            e.wait_ge(act.steps, act.at(f"r{i - 4}"))
                        if p_ < 2:
                            e.wait_ge(dve.steps, dve.at(f"m{l}{p_}"))
                        x = h[l][:] if p_ == 2 else masked[l][:, p_, :]
                        e.matmul(hidden(i), k.w["w1_2"][:, p_, ts(f, C)], x, start=True, stop=True).then_inc(pe.steps, pe.did(f"u{i}"))
                        if i >= 2:
                            down(i - 2)
                    down(22)
                    down(23)

                @block.scalar
                def _(e):
                    e.preload_act_table_set(EXP_LN)
                    for l in range(2):
                        n[l].scalar(e)
                    for i, (l, p_, f) in enumerate(order):
                        e.wait_ge(pe.steps, pe.at(f"u{i}"))
                        if i >= 4:
                            e.wait_ge(pe.steps, pe.at(f"d{i - 4}"))
                        e.activation(r[:, i % 4, :], hidden(i), ACT.Relu, bias=k.w["b1_2"][:, p_, f:f + 1]).then_inc(act.steps, act.did(f"r{i}"))

                @block.vector
                def _(e):
                    for l in range(2):
                        e.tensor_copy(modb[l][:], k.mod[:, :, :, batch(l)].rearrange("p l s a -> p l (s a)")).then_inc(dve.steps, dve.did())
                    e.wait_ge(dve.steps, dve.n)
                    for l in range(2):
                        n[l].vector(e)
                    for l in range(2):
                        e.wait_ge(pe.steps, pe.at(f"score{l}"))
                        e.wait_ge(dve.steps, dve.at(f"n{l}h"))
                        for x, op in ((0, ALU.is_le), (1, ALU.is_gt)):
                            e.scalar_tensor_tensor(masked[l][:, x, :], scores(l), 0.0, h[l][:], op, ALU.mult).then_inc(dve.steps, dve.did(f"m{l}{x}"))
                    for l in range(2):
                        e.wait_ge(pe.steps, pe.at(f"d{12 * l + 11}"))
                        e.tensor_scalar(h[l][:], total(l), bias[:, 0:1], None, ALU.add).then_inc(dve.steps, dve.did())
                        e.wait_ge(dve.steps, dve.n)
                        e.scalar_tensor_tensor(flat(k.X[:, batch(l), :]), h[l][:], m[l][:, GB:GB + 1], xb[l][:], ALU.mult, ALU.add).then_inc(dve.steps, dve.did())
            k.end()


def delta_rule(k):
    nc = k.nc
    TAPS, NH, NT = 4, 8, 4
    with ExitStack() as s:
        w_qk = k.sb("d_w_qk", [C, TAPS, 2, 8 * C], stack=s)
        w_v = k.sb("d_w_v", [C, TAPS, 256], stack=s)
        neg_a = k.sb("d_neg_a", [C, NH], stack=s)
        xb = k.sb("d_xb", [C, T], stack=s)
        hp = k.sb("d_hp", [C, T + 3], stack=s)
        QK = k.sb("d_QK", [C, 2, NH, T], stack=s)
        KT = k.sb("d_KT", [C, NT, NH, C], stack=s)
        VG = k.sb("d_values_gates", [C, 2, NT, 256], stack=s)
        V, G = VG[:, 0], VG[:, 1]
        O = k.sb("d_O", [C, NT, NH, 32], stack=s)
        sq = k.sb("d_sq", [C, 2, 2, T], stack=s)
        small = {n: k.sb("d_" + n, [C, NT, NH], stack=s) for n in
                 ("beta", "z", "g", "t", "gc", "gam", "end", "ga", "qn", "kn", "gtot", "n2", "ss", "sp", "eq", "ek")}
        ssq = k.sb("d_ssq", [C, 2, NT, NH], stack=s)
        S = k.sb("d_S", [C, NH, 32], stack=s)
        D = k.sb("d_D", [C, 2, 4, C], stack=s)
        A, Pm = (k.sb("d_" + n, [C, 6, 4, C], stack=s) for n in ("A", "P"))
        M = k.sb("d_M", [C, 4, 5, 4, 32], stack=s)
        A32, Y = (k.sb("d_" + n, [C, 4, 4, 32], stack=s) for n in ("A32", "Y"))
        F, X, W = (k.sb("d_" + n, [C, 2, 4, 32], stack=s) for n in ("F", "X", "W"))
        rv, zz, ze, o1 = (k.sb("d_" + n, [C, 2, 4, 32], stack=s) for n in ("r", "zz", "ze", "o1"))
        P = [k.ps[:, i, :] for i in range(8)]
        m = k.modb[:, 3, :]

        pe, act, dve, pool, dma = k.stage("delta_start")
        with nc.Block() as block:
            @block.scalar
            def _(e):
                e.activation(neg_a[:], k.w["A_log"][:], ACT.Exp).then_inc(act.steps, act.did("a"))

            @block.vector
            def _(e):
                e.memset(hp[:, 0:3], 0.0).then_inc(dve.steps, dve.did())
                for j in range(TAPS):
                    e.tensor_tensor(w_v[:, j], k.w["Wv3"][:], k.w["conv_v"][:, j], ALU.mult).then_inc(dve.steps, dve.did())
                e.wait_ge(act.steps, act.at("a"))
                e.tensor_scalar(neg_a[:], neg_a[:], -1.0, None, ALU.mult).then_inc(dve.steps, dve.did())
        k.end()
        taps = QK[:].rearrange("p c h t -> p (c h t)")[:, 0:TAPS * 8 * C].rearrange("p (j f) -> p j f", j=TAPS)
        for n in range(2):
            pe, act, dve, pool, dma = k.stage(f"delta_taps{n}")
            with nc.Block() as block:
                @block.sync
                def _(e):
                    src = k.dram["conv_qk"][n].rearrange("(a j) f -> a j f", a=1)
                    e.dma_start(taps, src.to_broadcast([C, TAPS, 8 * C])).then_inc(dma.steps, dma.did("taps"))

                @block.vector
                def _(e):
                    e.wait_ge(dma.steps, dma.at("taps"))
                    for j in range(TAPS):
                        e.tensor_tensor(w_qk[:, j, n], k.w["Wqk3"][:, n], taps[:, j], ALU.mult).then_inc(dve.steps, dve.did())
            k.end()

        f4 = lambda ap: ap.rearrange("p h t -> p (h t)")
        v4 = lambda ap: ap.rearrange("p (h t) -> p h t", h=4)
        p32 = lambda bank: v4(P[bank][:, 0:128])
        p_inv = lambda step, u: p32(4 * u + (1 if step == "y" else 0))
        INVERT = [("x", 0)] + [(step, l) for l in range(1, 5) for step in "fxy" if (step, l) != ("x", 4)]
        SOLVE = [("state", 0), ("solve", 0)] + [(step, j) for j in range(1, 4) for step in ("before", "solve")] + [("finish", 0)]
        MAKE = {0: 0, 3: 1, 6: 2}
        TURNS = (NT + 1) * len(INVERT)
        PIECES = [("norm", 0), ("small", 0), ("gate", 0), ("values", 0), ("gate", 1), ("values", 1), ("gate", 2), ("values", 2), ("gate", 3),
                  ("gate", 4), ("finish", 0), ("values", 3), ("finish", 1), ("finish", 2)]
        for run in range(4, 12):
            PIECES += [("first_taps", run - 4), ("last_taps", run - 4), ("finish", run - 1)]
            PIECES += [("squares", run - 7)] if run >= 7 else []
        PIECES += [("finish", 11), ("squares", 5), ("squares", 6), ("squares", 7)]
        PIECES += [("norms", 0), ("norms", 1), ("norms", 2)] + [("keys", i) for i in range(NT)]

        def stage(name, sg, pb, g):
            st = pe, act, dve, pool, dma = k.stage(name)
            q = small
            norm_tmp = A[:].rearrange("p (a x) h t -> p x a (h t)", x=2)[:, 0]
            norm = Norm(k, st, "n", 0, 1, xb[:], hp[:, 3:], m, SA, CA, norm_tmp)
            hs = slice(4 * (g or 0), 4 * (g or 0) + 4)
            four = lambda name_: q[name_][:, :, hs]
            run_bank = lambda run: P[4 * g + (0, 1, 3)[run % 3]]
            few = P[4 * g + 2] if g is not None else None
            made = lambda x: VG[:, :, x, ts(g, 128)] if x < 4 else QK[:, x % 2, 4 * g + (x - 4) // 2]
            products = lambda x: run_bank(x)[:, 0:256].rearrange("p (v x) -> p v x", v=2) if x < 4 else run_bank(x)
            pieces = [] if g is None else PIECES[0 if g == 0 else 1:]

            def in_turn(make, invert, solve, prepare):
                begun = 0
                if sg is not None:
                    for part in range(3):
                        make(sg, part)
                        if begun < len(pieces):
                            prepare(*pieces[begun])
                            begun += 1
                    for i in range(NT + 1):
                        for turn, (step, l) in enumerate(INVERT):
                            if i and turn < len(SOLVE):
                                solve(2 * (i - 1) + sg, *SOLVE[turn])
                            if i + 1 < NT and turn in MAKE:
                                make(2 * (i + 1) + sg, MAKE[turn])
                            if i < NT:
                                invert(2 * i + sg, step, l)
                            while begun < len(pieces) and begun * (TURNS - 18) <= len(pieces) * (i * len(INVERT) + turn):
                                prepare(*pieces[begun])
                                begun += 1
                for piece in pieces[begun:]:
                    prepare(*piece)

            with nc.Block() as block:
                @block.tensor
                def _(e):
                    def make(n, part):
                        i, u = n // 2, n % 2
                        t = ts(i, C)
                        if part == 0:
                            if n >= 2:
                                e.wait_ge(dve.steps, dve.at(f"A{n - 2}"))
                            for h in range(4):
                                H = 4 * u + h
                                ins = e.matmul(P[4 * u + 2][:, ts(h, C)], q["g"][:, i, H:H + 1].to_broadcast([C, C]), k.w["upto3"][:], start=True, stop=True)
                            ins.then_inc(pe.steps, pe.did(f"gb{n}"))
                        else:
                            e.wait_ge(dve.steps, dve.at((f"d{n}", f"P{n}")[part - 1]))
                            for h in range(4):
                                H = 4 * u + h
                                ins = e.matmul(P[4 * u + 2][:, ts(h, C)], QK[:, 1, H, t], QK[:, part - 1, H, t], start=True, stop=True)
                            ins.then_inc(pe.steps, pe.did((f"kq{n}", f"kk{n}")[part - 1]))

                    def products(step, stationary, moving, u):
                        for h in range(4):
                            for j in range(4):
                                rows = ts(j, 32)
                                ins = e.matmul(p_inv(step, u)[rows, h], stationary[rows, h], moving(rows, h), start=True, stop=True,
                                               tile_position=(32 * j, 32 * j))
                        return ins

                    def invert(n, step, l):
                        u = n % 2
                        if l == 0:
                            e.wait_ge(pool.steps, pool.at(f"c0{n}"))
                            products("x", M[:, n % 4, 0], lambda rows, h: k.w["eye32"][rows], u).then_inc(pe.steps, pe.did(f"x0{n}"))
                        elif step == "f":
                            if l == 1:
                                e.wait_ge(pool.steps, pool.at(f"c1{n}"))
                            e.wait_ge(dve.steps, dve.at(f"x{l - 1}{n}"))
                            products("f", M[:, n % 4, l], lambda rows, h: X[rows, u, h], u).then_inc(pe.steps, pe.did(f"f{l}{n}"))
                        elif step == "x":
                            e.wait_ge(act.steps, act.at(f"f{l}{n}"))
                            e.wait_ge(dve.steps, dve.at(f"y{l - 1}{n}"))
                            products("x", Y[:, n % 4], lambda rows, h: F[rows, u, h], u).then_inc(pe.steps, pe.did(f"x{l}{n}"))
                        else:
                            e.wait_ge(act.steps, act.at(f"f{l}{n}"))
                            e.wait_ge(dve.steps, dve.at(f"y{l - 1}{n}"))
                            products("y", F[:, u], lambda rows, h: Y[rows, n % 4, h], u).then_inc(pe.steps, pe.did(f"y{l}{n}"))

                    def solve(n, step, j):
                        i, u, rows = n // 2, n % 2, ts(j, 32)
                        if step == "state":
                            if n >= 2:
                                e.wait_ge(dve.steps, dve.at(f"out{n - 2}"))
                            for bank_half, c in ((0, 1), (1, 0)):
                                for h in range(4):
                                    H = 4 * u + h
                                    ins = e.matmul(P[4 * u + 3][:, bank_half * 128 + 32 * h:bank_half * 128 + 32 * h + 32], QK[:, c, H, ts(i, C)],
                                                   S[:, H], start=True, stop=True)
                            ins.then_inc(pe.steps, pe.did(f"s{n}"))
                        elif step == "before":
                            e.wait_ge(dve.steps, dve.at(f"w{j - 1}{n}"))
                            for h in range(4):
                                ins = e.matmul(P[4 * u + 3][rows, ts(h, 32)], A[:, n % 6, h, rows], W[:, u, h], start=True, stop=True,
                                               tile_position=(0, 32 * j))
                            ins.then_inc(pe.steps, pe.did(f"b{j}{n}"))
                        elif step == "solve":
                            e.wait_ge(dve.steps, dve.at(f"y4{n}"))
                            e.wait_ge(dve.steps, dve.at(f"r{j}{n}"))
                            for h in range(4):
                                ins = e.matmul(P[4 * u + 3][rows, 256 + 32 * h:288 + 32 * h], Y[rows, n % 4, h], rv[rows, u, h], start=True,
                                               stop=True, tile_position=(32 * j, 32 * j))
                            ins.then_inc(pe.steps, pe.did(f"w{j}{n}"))
                        else:
                            e.wait_ge(dve.steps, dve.at(f"z{n}"))
                            for h in range(4):
                                ins = e.matmul(P[4 * u + 3][:, 384 + 32 * h:416 + 32 * h], Pm[:, n % 6, h], zz[:, u, h], start=True, stop=True)
                            for h in range(4):
                                ins = e.matmul(P[4 * u + 3][:, 256 + 32 * h:288 + 32 * h], KT[:, i, 4 * u + h], ze[:, u, h], start=True, stop=True)
                            ins.then_inc(pe.steps, pe.did(f"o{n}"))

                    def prepare(what, x):
                        def free(run):
                            if run >= 3:
                                e.wait_ge(act.steps, act.at(f"p_run{run - 3}"))

                        if what == "norm":
                            e.wait_ge(pool.steps, pool.at("p_xb"))
                            norm.tensor(e)
                        elif what == "small":
                            if g == 0:
                                e.wait_ge(dve.steps, dve.at("nh"))
                            for i in range(NT):
                                ins = e.matmul(few[:, ts(i, 16)], hp[:, 3 + i * C:3 + i * C + C], k.w["Wab3"][:], start=True, stop=True)
                            ins.then_inc(pe.steps, pe.did("p_ab"))
                        elif what == "values":
                            free(x)
                            cols = ts(g, 128)
                            for j in range(TAPS):
                                e.matmul(run_bank(x)[:, 0:128], hp[:, j + x * C:j + x * C + C], w_v[:, j, cols], start=(j == 0), stop=(j == TAPS - 1))
                            e.matmul(run_bank(x)[:, 128:256], hp[:, 3 + x * C:3 + x * C + C], k.w["Wg3"][:, cols], start=True,
                                     stop=True).then_inc(pe.steps, pe.did(f"p_run{x}"))
                        elif what in ("first_taps", "last_taps"):
                            run, c, H = 4 + x, x % 2, 4 * g + x // 2
                            if what == "first_taps":
                                free(run)
                            for j in ((0, 1) if what == "first_taps" else (2, 3)):
                                ins = e.matmul(run_bank(run), w_qk[:, j, c, ts(H, C)], hp[:, j:j + T], start=(j == 0), stop=(j == TAPS - 1))
                            if what == "last_taps":
                                ins.then_inc(pe.steps, pe.did(f"p_run{run}"))
                        elif what == "squares":
                            e.wait_ge(pool.steps, pool.at(f"p_sq{x}"))
                            if x == 0:
                                e.wait_ge(dve.steps, dve.at("p_gc"))
                            for i in range(NT):
                                col = (x % 2) * 16 + i * 4 + x // 2
                                ins = e.matmul(few[:, col:col + 1], squares(x)[:, ts(i, C)], k.w["ones3"][:, 0:1], start=True, stop=True)
                            ins.then_inc(pe.steps, pe.did(f"p_ss{x}"))
                        elif what == "gate" and x == 2:
                            e.wait_ge(dve.steps, dve.at("p_g"))
                            e.matmul(few[:, 64:80], k.w["upto3"][:], four("g"), start=True, stop=True)
                            e.matmul(few[:, 80:96], k.w["ones3"][:], four("g"), start=True, stop=True).then_inc(pe.steps, pe.did("p_cum"))
                        elif what == "keys":
                            free(12 + x)
                            for h in range(4):
                                ins = e.transpose(run_bank(12 + x)[:, ts(h, C)], QK[:, 1, 4 * g + h, ts(x, C)], k.w["ident"][:])
                            ins.then_inc(pe.steps, pe.did(f"p_run{12 + x}"))

                    in_turn(make, invert, solve, prepare)

                @block.gpsimd
                def _(e):
                    def make(n, part):
                        u = n % 2
                        if part == 0:
                            e.wait_ge(act.steps, act.at(f"d{n}"))
                            e.tensor_tensor(D[:, u], D[:, u], k.w["upto3"][:].unsqueeze(1).to_broadcast([C, 4, C]), ALU.mult).then_inc(pool.steps, pool.did(f"d{n}"))
                        elif part == 2:
                            e.wait_ge(act.steps, act.at(f"a{n}"))
                            for l, levels in enumerate((slice(0, 1), slice(1, 5))):
                                many = levels.stop - levels.start
                                e.tensor_tensor(M[:, n % 4, levels], A32[:, n % 4].unsqueeze(1).to_broadcast([C, many, 4, 32]),
                                                k.w["joins"][:, levels].unsqueeze(2).to_broadcast([C, many, 4, 32]), ALU.mult).then_inc(pool.steps, pool.did(f"c{l}{n}"))

                    def prepare(what, x):
                        if what == "norm":
                            e.tensor_copy(xb[:], flat(k.X[:, bass.ds(pb, 1), :])).then_inc(pool.steps, pool.did("p_xb"))
                        elif what == "small":
                            e.memset(S[:, hs], 0.0).then_inc(pool.steps, pool.did())
                        elif what == "finish" and x >= 4:
                            y = x - 4
                            if y >= 4:
                                e.wait_ge(pe.steps, pe.at(f"p_ss{y - 4}"))
                            e.wait_ge(act.steps, act.at(f"p_run{x}"))
                            e.tensor_tensor(squares(y), made(x), made(x), ALU.mult).then_inc(pool.steps, pool.did(f"p_sq{y}"))

                    in_turn(make, lambda n, step, l: None, lambda n, step, j: None, prepare)

                @block.scalar
                def _(e):
                    def make(n, part):
                        u = n % 2
                        if part == 0:
                            e.wait_ge(dve.steps, dve.at(f"d{n}"))
                            e.activation(D[:, u], D[:, u], ACT.Exp).then_inc(act.steps, act.did(f"d{n}"))
                        elif part == 2:
                            e.wait_ge(dve.steps, dve.at(f"A{n}"))
                            for j in range(4):
                                e.activation(A32[ts(j, 32), n % 4], A[ts(j, 32), n % 6, :, ts(j, 32)], ACT.Copy).then_inc(act.steps, act.did(f"a{n}"))

                    def invert(n, step, l):
                        if step == "f":
                            e.wait_ge(pe.steps, pe.at(f"f{l}{n}"))
                            e.activation(F[:, n % 2], p_inv("f", n % 2), ACT.Copy).then_inc(act.steps, act.did(f"f{l}{n}"))

                    def prepare(what, x):
                        if what == "norm":
                            norm.scalar(e)
                        elif what == "finish":
                            e.wait_ge(pe.steps, pe.at(f"p_run{x}"))
                            e.activation(made(x), products(x), ACT.Silu).then_inc(act.steps, act.did(f"p_run{x}"))
                        elif what == "gate" and x == 0:
                            e.wait_ge(dve.steps, dve.at("p_negabs"))
                            e.activation(four("beta"), four("beta"), ACT.Exp, scale=-1.0).then_inc(act.steps, act.did())
                            e.activation(four("t"), four("t"), ACT.Exp).then_inc(act.steps, act.did())
                            e.wait_ge(act.steps, act.n)
                            e.activation(four("beta"), four("beta"), ACT.Ln, bias=1.0).then_inc(act.steps, act.did())
                            e.activation(four("sp"), four("t"), ACT.Ln, bias=1.0).then_inc(act.steps, act.did("p_sp"))
                            e.wait_ge(act.steps, act.n)
                            e.activation(four("beta"), four("beta"), ACT.Exp, scale=-1.0).then_inc(act.steps, act.did("p_beta"))
                        elif what == "gate" and x == 4:
                            e.wait_ge(dve.steps, dve.at("p_gc"))
                            e.activation(four("ga"), four("gc"), ACT.Exp).then_inc(act.steps, act.did())
                            e.activation(four("end"), four("end"), ACT.Exp).then_inc(act.steps, act.did())
                            e.activation(four("gtot"), four("gtot"), ACT.Exp).then_inc(act.steps, act.did())
                        elif what == "norms" and x == 1:
                            e.wait_ge(dve.steps, dve.at("p_ssq"))
                            e.activation(ssq[:, :, :, hs], ssq[:, :, :, hs], ACT.Ln).then_inc(act.steps, act.did())
                            e.wait_ge(act.steps, act.n)
                            e.activation(four("qn"), ssq[:, 0, :, hs], ACT.Exp, scale=-0.5).then_inc(act.steps, act.did())
                            e.activation(four("n2"), ssq[:, 1, :, hs], ACT.Exp, scale=-1.0).then_inc(act.steps, act.did())
                            e.activation(four("kn"), ssq[:, 1, :, hs], ACT.Exp, scale=0.5).then_inc(act.steps, act.did("p_norms"))
                        elif what == "keys":
                            e.wait_ge(pe.steps, pe.at(f"p_run{12 + x}"))
                            e.activation(KT[:, x, hs].rearrange("p h x -> p (h x)"), run_bank(12 + x), ACT.Copy).then_inc(act.steps, act.did(f"p_run{12 + x}"))

                    e.preload_act_table_set(EXP_LN)
                    in_turn(make, invert, lambda n, step, j: None, prepare)
                    if sg is not None:
                        ms = q["t"][:, :, ts(sg, 4)]
                        e.preload_act_table_set(EXP_LN)
                        e.wait_ge(dve.steps, dve.at("ms"))
                        e.activation(ms, ms, ACT.Ln).then_inc(act.steps, act.did())
                        e.wait_ge(act.steps, act.n)
                        e.activation(ms, ms, ACT.Exp, scale=-0.5).then_inc(act.steps, act.did("rms"))

                @block.vector
                def _(e):
                    wide = lambda name, i, u, w: q[name][:, i, 4 * u:4 * u + 4].unsqueeze(2).to_broadcast([C, 4, w])
                    eye32 = k.w["eye32"][:].unsqueeze(1).to_broadcast([C, 4, 32])

                    def make(n, part):
                        i, u = n // 2, n % 2
                        if part == 0:
                            e.wait_ge(pe.steps, pe.at(f"gb{n}"))
                            for h in range(4):
                                e.tensor_scalar(D[:, u, h], P[4 * u + 2][:, ts(h, C)], q["gc"][:, i, 4 * u + h:4 * u + h + 1], 0.0,
                                                ALU.subtract, ALU.min).then_inc(dve.steps, dve.did(f"d{n}"))
                        elif part == 1:
                            e.wait_ge(pe.steps, pe.at(f"kq{n}"))
                            e.wait_ge(pool.steps, pool.at(f"d{n}"))
                            e.tensor_tensor(Pm[:, n % 6], v4(P[4 * u + 2]), D[:, u], ALU.mult).then_inc(dve.steps, dve.did(f"P{n}"))
                            e.tensor_tensor(D[:, u], D[:, u], wide("gam", i, u, C), ALU.mult).then_inc(dve.steps, dve.did(f"dg{n}"))
                        else:
                            e.wait_ge(pe.steps, pe.at(f"kk{n}"))
                            e.wait_ge(dve.steps, dve.at(f"dg{n}"))
                            e.tensor_tensor(A[:, n % 6], v4(P[4 * u + 2]), D[:, u], ALU.mult).then_inc(dve.steps, dve.did(f"A{n}"))

                    def invert(n, step, l):
                        u = n % 2
                        if l == 0:
                            e.wait_ge(pe.steps, pe.at(f"x0{n}"))
                            e.tensor_tensor(X[:, u], eye32, p_inv("x", u), ALU.subtract).then_inc(dve.steps, dve.did(f"x0{n}"))
                            e.tensor_tensor(Y[:, n % 4], eye32, M[:, n % 4, 0], ALU.subtract).then_inc(dve.steps, dve.did(f"y0{n}"))
                        elif step == "x":
                            e.wait_ge(pe.steps, pe.at(f"x{l}{n}"))
                            e.tensor_tensor(X[:, u], X[:, u], p_inv("x", u), ALU.subtract).then_inc(dve.steps, dve.did(f"x{l}{n}"))
                        elif step == "y":
                            e.wait_ge(pe.steps, pe.at(f"y{l}{n}"))
                            e.tensor_tensor(Y[:, n % 4], Y[:, n % 4], p_inv("y", u), ALU.subtract).then_inc(dve.steps, dve.did(f"y{l}{n}"))

                    def solve(n, step, j):
                        i, u, rows = n // 2, n % 2, ts(j, 32)
                        s_u = S[:, ts(u, 4)]
                        if step == "state":
                            e.memset(W[:, u], 0.0).then_inc(dve.steps, dve.did())
                            e.wait_ge(pe.steps, pe.at(f"s{n}"))
                            e.tensor_tensor(rv[:, u], v4(P[4 * u + 3][:, 0:128]), wide("ga", i, u, 32), ALU.mult).then_inc(dve.steps, dve.did())
                            e.tensor_tensor(o1[:, u], v4(P[4 * u + 3][:, 128:256]), wide("ga", i, u, 32), ALU.mult).then_inc(dve.steps, dve.did())
                            e.wait_ge(dve.steps, dve.n)
                            e.tensor_tensor(rv[:, u], v4(V[:, i, ts(u, 128)]), rv[:, u], ALU.subtract).then_inc(dve.steps, dve.did(f"r0{n}"))
                            e.tensor_tensor(s_u, s_u, wide("gtot", i, u, 32), ALU.mult).then_inc(dve.steps, dve.did())
                        elif step == "before":
                            e.wait_ge(pe.steps, pe.at(f"b{j}{n}"))
                            e.tensor_tensor(rv[rows, u], rv[rows, u], p32(4 * u + 3)[rows], ALU.subtract).then_inc(dve.steps, dve.did(f"r{j}{n}"))
                        elif step == "solve":
                            e.wait_ge(pe.steps, pe.at(f"w{j}{n}"))
                            e.tensor_copy(W[rows, u], v4(P[4 * u + 3][rows, 256:384])).then_inc(dve.steps, dve.did(f"w{j}{n}"))
                            if j == 3:
                                e.wait_ge(dve.steps, dve.n)
                                e.tensor_tensor(zz[:, u], W[:, u], wide("gam", i, u, 32), ALU.mult).then_inc(dve.steps, dve.did())
                                e.wait_ge(dve.steps, dve.n)
                                e.tensor_tensor(ze[:, u], zz[:, u], wide("end", i, u, 32), ALU.mult).then_inc(dve.steps, dve.did(f"z{n}"))
                        else:
                            e.wait_ge(pe.steps, pe.at(f"o{n}"))
                            e.tensor_tensor(s_u, s_u, v4(P[4 * u + 3][:, 256:384]), ALU.add).then_inc(dve.steps, dve.did())
                            e.tensor_tensor(o1[:, u], o1[:, u], v4(P[4 * u + 3][:, 384:512]), ALU.add).then_inc(dve.steps, dve.did())
                            e.wait_ge(dve.steps, dve.n)
                            e.tensor_tensor(O[:, i, ts(u, 4)], o1[:, u], wide("qn", i, u, 32), ALU.mult).then_inc(dve.steps, dve.did(f"out{n}"))

                    def prepare(what, x):
                        if what == "norm":
                            e.tensor_copy(k.modb[:], k.mod[:, :, :, bass.ds(pb, 1)].rearrange("p l s a -> p l (s a)")).then_inc(dve.steps, dve.did())
                            e.wait_ge(dve.steps, dve.n)
                            norm.vector(e)
                        elif what == "gate" and x == 0:
                            e.wait_ge(pe.steps, pe.at("p_ab"))
                            ab = few[:, 0:64].rearrange("p (i x) -> p i x", i=NT)
                            e.tensor_tensor(four("z"), ab[:, :, hs], k.w["dt_bias"][:, hs].unsqueeze(1).to_broadcast([C, NT, 4]), ALU.add).then_inc(dve.steps, dve.did())
                            e.tensor_scalar(four("beta"), ab[:, :, 8 + 4 * g:12 + 4 * g], LEAST, None, ALU.max).then_inc(dve.steps, dve.did())
                            e.wait_ge(dve.steps, dve.n)
                            e.tensor_scalar(four("t"), four("z"), -1.0, None, ALU.mult).then_inc(dve.steps, dve.did())
                            e.wait_ge(dve.steps, dve.n)
                            e.tensor_tensor(four("t"), four("t"), four("z"), ALU.min).then_inc(dve.steps, dve.did("p_negabs"))
                            e.tensor_scalar(four("z"), four("z"), 0.0, None, ALU.max).then_inc(dve.steps, dve.did("p_z"))
                        elif what == "gate" and x == 1:
                            e.wait_ge(act.steps, act.at("p_sp"))
                            e.wait_ge(dve.steps, dve.at("p_z"))
                            e.tensor_tensor(four("g"), four("z"), four("sp"), ALU.add).then_inc(dve.steps, dve.did())
                            e.wait_ge(dve.steps, dve.n)
                            e.tensor_tensor(four("g"), four("g"), neg_a[:, hs].unsqueeze(1).to_broadcast([C, NT, 4]), ALU.mult).then_inc(dve.steps, dve.did("p_g"))
                        elif what == "gate" and x == 3:
                            e.wait_ge(pe.steps, pe.at("p_cum"))
                            sums = lambda at: few[:, at:at + 16].rearrange("p (i h) -> p i h", i=NT)
                            e.tensor_copy(four("gc"), sums(64)).then_inc(dve.steps, dve.did())
                            e.tensor_copy(four("gtot"), sums(80)).then_inc(dve.steps, dve.did())
                            e.wait_ge(dve.steps, dve.n)
                            e.tensor_tensor(four("end"), four("gtot"), four("gc"), ALU.subtract).then_inc(dve.steps, dve.did("p_gc"))
                        elif what == "norms" and x == 0:
                            e.wait_ge(pe.steps, pe.at("p_ss7"))
                            for c in range(2):
                                e.tensor_scalar(ssq[:, c, :, hs], few[:, ts(c, 16)].rearrange("p (i h) -> p i h", i=NT), 1e-12, None, ALU.max).then_inc(dve.steps, dve.did("p_ssq"))
                        elif what == "norms" and x == 2:
                            e.wait_ge(act.steps, act.at("p_norms"))
                            e.scalar_tensor_tensor(four("gam"), four("n2"), 2.0, four("beta"), ALU.mult, ALU.mult).then_inc(dve.steps, dve.did())
                            vals = V.rearrange("p i (h x) -> p i h x", h=NH)[:, :, hs]
                            e.tensor_tensor(vals, vals, four("kn").unsqueeze(3).to_broadcast([C, NT, 4, 32]), ALU.mult).then_inc(dve.steps, dve.did())

                    in_turn(make, invert, solve, prepare)
                    if sg is not None:
                        ms, og = q["t"][:, :, ts(sg, 4)], O[:, :, ts(sg, 4)]
                        gate = G.rearrange("p i (h x) -> p i h x", h=NH)[:, :, ts(sg, 4)]
                        o2 = f4(D[:, sg]).rearrange("p (i h x) -> p i h x", i=NT, h=4)
                        e.wait_ge(dve.steps, dve.n)
                        e.tensor_tensor(o2, og, og, ALU.mult).then_inc(dve.steps, dve.did())
                        e.wait_ge(dve.steps, dve.n)
                        e.tensor_reduce(ms, o2, AX.X, ALU.add).then_inc(dve.steps, dve.did())
                        e.wait_ge(dve.steps, dve.n)
                        e.tensor_scalar(ms, ms, 1.0 / 32, 1e-5, ALU.mult, ALU.add).then_inc(dve.steps, dve.did("ms"))
                        for i in range(NT):
                            e.tensor_tensor(gate[:, i], gate[:, i], k.w["o_norm_w"][:].unsqueeze(1).to_broadcast([C, 4, 32]), ALU.mult).then_inc(dve.steps, dve.did())
                        e.wait_ge(dve.steps, dve.n)
                        e.tensor_tensor(og, og, gate, ALU.mult).then_inc(dve.steps, dve.did())
                        e.wait_ge(act.steps, act.at("rms"))
                        e.wait_ge(dve.steps, dve.n)
                        e.tensor_tensor(og, og, ms.unsqueeze(3).to_broadcast([C, NT, 4, 32]), ALU.mult).then_inc(dve.steps, dve.did())
            k.end()

        def out(name, b):
            st = pe, act, dve, pool, dma = k.stage(name)
            OT = sq[:].rearrange("p a c t -> p (a c) t")
            with nc.Block() as block:
                @block.vector
                def _(e):
                    e.tensor_copy(k.modb[:], k.mod[:, :, :, bass.ds(b, 1)].rearrange("p l s a -> p l (s a)")).then_inc(dve.steps, dve.did())
                    e.wait_ge(pe.steps, pe.at("oT0"))
                    e.tensor_copy(OT[:, 0], P[0]).then_inc(dve.steps, dve.did("oT"))
                    e.wait_ge(pe.steps, pe.at("att"))
                    x = flat(k.X[:, bass.ds(b, 1), :])
                    e.scalar_tensor_tensor(x, P[2], m[:, GA:GA + 1], x, ALU.mult, ALU.add).then_inc(dve.steps, dve.did())

                @block.scalar
                def _(e):
                    e.wait_ge(pe.steps, pe.at("oT1"))
                    e.activation(OT[:, 1], P[1], ACT.Copy).then_inc(act.steps, act.did("oT"))

                @block.tensor
                def _(e):
                    for u in range(2):
                        for i in range(NT):
                            ins = e.transpose(P[u][:, ts(i, C)], O[:, i, ts(u, 4)].rearrange("p h x -> p (h x)"), k.w["ident"][:])
                        ins.then_inc(pe.steps, pe.did(f"oT{u}"))
                    for u, copied in ((0, dve), (1, act)):
                        e.wait_ge(copied.steps, copied.at("oT"))
                        ins = e.matmul(P[2], k.w["Wo3"][:, u, :], OT[:, u], start=(u == 0), stop=(u == 1))
                    ins.then_inc(pe.steps, pe.did("att"))
            k.end()

        squares = lambda x: sq[:, x % 4 // 2, x % 2]
        stage("delta_first", None, 0, 0)
        with nc.Fori(0, B - 1) as b:
            stage("delta_group0", 0, b, 1)
            stage("delta_group1", 1, b + 1, 0)
            out("delta_out", b)
        stage("delta_group0_last", 0, B - 1, 1)
        stage("delta_group1_last", 1, None, None)
        out("delta_out_last", B - 1)


def channel_mix(k):
    nc = k.nc
    with ExitStack() as s:
        lanes = lambda name, shape: [k.sb(f"c_{name}{l}", shape, stack=s) for l in range(2)]
        xb, dl, xr, xk, kk, rr = (lanes(n, [C, T]) for n in ("xb", "dl", "xr", "xk", "kk", "rr"))
        hp, tmp, modb = lanes("hp", [C, T + 1]), lanes("tmp", [C, 3, T]), lanes("modb", [C, 4, 6])
        bank = lambda l, i: k.ps[:, 4 * l + i, :]
        m = [modb[l][:, 3, :] for l in range(2)]
        with nc.Fori(0, B // 2) as pair:
            st = pe, act, dve, pool, dma = k.stage("mix")
            batch = lambda l: bass.ds(pair * 2 + l, 1)
            n = [Norm(k, st, f"n{l}", 4 * l, 4 * l + 1, xb[l][:], hp[l][:, 1:], m[l], SB_, CB, tmp[l]) for l in range(2)]
            with nc.Block() as block:
                @block.gpsimd
                def _(e):
                    for l in range(2):
                        e.tensor_copy(xb[l][:], flat(k.X[:, batch(l), :])).then_inc(pool.steps, pool.did(f"xb{l}"))
                    for l in range(2):
                        e.wait_ge(act.steps, act.at(f"k{l}"))
                        e.tensor_tensor(kk[l][:], kk[l][:], kk[l][:], ALU.mult).then_inc(pool.steps, pool.did(f"k2{l}"))

                @block.tensor
                def _(e):
                    for l in range(2):
                        e.wait_ge(pool.steps, pool.at(f"xb{l}"))
                        n[l].tensor(e)
                    for l in range(2):
                        e.wait_ge(dve.steps, dve.at(f"xr{l}"))
                        e.matmul(bank(l, 2), k.w["W_r3"][:], xr[l][:], start=True, stop=True).then_inc(pe.steps, pe.did(f"r{l}"))
                        e.wait_ge(dve.steps, dve.at(f"xk{l}"))
                        e.matmul(bank(l, 3), k.w["W_k3"][:], xk[l][:], start=True, stop=True).then_inc(pe.steps, pe.did(f"k{l}"))
                    for l in range(2):
                        e.wait_ge(pool.steps, pool.at(f"k2{l}"))
                        e.matmul(bank(l, 0), k.w["W_v3"][:], kk[l][:], start=True, stop=True).then_inc(pe.steps, pe.did(f"v{l}"))

                @block.scalar
                def _(e):
                    e.preload_act_table_set(EXP_LN)
                    for l in range(2):
                        n[l].scalar(e)
                    for l in range(2):
                        e.wait_ge(pe.steps, pe.at(f"k{l}"))
                        e.activation(kk[l][:], bank(l, 3), ACT.Relu).then_inc(act.steps, act.did(f"k{l}"))
                        e.wait_ge(dve.steps, dve.at(f"r{l}"))
                        e.activation(rr[l][:], rr[l][:], ACT.Exp, scale=-1.0).then_inc(act.steps, act.did())
                        e.wait_ge(act.steps, act.n)
                        e.activation(rr[l][:], rr[l][:], ACT.Ln, bias=1.0).then_inc(act.steps, act.did())
                        e.wait_ge(act.steps, act.n)
                        e.activation(rr[l][:], rr[l][:], ACT.Exp, scale=-1.0).then_inc(act.steps, act.did(f"r{l}"))

                @block.vector
                def _(e):
                    for l in range(2):
                        e.memset(hp[l][:, 0:1], 0.0).then_inc(dve.steps, dve.did())
                        e.tensor_copy(modb[l][:], k.mod[:, :, :, batch(l)].rearrange("p l s a -> p l (s a)")).then_inc(dve.steps, dve.did())
                    e.wait_ge(dve.steps, dve.n)
                    for l in range(2):
                        n[l].vector(e)
                        e.wait_ge(dve.steps, dve.n)
                        e.tensor_tensor(dl[l][:], hp[l][:, 1:], hp[l][:, 0:T], ALU.subtract).then_inc(dve.steps, dve.did())
                        e.wait_ge(dve.steps, dve.n)
                        for x, dst in (("xr", xr), ("xk", xk)):
                            mu = k.w["mu"][:, 0:1] if x == "xr" else k.w["mu"][:, 1:2]
                            e.scalar_tensor_tensor(dst[l][:], dl[l][:], mu, hp[l][:, 0:T], ALU.mult, ALU.add).then_inc(dve.steps, dve.did(f"{x}{l}"))
                    for l in range(2):
                        e.wait_ge(pe.steps, pe.at(f"r{l}"))
                        e.tensor_scalar(rr[l][:], bank(l, 2), LEAST, None, ALU.max).then_inc(dve.steps, dve.did(f"r{l}"))
                    for l in range(2):
                        e.wait_ge(act.steps, act.at(f"r{l}"))
                        e.wait_ge(pe.steps, pe.at(f"v{l}"))
                        e.tensor_tensor(rr[l][:], rr[l][:], bank(l, 0), ALU.mult).then_inc(dve.steps, dve.did())
                        e.wait_ge(dve.steps, dve.n)
                        e.scalar_tensor_tensor(flat(k.X[:, batch(l), :]), rr[l][:], m[l][:, GB:GB + 1], xb[l][:], ALU.mult, ALU.add).then_inc(dve.steps, dve.did())
            k.end()


def build(nc, a, counts, upto=99, first=0):
    k = Kernel(nc, counts)
    k.dram = a
    with k.stack:
        load_weights(k, a)
        if first <= 0:
            with ExitStack() as s:
                load(k, a, "layers01", s)
                wkv_mlp_prologue(k, s)
                q1 = k.sb("q1", [C, B, T], stack=s)
                k1 = k.sb("k1", [C, B, T], stack=s)
                v1 = k.sb("v1", [C, B, T], stack=s)
                qbar = k.sb("qbar", [C, B, 16], stack=s)
                kbar = k.sb("kbar", [C, B, 16], stack=s)
                idx_row = k.sb("idx_row", [1, 48], U32, stack=s)
                lg = k.sb("router_logits", [C, B, 32], stack=s)
                gates = k.sb("gates", [C, 32, 8], stack=s)
                layer0(k, q1, k1, v1, qbar, kbar)
                if upto >= 1:
                    choose_blocks(k, qbar, kbar, idx_row)
                    block_attention(k, q1, k1, v1, idx_row)
                    attention_out(k, q1, k1, lg)
                if upto >= 2:
                    route(k, lg, gates)
                    experts(k, k1, gates)
        if first <= 3 <= upto:
            with ExitStack() as s:
                load(k, a, "gla", s)
                gla(k)
        if first <= 4 <= upto:
            with ExitStack() as s:
                load(k, a, "mlp2", s)
                routed_mlp(k)
        if first <= 5 <= upto:
            with ExitStack() as s:
                load(k, a, "delta", s)
                delta_rule(k)
        if first <= 6 <= upto:
            with ExitStack() as s:
                load(k, a, "mix", s)
                channel_mix(k)
        pe, act, dve, pool, dma = k.stage("store")
        with nc.Block() as block:
            @block.sync
            def _(e):
                e.dma_start(a["out"], k.X[:]).then_inc(dma.steps, dma.did("out"))
                e.wait_ge(dma.steps, dma.at("out"))


def layouts(i):
    c = np.ascontiguousarray
    i = {n: np.asarray(v) for n, v in i.items()}
    o = {}
    o["x"] = c(i["L0_attn_x"].transpose(2, 0, 1))
    o["center"] = (np.eye(C) - 1.0 / C).astype(np.float32)
    o["mean"] = np.full((C, C), 1.0 / C, np.float32)
    o["ident"] = np.eye(C, dtype=np.float32)
    o["cT"] = c(np.stack([i[f"L{l}_c"].T for l in range(4)], 1))
    o["wmod"] = c(np.stack([i[f"L{l}_wmod"] for l in range(4)], 1))
    o["W_rvk"] = c(i["L0_attn_W_rvk"].T)
    o["W_out0"] = c(i["L0_attn_W_out"].T)
    o["decay"] = c(i["L0_attn_time_decay"][:, None])
    o["time_first"] = c(i["L0_attn_time_first"][:, None])
    two = lambda v: c(np.concatenate([v, v], 0))
    halves = lambda v: c(v.reshape(64, 8, 2).transpose(2, 0, 1).reshape(128, 8))
    o["Win0"] = c(np.concatenate([i["L0_ffn_Win"]] * 2, 1))
    o["bin_0"] = two(i["L0_ffn_bin_"][:, None])
    o["W1_0"], o["b1_0"], o["W2_0"] = halves(i["L0_ffn_W1"]), halves(i["L0_ffn_b1"]), halves(i["L0_ffn_W2"])
    o["b2_0"] = two(i["L0_ffn_b2"][:, None])
    o["Wout0"] = two(i["L0_ffn_Wout"])
    o["bout_0"] = c(i["L0_ffn_bout"][:, None])
    for n in "QKV":
        o[f"W_{n}"] = c(i[f"L1_attn_W_{n}"])
    o["W_O"] = c(i["L1_attn_W_O"])
    head = (np.arange(C)[:, None] % 32 // 8 == np.arange(4)[None]).astype(np.float32)
    o["head_mask"] = head
    o["head_scale"] = head * np.float32(1 / np.sqrt(8))
    o["w_gate1"] = c(i["L1_ffn_w_g"].T)
    o["rev8"] = np.broadcast_to(np.arange(8, 0, -1, dtype=np.float32), (C, 8)).copy()
    o["upto"] = np.triu(np.ones((C, C), np.float32))
    o["ones"] = np.ones((C, C), np.float32)
    o["c_fc"] = c(i["L1_ffn_c_fc"].transpose(1, 0, 2))
    o["c_proj"] = c(i["L1_ffn_c_proj"].reshape(8, 4, C, C).transpose(2, 0, 1, 3))
    o["W_in2"] = c(i["L2_attn_W_in"].T)
    o["b_in2"] = c(i["L2_attn_b_in"][:, None])
    wq = i["L2_attn_W_qkva"].reshape(2, 4, 32, 4, 2, C)
    bq = i["L2_attn_b_qkva"].reshape(2, 4, 32, 4, 2)
    sel = [0, 1, 3]
    o["W_qka"] = c(wq[:, :, :, sel].transpose(5, 3, 4, 0, 1, 2).reshape(C, 3, 2, 2, C))
    o["b_qka"] = c(bq[:, :, :, sel].transpose(1, 2, 3, 4, 0).reshape(C, 3, 2, 2))
    o["W_v2"] = c(wq[:, :, :, 2].transpose(4, 0, 1, 3, 2).reshape(C, 512))
    o["b_v2"] = c(np.broadcast_to(bq[:, :, :, 2].transpose(0, 1, 3, 2).reshape(1, 512), (C, 512)))
    o["W_y2"] = c(i["L2_attn_W_y"].reshape(C, 4, 2, 32, 2).transpose(2, 4, 3, 1, 0).reshape(C, 4, C))
    o["b_y2"] = c(i["L2_attn_b_y"][:, None])
    o["W_out2"] = c(i["L2_attn_W_out"].T)
    o["b_out2"] = c(i["L2_attn_b_out"][:, None])
    h0 = np.stack([i["L2_attn_h0_re"], i["L2_attn_h0_im"]], 2)
    o["h0"] = c(h0.reshape(2, 4, 32, 64).transpose(1, 2, 0, 3).reshape(C, 2, 64))
    s_, t_ = np.arange(C)[:, None] % 32, np.arange(32)[None]
    same8 = (s_ // 8 == t_ // 8) & (s_ <= t_)
    half8 = (s_ // 16 == t_ // 16) & (s_ // 8 < t_ // 8)
    o["gla_mask"] = c(np.stack([same8, half8], 1).astype(np.float32))
    o["gate_w2"] = c(i["L2_ffn_gate_w"].T)
    o["w1_2"] = c(np.stack([*i["L2_ffn_w1"], i["L2_ffn_sw1"]], 1))
    o["w2_2"] = c(np.stack([*i["L2_ffn_w2"], i["L2_ffn_sw2"]], 0).reshape(3, 4, C, C).transpose(2, 0, 1, 3))
    o["b1_2"] = c(np.stack([*i["L2_ffn_b1"], i["L2_ffn_sb1"]], 0).reshape(3, 4, C).transpose(2, 0, 1))
    o["b2_2"] = c(np.stack([*i["L2_ffn_b2"], i["L2_ffn_sb2"]], 1))
    rows = lambda v: c(np.broadcast_to(v[None], (C,) + v.shape))
    o["Wqk3"] = c(np.stack([i["L3_attn_Wq"], i["L3_attn_Wk"]], 1))
    o["conv_qk"] = c(np.stack([i["L3_attn_conv_q"].T, i["L3_attn_conv_k"].T], 0))
    o["Wv3"] = c(i["L3_attn_Wv"])
    o["conv_v"] = rows(c(i["L3_attn_conv_v"].T))
    o["Wg3"] = c(i["L3_attn_Wg"])
    o["Wab3"] = c(np.concatenate([i["L3_attn_Wa"], i["L3_attn_Wb"]], 1))
    o["Wo3"] = c(i["L3_attn_Wo"].reshape(2, C, C).transpose(1, 0, 2))
    for n in ("A_log", "dt_bias", "o_norm_w"):
        o[n] = rows(i["L3_attn_" + n])
    s_, t_ = np.arange(C)[:, None], np.arange(C)[None]
    joins = np.stack([(s_ // (2 * n) == t_ // (2 * n)) & (s_ // n < t_ // n) for n in (1, 2, 4, 8, 16)], 1)
    o["joins"] = np.tile(joins[0:32, :, 0:32].astype(np.float32), (4, 1, 1))
    o["eye32"] = np.tile(np.eye(32, dtype=np.float32), (4, 1))
    o["upto3"], o["ones3"] = o["upto"].copy(), o["ones"].copy()
    for n in "rkv":
        o[f"W_{n}3"] = c(i[f"L3_ffn_W_{n}"].T)
    o["mu"] = c(np.stack([i["L3_ffn_mu_r"], i["L3_ffn_mu_k"]], 1))
    return o


def kernel(**inputs):
    import concourse.bacc as _bacc
    from concourse.bass_utils import run_bass_kernel_spmd as _run

    counts, arrays = {}, layouts(inputs)

    def program():
        nc = _bacc.Bacc("TRN2", target_bir_lowering=False, num_devices=1)
        a = {n: nc.dram_tensor(f"in_{n}_dram", v.shape, mybir.dt.from_np(v.dtype), kind="ExternalInput").ap()
             for n, v in arrays.items()}
        a["out"] = nc.dram_tensor("out_0_dram", (C, B, T), F32, kind="ExternalOutput").ap()
        build(nc, a, counts)
        return nc

    program()
    result = _run(program(), [{f"in_{n}_dram": v for n, v in arrays.items()}], core_ids=[0])
    return np.ascontiguousarray(result.results[0]["out_0_dram"].transpose(1, 2, 0))
```
